# Optimizing a Trainium2 kernel written in Bass

```python
import numpy as np
import jax
import jax.numpy as jnp

def _softmax(x, axis=-1):
    return jax.nn.softmax(x, axis=axis)

def _gelu(x):
    return jax.nn.gelu(x, approximate=True)

def _silu(x):
    return jax.nn.silu(x)

def _sigmoid(x):
    return jax.nn.sigmoid(x)

def _layernorm(x, axis=-1, eps=1e-05):
    m = jnp.mean(x, axis=axis, keepdims=True)
    v = jnp.var(x, axis=axis, keepdims=True)
    return (x - m) / jnp.sqrt(v + eps)

def _scatter_add(tgt, idx, src, axis=0):
    return tgt.at[idx].add(src)

def _segment_sum(src, seg, n):
    return jax.ops.segment_sum(src, seg, n)
kernel_name = 'mk_hybrid_d4_jaxref_r8_189631'

def setup_inputs(seed: int=0):
    np.random.seed(seed)
    _w = jnp.asarray

    def _L0_attn_a_setup():
        import jax, jax.numpy as jnp
        import numpy as np
        B, S, D, H = (4, 256, 128, 512)
        EPS = 1e-12

        def _linear(x, W, b):
            return x @ W.T + b
        key = jax.random.key(seed)
        ks = jax.random.split(key, 14)
        s = lambda d: 1.0 / np.sqrt(d)
        return {'x': jax.random.normal(ks[0], (B, S, D), dtype=jnp.float32), 'Wq': jax.random.normal(ks[1], (D, D), dtype=jnp.float32) * s(D), 'bq': jax.random.normal(ks[2], (D,), dtype=jnp.float32) * 0.01, 'Wk': jax.random.normal(ks[3], (D, D), dtype=jnp.float32) * s(D), 'bk': jax.random.normal(ks[4], (D,), dtype=jnp.float32) * 0.01, 'Wv': jax.random.normal(ks[5], (D, D), dtype=jnp.float32) * s(D), 'bv': jax.random.normal(ks[6], (D,), dtype=jnp.float32) * 0.01, 'W1': jax.random.normal(ks[7], (D, D), dtype=jnp.float32) * s(D), 'b1': jax.random.normal(ks[8], (D,), dtype=jnp.float32) * 0.01, 'W2': jax.random.normal(ks[9], (H, D), dtype=jnp.float32) * s(D), 'b2': jax.random.normal(ks[10], (H,), dtype=jnp.float32) * 0.01, 'W3': jax.random.normal(ks[11], (D, H), dtype=jnp.float32) * s(H), 'b3': jax.random.normal(ks[12], (D,), dtype=jnp.float32) * 0.01}
    _L0_attn_a_in = _L0_attn_a_setup()

    def _L0_attn_b_setup():
        import jax, jax.numpy as jnp
        import numpy as np
        B, N, C, H, K = (4, 512, 128, 16, 2)
        D = C // H

        def _kernel(x):
            return jax.nn.silu(x) + 0.5
        key = jax.random.key(seed)
        ks = jax.random.split(key, 8)
        s = 0.02
        x = jax.random.normal(ks[0], (B, N, C), jnp.float32)
        Wq = jax.random.normal(ks[1], (C, C), jnp.float32) * s
        bq = jnp.zeros((C,), jnp.float32)
        Wk = jax.random.normal(ks[2], (K, C, C), jnp.float32) * s
        bk = jnp.zeros((K, C), jnp.float32)
        Wv = jax.random.normal(ks[3], (K, C, C), jnp.float32) * s
        bv = jnp.zeros((K, C), jnp.float32)
        Wo = jax.random.normal(ks[4], (C, C), jnp.float32) * s
        bo = jnp.zeros((C,), jnp.float32)
        ln_g = jnp.ones((C,), jnp.float32)
        ln_b = jnp.zeros((C,), jnp.float32)
        return dict(x=x, Wq=Wq, bq=bq, Wk=Wk, bk=bk, Wv=Wv, bv=bv, Wo=Wo, bo=bo, ln_g=ln_g, ln_b=ln_b)
    _L0_attn_b_in = _L0_attn_b_setup()

    def _L0_ffn_setup():
        import jax, jax.numpy as jnp
        import numpy as np
        B, S, D, E, K = (4, 256, 128, 8, 2)
        H = 4 * D
        key = jax.random.key(seed)
        k0, k1, k2, k3 = jax.random.split(key, 4)
        x = jax.random.normal(k0, (B, S, D), dtype=jnp.float32)
        router_w = jax.random.normal(k1, (E, D), dtype=jnp.float32) * 0.02
        w1 = jax.random.normal(k2, (E, H, D), dtype=jnp.float32) * 0.02
        w2 = jax.random.normal(k3, (E, D, H), dtype=jnp.float32) * 0.02
        return {'x': x, 'router_w': router_w, 'w1': w1, 'w2': w2}
    _L0_ffn_in = _L0_ffn_setup()

    def _L1_attn_a_setup():
        import jax, jax.numpy as jnp
        import numpy as np
        B, L, DM, ED, N, R, K = (2, 128, 128, 256, 16, 64, 4)
        key = jax.random.key(seed)
        ks = jax.random.split(key, 8)
        s = 0.02
        x = jax.random.normal(ks[0], (B, L, DM), jnp.float32)
        in_proj_w = jax.random.normal(ks[1], (2 * ED, DM), jnp.float32) * s
        conv_w = jax.random.normal(ks[2], (ED, 1, K), jnp.float32) * 0.3
        x_proj_w = jax.random.normal(ks[3], (R + 2 * N, ED), jnp.float32) * s
        dt_proj_w = jax.random.normal(ks[4], (ED, R), jnp.float32) * R ** (-0.5)
        dt_proj_b = jax.random.uniform(ks[5], (ED,), jnp.float32, minval=-4.6, maxval=-2.3)
        A_log = jnp.log(jnp.tile(jnp.arange(1, N + 1, dtype=jnp.float32), (ED, 1)))
        D = jnp.ones((ED,), jnp.float32)
        out_proj_w = jax.random.normal(ks[6], (DM, ED), jnp.float32) * s
        return dict(x=x, in_proj_w=in_proj_w, conv_w=conv_w, x_proj_w=x_proj_w, dt_proj_w=dt_proj_w, dt_proj_b=dt_proj_b, A_log=A_log, D=D, out_proj_w=out_proj_w)
    _L1_attn_a_in = _L1_attn_a_setup()

    def _L1_attn_b_setup():
        import jax, jax.numpy as jnp
        import numpy as np
        DIM = 128
        HEADS = 16
        HEAD_DIM = DIM // HEADS // 2
        DEPTH = 12
        LAMBDA_INIT = 0.8 - 0.6 * float(np.exp(-0.3 * DEPTH))
        EPS = 1e-05
        B, N = (2, 256)
        key = jax.random.key(seed)
        ks = jax.random.split(key, 9)
        s = 0.02
        return {'x': jax.random.normal(ks[0], (B, N, DIM), jnp.float32), 'W_qkv': jax.random.normal(ks[1], (DIM, 3 * DIM), jnp.float32) * s, 'W_proj': jax.random.normal(ks[2], (DIM, DIM), jnp.float32) * s, 'b_proj': jnp.zeros((DIM,), jnp.float32), 'lambda_q1': jax.random.normal(ks[3], (HEAD_DIM,), jnp.float32) * 0.1, 'lambda_k1': jax.random.normal(ks[4], (HEAD_DIM,), jnp.float32) * 0.1, 'lambda_q2': jax.random.normal(ks[5], (HEAD_DIM,), jnp.float32) * 0.1, 'lambda_k2': jax.random.normal(ks[6], (HEAD_DIM,), jnp.float32) * 0.1, 'subln_w': jnp.ones((2 * HEAD_DIM,), jnp.float32)}
    _L1_attn_b_in = _L1_attn_b_setup()

    def _L1_ffn_setup():
        import jax, jax.numpy as jnp
        import numpy as np
        key = jax.random.key(seed)
        k0, k1, k2, k3 = jax.random.split(key, 4)
        B, S, D, F, E = (8, 256, 128, 256, 8)
        x = jax.random.normal(k0, (B, S, D), dtype=jnp.float32)
        Wg = jax.random.normal(k1, (D, E), dtype=jnp.float32) * 0.02
        W1 = jax.random.normal(k2, (E, D, F), dtype=jnp.float32) * 0.02
        W2 = jax.random.normal(k3, (E, F, D), dtype=jnp.float32) * 0.02
        return {'x': x, 'Wg': Wg, 'W1': W1, 'W2': W2}
    _L1_ffn_in = _L1_ffn_setup()

    def _L2_attn_a_setup():
        import jax, jax.numpy as jnp
        import numpy as np
        B_SZ, SEQ, D_MODEL = (2, 256, 128)
        D_STATE, EXPAND = (16, 2)
        D_INNER = D_MODEL * EXPAND
        A_FLOOR = 0.0001
        RMS_EPS = float(np.finfo(np.float32).eps)

        def _rmsnorm(v, w):
            return v * jax.lax.rsqrt(jnp.mean(v * v, axis=-1, keepdims=True) + RMS_EPS) * w

        def _rope(v, cos_a, sin_a):
            ve, vo = (v[..., ::2], v[..., 1::2])
            re = ve * cos_a - vo * sin_a
            ro = ve * sin_a + vo * cos_a
            return jnp.stack([re, ro], axis=-1).reshape(v.shape)
        key = jax.random.key(seed)
        ks = jax.random.split(key, 6)
        x = jax.random.normal(ks[0], (B_SZ, SEQ, D_MODEL), dtype=jnp.float32)
        W_in = jax.random.normal(ks[1], (2 * D_INNER, D_MODEL), dtype=jnp.float32) * 0.02
        W_x = jax.random.normal(ks[2], (2 * D_STATE + 2, D_INNER), dtype=jnp.float32) * 0.02
        W_dt = jax.random.normal(ks[3], (D_INNER, 1), dtype=jnp.float32) * 0.1
        b_dt = jnp.zeros((D_INNER,), dtype=jnp.float32)
        A_log = jnp.broadcast_to(jnp.log(jnp.arange(1, D_STATE + 1, dtype=jnp.float32)), (D_INNER, D_STATE))
        B_bias = jnp.ones((D_STATE,), dtype=jnp.float32)
        C_bias = jnp.ones((D_STATE,), dtype=jnp.float32)
        B_norm_w = jnp.ones((D_STATE,), dtype=jnp.float32)
        C_norm_w = jnp.ones((D_STATE,), dtype=jnp.float32)
        rope_freqs = jax.random.normal(ks[4], (D_STATE // 2,), dtype=jnp.float32) * 0.01
        D = jnp.ones((D_INNER,), dtype=jnp.float32)
        W_out = jax.random.normal(ks[5], (D_MODEL, D_INNER), dtype=jnp.float32) * 0.02
        return {'x': x, 'W_in': W_in, 'W_x': W_x, 'W_dt': W_dt, 'b_dt': b_dt, 'A_log': A_log, 'B_bias': B_bias, 'C_bias': C_bias, 'B_norm_w': B_norm_w, 'C_norm_w': C_norm_w, 'rope_freqs': rope_freqs, 'D': D, 'W_out': W_out}
    _L2_attn_a_in = _L2_attn_a_setup()

    def _L2_attn_b_setup():
        import jax, jax.numpy as jnp
        import numpy as np
        H = 8
        ROPE_DIM = 64
        GAMMA = 0.96875
        GROUPS = 16
        EPS = 1e-05

        def _rope(x, offset=0):
            T = x.shape[-2]
            inv_freq = 1.0 / 10000.0 ** (np.arange(0, ROPE_DIM, 2, dtype=np.float32) / ROPE_DIM)
            t = jnp.arange(T, dtype=jnp.float32) + offset
            freqs = t[:, None] * inv_freq[None, :]
            freqs = jnp.repeat(freqs, 2, axis=-1)
            cos, sin = (jnp.cos(freqs), jnp.sin(freqs))
            xr, xp = (x[..., :ROPE_DIM], x[..., ROPE_DIM:])
            x1, x2 = (xr[..., 0::2], xr[..., 1::2])
            rot = jnp.stack([-x2, x1], axis=-1).reshape(xr.shape)
            return jnp.concatenate([xr * cos + rot * sin, xp], axis=-1)

        def _to_scores(X, W):
            B, T, C = X.shape
            return (X @ W).reshape(B, T, H, C).transpose(0, 2, 1, 3)
        key = jax.random.key(seed)
        ks = jax.random.split(key, 4)
        B, T, C = (1, 256, 128)
        return {'X_Q': jax.random.normal(ks[0], (B, T, C), jnp.float32), 'W_Q': jax.random.normal(ks[1], (C, C * H), jnp.float32) / C, 'W_K': jax.random.normal(ks[2], (C, C * H), jnp.float32) / C, 'W_V': jax.random.normal(ks[3], (C, C * H), jnp.float32) / C, 'gn_weight': jnp.ones((C,), jnp.float32), 'gn_bias': jnp.zeros((C,), jnp.float32)}
    _L2_attn_b_in = _L2_attn_b_setup()

    def _L2_ffn_setup():
        import jax, jax.numpy as jnp
        import numpy as np
        D_MODEL = 128
        NUM_TILES = 64
        TPC = 8
        NUM_CLUSTERS = NUM_TILES // TPC
        GRID = 16
        COMP_H = 32
        NUM_KNOTS = 8
        EPS_LN = 1e-05

        def _calibrate(scores, knots, temperature):
            K = knots.shape[0]
            normalized = jax.nn.sigmoid(scores / (temperature[0] + 1e-06))
            idx_float = normalized * (K - 1)
            idx_low = jnp.clip(idx_float.astype(jnp.int32), 0, K - 2)
            idx_high = idx_low + 1
            t = idx_float - idx_low.astype(scores.dtype)
            val_low = knots[idx_low]
            val_high = knots[idx_high]
            return val_low + t * (val_high - val_low)

        def _forward(x, signatures_raw, knot_values, temperature, compress_w1, compress_b1, compress_w2, compress_b2, spline_w1, spline_b1, spline_w2, spline_b2, directions, norm_gamma, norm_beta, output_scale):
            B, T, D = x.shape
            xf = x.reshape(-1, D)
            q = jnp.where(signatures_raw > 0.3, 1.0, jnp.where(signatures_raw < -0.3, -1.0, 0.0)).astype(signatures_raw.dtype)
            sigs = signatures_raw + jax.lax.stop_gradient(q - signatures_raw)
            cluster_sigs = jnp.sign(sigs.reshape(NUM_CLUSTERS, TPC, D).mean(axis=1))
            cluster_scores = xf @ cluster_sigs.T
            cluster_gates = _calibrate(cluster_scores, knot_values, temperature)
            cluster_idx = jnp.argmax(cluster_gates, axis=-1)
            tile_scores = xf @ sigs.T
            tile_gates = _calibrate(tile_scores, knot_values, temperature)
            gates_by_cluster = tile_gates.reshape(-1, NUM_CLUSTERS, TPC)
            sel_gates = jnp.take_along_axis(gates_by_cluster, cluster_idx[:, None, None], axis=1)[:, 0, :]
            local_idx = jnp.argmax(sel_gates, axis=-1)
            tile_idx = cluster_idx * TPC + local_idx
            h = jax.nn.gelu(xf @ compress_w1 + compress_b1, approximate=False)
            comp = jnp.tanh(h @ compress_w2 + compress_b2)
            w1 = spline_w1[tile_idx]
            b1 = spline_b1[tile_idx]
            hh = jax.nn.relu(jnp.einsum('ni,nig->ng', comp, w1) + b1)
            w2 = spline_w2[tile_idx]
            b2 = spline_b2[tile_idx]
            mag = jnp.einsum('ng,ngo->no', hh, w2) + b2
            ffn_out = mag * directions[tile_idx] * output_scale[0]
            y = xf + ffn_out
            mu = y.mean(axis=-1, keepdims=True)
            var = ((y - mu) ** 2).mean(axis=-1, keepdims=True)
            y = (y - mu) / jnp.sqrt(var + EPS_LN) * norm_gamma + norm_beta
            return y.reshape(B, T, D)
        key = jax.random.key(seed)
        ks = jax.random.split(key, 12)
        B, T = (4, 512)
        x = jax.random.normal(ks[0], (B, T, D_MODEL), dtype=jnp.float32)
        signatures_raw = jax.random.normal(ks[1], (NUM_TILES, D_MODEL), dtype=jnp.float32) * 0.5
        knot_values = jax.nn.sigmoid(jnp.linspace(-3.0, 3.0, NUM_KNOTS).astype(jnp.float32))
        temperature = jnp.ones((1,), dtype=jnp.float32)
        compress_w1 = jax.random.normal(ks[2], (D_MODEL, COMP_H), dtype=jnp.float32) * (1.0 / np.sqrt(D_MODEL))
        compress_b1 = jnp.zeros((COMP_H,), dtype=jnp.float32)
        compress_w2 = jax.random.normal(ks[3], (COMP_H, 2), dtype=jnp.float32) * (1.0 / np.sqrt(COMP_H))
        compress_b2 = jnp.zeros((2,), dtype=jnp.float32)
        spline_w1 = jax.random.normal(ks[4], (NUM_TILES, 2, GRID), dtype=jnp.float32) * (1.0 / np.sqrt(2.0))
        spline_b1 = jnp.zeros((NUM_TILES, GRID), dtype=jnp.float32)
        spline_w2 = jax.random.normal(ks[5], (NUM_TILES, GRID, 1), dtype=jnp.float32) * (1.0 / np.sqrt(GRID))
        spline_b2 = jnp.zeros((NUM_TILES, 1), dtype=jnp.float32)
        directions = jax.random.normal(ks[6], (NUM_TILES, D_MODEL), dtype=jnp.float32) * 0.02
        norm_gamma = jnp.ones((D_MODEL,), dtype=jnp.float32)
        norm_beta = jnp.zeros((D_MODEL,), dtype=jnp.float32)
        output_scale = jnp.ones((1,), dtype=jnp.float32) * 0.1
        return dict(x=x, signatures_raw=signatures_raw, knot_values=knot_values, temperature=temperature, compress_w1=compress_w1, compress_b1=compress_b1, compress_w2=compress_w2, compress_b2=compress_b2, spline_w1=spline_w1, spline_b1=spline_b1, spline_w2=spline_w2, spline_b2=spline_b2, directions=directions, norm_gamma=norm_gamma, norm_beta=norm_beta, output_scale=output_scale)
    _L2_ffn_in = _L2_ffn_setup()

    def _L3_attn_a_setup():
        import jax, jax.numpy as jnp
        import numpy as np
        DIM = 128
        NUM_HEADS = 16
        HEAD_DIM = DIM // NUM_HEADS
        WINDOW = 32
        SCALE = HEAD_DIM ** (-0.5)
        key = jax.random.key(seed)
        ks = jax.random.split(key, 5)
        B, L = (4, 512)
        x = jax.random.normal(ks[0], (B, L, DIM), dtype=jnp.float32)
        q_w = jax.random.normal(ks[1], (DIM, DIM), dtype=jnp.float32) * DIM ** (-0.5)
        kv_w = jax.random.normal(ks[2], (2 * HEAD_DIM, DIM), dtype=jnp.float32) * DIM ** (-0.5)
        proj_w = jax.random.normal(ks[3], (DIM, DIM), dtype=jnp.float32) * DIM ** (-0.5)
        proj_b = jax.random.normal(ks[4], (DIM,), dtype=jnp.float32) * 0.01
        return {'x': x, 'q_w': q_w, 'kv_w': kv_w, 'proj_w': proj_w, 'proj_b': proj_b}
    _L3_attn_a_in = _L3_attn_a_setup()

    def _L3_attn_b_setup():
        import math
        import jax, jax.numpy as jnp
        import numpy as np
        H = 128
        NH = 16
        HD = H // NH
        FF = 512
        EPS = 1e-12

        def _lin(key, fan_in, fan_out):
            k1, k2 = jax.random.split(key)
            bound = 1.0 / math.sqrt(fan_in)
            W = jax.random.uniform(k1, (fan_in, fan_out), jnp.float32, -bound, bound)
            b = jax.random.uniform(k2, (fan_out,), jnp.float32, -bound, bound)
            return (W, b)

        def _layernorm(x, g, b):
            mu = jnp.mean(x, axis=-1, keepdims=True)
            var = jnp.mean((x - mu) ** 2, axis=-1, keepdims=True)
            return (x - mu) * jax.lax.rsqrt(var + EPS) * g + b

        def _gelu(x):
            return x * 0.5 * (1.0 + jax.lax.erf(x / jnp.sqrt(jnp.float32(2.0))))
        key = jax.random.key(seed)
        ks = jax.random.split(key, 8)
        x = jax.random.normal(ks[0], (4, 512, H), jnp.float32)
        Wq, bq = _lin(ks[1], H, H)
        Wk, bk = _lin(ks[2], H, H)
        Wv, bv = _lin(ks[3], H, H)
        Wo, bo = _lin(ks[4], H, H)
        W1, b1 = _lin(ks[5], H, FF)
        W2, b2 = _lin(ks[6], FF, H)
        g1 = jnp.ones((H,), jnp.float32)
        be1 = jnp.zeros((H,), jnp.float32)
        g2 = jnp.ones((H,), jnp.float32)
        be2 = jnp.zeros((H,), jnp.float32)
        return dict(x=x, Wq=Wq, bq=bq, Wk=Wk, bk=bk, Wv=Wv, bv=bv, Wo=Wo, bo=bo, g1=g1, be1=be1, W1=W1, b1=b1, W2=W2, b2=b2, g2=g2, be2=be2)
    _L3_attn_b_in = _L3_attn_b_setup()

    def _L3_ffn_setup():
        import jax, jax.numpy as jnp
        import numpy as np
        DIM = 128
        HIDDEN = 512
        N_EXPERTS = 8
        K = 2
        TEMP = 1.0

        def _expert_ffn(xf, wa, ba, wb, bb):
            h = xf @ wa.T + ba
            h1, h2 = jnp.split(h, 2, axis=-1)
            h = jax.nn.silu(h1) * h2
            return h @ wb.T + bb
        key = jax.random.key(seed)
        ks = jax.random.split(key, 7)
        s = 0.02
        x = jax.random.normal(ks[0], (4, 256, DIM), dtype=jnp.float32)
        router_w = jax.random.normal(ks[1], (N_EXPERTS, DIM), dtype=jnp.float32) * s
        router_b = jnp.zeros((N_EXPERTS,), dtype=jnp.float32)
        w1 = jax.random.normal(ks[2], (N_EXPERTS, 2 * HIDDEN, DIM), dtype=jnp.float32) * s
        b1 = jnp.zeros((N_EXPERTS, 2 * HIDDEN), dtype=jnp.float32)
        w2 = jax.random.normal(ks[3], (N_EXPERTS, DIM, HIDDEN), dtype=jnp.float32) * s
        b2 = jnp.zeros((N_EXPERTS, DIM), dtype=jnp.float32)
        return {'x': x, 'router_w': router_w, 'router_b': router_b, 'w1': w1, 'b1': b1, 'w2': w2, 'b2': b2}
    _L3_ffn_in = _L3_ffn_setup()
    _d = {'L0_attn_a_x': _L0_attn_a_in['x'], 'L0_attn_a_Wq': _L0_attn_a_in['Wq'], 'L0_attn_a_bq': _L0_attn_a_in['bq'], 'L0_attn_a_Wk': _L0_attn_a_in['Wk'], 'L0_attn_a_bk': _L0_attn_a_in['bk'], 'L0_attn_a_Wv': _L0_attn_a_in['Wv'], 'L0_attn_a_bv': _L0_attn_a_in['bv'], 'L0_attn_a_W1': _L0_attn_a_in['W1'], 'L0_attn_a_b1': _L0_attn_a_in['b1'], 'L0_attn_a_W2': _L0_attn_a_in['W2'], 'L0_attn_a_b2': _L0_attn_a_in['b2'], 'L0_attn_a_W3': _L0_attn_a_in['W3'], 'L0_attn_a_b3': _L0_attn_a_in['b3'], 'L0_attn_b_Wq': _L0_attn_b_in['Wq'], 'L0_attn_b_bq': _L0_attn_b_in['bq'], 'L0_attn_b_Wk': _L0_attn_b_in['Wk'], 'L0_attn_b_bk': _L0_attn_b_in['bk'], 'L0_attn_b_Wv': _L0_attn_b_in['Wv'], 'L0_attn_b_bv': _L0_attn_b_in['bv'], 'L0_attn_b_Wo': _L0_attn_b_in['Wo'], 'L0_attn_b_bo': _L0_attn_b_in['bo'], 'L0_attn_b_ln_g': _L0_attn_b_in['ln_g'], 'L0_attn_b_ln_b': _L0_attn_b_in['ln_b'], 'L0_ffn_router_w': _L0_ffn_in['router_w'], 'L0_ffn_w1': _L0_ffn_in['w1'], 'L0_ffn_w2': _L0_ffn_in['w2'], 'L1_attn_a_in_proj_w': _L1_attn_a_in['in_proj_w'], 'L1_attn_a_conv_w': _L1_attn_a_in['conv_w'], 'L1_attn_a_x_proj_w': _L1_attn_a_in['x_proj_w'], 'L1_attn_a_dt_proj_w': _L1_attn_a_in['dt_proj_w'], 'L1_attn_a_dt_proj_b': _L1_attn_a_in['dt_proj_b'], 'L1_attn_a_A_log': _L1_attn_a_in['A_log'], 'L1_attn_a_D': _L1_attn_a_in['D'], 'L1_attn_a_out_proj_w': _L1_attn_a_in['out_proj_w'], 'L1_attn_b_W_qkv': _L1_attn_b_in['W_qkv'], 'L1_attn_b_W_proj': _L1_attn_b_in['W_proj'], 'L1_attn_b_b_proj': _L1_attn_b_in['b_proj'], 'L1_attn_b_lambda_q1': _L1_attn_b_in['lambda_q1'], 'L1_attn_b_lambda_k1': _L1_attn_b_in['lambda_k1'], 'L1_attn_b_lambda_q2': _L1_attn_b_in['lambda_q2'], 'L1_attn_b_lambda_k2': _L1_attn_b_in['lambda_k2'], 'L1_attn_b_subln_w': _L1_attn_b_in['subln_w'], 'L1_ffn_Wg': _L1_ffn_in['Wg'], 'L1_ffn_W1': _L1_ffn_in['W1'], 'L1_ffn_W2': _L1_ffn_in['W2'], 'L2_attn_a_W_in': _L2_attn_a_in['W_in'], 'L2_attn_a_W_x': _L2_attn_a_in['W_x'], 'L2_attn_a_W_dt': _L2_attn_a_in['W_dt'], 'L2_attn_a_b_dt': _L2_attn_a_in['b_dt'], 'L2_attn_a_A_log': _L2_attn_a_in['A_log'], 'L2_attn_a_B_bias': _L2_attn_a_in['B_bias'], 'L2_attn_a_C_bias': _L2_attn_a_in['C_bias'], 'L2_attn_a_B_norm_w': _L2_attn_a_in['B_norm_w'], 'L2_attn_a_C_norm_w': _L2_attn_a_in['C_norm_w'], 'L2_attn_a_rope_freqs': _L2_attn_a_in['rope_freqs'], 'L2_attn_a_D': _L2_attn_a_in['D'], 'L2_attn_a_W_out': _L2_attn_a_in['W_out'], 'L2_attn_b_W_Q': _L2_attn_b_in['W_Q'], 'L2_attn_b_W_K': _L2_attn_b_in['W_K'], 'L2_attn_b_W_V': _L2_attn_b_in['W_V'], 'L2_attn_b_gn_weight': _L2_attn_b_in['gn_weight'], 'L2_attn_b_gn_bias': _L2_attn_b_in['gn_bias'], 'L2_ffn_signatures_raw': _L2_ffn_in['signatures_raw'], 'L2_ffn_knot_values': _L2_ffn_in['knot_values'], 'L2_ffn_temperature': _L2_ffn_in['temperature'], 'L2_ffn_compress_w1': _L2_ffn_in['compress_w1'], 'L2_ffn_compress_b1': _L2_ffn_in['compress_b1'], 'L2_ffn_compress_w2': _L2_ffn_in['compress_w2'], 'L2_ffn_compress_b2': _L2_ffn_in['compress_b2'], 'L2_ffn_spline_w1': _L2_ffn_in['spline_w1'], 'L2_ffn_spline_b1': _L2_ffn_in['spline_b1'], 'L2_ffn_spline_w2': _L2_ffn_in['spline_w2'], 'L2_ffn_spline_b2': _L2_ffn_in['spline_b2'], 'L2_ffn_directions': _L2_ffn_in['directions'], 'L2_ffn_norm_gamma': _L2_ffn_in['norm_gamma'], 'L2_ffn_norm_beta': _L2_ffn_in['norm_beta'], 'L2_ffn_output_scale': _L2_ffn_in['output_scale'], 'L3_attn_a_q_w': _L3_attn_a_in['q_w'], 'L3_attn_a_kv_w': _L3_attn_a_in['kv_w'], 'L3_attn_a_proj_w': _L3_attn_a_in['proj_w'], 'L3_attn_a_proj_b': _L3_attn_a_in['proj_b'], 'L3_attn_b_Wq': _L3_attn_b_in['Wq'], 'L3_attn_b_bq': _L3_attn_b_in['bq'], 'L3_attn_b_Wk': _L3_attn_b_in['Wk'], 'L3_attn_b_bk': _L3_attn_b_in['bk'], 'L3_attn_b_Wv': _L3_attn_b_in['Wv'], 'L3_attn_b_bv': _L3_attn_b_in['bv'], 'L3_attn_b_Wo': _L3_attn_b_in['Wo'], 'L3_attn_b_bo': _L3_attn_b_in['bo'], 'L3_attn_b_g1': _L3_attn_b_in['g1'], 'L3_attn_b_be1': _L3_attn_b_in['be1'], 'L3_attn_b_W1': _L3_attn_b_in['W1'], 'L3_attn_b_b1': _L3_attn_b_in['b1'], 'L3_attn_b_W2': _L3_attn_b_in['W2'], 'L3_attn_b_b2': _L3_attn_b_in['b2'], 'L3_attn_b_g2': _L3_attn_b_in['g2'], 'L3_attn_b_be2': _L3_attn_b_in['be2'], 'L3_ffn_router_w': _L3_ffn_in['router_w'], 'L3_ffn_router_b': _L3_ffn_in['router_b'], 'L3_ffn_w1': _L3_ffn_in['w1'], 'L3_ffn_b1': _L3_ffn_in['b1'], 'L3_ffn_w2': _L3_ffn_in['w2'], 'L3_ffn_b2': _L3_ffn_in['b2']}
    _x0 = _d['L0_attn_a_x']
    _d['L0_attn_a_x'] = jax.random.normal(jax.random.fold_in(jax.random.key(seed), 1), (16, 256, 128), dtype=_x0.dtype)
    del _x0
    return _d

def reference(L0_attn_a_x, L0_attn_a_Wq, L0_attn_a_bq, L0_attn_a_Wk, L0_attn_a_bk, L0_attn_a_Wv, L0_attn_a_bv, L0_attn_a_W1, L0_attn_a_b1, L0_attn_a_W2, L0_attn_a_b2, L0_attn_a_W3, L0_attn_a_b3, L0_attn_b_Wq, L0_attn_b_bq, L0_attn_b_Wk, L0_attn_b_bk, L0_attn_b_Wv, L0_attn_b_bv, L0_attn_b_Wo, L0_attn_b_bo, L0_attn_b_ln_g, L0_attn_b_ln_b, L0_ffn_router_w, L0_ffn_w1, L0_ffn_w2, L1_attn_a_in_proj_w, L1_attn_a_conv_w, L1_attn_a_x_proj_w, L1_attn_a_dt_proj_w, L1_attn_a_dt_proj_b, L1_attn_a_A_log, L1_attn_a_D, L1_attn_a_out_proj_w, L1_attn_b_W_qkv, L1_attn_b_W_proj, L1_attn_b_b_proj, L1_attn_b_lambda_q1, L1_attn_b_lambda_k1, L1_attn_b_lambda_q2, L1_attn_b_lambda_k2, L1_attn_b_subln_w, L1_ffn_Wg, L1_ffn_W1, L1_ffn_W2, L2_attn_a_W_in, L2_attn_a_W_x, L2_attn_a_W_dt, L2_attn_a_b_dt, L2_attn_a_A_log, L2_attn_a_B_bias, L2_attn_a_C_bias, L2_attn_a_B_norm_w, L2_attn_a_C_norm_w, L2_attn_a_rope_freqs, L2_attn_a_D, L2_attn_a_W_out, L2_attn_b_W_Q, L2_attn_b_W_K, L2_attn_b_W_V, L2_attn_b_gn_weight, L2_attn_b_gn_bias, L2_ffn_signatures_raw, L2_ffn_knot_values, L2_ffn_temperature, L2_ffn_compress_w1, L2_ffn_compress_b1, L2_ffn_compress_w2, L2_ffn_compress_b2, L2_ffn_spline_w1, L2_ffn_spline_b1, L2_ffn_spline_w2, L2_ffn_spline_b2, L2_ffn_directions, L2_ffn_norm_gamma, L2_ffn_norm_beta, L2_ffn_output_scale, L3_attn_a_q_w, L3_attn_a_kv_w, L3_attn_a_proj_w, L3_attn_a_proj_b, L3_attn_b_Wq, L3_attn_b_bq, L3_attn_b_Wk, L3_attn_b_bk, L3_attn_b_Wv, L3_attn_b_bv, L3_attn_b_Wo, L3_attn_b_bo, L3_attn_b_g1, L3_attn_b_be1, L3_attn_b_W1, L3_attn_b_b1, L3_attn_b_W2, L3_attn_b_b2, L3_attn_b_g2, L3_attn_b_be2, L3_ffn_router_w, L3_ffn_router_b, L3_ffn_w1, L3_ffn_b1, L3_ffn_w2, L3_ffn_b2):

    def _L0_attn_a_ref(x, Wq, bq, Wk, bk, Wv, bv, W1, b1, W2, b2, W3, b3):
        import jax, jax.numpy as jnp
        import numpy as np
        B, S, D, H = (4, 256, 128, 512)
        EPS = 1e-12

        def _linear(x, W, b):
            return x @ W.T + b
        Q = _linear(x, Wq, bq)
        K = _linear(x, Wk, bk)
        V = _linear(x, Wv, bv)
        Q = Q / jnp.maximum(jnp.linalg.norm(Q, axis=2, keepdims=True), EPS)
        K = K / jnp.maximum(jnp.linalg.norm(K, axis=2, keepdims=True), EPS)
        sim = jnp.einsum('bqd,bkd->bqk', Q, K)
        attn = jax.nn.softmax(sim, axis=2)
        out = jnp.einsum('bqk,bkd->bqd', attn, V)
        h = jax.nn.relu(_linear(out, W1, b1))
        h = jax.nn.relu(_linear(h, W2, b2))
        return _linear(h, W3, b3)

    def _L0_attn_b_ref(x, Wq, bq, Wk, bk, Wv, bv, Wo, bo, ln_g, ln_b):
        import jax, jax.numpy as jnp
        import numpy as np
        B, N, C, H, K = (4, 512, 128, 16, 2)
        D = C // H

        def _kernel(x):
            return jax.nn.silu(x) + 0.5
        dtype = x.dtype
        Bn, Nn, Cn = x.shape
        q = x + x @ Wq.T + bq
        ks = x[None] + jnp.einsum('bnc,kdc->kbnd', x, Wk) + bk[:, None, None, :]
        vs = x[None] + jnp.einsum('bnc,kdc->kbnd', x, Wv) + bv[:, None, None, :]
        q = q.reshape(Bn, Nn, H, D).transpose(0, 2, 1, 3)
        ks = ks.reshape(K, Bn, Nn, H, D).transpose(0, 1, 3, 2, 4)
        vs = vs.reshape(K, Bn, Nn, H, D).transpose(0, 1, 3, 2, 4)
        q = _kernel(q)
        ks = _kernel(ks)
        q = q / (jnp.linalg.norm(q, axis=-1, keepdims=True) + 1e-06)
        ks = ks / (jnp.linalg.norm(ks, axis=-1, keepdims=True) + 1e-06)
        scale = Nn ** (-0.5)
        ks = ks.astype(jnp.float32) * scale
        vs = vs.astype(jnp.float32) * scale
        states = jnp.einsum('kbhnd,kbhne->kbhde', ks, vs)
        state = jnp.prod(states, axis=0)
        out = jnp.einsum('bhnd,bhde->bhne', q.astype(jnp.float32), state)
        out = out.astype(dtype)
        out = out.transpose(0, 2, 1, 3).reshape(Bn, Nn, Cn)
        mu = out.mean(axis=-1, keepdims=True)
        var = out.var(axis=-1, keepdims=True)
        out = (out - mu) * jax.lax.rsqrt(var + 1e-05) * ln_g + ln_b
        out = out @ Wo.T + bo
        return out

    def _L0_ffn_ref(x, router_w, w1, w2):
        import jax, jax.numpy as jnp
        import numpy as np
        B, S, D, E, K = (4, 256, 128, 8, 2)
        H = 4 * D
        b, s, d = x.shape
        e = router_w.shape[0]
        logits = jnp.einsum('bsd,ed->bse', x, router_w)
        probs = jax.nn.softmax(logits, axis=-1)
        topk_vals, topk_idx = jax.lax.top_k(probs, K)
        x_flat = x.reshape(b * s, d)
        vals = topk_vals.reshape(b * s, K)
        idx = topk_idx.reshape(b * s, K)
        out = jnp.zeros_like(x_flat)
        for eid in range(e):
            w = jnp.sum(jnp.where(idx == eid, vals, jnp.zeros((), x.dtype)), axis=-1)
            h = jax.nn.gelu(x_flat @ w1[eid].T, approximate=False)
            y = h @ w2[eid].T
            out = out + w[:, None] * y
        return out.reshape(b, s, d)

    def _L1_attn_a_ref(x, in_proj_w, conv_w, x_proj_w, dt_proj_w, dt_proj_b, A_log, D, out_proj_w):
        import jax, jax.numpy as jnp
        import numpy as np
        B, L, DM, ED, N, R, K = (2, 128, 128, 256, 16, 64, 4)
        xz = jnp.einsum('bld,ed->ble', x, in_proj_w)
        xp, z = (xz[..., :ED], xz[..., ED:])
        xc = jax.lax.conv_general_dilated(xp.transpose(0, 2, 1), conv_w, window_strides=(1,), padding=[(K - 1, 0)], feature_group_count=ED, dimension_numbers=('NCH', 'OIH', 'NCH'))
        xc = jax.nn.silu(xc.transpose(0, 2, 1))
        dBC = jnp.einsum('ble,fe->blf', xc, x_proj_w)
        dt, Bm, Cm = (dBC[..., :R], dBC[..., R:R + N], dBC[..., R + N:])
        delta = jax.nn.softplus(jnp.einsum('blr,er->ble', dt, dt_proj_w) + dt_proj_b)
        A = -jnp.exp(A_log)
        dA = jnp.exp(delta[..., None] * A)
        BX = delta[..., None] * Bm[:, :, None, :] * xc[..., None]

        def comb(c1, c2):
            a1, b1 = c1
            a2, b2 = c2
            return (a1 * a2, b1 * a2 + b2)
        _, hs = jax.lax.associative_scan(comb, (dA, BX), axis=1)
        y = jnp.einsum('blen,bln->ble', hs, Cm) + D * xc
        out = jnp.einsum('ble,de->bld', y * jax.nn.silu(z), out_proj_w)
        return out

    def _L1_attn_b_ref(x, W_qkv, W_proj, b_proj, lambda_q1, lambda_k1, lambda_q2, lambda_k2, subln_w):
        import jax, jax.numpy as jnp
        import numpy as np
        DIM = 128
        HEADS = 16
        HEAD_DIM = DIM // HEADS // 2
        DEPTH = 12
        LAMBDA_INIT = 0.8 - 0.6 * float(np.exp(-0.3 * DEPTH))
        EPS = 1e-05
        B, N = (2, 256)
        Bm, Nm, C = x.shape
        H, hd = (HEADS, HEAD_DIM)
        scale = hd ** (-0.5)
        qkv = (x @ W_qkv).reshape(Bm, Nm, 3, H, 2 * hd)
        q, k, v = (qkv[:, :, 0], qkv[:, :, 1], qkv[:, :, 2])
        q = q.reshape(Bm, Nm, 2 * H, hd).transpose(0, 2, 1, 3)
        k = k.reshape(Bm, Nm, 2 * H, hd).transpose(0, 2, 1, 3)
        v = v.transpose(0, 2, 1, 3)
        q1, q2 = (q[:, :H], q[:, H:])
        k1, k2 = (k[:, :H], k[:, H:])

        def sdpa(qh, kh):
            scores = jnp.einsum('bhqd,bhkd->bhqk', qh, kh) * scale
            a = jax.nn.softmax(scores, axis=-1)
            return jnp.einsum('bhqk,bhkd->bhqd', a, v)
        attn1 = sdpa(q1, k1)
        attn2 = sdpa(q2, k2)
        lam1 = jnp.exp(jnp.sum(lambda_q1 * lambda_k1))
        lam2 = jnp.exp(jnp.sum(lambda_q2 * lambda_k2))
        lam = lam1 - lam2 + LAMBDA_INIT
        o = attn1 - lam * attn2
        o = o * jax.lax.rsqrt(jnp.mean(o * o, axis=-1, keepdims=True) + EPS)
        o = o * subln_w
        o = o * (1.0 - LAMBDA_INIT)
        o = o.transpose(0, 2, 1, 3).reshape(Bm, Nm, C)
        return o @ W_proj + b_proj

    def _L1_ffn_ref(x, Wg, W1, W2):
        import jax, jax.numpy as jnp
        import numpy as np
        B, S, D = x.shape
        E = Wg.shape[1]
        T = B * S
        cap = max(1, T // E)
        xt = x.reshape(T, D)
        logits = xt @ Wg
        probs = jax.nn.softmax(logits, axis=-1)
        pT = probs.T
        _, top_idx = jax.lax.top_k(pT, cap)
        sel = jnp.zeros((E, T), dtype=bool).at[jnp.arange(E)[:, None], top_idx].set(True)
        masked = jnp.where(sel, pT, -jnp.inf)
        assigned = sel.any(axis=0)
        tok2exp = jnp.where(assigned, jnp.argmax(masked, axis=0), jnp.argmax(pT, axis=0))
        weights = jnp.take_along_axis(probs, tok2exp[:, None], axis=1)[:, 0]
        out = jnp.zeros_like(xt)
        for e in range(E):
            gate = jnp.where(tok2exp == e, weights, 0.0)
            h = jax.nn.gelu(xt @ W1[e], approximate=False) @ W2[e]
            out = out + gate[:, None] * h
        return out.reshape(B, S, D)

    def _L2_attn_a_ref(x, W_in, W_x, W_dt, b_dt, A_log, B_bias, C_bias, B_norm_w, C_norm_w, rope_freqs, D, W_out):
        import jax, jax.numpy as jnp
        import numpy as np
        B_SZ, SEQ, D_MODEL = (2, 256, 128)
        D_STATE, EXPAND = (16, 2)
        D_INNER = D_MODEL * EXPAND
        A_FLOOR = 0.0001
        RMS_EPS = float(np.finfo(np.float32).eps)

        def _rmsnorm(v, w):
            return v * jax.lax.rsqrt(jnp.mean(v * v, axis=-1, keepdims=True) + RMS_EPS) * w

        def _rope(v, cos_a, sin_a):
            ve, vo = (v[..., ::2], v[..., 1::2])
            re = ve * cos_a - vo * sin_a
            ro = ve * sin_a + vo * cos_a
            return jnp.stack([re, ro], axis=-1).reshape(v.shape)
        xz = jnp.einsum('bld,ed->ble', x, W_in)
        x_path, z = jnp.split(xz, 2, axis=-1)
        x_path = jax.nn.silu(x_path)
        ssm = jnp.einsum('ble,se->bls', x_path, W_x)
        B_raw = ssm[..., :D_STATE]
        C_raw = ssm[..., D_STATE:2 * D_STATE]
        dt_in = ssm[..., -2:-1]
        lam_in = ssm[..., -1:]
        Bn = _rmsnorm(B_raw + B_bias, B_norm_w)
        Cn = _rmsnorm(C_raw + C_bias, C_norm_w)
        dt = jax.nn.softplus(dt_in * W_dt[:, 0] + b_dt)
        lam = jax.nn.sigmoid(lam_in)
        freqs = jax.nn.softplus(rope_freqs)
        cum_dt = jnp.cumsum(jnp.mean(dt, axis=-1, keepdims=True), axis=1)
        angles = cum_dt * freqs
        cos_a, sin_a = (jnp.cos(angles), jnp.sin(angles))
        Br = _rope(Bn, cos_a, sin_a)
        Cr = _rope(Cn, cos_a, sin_a)
        A = jnp.minimum(-jnp.exp(A_log), -A_FLOOR)
        dA = jnp.exp(A[None, None] * dt[..., None])
        Bx = Br[:, :, None, :] * x_path[..., None]
        lam_e = lam[..., None]
        dt_e = dt[..., None]
        Bx_prev = jnp.concatenate([jnp.zeros_like(Bx[:, :1]), Bx[:, :-1]], axis=1)
        u = (1.0 - lam_e) * dt_e * dA * Bx_prev + lam_e * dt_e * Bx
        u = u.at[:, 0].set(dt_e[:, 0] * Bx[:, 0])
        dA_t = jnp.moveaxis(dA, 1, 0)
        u_t = jnp.moveaxis(u, 1, 0)
        C_t = jnp.moveaxis(Cr, 1, 0)

        def step(h, inp):
            dA_, u_, C_ = inp
            h = dA_ * h + u_
            y = jnp.sum(h * C_[:, None, :], axis=-1)
            return (h, y)
        h0 = jnp.zeros((x.shape[0], D_INNER, D_STATE), dtype=x.dtype)
        _, ys = jax.lax.scan(step, h0, (dA_t, u_t, C_t))
        y = jnp.moveaxis(ys, 0, 1)
        y = y + x_path * D
        y = y * jax.nn.silu(z)
        return jnp.einsum('ble,de->bld', y, W_out)

    def _L2_attn_b_ref(X_Q, W_Q, W_K, W_V, gn_weight, gn_bias):
        import jax, jax.numpy as jnp
        import numpy as np
        H = 8
        ROPE_DIM = 64
        GAMMA = 0.96875
        GROUPS = 16
        EPS = 1e-05

        def _rope(x, offset=0):
            T = x.shape[-2]
            inv_freq = 1.0 / 10000.0 ** (np.arange(0, ROPE_DIM, 2, dtype=np.float32) / ROPE_DIM)
            t = jnp.arange(T, dtype=jnp.float32) + offset
            freqs = t[:, None] * inv_freq[None, :]
            freqs = jnp.repeat(freqs, 2, axis=-1)
            cos, sin = (jnp.cos(freqs), jnp.sin(freqs))
            xr, xp = (x[..., :ROPE_DIM], x[..., ROPE_DIM:])
            x1, x2 = (xr[..., 0::2], xr[..., 1::2])
            rot = jnp.stack([-x2, x1], axis=-1).reshape(xr.shape)
            return jnp.concatenate([xr * cos + rot * sin, xp], axis=-1)

        def _to_scores(X, W):
            B, T, C = X.shape
            return (X @ W).reshape(B, T, H, C).transpose(0, 2, 1, 3)
        B, T, C = X_Q.shape
        Q = _rope(_to_scores(X_Q, W_Q))
        K = _rope(_to_scores(X_Q, W_K))
        V = _to_scores(X_Q, W_V)
        Q, K, V = (jax.nn.silu(Q), jax.nn.silu(K), jax.nn.silu(V))
        n = jnp.arange(T)
        diff = n[:, None] - n[None, :]
        D = jnp.where(diff >= 0, GAMMA ** jnp.maximum(diff, 0).astype(jnp.float32), 0.0)
        A = jnp.einsum('bhqc,bhkc->bhqk', Q, K)
        A = A * D
        A = jnp.swapaxes(A, -2, -1)
        out = A @ V
        out = out.sum(axis=1)
        x = out.reshape(B * T, GROUPS, C // GROUPS)
        mu = x.mean(-1, keepdims=True)
        var = x.var(-1, keepdims=True)
        xn = (x - mu) * jax.lax.rsqrt(var + EPS)
        out = xn.reshape(B * T, C) * gn_weight + gn_bias
        return out.reshape(B, T, C)

    def _L2_ffn_ref(x, signatures_raw, knot_values, temperature, compress_w1, compress_b1, compress_w2, compress_b2, spline_w1, spline_b1, spline_w2, spline_b2, directions, norm_gamma, norm_beta, output_scale):
        import jax, jax.numpy as jnp
        import numpy as np
        D_MODEL = 128
        NUM_TILES = 64
        TPC = 8
        NUM_CLUSTERS = NUM_TILES // TPC
        GRID = 16
        COMP_H = 32
        NUM_KNOTS = 8
        EPS_LN = 1e-05

        def _calibrate(scores, knots, temperature):
            K = knots.shape[0]
            normalized = jax.nn.sigmoid(scores / (temperature[0] + 1e-06))
            idx_float = normalized * (K - 1)
            idx_low = jnp.clip(idx_float.astype(jnp.int32), 0, K - 2)
            idx_high = idx_low + 1
            t = idx_float - idx_low.astype(scores.dtype)
            val_low = knots[idx_low]
            val_high = knots[idx_high]
            return val_low + t * (val_high - val_low)

        def _forward(x, signatures_raw, knot_values, temperature, compress_w1, compress_b1, compress_w2, compress_b2, spline_w1, spline_b1, spline_w2, spline_b2, directions, norm_gamma, norm_beta, output_scale):
            B, T, D = x.shape
            xf = x.reshape(-1, D)
            q = jnp.where(signatures_raw > 0.3, 1.0, jnp.where(signatures_raw < -0.3, -1.0, 0.0)).astype(signatures_raw.dtype)
            sigs = signatures_raw + jax.lax.stop_gradient(q - signatures_raw)
            cluster_sigs = jnp.sign(sigs.reshape(NUM_CLUSTERS, TPC, D).mean(axis=1))
            cluster_scores = xf @ cluster_sigs.T
            cluster_gates = _calibrate(cluster_scores, knot_values, temperature)
            cluster_idx = jnp.argmax(cluster_gates, axis=-1)
            tile_scores = xf @ sigs.T
            tile_gates = _calibrate(tile_scores, knot_values, temperature)
            gates_by_cluster = tile_gates.reshape(-1, NUM_CLUSTERS, TPC)
            sel_gates = jnp.take_along_axis(gates_by_cluster, cluster_idx[:, None, None], axis=1)[:, 0, :]
            local_idx = jnp.argmax(sel_gates, axis=-1)
            tile_idx = cluster_idx * TPC + local_idx
            h = jax.nn.gelu(xf @ compress_w1 + compress_b1, approximate=False)
            comp = jnp.tanh(h @ compress_w2 + compress_b2)
            w1 = spline_w1[tile_idx]
            b1 = spline_b1[tile_idx]
            hh = jax.nn.relu(jnp.einsum('ni,nig->ng', comp, w1) + b1)
            w2 = spline_w2[tile_idx]
            b2 = spline_b2[tile_idx]
            mag = jnp.einsum('ng,ngo->no', hh, w2) + b2
            ffn_out = mag * directions[tile_idx] * output_scale[0]
            y = xf + ffn_out
            mu = y.mean(axis=-1, keepdims=True)
            var = ((y - mu) ** 2).mean(axis=-1, keepdims=True)
            y = (y - mu) / jnp.sqrt(var + EPS_LN) * norm_gamma + norm_beta
            return y.reshape(B, T, D)
        return _forward(x, signatures_raw, knot_values, temperature, compress_w1, compress_b1, compress_w2, compress_b2, spline_w1, spline_b1, spline_w2, spline_b2, directions, norm_gamma, norm_beta, output_scale)

    def _L3_attn_a_ref(x, q_w, kv_w, proj_w, proj_b):
        import jax, jax.numpy as jnp
        import numpy as np
        DIM = 128
        NUM_HEADS = 16
        HEAD_DIM = DIM // NUM_HEADS
        WINDOW = 32
        SCALE = HEAD_DIM ** (-0.5)
        B, L, D = x.shape
        H, hd, ws = (NUM_HEADS, HEAD_DIM, WINDOW)
        q = x @ q_w.T
        kv = x @ kv_w.T
        k, v = (kv[..., :hd], kv[..., hd:])
        q = q.reshape(B, L, H, hd).transpose(0, 2, 1, 3)
        pad = (ws - L % ws) % ws
        Lp = L + pad
        if pad > 0:
            q = jnp.pad(q, ((0, 0), (0, 0), (0, pad), (0, 0)))
            k = jnp.pad(k, ((0, 0), (0, pad), (0, 0)))
            v = jnp.pad(v, ((0, 0), (0, pad), (0, 0)))
        n = Lp // ws
        qb = q.reshape(B, H, n, ws, hd)
        kb = k.reshape(B, n, ws, hd)
        vb = v.reshape(B, n, ws, hd)
        attn = jnp.einsum('bhnwd,bnud->bhnwu', qb, kb) * SCALE
        attn = jax.nn.softmax(attn, axis=-1)
        out = jnp.einsum('bhnwu,bnud->bhnwd', attn, vb)
        out = out.reshape(B, H, Lp, hd)[:, :, :L, :]
        out = out.transpose(0, 2, 1, 3).reshape(B, L, D)
        return out @ proj_w.T + proj_b

    def _L3_attn_b_ref(x, Wq, bq, Wk, bk, Wv, bv, Wo, bo, g1, be1, W1, b1, W2, b2, g2, be2):
        import math
        import jax, jax.numpy as jnp
        import numpy as np
        H = 128
        NH = 16
        HD = H // NH
        FF = 512
        EPS = 1e-12

        def _lin(key, fan_in, fan_out):
            k1, k2 = jax.random.split(key)
            bound = 1.0 / math.sqrt(fan_in)
            W = jax.random.uniform(k1, (fan_in, fan_out), jnp.float32, -bound, bound)
            b = jax.random.uniform(k2, (fan_out,), jnp.float32, -bound, bound)
            return (W, b)

        def _layernorm(x, g, b):
            mu = jnp.mean(x, axis=-1, keepdims=True)
            var = jnp.mean((x - mu) ** 2, axis=-1, keepdims=True)
            return (x - mu) * jax.lax.rsqrt(var + EPS) * g + b

        def _gelu(x):
            return x * 0.5 * (1.0 + jax.lax.erf(x / jnp.sqrt(jnp.float32(2.0))))
        B, S, _ = x.shape

        def heads(W, b):
            return (x @ W + b).reshape(B, S, NH, HD).transpose(0, 2, 1, 3)
        q, k, v = (heads(Wq, bq), heads(Wk, bk), heads(Wv, bv))
        eq = jax.nn.elu(q)
        ek = jax.nn.elu(k)
        qn = eq / jnp.linalg.norm(eq, axis=-1, keepdims=True)
        kn = ek / jnp.linalg.norm(ek, axis=-1, keepdims=True)
        kv = jnp.einsum('bhsd,bhse->bhde', kn, v)
        ctx = jnp.einsum('bhsd,bhde->bhse', qn, kv) / jnp.float32(math.sqrt(HD))
        ctx = ctx.transpose(0, 2, 1, 3).reshape(B, S, H)
        attn_out = _layernorm(ctx @ Wo + bo + x, g1, be1)
        h = _gelu(attn_out @ W1 + b1)
        out = _layernorm(h @ W2 + b2 + attn_out, g2, be2)
        return out

    def _L3_ffn_ref(x, router_w, router_b, w1, b1, w2, b2):
        import jax, jax.numpy as jnp
        import numpy as np
        DIM = 128
        HIDDEN = 512
        N_EXPERTS = 8
        K = 2
        TEMP = 1.0

        def _expert_ffn(xf, wa, ba, wb, bb):
            h = xf @ wa.T + ba
            h1, h2 = jnp.split(h, 2, axis=-1)
            h = jax.nn.silu(h1) * h2
            return h @ wb.T + bb
        b, t, d = x.shape
        logits = (x @ router_w.T + router_b) / TEMP
        topk_val, topk_idx = jax.lax.top_k(logits, K)
        weights = jax.nn.softmax(topk_val, axis=-1)
        xf = x.reshape(-1, d)
        outs = jax.vmap(_expert_ffn, in_axes=(None, 0, 0, 0, 0))(xf, w1, b1, w2, b2)
        outs = jnp.transpose(outs, (1, 0, 2))
        idx = topk_idx.reshape(-1, K)
        gathered = jnp.take_along_axis(outs, idx[:, :, None], axis=1)
        combined = (gathered * weights.reshape(-1, K, 1)).sum(axis=1)
        return combined.reshape(b, t, d)
    x = L0_attn_a_x
    x = x + _L0_attn_a_ref(_layernorm(x, axis=-1), L0_attn_a_Wq, L0_attn_a_bq, L0_attn_a_Wk, L0_attn_a_bk, L0_attn_a_Wv, L0_attn_a_bv, L0_attn_a_W1, L0_attn_a_b1, L0_attn_a_W2, L0_attn_a_b2, L0_attn_a_W3, L0_attn_a_b3)
    x = x + _L0_ffn_ref(_layernorm(x, axis=-1), L0_ffn_router_w, L0_ffn_w1, L0_ffn_w2)
    x = x + _L0_attn_b_ref(_layernorm(x, axis=-1), L0_attn_b_Wq, L0_attn_b_bq, L0_attn_b_Wk, L0_attn_b_bk, L0_attn_b_Wv, L0_attn_b_bv, L0_attn_b_Wo, L0_attn_b_bo, L0_attn_b_ln_g, L0_attn_b_ln_b)
    x = x + _L0_ffn_ref(_layernorm(x, axis=-1), L0_ffn_router_w, L0_ffn_w1, L0_ffn_w2)
    x = x + _L1_attn_a_ref(_layernorm(x, axis=-1), L1_attn_a_in_proj_w, L1_attn_a_conv_w, L1_attn_a_x_proj_w, L1_attn_a_dt_proj_w, L1_attn_a_dt_proj_b, L1_attn_a_A_log, L1_attn_a_D, L1_attn_a_out_proj_w)
    x = x + _L1_ffn_ref(_layernorm(x, axis=-1), L1_ffn_Wg, L1_ffn_W1, L1_ffn_W2)
    x = x + _L1_attn_b_ref(_layernorm(x, axis=-1), L1_attn_b_W_qkv, L1_attn_b_W_proj, L1_attn_b_b_proj, L1_attn_b_lambda_q1, L1_attn_b_lambda_k1, L1_attn_b_lambda_q2, L1_attn_b_lambda_k2, L1_attn_b_subln_w)
    x = x + _L1_ffn_ref(_layernorm(x, axis=-1), L1_ffn_Wg, L1_ffn_W1, L1_ffn_W2)
    x = x + _L2_attn_a_ref(_layernorm(x, axis=-1), L2_attn_a_W_in, L2_attn_a_W_x, L2_attn_a_W_dt, L2_attn_a_b_dt, L2_attn_a_A_log, L2_attn_a_B_bias, L2_attn_a_C_bias, L2_attn_a_B_norm_w, L2_attn_a_C_norm_w, L2_attn_a_rope_freqs, L2_attn_a_D, L2_attn_a_W_out)
    x = x + _L2_ffn_ref(_layernorm(x, axis=-1), L2_ffn_signatures_raw, L2_ffn_knot_values, L2_ffn_temperature, L2_ffn_compress_w1, L2_ffn_compress_b1, L2_ffn_compress_w2, L2_ffn_compress_b2, L2_ffn_spline_w1, L2_ffn_spline_b1, L2_ffn_spline_w2, L2_ffn_spline_b2, L2_ffn_directions, L2_ffn_norm_gamma, L2_ffn_norm_beta, L2_ffn_output_scale)
    x = x + _L2_attn_b_ref(_layernorm(x, axis=-1), L2_attn_b_W_Q, L2_attn_b_W_K, L2_attn_b_W_V, L2_attn_b_gn_weight, L2_attn_b_gn_bias)
    x = x + _L2_ffn_ref(_layernorm(x, axis=-1), L2_ffn_signatures_raw, L2_ffn_knot_values, L2_ffn_temperature, L2_ffn_compress_w1, L2_ffn_compress_b1, L2_ffn_compress_w2, L2_ffn_compress_b2, L2_ffn_spline_w1, L2_ffn_spline_b1, L2_ffn_spline_w2, L2_ffn_spline_b2, L2_ffn_directions, L2_ffn_norm_gamma, L2_ffn_norm_beta, L2_ffn_output_scale)
    x = x + _L3_attn_a_ref(_layernorm(x, axis=-1), L3_attn_a_q_w, L3_attn_a_kv_w, L3_attn_a_proj_w, L3_attn_a_proj_b)
    x = x + _L3_ffn_ref(_layernorm(x, axis=-1), L3_ffn_router_w, L3_ffn_router_b, L3_ffn_w1, L3_ffn_b1, L3_ffn_w2, L3_ffn_b2)
    x = x + _L3_attn_b_ref(_layernorm(x, axis=-1), L3_attn_b_Wq, L3_attn_b_bq, L3_attn_b_Wk, L3_attn_b_bk, L3_attn_b_Wv, L3_attn_b_bv, L3_attn_b_Wo, L3_attn_b_bo, L3_attn_b_g1, L3_attn_b_be1, L3_attn_b_W1, L3_attn_b_b1, L3_attn_b_W2, L3_attn_b_b2, L3_attn_b_g2, L3_attn_b_be2)
    x = x + _L3_ffn_ref(_layernorm(x, axis=-1), L3_ffn_router_w, L3_ffn_router_b, L3_ffn_w1, L3_ffn_b1, L3_ffn_w2, L3_ffn_b2)
    return x

_drawn_inputs = setup_inputs


def setup_inputs(seed=0):
    import zlib

    import numpy as np

    out = dict(_drawn_inputs(seed))
    spreads = {'L0_attn_b_bq': (0.0, 0.1),
     'L0_attn_b_bk': (0.0, 0.1),
     'L0_attn_b_bv': (0.0, 0.1),
     'L0_attn_b_bo': (0.0, 0.1),
     'L0_attn_b_ln_g': (1.0, 0.2),
     'L0_attn_b_ln_b': (0.0, 0.1),
     'L1_attn_a_D': (1.0, 0.2),
     'L1_attn_b_b_proj': (0.0, 0.1),
     'L1_attn_b_subln_w': (1.0, 0.2),
     'L2_attn_a_b_dt': (0.0, 0.1),
     'L2_attn_a_B_bias': (1.0, 0.2),
     'L2_attn_a_C_bias': (1.0, 0.2),
     'L2_attn_a_B_norm_w': (1.0, 0.2),
     'L2_attn_a_C_norm_w': (1.0, 0.2),
     'L2_attn_a_D': (1.0, 0.2),
     'L2_attn_b_gn_weight': (1.0, 0.2),
     'L2_attn_b_gn_bias': (0.0, 0.1),
     'L2_ffn_compress_b1': (0.0, 0.1),
     'L2_ffn_compress_b2': (0.0, 0.1),
     'L2_ffn_spline_b1': (0.0, 0.1),
     'L2_ffn_spline_b2': (0.0, 0.1),
     'L2_ffn_norm_gamma': (1.0, 0.2),
     'L2_ffn_norm_beta': (0.0, 0.1),
     'L3_attn_b_g1': (1.0, 0.2),
     'L3_attn_b_be1': (0.0, 0.1),
     'L3_attn_b_g2': (1.0, 0.2),
     'L3_attn_b_be2': (0.0, 0.1),
     'L3_ffn_router_b': (0.0, 0.1),
     'L3_ffn_b1': (0.0, 0.1),
     'L3_ffn_b2': (0.0, 0.1)}
    factors = {}
    for name, (base, spread) in spreads.items():
        noise = np.random.default_rng([zlib.crc32(name.encode()), seed]).standard_normal(out[name].shape)
        drawn = base * np.exp(spread * noise) if base else spread * noise
        out[name] = jnp.asarray(drawn.astype(out[name].dtype))
    for name, factor in factors.items():
        out[name] = (out[name] * factor).astype(out[name].dtype)
    return out
```

```python
from contextlib import ExitStack

import numpy as np

import concourse.bass as bass
from concourse import mybir

F32 = mybir.dt.float32
U32 = mybir.dt.uint32
I32 = mybir.dt.int32
ALU = mybir.AluOpType
ACT = mybir.ActivationFunctionType
AX = mybir.AxisListType

P = 128
BATCH, SEQ, D = 16, 256, 128
TOKENS = BATCH * SEQ
TILES = TOKENS // P
GT = 4
GROUP = GT * P
GROUPS = TILES // GT
BPG = GROUP // SEQ
TPB = SEQ // P
LN_EPS = 1e-5


class Scope:

    def __init__(self, nc, name):
        self.nc, self.name, self.stack = nc, name, ExitStack()
        self.sems = []

    def __enter__(self):
        self.stack.__enter__()
        return self

    def __exit__(self, *a):
        return self.stack.__exit__(*a)

    def sb(self, name, shape, dt=F32):
        return self.stack.enter_context(self.nc.sbuf_tensor(f"{self.name}_{name}", shape, dt))

    def ps(self, name, shape, dt=F32):
        return self.stack.enter_context(self.nc.psum_tensor(f"{self.name}_{name}", shape, dt))

    def sem(self, name):
        self.sems.append(self.stack.enter_context(self.nc.semaphore(f"{self.name}_{name}")))
        return self.sems[-1]

    def clear(self):
        for sem in self.sems:
            self.nc.gpsimd.sem_clear(sem)

    def block(self):
        self.stack.callback(self.clear)
        return self.stack.enter_context(self.nc.Block())


class Core:

    def __init__(self, nc, dram):
        self.nc, self.dram = nc, dram
        self.stack = ExitStack()
        self.bufs = {}
        self.loads_started = 0

    def keep(self, name, shape, dt=F32):
        self.bufs[name] = self.stack.enter_context(self.nc.sbuf_tensor(name, shape, dt))
        return self.bufs[name]


def flat(ap):
    return ap.rearrange("p a n -> p (a n)")


def tile(buf, t):
    return flat(buf[:, bass.ds(t, 1), :])


def load_all(nc, k, weights):
    with Scope(nc, "load") as s:
        loaded = s.sem("loaded")
        block = s.block()

        @block.sync
        def _(sp):
            n = 0
            sp.dma_start(k.X[:], k.dram["x"]).then_inc(loaded, 16)
            for name in weights:
                sp.dma_start(k.bufs[name][:], k.dram[name]).then_inc(loaded, 16)
                n += 16
            sp.wait_ge(loaded, n + 16)

        @block.vector
        def _(dve):
            nc.vector.memset(k.neg_half[:], -0.5)
            nc.vector.memset(k.ones[:], 1.0)
            nc.vector.memset(k.ones_row[:], 1.0)


def start_expert_load(nc, k, step):
    k.loads_started += 2
    layer = step[:2].upper()
    with Scope(nc, f"{step}_load{k.loads_started}") as s:
        block = s.block()

        @block.sync
        def _(sp):
            for buf, name in ((k.up, "w1"), (k.down, "w2")):
                src = k.dram[f"{layer}_ffn_{name}"]
                sp.dma_start(buf[:, 0:src.shape[1]], src).then_inc(k.weights_landed, 16)


def finish_expert_load(nc, k):
    with Scope(nc, f"landed{k.loads_started}") as s:
        block = s.block()

        @block.sync
        def _(sp):
            sp.wait_ge(k.weights_landed, 16 * k.loads_started)


def store(nc, k, out):
    with Scope(nc, "store") as s:
        stored = s.sem("stored")
        block = s.block()

        @block.sync
        def _(sp):
            sp.dma_start(out, k.X[:]).then_inc(stored, 16)
            sp.wait_ge(stored, 16)


def layer_norm(nc, k, name, project=None, n_out=0, keep_rows=False):
    with Scope(nc, name) as s:
        stats = s.sb("stats", [P, TILES, 6])
        meanvar = s.sb("meanvar", [P, TILES, 1])
        rstd = s.sb("rstd", [P, TILES])
        half_gap = s.sb("half_gap", [P, TILES])
        rows = [s.sb(f"rows{i}", [P, GT, D]) for i in range(2)]
        cols = [s.sb(f"cols{i}", [P, GROUP]) for i in range(2)]
        turned = [s.ps(f"turned{i}", [P, GROUP]) for i in range(2)]
        proj = [s.ps(f"proj{i}", [P, 512]) for i in range(2)]
        moments, ready = s.sem("moments"), s.sem("ready")
        rows_ready, rows_free = s.sem("rows_ready"), s.sem("rows_free")
        turned_ready = s.sem("turned_ready")
        turned_free, cols_ready = s.sem("turned_free"), s.sem("cols_ready")
        proj_ready, logits_kept = s.sem("proj_ready"), s.sem("logits_kept")
        rows_kept = s.sem("rows_kept")
        block = s.block()

        @block.vector
        def _(dve):
            with dve.Fori(0, TILES) as t:
                nc.vector.bn_stats(tile(stats, t), tile(k.X, t))
            dve.drain()
            nc.vector.tensor_tensor(meanvar[:, :, 0], stats[:, :, 1], stats[:, :, 4], ALU.add)
            nc.vector.tensor_tensor(half_gap[:], stats[:, :, 1], stats[:, :, 4], ALU.subtract)
            nc.vector.tensor_tensor(rstd[:], stats[:, :, 2], stats[:, :, 5], ALU.add)
            dve.drain()
            nc.vector.tensor_scalar(meanvar[:, :, 0], meanvar[:, :, 0], 0.5, None, ALU.mult)
            nc.vector.scalar_tensor_tensor(out=half_gap[:], in0=half_gap[:], scalar=0.25, in1=half_gap[:],
                                           op0=ALU.mult, op1=ALU.mult)
            nc.vector.tensor_scalar(rstd[:], rstd[:], 1.0 / D, LN_EPS, ALU.mult, ALU.add)
            dve.drain()
            nc.vector.tensor_tensor(rstd[:], rstd[:], half_gap[:], ALU.add).then_inc(moments, 1)
            dve.wait_ge(ready, 1)
            nc.vector.reciprocal(rstd[:], rstd[:])
            dve.drain()
            with dve.Fori(0, GROUPS // 2) as pair:
                g = pair * 2
                for i in range(2):
                    dve.wait_ge(rows_free, g + (i + 1))
                    if keep_rows:
                        dve.wait_ge(rows_kept, g + (i + 1))
                    for j in range(GT):
                        last = nc.vector.tensor_scalar(
                            rows[i][:, j, :], tile(k.X, g * GT + (i * GT + j)),
                            flat(meanvar[:, bass.ds(g * GT + (i * GT + j), 1), 0:1]),
                            rstd[:, bass.ds(g * GT + (i * GT + j), 1)], ALU.subtract, ALU.mult)
                    last.then_inc(rows_ready, 1)

        if keep_rows:
            @block.gpsimd
            def _(pool):
                pool.sem_inc(rows_kept, 2)
                with pool.Fori(0, GROUPS // 2) as pair:
                    for i in range(2):
                        pool.wait_ge(rows_ready, pair * 2 + (i + 1))
                        nc.gpsimd.tensor_copy(k.XN[:, bass.ds(pair * 2 * GT + i * GT, GT), :], rows[i][:]).then_inc(rows_kept, 1)

        @block.tensor
        def _(pe):
            pe.sem_inc(rows_free, 2)
            with pe.Fori(0, GROUPS // 2) as pair:
                g = pair * 2
                for i in range(2):
                    pe.wait_ge(rows_ready, g + (i + 1))
                    pe.wait_ge(turned_free, g + (i + 1))
                    for j in range(GT):
                        last = nc.tensor.transpose(turned[i][:, j * P:(j + 1) * P], rows[i][:, j, :], k.ident[:])
                    last.then_inc(turned_ready, 1)
                if project is not None:
                    for i in range(2):
                        pe.wait_ge(cols_ready, g + (i + 1))
                        for j in range(GT):
                            last = nc.tensor.matmul(proj[i][:, j * n_out:(j + 1) * n_out], cols[i][:, j * P:(j + 1) * P],
                                                    project[:, 0:n_out], start=True, stop=True)
                        last.then_inc(proj_ready, 1)

        @block.scalar
        def _(act):
            act.wait_ge(moments, 1)
            nc.scalar.activation(rstd[:], rstd[:], ACT.Sqrt).then_inc(ready, 1)
            act.sem_inc(turned_free, 2)
            with act.Fori(0, GROUPS // 2) as pair:
                g = pair * 2
                for i in range(2):
                    act.wait_ge(turned_ready, g + (i + 1))
                    act.sem_inc(rows_free, 1)
                    xnt = k.XNT[:, bass.ds(g * GROUP + i * GROUP, GROUP)]
                    if project is not None:
                        nc.scalar.copy(cols[i][:], turned[i][:]).then_inc(cols_ready, 1)
                    nc.scalar.copy(xnt, turned[i][:]).then_inc(turned_free, 1)
                if project is not None:
                    for i in range(2):
                        act.wait_ge(proj_ready, g + (i + 1))
                        nc.scalar.copy(k.LOG[:, bass.ds(g * GT + i * GT, GT), 0:n_out],
                                       proj[i][:, 0:GT * n_out].rearrange("p (t n) -> p t n", n=n_out)).then_inc(logits_kept, 1)


def rank_below_two(nc, dve, s, probs, keep):
    ahead = s.sb("ahead", [P, TILES, 8])
    cmp = s.sb("cmp", [P, TILES, 8])
    nc.vector.memset(ahead[:], 0.0)
    for j in range(8):
        pj = probs[:, :, j:j + 1]
        dve.drain()
        if j > 0:
            nc.vector.tensor_tensor(cmp[:, :, 0:j], pj.to_broadcast([P, TILES, j]), probs[:, :, 0:j], ALU.is_gt)
        if j < 7:
            nc.vector.tensor_tensor(cmp[:, :, j + 1:8], pj.to_broadcast([P, TILES, 7 - j]), probs[:, :, j + 1:8], ALU.is_ge)
        nc.vector.memset(cmp[:, :, j:j + 1], 0.0)
        dve.drain()
        nc.vector.tensor_tensor(ahead[:], ahead[:], cmp[:], ALU.add)
    dve.drain()
    nc.vector.tensor_scalar(keep[:], ahead[:], 2.0, None, ALU.is_lt)
    dve.drain()


def softmax8(nc, k, name, top2_first, bias=None):
    with Scope(nc, name) as s:
        shifted = s.sb("shifted", [P, TILES, 8])
        e = s.sb("e", [P, TILES, 8])
        keep = s.sb("keep", [P, TILES, 8])
        top = s.sb("top", [P, TILES])
        total = s.sb("total", [P, TILES])
        shift_ready, exp_ready = s.sem("shift_ready"), s.sem("exp_ready")
        block = s.block()
        logits = k.LOG[:, :, 0:8]

        def per_tile(ap):
            return ap.rearrange("p (t a) -> p t a", a=1).to_broadcast([P, TILES, 8])

        @block.vector
        def _(dve):
            if bias is not None:
                nc.vector.tensor_tensor(logits, logits, bias[:].rearrange("p (a e) -> p a e", a=1)
                                        .to_broadcast([P, TILES, 8]), ALU.add)
                dve.drain()
            nc.vector.tensor_reduce(top[:], logits, AX.X, ALU.max)
            if top2_first:
                rank_below_two(nc, dve, s, k.LOG[:, :, 0:8], keep)
            dve.drain()
            nc.vector.tensor_tensor(shifted[:], logits, per_tile(top[:]), ALU.subtract).then_inc(shift_ready, 1)
            dve.wait_ge(exp_ready, 1)
            if top2_first:
                nc.vector.tensor_tensor(e[:], e[:], keep[:], ALU.mult)
                dve.drain()
            nc.vector.tensor_reduce(total[:], e[:], AX.X, ALU.add)
            dve.drain()
            nc.vector.reciprocal(total[:], total[:])
            dve.drain()
            nc.vector.tensor_tensor(k.GATE[:], e[:], per_tile(total[:]), ALU.mult)
            if top2_first is False:
                dve.drain()
                rank_below_two(nc, dve, s, k.GATE, keep)
                nc.vector.tensor_tensor(k.GATE[:], k.GATE[:], keep[:], ALU.mult)

        @block.scalar
        def _(act):
            act.wait_ge(shift_ready, 1)
            nc.scalar.activation(e[:], shifted[:], ACT.Exp).then_inc(exp_ready, 1)


def gelu_experts(nc, k, name, w1, w2, chunks):
    with Scope(nc, name) as s:
        up = [s.ps(f"up{i}", [P, GROUP]) for i in range(2)]
        down = [s.ps(f"down{i}", [P, GT, D]) for i in range(2)]
        hid = [s.sb(f"hid{i}", [P, GROUP]) for i in range(2)]
        up_ready, hid_ready = s.sem("up_ready"), s.sem("hid_ready")
        down_ready, down_free = s.sem("down_ready"), s.sem("down_free")
        block = s.block()
        steps = 8 * chunks

        @block.tensor
        def _(pe):
            def go_up(g, c):
                nc.tensor.matmul(up[c % 2][:], w1[:, c * P:(c + 1) * P], k.XNT[:, bass.ds(g * GROUP, GROUP)],
                                 start=True, stop=True).then_inc(up_ready, 1)

            def go_down(g, c):
                e, j = divmod(c, chunks)
                pe.wait_ge(hid_ready, g * steps + (c + 1))
                if j == 0:
                    pe.wait_ge(down_free, g * 8 + (e + 1))
                for t in range(GT):
                    last = nc.tensor.matmul(down[e % 2][:, t, :], hid[c % 2][:, t * P:(t + 1) * P],
                                            w2[:, c * D:(c + 1) * D], start=(j == 0 and t == 0),
                                            stop=(j == chunks - 1), skip_group_check=True)
                if j == chunks - 1:
                    last.then_inc(down_ready, 1)

            with pe.Fori(0, GROUPS) as g:
                go_up(g, 0)
                for c in range(steps):
                    if c + 1 < steps:
                        go_up(g, c + 1)
                    go_down(g, c)

        @block.scalar
        def _(act):
            with act.Fori(0, GROUPS) as g:
                for c in range(steps):
                    act.wait_ge(up_ready, g * steps + (c + 1))
                    nc.scalar.activation(hid[c % 2][:], up[c % 2][:], ACT.Gelu).then_inc(hid_ready, 1)

        @block.vector
        def _(dve):
            dve.sem_inc(down_free, 2)
            with dve.Fori(0, GROUPS) as g:
                for e in range(8):
                    dve.wait_ge(down_ready, g * 8 + (e + 1))
                    for t in range(GT):
                        xt = tile(k.X, g * GT + t)
                        last = nc.vector.scalar_tensor_tensor(
                            out=xt, in0=down[e % 2][:, t, :], scalar=flat(k.GATE[:, bass.ds(g * GT + t, 1), e:e + 1]),
                            in1=xt, op0=ALU.mult, op1=ALU.add)
                    last.then_inc(down_free, 1)
                    dve.drain()


def l0_ffn(nc, k, name):
    layer_norm(nc, k, name + "_ln", k.bufs["L0_ffn_router"], 8)
    softmax8(nc, k, name + "_gate", False)
    gelu_experts(nc, k, name + "_ffn", k.up, k.down, 4)


def silu_experts(nc, k, name):
    w1, b1, w2 = k.up, k.bufs["L3_ffn_b1"], k.down
    chunks = 4
    steps = 8 * chunks
    with Scope(nc, name) as s:
        up_a = [s.ps(f"up_a{i}", [P, GROUP]) for i in range(2)]
        up_b = [s.ps(f"up_b{i}", [P, GROUP]) for i in range(2)]
        down = [s.ps(f"down{i}", [P, GT, D]) for i in range(2)]
        gated = [s.sb(f"gated{i}", [P, GROUP]) for i in range(2)]
        hid = [s.sb(f"hid{i}", [P, GROUP]) for i in range(2)]
        up_ready, gated_ready, hid_ready = s.sem("up_ready"), s.sem("gated_ready"), s.sem("hid_ready")
        down_ready, down_free = s.sem("down_ready"), s.sem("down_free")
        block = s.block()

        @block.tensor
        def _(pe):
            def go_up(g, c):
                e, j = divmod(c, chunks)
                xn = k.XNT[:, bass.ds(g * GROUP, GROUP)]
                a, b = (2 * e * chunks + j) * P, ((2 * e + 1) * chunks + j) * P
                nc.tensor.matmul(up_a[c % 2][:], w1[:, a:a + P], xn, start=True, stop=True)
                nc.tensor.matmul(up_b[c % 2][:], w1[:, b:b + P], xn, start=True, stop=True).then_inc(up_ready, 1)

            def go_down(g, c):
                e, j = divmod(c, chunks)
                pe.wait_ge(hid_ready, g * steps + (c + 1))
                if j == 0:
                    pe.wait_ge(down_free, g * 8 + (e + 1))
                for t in range(GT):
                    last = nc.tensor.matmul(down[e % 2][:, t, :], hid[c % 2][:, t * P:(t + 1) * P],
                                            w2[:, c * D:(c + 1) * D], start=(j == 0 and t == 0),
                                            stop=(j == chunks - 1), skip_group_check=True)
                if j == chunks - 1:
                    last.then_inc(down_ready, 1)

            with pe.Fori(0, GROUPS) as g:
                go_up(g, 0)
                for c in range(steps):
                    if c + 1 < steps:
                        go_up(g, c + 1)
                    go_down(g, c)

        @block.scalar
        def _(act):
            with act.Fori(0, GROUPS) as g:
                for c in range(steps):
                    e, j = divmod(c, chunks)
                    act.wait_ge(up_ready, g * steps + (c + 1))
                    nc.scalar.activation(gated[c % 2][:], up_a[c % 2][:], ACT.Silu,
                                         bias=b1[:, 2 * e * chunks + j:2 * e * chunks + j + 1]).then_inc(gated_ready, 1)

        @block.vector
        def _(dve):
            dve.sem_inc(down_free, 2)

            def add_expert(g, e):
                dve.wait_ge(down_ready, g * 8 + (e + 1))
                for t in range(GT):
                    xt = tile(k.X, g * GT + t)
                    last = nc.vector.scalar_tensor_tensor(
                        out=xt, in0=down[e % 2][:, t, :], scalar=flat(k.GATE[:, bass.ds(g * GT + t, 1), e:e + 1]),
                        in1=xt, op0=ALU.mult, op1=ALU.add)
                last.then_inc(down_free, 1)
                dve.drain()

            with dve.Fori(0, GROUPS) as g:
                for c in range(steps):
                    e, j = divmod(c, chunks)
                    b = (2 * e + 1) * chunks + j
                    dve.wait_ge(gated_ready, g * steps + (c + 1))
                    nc.vector.scalar_tensor_tensor(out=hid[c % 2][:], in0=up_b[c % 2][:], scalar=b1[:, b:b + 1],
                                                   in1=gated[c % 2][:], op0=ALU.add, op1=ALU.mult).then_inc(hid_ready, 1)
                    if j == 1 and e > 0:
                        add_expert(g, e - 1)
                add_expert(g, 7)


def expert_bias(nc, k, name):
    half = TILES // 2
    with Scope(nc, name) as s:
        turned = s.ps("turned", [P, 2, P])
        gates = s.sb("gates", [P, 2, P])
        spread = s.sb("spread", [P, half, D])
        added = [s.ps(f"added{i}", [P, GT, D]) for i in range(4)]
        turned_ready, gates_ready = s.sem("turned_ready"), s.sem("gates_ready")
        spread_ready, added_ready, added_free = s.sem("spread_ready"), s.sem("added_ready"), s.sem("added_free")
        block = s.block()

        @block.gpsimd
        def _(pool):
            nc.gpsimd.tensor_tensor(spread[:],
                                    k.bufs["L3_ffn_b2"][:].rearrange("p (a d) -> p a d", a=1).to_broadcast([P, half, D]),
                                    k.bufs["c_own_tile"][:].rearrange("p (t a) -> p t a", a=1).to_broadcast([P, half, D]),
                                    ALU.mult).then_inc(spread_ready, 1)

        @block.tensor
        def _(pe):
            for h in range(2):
                nc.tensor.transpose(turned[:, h, :], k.GATE[:, h * half:(h + 1) * half, :].rearrange("p t e -> p (t e)"),
                                    k.ident[:]).then_inc(turned_ready, 1)
            pe.wait_ge(gates_ready, 1)
            pe.wait_ge(spread_ready, 1)
            for g in range(GROUPS):
                if g >= 4:
                    pe.wait_ge(added_free, g - 3)
                h, q = divmod(g * GT, half)
                nc.tensor.matmul(added[g % 4][:], gates[:, h, :], spread[:, q:q + GT, :], start=True, stop=True)\
                    .then_inc(added_ready, 1)

        @block.scalar
        def _(act):
            act.wait_ge(turned_ready, 2)
            nc.scalar.copy(gates[:], turned[:]).then_inc(gates_ready, 1)

        @block.vector
        def _(dve):
            for g in range(GROUPS):
                dve.wait_ge(added_ready, g + 1)
                xg = k.X[:, g * GT:(g + 1) * GT, :]
                nc.vector.tensor_tensor(xg, xg, added[g % 4][:], ALU.add).then_inc(added_free, 1)


def l3_ffn(nc, k, name):
    layer_norm(nc, k, name + "_ln", k.bufs["L3_ffn_router"], 8)
    softmax8(nc, k, name + "_gate", True, k.bufs["L3_ffn_rb"])
    expert_bias(nc, k, name + "_bias")
    silu_experts(nc, k, name + "_ffn")


def claim_by_capacity(nc, k, name):
    cap = TOKENS // 8
    with Scope(nc, name) as s:
        before, carry, weight = s.sb("before", [P, P]), s.sb("carry", [P, 8 * TILES]), s.sb("weight", [P, 8, TILES])
        p = s.sb("p", [P, 8, TILES])
        floor, cand, bit = s.sb("floor", [P, 8], U32), s.sb("cand", [P, 8], U32), s.sb("bit", [P, 8], U32)
        take = s.sb("take", [P, 8], U32)
        cmp, tie = s.sb("cmp", [P, 8, TILES]), s.sb("tie", [P, 8, TILES])
        rank, claim, q = s.sb("rank", [P, 8, TILES]), s.sb("claim", [P, 8, TILES]), s.sb("q", [P, 8, TILES])
        some, count, room = s.sb("some", [P, TILES]), s.sb("count", [P, 8]), s.sb("room", [P, 8])
        total = s.ps("total", [P, 8])
        ties_before, ties_tile = s.ps("ties_before", [P, 8 * TILES]), s.ps("ties_tile", [P, 8 * TILES])
        loaded, counted, totalled = s.sem("loaded"), s.sem("counted"), s.sem("totalled")
        tied, ranked = s.sem("tied"), s.sem("ranked")
        block = s.block()
        BITS = 30

        def over_tiles(ap):
            return ap.rearrange("p (e a) -> p e a", a=1).to_broadcast([P, 8, TILES])

        def over_experts(ap):
            return ap.rearrange("p (a t) -> p a t", a=1).to_broadcast([P, 8, TILES])

        def by_token(ap):
            return ap.rearrange("p e t -> p t e")

        @block.sync
        def _(sp):
            sp.dma_start(before[:], k.dram["c_before"]).then_inc(loaded, 16)
            sp.dma_start(carry[:], k.dram["c_not_first_tile"]).then_inc(loaded, 16)
            sp.dma_start(weight[:].rearrange("p e t -> p (e t)"), k.dram["c_early_first"]).then_inc(loaded, 16)

        @block.vector
        def _(dve):
            nc.vector.tensor_copy(by_token(p[:]), k.GATE[:])
            nc.vector.memset(floor[:], 0)
            nc.vector.memset(bit[:], 1 << (BITS - 1))
            dve.drain()
            with dve.Fori(0, BITS) as b:
                nc.vector.tensor_tensor(cand[:], floor[:], bit[:], ALU.bitwise_or)
                dve.drain()
                nc.vector.tensor_tensor(cmp[:], p[:], over_tiles(cand[:].bitcast(F32)), ALU.is_ge)
                nc.vector.tensor_scalar(bit[:], bit[:], 1, None, ALU.logical_shift_right)
                dve.drain()
                nc.vector.tensor_reduce(count[:], cmp[:], AX.X, ALU.add).then_inc(counted, 1)
                dve.wait_ge(totalled, b + 1)
                nc.vector.tensor_scalar(take[:], total[:], float(cap), None, ALU.is_ge)
                dve.drain()
                nc.vector.copy_predicated(floor[:], take[:], cand[:])
                dve.drain()
            nc.vector.tensor_tensor(claim[:], p[:], over_tiles(floor[:].bitcast(F32)), ALU.is_gt)
            nc.vector.tensor_tensor(tie[:], p[:], over_tiles(floor[:].bitcast(F32)), ALU.is_equal)
            dve.drain()
            nc.vector.tensor_reduce(count[:], claim[:], AX.X, ALU.add).then_inc(tied, 1)
            dve.wait_ge(loaded, 48)
            dve.wait_ge(ranked, 1)
            nc.vector.tensor_scalar(room[:], total[:], -1.0, float(cap), ALU.mult, ALU.add)
            nc.vector.tensor_tensor_scan(rank[:].rearrange("p e t -> p (e t)"), carry[:], ties_tile[:], 0.0, ALU.mult, ALU.add)
            dve.drain()
            nc.vector.tensor_tensor(rank[:].rearrange("p e t -> p (e t)"), rank[:].rearrange("p e t -> p (e t)"), ties_tile[:], ALU.subtract)
            dve.drain()
            nc.vector.tensor_tensor(rank[:].rearrange("p e t -> p (e t)"), rank[:].rearrange("p e t -> p (e t)"), ties_before[:], ALU.add)
            dve.drain()
            nc.vector.tensor_tensor(cmp[:], rank[:], over_tiles(room[:]), ALU.is_lt)
            dve.drain()
            nc.vector.tensor_tensor(cmp[:], cmp[:], tie[:], ALU.mult)
            dve.drain()
            nc.vector.tensor_tensor(claim[:], claim[:], cmp[:], ALU.add)
            dve.drain()
            nc.vector.tensor_reduce(some[:], by_token(claim[:]), AX.X, ALU.max)
            dve.drain()
            nc.vector.tensor_scalar(some[:], some[:], -1.0, 1.0, ALU.mult, ALU.add)
            dve.drain()
            nc.vector.tensor_tensor(claim[:], claim[:], over_experts(some[:]), ALU.max)
            dve.drain()
            nc.vector.tensor_tensor(q[:], p[:], claim[:], ALU.mult)
            dve.drain()
            nc.vector.scalar_tensor_tensor(out=q[:].rearrange("p e t -> p (e t)"), in0=claim[:].rearrange("p e t -> p (e t)"),
                                           scalar=-1.0, in1=q[:].rearrange("p e t -> p (e t)"), op0=ALU.add, op1=ALU.add)
            dve.drain()
            nc.vector.tensor_reduce(some[:], by_token(q[:]), AX.X, ALU.max)
            dve.drain()
            nc.vector.tensor_tensor(cmp[:], q[:], over_experts(some[:]), ALU.is_equal)
            dve.drain()
            nc.vector.tensor_tensor(cmp[:], cmp[:], weight[:], ALU.mult)
            dve.drain()
            nc.vector.tensor_reduce(some[:], by_token(cmp[:]), AX.X, ALU.max)
            dve.drain()
            nc.vector.tensor_tensor(cmp[:], cmp[:], over_experts(some[:]), ALU.is_equal)
            dve.drain()
            nc.vector.tensor_tensor(k.GATE[:], by_token(cmp[:]), by_token(p[:]), ALU.mult)

        @block.tensor
        def _(pe):
            with pe.Fori(0, BITS) as b:
                pe.wait_ge(counted, b + 1)
                nc.tensor.matmul(total[:], k.ones[:], count[:], start=True, stop=True).then_inc(totalled, 1)
            pe.wait_ge(tied, 1)
            pe.wait_ge(loaded, 48)
            ties = tie[:].rearrange("p e t -> p (e t)")
            nc.tensor.matmul(total[:], k.ones[:], count[:], start=True, stop=True)
            nc.tensor.matmul(ties_before[:], before[:], ties, start=True, stop=True)
            nc.tensor.matmul(ties_tile[:], k.ones[:], ties, start=True, stop=True).then_inc(ranked, 1)


def l1_ffn(nc, k, name):
    layer_norm(nc, k, name + "_ln", k.bufs["L1_ffn_router"], 8)
    softmax8(nc, k, name + "_probs", None)
    claim_by_capacity(nc, k, name + "_claim")
    gelu_experts(nc, k, name + "_ffn", k.up, k.down, 2)


def group_norm_rows(nc, dve, rows_ps, stats, mv):
    for t in range(GT):
        nc.vector.bn_stats(stats[:, t, :], rows_ps[:, t, :])
    dve.drain()
    for t in range(GT):
        nc.vector.bn_aggr(mv[:, t, :], stats[:, t, :])
    dve.drain()


def per_row(ap, n):
    return ap.rearrange("p (m a) -> p m a", a=1).to_broadcast([P, ap.shape[1], n])


def l0_attn_a(nc, k, name):
    layer_norm(nc, k, name + "_ln")
    with Scope(nc, name) as s:
        names = [("L0a_wqkv", [P, 3 * D]), ("L0a_bqkv", [P, 3 * D]), ("L0a_w1", [P, D]), ("L0a_b1", [P, 1]), ("L0a_w2", [P, 512]), ("L0a_b2", [P, 4]),
                 ("L0a_w3", [P, 512]), ("L0a_b3", [1, GROUP])]
        w = {n: s.sb(n, shape) for n, shape in names}
        xg, qkv = s.sb("xg", [P, GROUP]), s.sb("qkv", [P, GT, 3 * D])
        sq, norm = s.sb("sq", [P, GT, 2 * D]), s.sb("norm", [P, GT * 2])
        qk = s.sb("qk", [P, 2, GROUP])
        e = s.sb("e", [P, BPG, TPB, SEQ])
        rden, o, h1, h2 = s.sb("rden", [P, GROUP]), s.sb("o", [P, GROUP]), s.sb("h1", [P, GROUP]), s.sb("h2", [P, 4, GROUP])
        proj = s.ps("proj", [P, GT, 512])
        qkt_ps, s_ps = proj[:, 0:2, :], proj[:, 2:4, :]
        den_ps, o_ps = s.ps("den_ps", [P, GROUP]), s.ps("o_ps", [P, GROUP])
        y_ps, h1_ps = s.ps("y_ps", [P, GT, D]), s.ps("h1_ps", [P, GROUP])
        loaded, xg_ready, projected, squared = s.sem("loaded"), s.sem("xg_ready"), s.sem("projected"), s.sem("squared")
        rooted, unit, turned, qk_ready = s.sem("rooted"), s.sem("unit"), s.sem("turned"), s.sem("qk_ready")
        scored, exped, summed, mixed = s.sem("scored"), s.sem("exped"), s.sem("summed"), s.sem("mixed")
        h1_up, h1_ready, h2_up, h2_ready = s.sem("h1_up"), s.sem("h1_ready"), s.sem("h2_up"), s.sem("h2_ready")
        y_ready, done = s.sem("y_ready"), s.sem("done")
        block = s.block()

        @block.sync
        def _(sp):
            for n, _ in names:
                sp.dma_start(w[n][:], k.dram[n]).then_inc(loaded, 16)

        @block.tensor
        def _(pe):
            pe.wait_ge(loaded, 16 * len(names))
            with pe.Fori(0, GROUPS) as g:
                pe.wait_ge(xg_ready, g + 1)
                for t in range(GT):
                    last = nc.tensor.matmul(proj[:, t, 0:3 * D], xg[:, t * P:(t + 1) * P], w["L0a_wqkv"][:], start=True, stop=True)
                last.then_inc(projected, 1)
                pe.wait_ge(unit, g + 1)
                for i in range(2):
                    for t in range(GT):
                        last = nc.tensor.transpose(qkt_ps[:, i, t * P:(t + 1) * P], qkv[:, t, i * D:(i + 1) * D], k.ident[:])
                last.then_inc(turned, 1)
                pe.wait_ge(qk_ready, g + 1)
                for b in range(BPG):
                    for kt in range(TPB):
                        c = b * SEQ + kt * P
                        last = nc.tensor.matmul(s_ps[:, b, kt * SEQ:(kt + 1) * SEQ], qk[:, 1, c:c + P],
                                                qk[:, 0, b * SEQ:(b + 1) * SEQ], start=True, stop=True)
                    last.then_inc(scored, 1)
                for b in range(BPG):
                    pe.wait_ge(exped, g * BPG + (b + 1))
                    for kt in range(TPB):
                        nc.tensor.matmul(den_ps[:, b * SEQ:(b + 1) * SEQ], k.ones[:], e[:, b, kt, :],
                                         start=(kt == 0), stop=(kt == TPB - 1))
                    for kt in range(TPB):
                        last = nc.tensor.matmul(o_ps[:, b * SEQ:(b + 1) * SEQ], qkv[:, b * TPB + kt, 2 * D:3 * D], e[:, b, kt, :],
                                                start=(kt == 0), stop=(kt == TPB - 1))
                last.then_inc(summed, 1)
                nc.tensor.matmul(y_ps[:], k.ones_row[0:1, 0:P], w["L0a_b3"][:], start=True, stop=False, skip_group_check=True)
                pe.wait_ge(mixed, g + 1)
                nc.tensor.matmul(h1_ps[:], w["L0a_w1"][:], o[:], start=True, stop=True).then_inc(h1_up, 1)
                pe.wait_ge(h1_ready, g + 1)
                for j in range(4):
                    nc.tensor.matmul(proj[:, j, :], w["L0a_w2"][:, j * P:(j + 1) * P], h1[:], start=True, stop=True)\
                        .then_inc(h2_up, 1)
                for j in range(4):
                    pe.wait_ge(h2_ready, g * 4 + (j + 1))
                    for t in range(GT):
                        last = nc.tensor.matmul(y_ps[:, t, :], h2[:, j, t * P:(t + 1) * P], w["L0a_w3"][:, j * D:(j + 1) * D],
                                                start=False, stop=(j == 3), skip_group_check=True)
                last.then_inc(y_ready, 1)

        @block.scalar
        def _(act):
            act.wait_ge(loaded, 16 * len(names))
            with act.Fori(0, GROUPS) as g:
                act.wait_ge(done, g)
                nc.scalar.copy(xg[:], k.XNT[:, bass.ds(g * GROUP, GROUP)]).then_inc(xg_ready, 1)
                act.wait_ge(squared, g + 1)
                nc.scalar.activation(norm[:], norm[:], ACT.Sqrt).then_inc(rooted, 1)
                act.wait_ge(turned, g + 1)
                nc.scalar.copy(qk[:], qkt_ps).then_inc(qk_ready, 1)
                for b in range(BPG):
                    act.wait_ge(scored, g * BPG + (b + 1))
                    nc.scalar.activation(e[:, b, :, :], s_ps[:, b, :], ACT.Exp).then_inc(exped, 1)
                act.wait_ge(h1_up, g + 1)
                nc.scalar.activation(h1[:], h1_ps[:], ACT.Relu, bias=w["L0a_b1"][:]).then_inc(h1_ready, 1)
                for j in range(4):
                    act.wait_ge(h2_up, g * 4 + (j + 1))
                    nc.scalar.activation(h2[:, j, :], proj[:, j, :], ACT.Relu, bias=w["L0a_b2"][:, j:j + 1]).then_inc(h2_ready, 1)

        @block.vector
        def _(dve):
            dve.wait_ge(loaded, 16 * len(names))
            with dve.Fori(0, GROUPS) as g:
                dve.wait_ge(projected, g + 1)
                nc.vector.tensor_tensor(qkv[:], proj[:, :, 0:3 * D],
                                        w["L0a_bqkv"][:].rearrange("p (a n) -> p a n", a=1).to_broadcast([P, GT, 3 * D]), ALU.add)
                dve.drain()
                nc.vector.tensor_tensor(sq[:], qkv[:, :, 0:2 * D], qkv[:, :, 0:2 * D], ALU.mult)
                dve.drain()
                nc.vector.tensor_reduce(norm[:], sq[:].rearrange("p t (i d) -> p (t i) d", d=D), AX.X, ALU.add).then_inc(squared, 1)
                dve.wait_ge(rooted, g + 1)
                nc.vector.tensor_scalar(norm[:], norm[:], 1e-12, None, ALU.max)
                dve.drain()
                nc.vector.reciprocal(norm[:], norm[:])
                dve.drain()
                for t in range(GT):
                    rows = qkv[:, t, 0:2 * D].rearrange("p (i d) -> p i d", d=D)
                    last = nc.vector.tensor_tensor(rows, rows, per_row(norm[:, 2 * t:2 * t + 2], D), ALU.mult)
                last.then_inc(unit, 1)
                dve.wait_ge(summed, g + 1)
                nc.vector.reciprocal(rden[:], den_ps[:])
                dve.drain()
                nc.vector.tensor_tensor(o[:], o_ps[:], rden[:], ALU.mult).then_inc(mixed, 1)
                dve.wait_ge(y_ready, g + 1)
                x = k.X[:, bass.ds(g * GT, GT), :]
                nc.vector.tensor_tensor(x, x, y_ps[:], ALU.add).then_inc(done, 1)


def l0_attn_b(nc, k, name):
    layer_norm(nc, k, name + "_ln")
    QK = 3 * D
    HD = 8
    with Scope(nc, name) as s:
        names = [("L0b_w", [P, 5 * D]), ("L0b_b", [P, 5 * D]), ("L0b_wo", [P, D]), ("L0b_bo", [1, GROUP]),
                 ("L0b_g", [P, 1]), ("L0b_be", [P, 1]), ("c_heads8", [P, P])]
        w = {n: s.sb(n, shape) for n, shape in names}
        xg, z = s.sb("xg", [P, GROUP]), s.sb("z", [P, GT, 5 * D])
        a, sq = s.sb("a", [P, GT, QK]), s.sb("sq", [P, GT, QK])
        norm = s.sb("norm", [P, GT * QK // HD])
        minus = s.sb("minus", [P, GT])
        qt, state, half_state = s.sb("qt", [P, GROUP]), s.sb("state", [P, BPG, P]), s.sb("half_state", [P, BPG, P])
        stats, mv, rstd = s.sb("stats", [P, GT, 6]), s.sb("mv", [P, GT, 2]), s.sb("rstd", [P, GT])
        on, ont = s.sb("on", [P, GT, D]), s.sb("ont", [P, GROUP])
        proj = s.ps("proj", [P, GT, 4 * D])
        proj_v = s.ps("proj_v", [P, GT, D])
        turned, st_ps, o_ps = s.ps("turned", [P, GROUP]), s.ps("st_ps", [P, BPG, 2, P]), s.ps("o_ps", [P, GT, D])
        loaded, w_ready, xg_ready, projected = s.sem("loaded"), s.sem("w_ready"), s.sem("xg_ready"), s.sem("projected")
        biased, activated, squared, rooted, unit = s.sem("biased"), s.sem("activated"), s.sem("squared"), s.sem("rooted"), s.sem("unit")
        turned_q, qt_ready, stated, state_ready = s.sem("turned_q"), s.sem("qt_ready"), s.sem("stated"), s.sem("state_ready")
        o_ready, var_ready, rstd_ready, on_ready = s.sem("o_ready"), s.sem("var_ready"), s.sem("rstd_ready"), s.sem("on_ready")
        turned_o, ont_ready, y_ready, done = s.sem("turned_o"), s.sem("ont_ready"), s.sem("y_ready"), s.sem("done")
        block = s.block()

        @block.sync
        def _(sp):
            for n, _ in names:
                sp.dma_start(w[n][:], k.dram[n]).then_inc(loaded, 16)

        @block.gpsimd
        def _(pool):
            nc.gpsimd.memset(minus[:], -0.5)
            pool.drain()
            with pool.Fori(0, GROUPS) as g:
                pool.wait_ge(var_ready, g + 1)
                nc.gpsimd.tensor_tensor(rstd[:], rstd[:], minus[:], ALU.pow).then_inc(rstd_ready, 1)

        @block.tensor
        def _(pe):
            pe.wait_ge(w_ready, 1)
            with pe.Fori(0, GROUPS) as g:
                pe.wait_ge(xg_ready, g + 1)
                for t in range(GT):
                    xt = xg[:, t * P:(t + 1) * P]
                    nc.tensor.matmul(proj[:, t, :], xt, w["L0b_w"][:, 0:4 * D], start=True, stop=True)
                    last = nc.tensor.matmul(proj_v[:, t, :], xt, w["L0b_w"][:, 4 * D:5 * D], start=True, stop=True)
                last.then_inc(projected, 1)
                pe.wait_ge(unit, g + 1)
                for t in range(GT):
                    last = nc.tensor.transpose(turned[:, t * P:(t + 1) * P], a[:, t, 0:D], k.ident[:])
                last.then_inc(turned_q, 1)
                for b in range(BPG):
                    for i in range(2):
                        for t in range(TPB):
                            last = nc.tensor.matmul(st_ps[:, b, i, :], a[:, b * TPB + t, (1 + i) * D:(2 + i) * D],
                                                    z[:, b * TPB + t, (3 + i) * D:(4 + i) * D], start=(t == 0), stop=(t == TPB - 1))
                last.then_inc(stated, 1)
                pe.wait_ge(state_ready, g + 1)
                pe.wait_ge(qt_ready, g + 1)
                for t in range(GT):
                    last = nc.tensor.matmul(o_ps[:, t, :], qt[:, t * P:(t + 1) * P], state[:, t // TPB, :], start=True, stop=True)
                last.then_inc(o_ready, 1)
                pe.wait_ge(on_ready, g + 1)
                for t in range(GT):
                    last = nc.tensor.transpose(turned[:, t * P:(t + 1) * P], on[:, t, :], k.ident[:])
                last.then_inc(turned_o, 1)
                nc.tensor.matmul(proj_v[:], k.ones_row[0:1, 0:P], w["L0b_bo"][:], start=True, stop=False, skip_group_check=True)
                pe.wait_ge(ont_ready, g + 1)
                for t in range(GT):
                    last = nc.tensor.matmul(proj_v[:, t, :], ont[:, t * P:(t + 1) * P], w["L0b_wo"][:], start=False, stop=True,
                                            skip_group_check=True)
                last.then_inc(y_ready, 1)

        @block.scalar
        def _(act):
            act.wait_ge(loaded, 16 * len(names))
            with act.Fori(0, GROUPS) as g:
                act.wait_ge(done, g)
                nc.scalar.copy(xg[:], k.XNT[:, bass.ds(g * GROUP, GROUP)]).then_inc(xg_ready, 1)
                act.wait_ge(biased, g + 1)
                nc.scalar.activation(a[:], z[:, :, 0:QK], ACT.Silu).then_inc(activated, 1)
                act.wait_ge(squared, g + 1)
                nc.scalar.activation(norm[:], norm[:], ACT.Sqrt).then_inc(rooted, 1)
                act.wait_ge(turned_q, g + 1)
                nc.scalar.copy(qt[:], turned[:]).then_inc(qt_ready, 1)
                act.wait_ge(turned_o, g + 1)
                nc.scalar.activation(ont[:], turned[:], ACT.Identity, bias=w["L0b_be"][:], scale=w["L0b_g"][:]).then_inc(ont_ready, 1)

        @block.vector
        def _(dve):
            dve.wait_ge(loaded, 16 * len(names))
            for i in range(5):
                last = nc.vector.tensor_tensor(w["L0b_w"][:, i * D:(i + 1) * D], w["L0b_w"][:, i * D:(i + 1) * D], k.ident[:], ALU.add)
            last.then_inc(w_ready, 1)
            with dve.Fori(0, GROUPS) as g:
                dve.wait_ge(projected, g + 1)
                for t in range(GT):
                    nc.vector.tensor_tensor(z[:, t, 0:4 * D], proj[:, t, :], w["L0b_b"][:, 0:4 * D], ALU.add)
                nc.vector.tensor_tensor(z[:, :, 4 * D:5 * D], proj_v[:],
                                        w["L0b_b"][:, 4 * D:5 * D].rearrange("p (a d) -> p a d", a=1).to_broadcast([P, GT, D]),
                                        ALU.add).then_inc(biased, 1)
                dve.wait_ge(activated, g + 1)
                nc.vector.tensor_scalar(a[:], a[:], 0.5, None, ALU.add)
                dve.drain()
                nc.vector.tensor_tensor(sq[:], a[:], a[:], ALU.mult)
                dve.drain()
                nc.vector.tensor_reduce(norm[:], sq[:].rearrange("p t (h d) -> p (t h) d", d=HD), AX.X, ALU.add).then_inc(squared, 1)
                dve.wait_ge(rooted, g + 1)
                nc.vector.tensor_scalar(norm[:], norm[:], 1e-6, None, ALU.add)
                dve.drain()
                nc.vector.reciprocal(norm[:], norm[:])
                dve.drain()
                heads = a[:].rearrange("p t (h d) -> p (t h) d", d=HD)
                nc.vector.tensor_tensor(heads, heads, per_row(norm[:], HD), ALU.mult).then_inc(unit, 1)
                dve.wait_ge(stated, g + 1)
                for b in range(BPG):
                    nc.vector.scalar_tensor_tensor(out=half_state[:, b, :], in0=st_ps[:, b, 0, :], scalar=1.0 / SEQ ** 2,
                                                   in1=w["c_heads8"][:], op0=ALU.mult, op1=ALU.mult)
                dve.drain()
                for b in range(BPG):
                    last = nc.vector.tensor_tensor(state[:, b, :], half_state[:, b, :], st_ps[:, b, 1, :], ALU.mult)
                last.then_inc(state_ready, 1)
                dve.wait_ge(o_ready, g + 1)
                group_norm_rows(nc, dve, o_ps, stats, mv)
                nc.vector.tensor_scalar(rstd[:], mv[:, :, 1], 1e-5, None, ALU.add).then_inc(var_ready, 1)
                dve.wait_ge(rstd_ready, g + 1)
                for t in range(GT):
                    last = nc.vector.tensor_scalar(on[:, t, :], o_ps[:, t, :], mv[:, t, 0:1], rstd[:, t:t + 1], ALU.subtract, ALU.mult)
                last.then_inc(on_ready, 1)
                dve.wait_ge(y_ready, g + 1)
                x = k.X[:, bass.ds(g * GT, GT), :]
                nc.vector.tensor_tensor(x, x, proj_v[:], ALU.add).then_inc(done, 1)


def l3_attn_b(nc, k, name):
    layer_norm(nc, k, name + "_ln")
    HD, CH = 8, 4
    with Scope(nc, name) as s:
        names = [("L3b_w", [P, 3 * D]), ("L3b_b", [P, 3 * D]), ("L3b_wo", [P, D]), ("L3b_bo", [1, GROUP]),
                 ("L3b_g1", [P, 1]), ("L3b_be1", [P, 1]), ("L3b_g2", [P, D]), ("L3b_be2", [P, D]),
                 ("L3b_w1", [P, CH * P]), ("L3b_b1", [P, CH]), ("L3b_w2", [P, CH * D]), ("L3b_b2", [1, GROUP]),
                 ("c_heads8", [P, P])]
        w = {n: s.sb(n, shape) for n, shape in names}
        xg, z = s.sb("xg", [P, GROUP]), s.sb("z", [P, GT, 3 * D])
        low, sq = s.sb("low", [P, GT, 2 * D]), s.sb("sq", [P, GT, 2 * D])
        norm, minus = s.sb("norm", [P, GT * 2 * D // HD]), s.sb("minus", [P, GT])
        qt, state, ctxt = s.sb("qt", [P, GROUP]), s.sb("state", [P, BPG, P]), s.sb("ctxt", [P, GROUP])
        stats, mv, rstd = s.sb("stats", [P, GT, 6]), s.sb("mv", [P, GT, 2]), s.sb("rstd", [P, GT])
        rows, at, hid = s.sb("rows", [P, GT, D]), s.sb("at", [P, GROUP]), s.sb("hid", [P, CH, GROUP])
        proj = s.ps("proj", [P, GT, 512])
        turned, st_ps, ctx_ps, y_ps = s.ps("turned", [P, GROUP]), s.ps("st_ps", [P, BPG, P]), s.ps("ctx_ps", [P, GROUP]), s.ps("y_ps", [P, GT, D])
        loaded, xg_ready, projected, clipped = s.sem("loaded"), s.sem("xg_ready"), s.sem("projected"), s.sem("clipped")
        exped, squared, rooted, unit = s.sem("exped"), s.sem("squared"), s.sem("rooted"), s.sem("unit")
        turned_q, qt_ready, stated, state_ready = s.sem("turned_q"), s.sem("qt_ready"), s.sem("stated"), s.sem("state_ready")
        ctx_up, ctx_ready, y1_ready, var_ready = s.sem("ctx_up"), s.sem("ctx_ready"), s.sem("y1_ready"), s.sem("var_ready")
        rstd_ready, rows_ready, turned_a, at_ready = s.sem("rstd_ready"), s.sem("rows_ready"), s.sem("turned_a"), s.sem("at_ready")
        hid_up, hid_ready, y2_ready, done = s.sem("hid_up"), s.sem("hid_ready"), s.sem("y2_ready"), s.sem("done")
        block = s.block()

        @block.sync
        def _(sp):
            for n, _ in names:
                sp.dma_start(w[n][:], k.dram[n]).then_inc(loaded, 16)

        @block.gpsimd
        def _(pool):
            nc.gpsimd.memset(minus[:], -0.5)
            pool.drain()
            with pool.Fori(0, GROUPS) as g:
                for i in range(2):
                    pool.wait_ge(var_ready, g * 2 + (i + 1))
                    nc.gpsimd.tensor_tensor(rstd[:], rstd[:], minus[:], ALU.pow).then_inc(rstd_ready, 1)

        @block.tensor
        def _(pe):
            pe.wait_ge(loaded, 16 * len(names))
            with pe.Fori(0, GROUPS) as g:
                pe.wait_ge(xg_ready, g + 1)
                for t in range(GT):
                    last = nc.tensor.matmul(proj[:, t, 0:3 * D], xg[:, t * P:(t + 1) * P], w["L3b_w"][:], start=True, stop=True)
                last.then_inc(projected, 1)
                pe.wait_ge(unit, g + 1)
                for t in range(GT):
                    last = nc.tensor.transpose(turned[:, t * P:(t + 1) * P], low[:, t, 0:D], k.ident[:])
                last.then_inc(turned_q, 1)
                for b in range(BPG):
                    for t in range(TPB):
                        r = b * TPB + t
                        last = nc.tensor.matmul(st_ps[:, b, :], low[:, r, D:2 * D], z[:, r, 2 * D:3 * D], start=(t == 0), stop=(t == TPB - 1))
                last.then_inc(stated, 1)
                pe.wait_ge(state_ready, g + 1)
                pe.wait_ge(qt_ready, g + 1)
                for b in range(BPG):
                    last = nc.tensor.matmul(ctx_ps[:, b * SEQ:(b + 1) * SEQ], state[:, b, :], qt[:, b * SEQ:(b + 1) * SEQ], start=True, stop=True)
                last.then_inc(ctx_up, 1)
                nc.tensor.matmul(y_ps[:], k.ones_row[0:1, 0:P], w["L3b_bo"][:], start=True, stop=False, skip_group_check=True)
                for t in range(GT):
                    nc.tensor.matmul(y_ps[:, t, :], xg[:, t * P:(t + 1) * P], k.ident[:], start=False, stop=False, skip_group_check=True)
                pe.wait_ge(ctx_ready, g + 1)
                for t in range(GT):
                    last = nc.tensor.matmul(y_ps[:, t, :], ctxt[:, t * P:(t + 1) * P], w["L3b_wo"][:], start=False, stop=True,
                                            skip_group_check=True)
                last.then_inc(y1_ready, 1)
                pe.wait_ge(rows_ready, g + 1)
                for t in range(GT):
                    last = nc.tensor.transpose(turned[:, t * P:(t + 1) * P], rows[:, t, :], k.ident[:])
                last.then_inc(turned_a, 1)
                pe.wait_ge(at_ready, g + 1)
                for j in range(CH):
                    nc.tensor.matmul(proj[:, j, :], w["L3b_w1"][:, j * P:(j + 1) * P], at[:], start=True, stop=True).then_inc(hid_up, 1)
                nc.tensor.matmul(y_ps[:], k.ones_row[0:1, 0:P], w["L3b_b2"][:], start=True, stop=False, skip_group_check=True)
                for t in range(GT):
                    nc.tensor.matmul(y_ps[:, t, :], at[:, t * P:(t + 1) * P], k.ident[:], start=False, stop=False, skip_group_check=True)
                for j in range(CH):
                    pe.wait_ge(hid_ready, g * CH + (j + 1))
                    for t in range(GT):
                        last = nc.tensor.matmul(y_ps[:, t, :], hid[:, j, t * P:(t + 1) * P], w["L3b_w2"][:, j * D:(j + 1) * D],
                                                start=False, stop=(j == CH - 1), skip_group_check=True)
                last.then_inc(y2_ready, 1)

        @block.scalar
        def _(act):
            act.wait_ge(loaded, 16 * len(names))
            with act.Fori(0, GROUPS) as g:
                act.wait_ge(done, g)
                nc.scalar.copy(xg[:], k.XNT[:, bass.ds(g * GROUP, GROUP)]).then_inc(xg_ready, 1)
                act.wait_ge(clipped, g + 1)
                nc.scalar.activation(low[:], low[:], ACT.Exp).then_inc(exped, 1)
                act.wait_ge(squared, g + 1)
                nc.scalar.activation(norm[:], norm[:], ACT.Sqrt).then_inc(rooted, 1)
                act.wait_ge(turned_q, g + 1)
                nc.scalar.copy(qt[:], turned[:]).then_inc(qt_ready, 1)
                act.wait_ge(ctx_up, g + 1)
                nc.scalar.copy(ctxt[:], ctx_ps[:]).then_inc(ctx_ready, 1)
                act.wait_ge(turned_a, g + 1)
                nc.scalar.activation(at[:], turned[:], ACT.Identity, bias=w["L3b_be1"][:], scale=w["L3b_g1"][:]).then_inc(at_ready, 1)
                for j in range(CH):
                    act.wait_ge(hid_up, g * CH + (j + 1))
                    nc.scalar.activation(hid[:, j, :], proj[:, j, :], ACT.Gelu, bias=w["L3b_b1"][:, j:j + 1]).then_inc(hid_ready, 1)

        @block.vector
        def _(dve):
            def normalise(g, i):
                group_norm_rows(nc, dve, y_ps, stats, mv)
                nc.vector.tensor_scalar(rstd[:], mv[:, :, 1], 1e-12, None, ALU.add).then_inc(var_ready, 1)
                dve.wait_ge(rstd_ready, g * 2 + (i + 1))
                for t in range(GT):
                    last = nc.vector.tensor_scalar(rows[:, t, :], y_ps[:, t, :], mv[:, t, 0:1], rstd[:, t:t + 1], ALU.subtract, ALU.mult)
                return last

            def over_tiles(ap):
                return ap.rearrange("p (a n) -> p a n", a=1).to_broadcast([P, GT, ap.shape[1]])

            dve.wait_ge(loaded, 16 * len(names))
            with dve.Fori(0, GROUPS) as g:
                dve.wait_ge(projected, g + 1)
                nc.vector.tensor_tensor(z[:], proj[:, :, 0:3 * D], over_tiles(w["L3b_b"][:]), ALU.add)
                dve.drain()
                nc.vector.tensor_scalar(low[:], z[:, :, 0:2 * D], 0.0, None, ALU.min).then_inc(clipped, 1)
                nc.vector.tensor_scalar(z[:, :, 0:2 * D], z[:, :, 0:2 * D], 0.0, None, ALU.max)
                dve.drain()
                dve.wait_ge(exped, g + 1)
                nc.vector.scalar_tensor_tensor(out=low[:], in0=low[:], scalar=-1.0, in1=z[:, :, 0:2 * D], op0=ALU.add, op1=ALU.add)
                dve.drain()
                nc.vector.tensor_tensor(sq[:], low[:], low[:], ALU.mult)
                dve.drain()
                nc.vector.tensor_reduce(norm[:], sq[:].rearrange("p t (h d) -> p (t h) d", d=HD), AX.X, ALU.add).then_inc(squared, 1)
                dve.wait_ge(rooted, g + 1)
                nc.vector.reciprocal(norm[:], norm[:])
                dve.drain()
                heads = low[:].rearrange("p t (h d) -> p (t h) d", d=HD)
                nc.vector.tensor_tensor(heads, heads, per_row(norm[:], HD), ALU.mult).then_inc(unit, 1)
                dve.wait_ge(stated, g + 1)
                for b in range(BPG):
                    last = nc.vector.scalar_tensor_tensor(out=state[:, b, :], in0=st_ps[:, b, :], scalar=HD ** -0.5, in1=w["c_heads8"][:],
                                                          op0=ALU.mult, op1=ALU.mult)
                last.then_inc(state_ready, 1)
                dve.wait_ge(y1_ready, g + 1)
                normalise(g, 0).then_inc(rows_ready, 1)
                dve.wait_ge(y2_ready, g + 1)
                normalise(g, 1)
                dve.drain()
                nc.vector.tensor_tensor(rows[:], rows[:], over_tiles(w["L3b_g2"][:]), ALU.mult)
                dve.drain()
                nc.vector.tensor_tensor(rows[:], rows[:], over_tiles(w["L3b_be2"][:]), ALU.add)
                dve.drain()
                x = k.X[:, bass.ds(g * GT, GT), :]
                nc.vector.tensor_tensor(x, x, rows[:], ALU.add).then_inc(done, 1)


def l3_attn_a(nc, k, name):
    layer_norm(nc, k, name + "_ln")
    H, HD, WIN = 16, 8, 32
    WPT, WPG = P // WIN, GROUP // WIN
    HB = P // WIN
    with Scope(nc, name) as s:
        names = [("L3a_wq", [P, D]), ("L3a_wk", [P, D]), ("L3a_wv", [P, HB * HD]), ("L3a_wo", [P, D]), ("L3a_bo", [1, GROUP]),
                 ("c_head_of_row8", [P, H]), ("c_blocks32x8", [P, HB * HD])]
        w = {n: s.sb(n, shape) for n, shape in names}
        xg, q, kk = s.sb("xg", [P, GROUP]), s.sb("q", [P, GROUP]), s.sb("kk", [P, GROUP])
        xrep = s.sb("xrep", [P, WPG, HB, WIN])
        keys, vals = s.sb("keys", [P, WPG, H, WIN]), s.sb("vals", [P, WPG, HB * HD])
        p, top, den = s.sb("p", [P, GT * H, WIN]), s.sb("top", [P, GT * H]), s.sb("den", [P, GT * H])
        pt, o, ot = s.sb("pt", [P, GT, H // HB, P]), s.sb("o", [P, GT, D]), s.sb("ot", [P, GROUP])
        big_a, big_b = s.ps("big_a", [P, GT, 512]), s.ps("big_b", [P, GT, 512])
        q_ps, k_ps, v_ps, y_ps = (big_a[:, i, :] for i in range(4))
        loaded, xg_ready, xrep_ready, projected = s.sem("loaded"), s.sem("xg_ready"), s.sem("xrep_ready"), s.sem("projected")
        k_ready, qv_ready, keys_ready, scored = s.sem("k_ready"), s.sem("qv_ready"), s.sem("keys_ready"), s.sem("scored")
        shifted, exped, probs_ready, turned = s.sem("shifted"), s.sem("exped"), s.sem("probs_ready"), s.sem("turned")
        pt_ready, o_up, o_ready, turned_o, ot_ready = s.sem("pt_ready"), s.sem("o_up"), s.sem("o_ready"), s.sem("turned_o"), s.sem("ot_ready")
        v_ready, y_ready, done = s.sem("v_ready"), s.sem("y_ready"), s.sem("done")
        block = s.block()

        @block.sync
        def _(sp):
            for n, _ in names:
                sp.dma_start(w[n][:], k.dram[n]).then_inc(loaded, 16)

        @block.tensor
        def _(pe):
            pe.wait_ge(loaded, 16 * len(names))
            with pe.Fori(0, GROUPS) as g:
                pe.wait_ge(xg_ready, g + 1)
                nc.tensor.matmul(k_ps, w["L3a_wk"][:], xg[:], start=True, stop=True)
                nc.tensor.matmul(q_ps, w["L3a_wq"][:], xg[:], start=True, stop=True)
                pe.wait_ge(xrep_ready, g + 1)
                for n in range(WPG):
                    last = nc.tensor.matmul(v_ps[:, n * HB * HD:(n + 1) * HB * HD], xrep[:, n, :, :].rearrange("p h u -> p (h u)"),
                                            w["L3a_wv"][:], start=True, stop=True)
                last.then_inc(projected, 1)
                pe.wait_ge(qv_ready, g + 1)
                pe.wait_ge(v_ready, g + 1)
                pe.wait_ge(keys_ready, g + 1)
                for t in range(GT):
                    for i in range(WPT):
                        n = t * WPT + i
                        last = nc.tensor.matmul(big_a[i * WIN:(i + 1) * WIN, t, :], q[:, n * WIN:(n + 1) * WIN],
                                                keys[:, n, :, :].rearrange("p h u -> p (h u)"), start=True, stop=True)
                last.then_inc(scored, 1)
                pe.wait_ge(probs_ready, g + 1)
                for t in range(GT):
                    for c in range(H // HB):
                        last = nc.tensor.transpose(big_b[:, t, c * P:(c + 1) * P],
                                                   p[:, t * H + c * HB:t * H + (c + 1) * HB, :].rearrange("p h u -> p (h u)"), k.ident[:])
                last.then_inc(turned, 1)
                pe.wait_ge(pt_ready, g + 1)
                for t in range(GT):
                    for c in range(H // HB):
                        for i in range(WPT):
                            last = nc.tensor.matmul(big_a[i * WIN:(i + 1) * WIN, 0, t * D + c * HB * HD:t * D + (c + 1) * HB * HD],
                                                    pt[:, t, c, i * WIN:(i + 1) * WIN], vals[:, t * WPT + i, :], start=True, stop=True)
                last.then_inc(o_up, 1)
                pe.wait_ge(o_ready, g + 1)
                for t in range(GT):
                    last = nc.tensor.transpose(big_a[:, 1, t * P:(t + 1) * P], o[:, t, :], k.ident[:])
                last.then_inc(turned_o, 1)
                nc.tensor.matmul(y_ps, k.ones_row[0:1, 0:P], w["L3a_bo"][:], start=True, stop=False, skip_group_check=True)
                pe.wait_ge(ot_ready, g + 1)
                for t in range(GT):
                    last = nc.tensor.matmul(y_ps[:, t * D:(t + 1) * D], ot[:, t * P:(t + 1) * P], w["L3a_wo"][:], start=False, stop=True,
                                            skip_group_check=True)
                last.then_inc(y_ready, 1)

        @block.scalar
        def _(act):
            with act.Fori(0, GROUPS) as g:
                act.wait_ge(done, g)
                xnt = k.XNT[:, bass.ds(g * GROUP, GROUP)]
                nc.scalar.copy(xg[:], xnt).then_inc(xg_ready, 1)
                act.wait_ge(projected, g + 1)
                nc.scalar.copy(kk[:], k_ps).then_inc(k_ready, 1)
                nc.scalar.copy(q[:], q_ps).then_inc(qv_ready, 1)
                act.wait_ge(shifted, g + 1)
                nc.scalar.activation(p[:], p[:], ACT.Exp, scale=HD ** -0.5).then_inc(exped, 1)
                act.wait_ge(turned, g + 1)
                nc.scalar.copy(pt[:].rearrange("p t c n -> p t (c n)"), big_b[:]).then_inc(pt_ready, 1)
                act.wait_ge(o_up, g + 1)
                nc.scalar.copy(o[:].rearrange("p t d -> p (t d)"), big_a[:, 0, :]).then_inc(o_ready, 1)
                act.wait_ge(turned_o, g + 1)
                nc.scalar.copy(ot[:], big_a[:, 1, :]).then_inc(ot_ready, 1)

        @block.vector
        def _(dve):
            dve.wait_ge(loaded, 16 * len(names))
            with dve.Fori(0, GROUPS) as g:
                dve.wait_ge(xg_ready, g + 1)
                for h in range(HB):
                    last = nc.vector.tensor_copy(xrep[:, :, h, :], xg[:].rearrange("p (n u) -> p n u", u=WIN))
                last.then_inc(xrep_ready, 1)
                dve.wait_ge(projected, g + 1)
                blocks = w["c_blocks32x8"][:].rearrange("p (a n) -> p a n", a=1).to_broadcast([P, WPG, HB * HD])
                nc.vector.tensor_tensor(vals[:], v_ps.rearrange("p (w n) -> p w n", w=WPG), blocks, ALU.mult).then_inc(v_ready, 1)
                dve.wait_ge(k_ready, g + 1)
                for h in range(H):
                    last = nc.vector.tensor_scalar(keys[:, :, h, :], kk[:].rearrange("p (n u) -> p n u", u=WIN),
                                                   w["c_head_of_row8"][:, h:h + 1], None, ALU.mult)
                last.then_inc(keys_ready, 1)
                dve.wait_ge(scored, g + 1)
                scores = big_a[:].rearrange("p t (h u) -> p (t h) u", u=WIN)
                nc.vector.tensor_reduce(top[:], scores, AX.X, ALU.max)
                dve.drain()
                nc.vector.tensor_tensor(p[:], scores, per_row(top[:], WIN), ALU.subtract).then_inc(shifted, 1)
                dve.wait_ge(exped, g + 1)
                nc.vector.tensor_reduce(den[:], p[:], AX.X, ALU.add)
                dve.drain()
                nc.vector.reciprocal(den[:], den[:])
                dve.drain()
                nc.vector.tensor_tensor(p[:], p[:], per_row(den[:], WIN), ALU.mult).then_inc(probs_ready, 1)
                dve.wait_ge(y_ready, g + 1)
                x = k.X[:, bass.ds(g * GT, GT), :]
                nc.vector.tensor_tensor(x, x, y_ps.rearrange("p (t d) -> p t d", d=D), ALU.add).then_inc(done, 1)

ED, CHH, NST = 256, 2, 16


class StateScan:

    def __init__(self, nc, k, s, bc, b_row, c_row, delta, dx, a, spread, y_ps):
        self.nc, self.k, self.bc, self.b_row, self.c_row = nc, k, bc, b_row, c_row
        self.delta, self.dx, self.a, self.spread, self.y_ps = delta, dx, a, spread, y_ps
        self.da = [s.sb(f"da{i}", [P, CHH, BPG, SEQ]) for i in range(2)]
        self.u, self.h = s.sb("u", [P, CHH, GROUP]), s.sb("h", [P, CHH, GROUP])
        self.hc = [s.sb(f"hc{i}", [P, CHH, GROUP]) for i in range(2)]
        self.zeros = s.sb("zeros", [P, CHH, BPG])
        self.spread_ready, self.da_ready, self.reset = s.sem("spread_ready"), s.sem("da_ready"), s.sem("reset")
        self.hc_ready, self.summed = s.sem("hc_ready"), s.sem("summed")

    def pe(self, pe, g):
        nc = self.nc

        def spread(n):
            rows = self.bc.shape[0]
            for i, row in enumerate((self.b_row + n, self.c_row + n)):
                last = nc.tensor.matmul(self.spread[:, 2 * (n % 2) + i, :], self.k.ident[0:rows, row:row + 1].to_broadcast([rows, P]),
                                        self.bc[:], start=True, stop=True)
            last.then_inc(self.spread_ready, 1)

        spread(0)
        spread(1)
        for n in range(NST):
            pe.wait_ge(self.hc_ready, g * NST + (n + 1))
            for i in range(CHH):
                last = nc.tensor.matmul(self.y_ps[:, i, :], self.k.ident[:], self.hc[n % 2][:, i, :], start=(n == 0), stop=(n == NST - 1))
            if n + 2 < NST:
                spread(n + 2)
        last.then_inc(self.summed, 1)

    def act(self, act, g):
        for n in range(NST):
            if n >= 2:
                act.wait_ge(self.hc_ready, g * NST + (n - 1))
            for i in range(CHH):
                last = self.nc.scalar.activation(self.da[n % 2][:, i, :, :].rearrange("p b t -> p (b t)"), self.delta[:, i, :], ACT.Exp,
                                                 scale=self.a[:, i * NST + n:i * NST + n + 1])
            last.then_inc(self.da_ready, 1)

    def pool(self, pool, g):
        for n in range(NST):
            pool.wait_ge(self.da_ready, g * NST + (n + 1))
            starts = self.da[n % 2][:, :, :, 0]
            self.nc.gpsimd.tensor_tensor(starts, starts, self.zeros[:], ALU.mult).then_inc(self.reset, 1)

    def dve(self, dve, g):
        nc = self.nc
        for n in range(NST):
            def spread(i):
                return self.spread[:, 2 * (n % 2) + i, :].rearrange("p (a t) -> p a t", a=1).to_broadcast([P, CHH, GROUP])
            dve.wait_ge(self.spread_ready, g * NST + (n + 1))
            nc.vector.tensor_tensor(self.u[:], self.dx[:], spread(0), ALU.mult)
            dve.drain()
            dve.wait_ge(self.reset, g * NST + (n + 1))
            nc.vector.tensor_tensor_scan(self.h[:].rearrange("p i t -> p (i t)"), self.da[n % 2][:].rearrange("p i b t -> p (i b t)"),
                                         self.u[:].rearrange("p i t -> p (i t)"), 0.0, ALU.mult, ALU.add)
            dve.drain()
            nc.vector.tensor_tensor(self.hc[n % 2][:], self.h[:], spread(1), ALU.mult).then_inc(self.hc_ready, 1)


def l1_attn_a(nc, k, name):
    layer_norm(nc, k, name + "_ln")
    R, TAPS = 64, 4
    with Scope(nc, name) as s:
        names = [("L1a_win", [P, 4 * P]), ("L1a_conv", [P, CHH * TAPS]), ("L1a_wx", [P, CHH * (R + 2 * NST)]), ("L1a_wdt", [R, ED]),
                 ("L1a_bdt", [P, CHH]), ("L1a_alog", [P, CHH * NST]), ("L1a_d", [P, CHH]), ("L1a_wout", [P, CHH * D])]
        w = {n: s.sb(n, shape) for n, shape in names}
        F = R + 2 * NST
        a = s.sb("a", [P, CHH * NST])
        padded = s.sb("padded", [P, CHH, BPG, TAPS - 1 + SEQ])
        xc, z, bc = s.sb("xc", [P, CHH, BPG, SEQ]), s.sb("z", [P, CHH, GROUP]), s.sb("bc", [F, GROUP])
        raw, soft, delta, dx = s.sb("raw", [P, CHH, GROUP]), s.sb("soft", [P, CHH, GROUP]), s.sb("delta", [P, CHH, GROUP]), s.sb("dx", [P, CHH, GROUP])
        y = s.sb("y", [P, CHH, GROUP])
        big, y_ps = s.ps("big", [P, 4, GROUP]), s.ps("y_ps", [P, CHH, GROUP])
        bc_ps, out_ps = s.ps("bc_ps", [F, GROUP]), s.ps("out_ps", [P, GT, D])
        scan = StateScan(nc, k, s, bc, R, R + NST, delta, dx, a, big, y_ps)
        loaded, a_exp, a_ready, cleared = s.sem("loaded"), s.sem("a_exp"), s.sem("a_ready"), s.sem("cleared")
        projected, padded_ready, conv_ready, xc_ready = s.sem("projected"), s.sem("padded_ready"), s.sem("conv_ready"), s.sem("xc_ready")
        bc_up, bc_ready, dt_up, raw_ready = s.sem("bc_up"), s.sem("bc_ready"), s.sem("dt_up"), s.sem("raw_ready")
        soft_ready, delta_ready, y_ready, out_ready, done = s.sem("soft_ready"), s.sem("delta_ready"), s.sem("y_ready"), s.sem("out_ready"), s.sem("done")
        block = s.block()

        @block.sync
        def _(sp):
            for n, _ in names:
                sp.dma_start(w[n][:], k.dram[n]).then_inc(loaded, 16)

        @block.tensor
        def _(pe):
            pe.wait_ge(loaded, 16 * len(names))
            with pe.Fori(0, GROUPS) as g:
                pe.wait_ge(done, g)
                xn = k.XNT[:, bass.ds(g * GROUP, GROUP)]
                for j in range(4):
                    last = nc.tensor.matmul(big[:, j, :], w["L1a_win"][:, j * P:(j + 1) * P], xn, start=True, stop=True)
                last.then_inc(projected, 1)
                pe.wait_ge(xc_ready, g + 1)
                for i in range(CHH):
                    last = nc.tensor.matmul(bc_ps[:], w["L1a_wx"][:, i * F:(i + 1) * F], xc[:, i, :, :].rearrange("p b t -> p (b t)"),
                                            start=(i == 0), stop=(i == 1))
                last.then_inc(bc_up, 1)
                pe.wait_ge(bc_ready, g + 1)
                for i in range(CHH):
                    last = nc.tensor.matmul(y_ps[:, i, :], w["L1a_wdt"][:, i * P:(i + 1) * P], bc[0:R, :], start=True, stop=True)
                last.then_inc(dt_up, 1)
                pe.wait_ge(delta_ready, g + 1)
                scan.pe(pe, g)
                pe.wait_ge(y_ready, g + 1)
                for i in range(CHH):
                    for t in range(GT):
                        last = nc.tensor.matmul(out_ps[:, t, :], y[:, i, t * P:(t + 1) * P], w["L1a_wout"][:, i * D:(i + 1) * D],
                                                start=(i == 0 and t == 0), stop=(i == 1), skip_group_check=True)
                last.then_inc(out_ready, 1)

        @block.gpsimd
        def _(pool):
            nc.gpsimd.memset(padded[:, :, :, 0:TAPS - 1], 0.0).then_inc(cleared, 1)
            nc.gpsimd.memset(scan.zeros[:], 0.0)
            pool.drain()
            with pool.Fori(0, GROUPS) as g:
                scan.pool(pool, g)

        @block.scalar
        def _(act):
            act.wait_ge(loaded, 16 * len(names))
            nc.scalar.activation(a[:], w["L1a_alog"][:], ACT.Exp).then_inc(a_exp, 1)
            act.wait_ge(a_ready, 1)
            with act.Fori(0, GROUPS) as g:
                act.wait_ge(projected, g + 1)
                nc.scalar.copy(padded[:, :, :, TAPS - 1:], big[:, 0:2, :].rearrange("p i (b t) -> p i b t", b=BPG)).then_inc(padded_ready, 1)
                nc.scalar.activation(z[:], big[:, 2:4, :], ACT.Silu)
                act.wait_ge(conv_ready, g + 1)
                nc.scalar.activation(xc[:], y[:].rearrange("p i (b t) -> p i b t", b=BPG), ACT.Silu).then_inc(xc_ready, 1)
                act.wait_ge(bc_up, g + 1)
                nc.scalar.copy(bc[:], bc_ps[:]).then_inc(bc_ready, 1)
                act.wait_ge(raw_ready, g + 1)
                nc.scalar.activation(soft[:], soft[:], ACT.Exp)
                act.drain()
                nc.scalar.activation(soft[:], soft[:], ACT.Ln, bias=1.0).then_inc(soft_ready, 1)
                act.wait_ge(delta_ready, g + 1)
                scan.act(act, g)

        @block.vector
        def _(dve):
            dve.wait_ge(a_exp, 1)
            nc.vector.tensor_scalar(a[:], a[:], -1.0, None, ALU.mult).then_inc(a_ready, 1)
            dve.wait_ge(loaded, 16 * len(names))
            dve.wait_ge(cleared, 1)
            with dve.Fori(0, GROUPS) as g:
                dve.wait_ge(padded_ready, g + 1)
                for j in range(TAPS):
                    for i in range(CHH):
                        out = y[:, i, :].rearrange("p (b t) -> p b t", b=BPG)
                        tap = w["L1a_conv"][:, i * TAPS + j:i * TAPS + j + 1]
                        if j == 0:
                            last = nc.vector.tensor_scalar(out, padded[:, i, :, j:j + SEQ], tap, None, ALU.mult)
                        else:
                            last = nc.vector.scalar_tensor_tensor(out=out, in0=padded[:, i, :, j:j + SEQ], scalar=tap, in1=out,
                                                                  op0=ALU.mult, op1=ALU.add)
                    if j < TAPS - 1:
                        dve.drain()
                last.then_inc(conv_ready, 1)
                dve.wait_ge(dt_up, g + 1)
                for i in range(CHH):
                    nc.vector.tensor_scalar(raw[:, i, :], y_ps[:, i, :], w["L1a_bdt"][:, i:i + 1], None, ALU.add)
                dve.drain()
                nc.vector.scalar_tensor_tensor(out=soft[:], in0=raw[:], scalar=-1.0, in1=raw[:], op0=ALU.mult, op1=ALU.min).then_inc(raw_ready, 1)
                dve.wait_ge(soft_ready, g + 1)
                nc.vector.scalar_tensor_tensor(out=delta[:], in0=raw[:], scalar=0.0, in1=soft[:], op0=ALU.max, op1=ALU.add)
                dve.drain()
                nc.vector.tensor_tensor(dx[:], delta[:], xc[:].rearrange("p i b t -> p i (b t)"), ALU.mult).then_inc(delta_ready, 1)
                dve.drain()
                scan.dve(dve, g)
                dve.wait_ge(scan.summed, g + 1)
                for i in range(CHH):
                    nc.vector.scalar_tensor_tensor(out=y[:, i, :], in0=xc[:, i, :, :].rearrange("p b t -> p (b t)"), scalar=w["L1a_d"][:, i:i + 1],
                                                   in1=y_ps[:, i, :], op0=ALU.mult, op1=ALU.add)
                dve.drain()
                nc.vector.tensor_tensor(y[:], y[:], z[:], ALU.mult).then_inc(y_ready, 1)
                dve.wait_ge(out_ready, g + 1)
                x = k.X[:, bass.ds(g * GT, GT), :]
                nc.vector.tensor_tensor(x, x, out_ps[:], ALU.add).then_inc(done, 1)


def l2_attn_a(nc, k, name):
    layer_norm(nc, k, name + "_ln")
    RMS_EPS, A_FLOOR = float(np.finfo(np.float32).eps), 1e-4
    HALF_TURN, TURN = float(np.pi), 2 * float(np.pi)
    TURN_HI = 6.28125
    TURN_LO = TURN - TURN_HI
    ROUND = 1.5 * 2.0 ** 23
    BC, DT, LAM = 2 * NST, 32, 64
    F = LAM + 1
    with Scope(nc, name) as s:
        names = [("L2a_win", [P, 4 * P]), ("L2a_wx", [P, CHH * F]), ("L2a_bdt", [P, CHH]), ("L2a_alog", [P, CHH * NST]),
                 ("L2a_d", [P, CHH]), ("L2a_wout", [P, CHH * D]), ("L2a_bias", [BC, 1]), ("L2a_norm", [BC, 1]), ("L2a_freq", [BC, 1]),
                 ("c_mean16", [BC, P]), ("c_quarter_turn", [BC, BC]), ("c_not_first", [BC, GROUP])]
        w = {n: s.sb(n, shape) for n, shape in names}
        wdt = s.sb("wdt", [DT + 1, ED])
        a, freq, fsoft = s.sb("a", [P, CHH * NST]), s.sb("freq", [BC, 1]), s.sb("fsoft", [BC, 1])
        xp, z, ssm = s.sb("xp", [P, CHH, GROUP]), s.sb("z", [P, CHH, GROUP]), s.sb("ssm", [F, GROUP])
        v, vsq, bc, cb = s.sb("v", [BC, GROUP]), s.sb("vsq", [BC, GROUP]), s.sb("bc", [BC, GROUP]), s.sb("cb", [NST, GROUP])
        cum, ang, turns = s.sb("cum", [BC, GROUP]), s.sb("ang", [BC, 2, GROUP]), s.sb("turns", [BC, 2, GROUP])
        raw, soft, delta = s.sb("raw", [P, CHH, GROUP]), s.sb("soft", [P, CHH, GROUP]), s.sb("delta", [P, CHH, GROUP])
        lam, ahead, dx = s.sb("lam", [P, GROUP]), s.sb("ahead", [P, CHH, BPG, SEQ]), s.sb("dx", [P, CHH, GROUP])
        y = s.sb("y", [P, CHH, GROUP])
        big, y_ps = s.ps("big", [P, 4, GROUP]), s.ps("y_ps", [P, CHH, GROUP])
        small, out_ps = s.ps("small", [P, GROUP]), s.ps("out_ps", [P, GT, D])
        scan = StateScan(nc, k, s, bc, 0, NST, delta, dx, a, big, y_ps)
        loaded, consts_exp, consts_ready, cleared = s.sem("loaded"), s.sem("consts_exp"), s.sem("consts_ready"), s.sem("cleared")
        projected, xp_ready, ssm_up, ssm_ready = s.sem("projected"), s.sem("xp_ready"), s.sem("ssm_up"), s.sem("ssm_ready")
        dt_up, raw_ready, soft_ready, lam_ready = s.sem("dt_up"), s.sem("raw_ready"), s.sem("soft_ready"), s.sem("lam_ready")
        delta_ready, vsq_ready, mean_up, root_ready = s.sem("delta_ready"), s.sem("vsq_ready"), s.sem("mean_up"), s.sem("root_ready")
        v_ready, turned, ang_ready, sin_ready = s.sem("v_ready"), s.sem("turned"), s.sem("ang_ready"), s.sem("sin_ready")
        bc_ready, c_up, cb_ready, cb_up = s.sem("bc_ready"), s.sem("c_up"), s.sem("cb_ready"), s.sem("cb_up")
        y_ready, out_ready, done = s.sem("y_ready"), s.sem("out_ready"), s.sem("done")
        block = s.block()
        n_loads = len(names) + 1

        @block.sync
        def _(sp):
            for n, _ in names:
                sp.dma_start(w[n][:], k.dram[n]).then_inc(loaded, 16)
            sp.dma_start(wdt[DT:DT + 1, :], k.dram["L2a_wdt"]).then_inc(loaded, 16)

        @block.tensor
        def _(pe):
            pe.wait_ge(loaded, 16 * n_loads)
            with pe.Fori(0, GROUPS) as g:
                pe.wait_ge(done, g)
                xn = k.XNT[:, bass.ds(g * GROUP, GROUP)]
                for j in range(4):
                    last = nc.tensor.matmul(big[:, j, :], w["L2a_win"][:, j * P:(j + 1) * P], xn, start=True, stop=True)
                last.then_inc(projected, 1)
                pe.wait_ge(xp_ready, g + 1)
                for i in range(CHH):
                    last = nc.tensor.matmul(small[0:F, :], w["L2a_wx"][:, i * F:(i + 1) * F], xp[:, i, :], start=(i == 0), stop=(i == 1))
                last.then_inc(ssm_up, 1)
                pe.wait_ge(ssm_ready, g + 1)
                for i in range(CHH):
                    nc.tensor.matmul(y_ps[:, i, :], wdt[DT:DT + 1, i * P:(i + 1) * P], ssm[DT:DT + 1, :], start=True, stop=True)
                nc.tensor.matmul(out_ps[:].rearrange("p t d -> p (t d)"), k.ones[LAM:LAM + 1, :], ssm[LAM:LAM + 1, :], start=True, stop=True)\
                    .then_inc(dt_up, 1)
                pe.wait_ge(vsq_ready, g + 1)
                nc.tensor.matmul(small[:], w["c_mean16"][:], vsq[:], start=True, stop=True).then_inc(mean_up, 1)
                pe.wait_ge(delta_ready, g + 1)
                pe.wait_ge(v_ready, g + 1)
                for i in range(CHH):
                    nc.tensor.matmul(big[0:BC, 0, :], k.ones[:, 0:BC], delta[:, i, :], start=(i == 0), stop=(i == 1))
                nc.tensor.matmul(big[0:BC, 1, :], w["c_quarter_turn"][:], v[:], start=True, stop=True).then_inc(turned, 1)
                pe.wait_ge(bc_ready, g + 1)
                nc.tensor.matmul(small[0:P - NST, :], k.ident[0:BC, NST:P], bc[:], start=True, stop=True).then_inc(c_up, 1)
                pe.wait_ge(cb_ready, g + 1)
                nc.tensor.matmul(small[:], k.ones[0:NST, :], cb[:], start=True, stop=True).then_inc(cb_up, 1)
                scan.pe(pe, g)
                pe.wait_ge(y_ready, g + 1)
                for i in range(CHH):
                    for t in range(GT):
                        last = nc.tensor.matmul(out_ps[:, t, :], y[:, i, t * P:(t + 1) * P], w["L2a_wout"][:, i * D:(i + 1) * D],
                                                start=(i == 0 and t == 0), stop=(i == 1), skip_group_check=True)
                last.then_inc(out_ready, 1)

        @block.gpsimd
        def _(pool):
            nc.gpsimd.memset(ahead[:, :, :, SEQ - 1:SEQ], 0.0).then_inc(cleared, 1)
            nc.gpsimd.memset(scan.zeros[:], 0.0)
            pool.drain()
            with pool.Fori(0, GROUPS) as g:
                scan.pool(pool, g)

        @block.scalar
        def _(act):
            act.wait_ge(loaded, 16 * n_loads)
            nc.scalar.activation(a[:], w["L2a_alog"][:], ACT.Exp)
            act.wait_ge(cleared, 2)
            nc.scalar.activation(fsoft[:], fsoft[:], ACT.Exp)
            act.drain()
            nc.scalar.activation(fsoft[:], fsoft[:], ACT.Ln, bias=1.0).then_inc(consts_exp, 1)
            act.wait_ge(consts_ready, 1)
            with act.Fori(0, GROUPS) as g:
                act.wait_ge(projected, g + 1)
                nc.scalar.activation(xp[:], big[:, 0:2, :], ACT.Silu).then_inc(xp_ready, 1)
                nc.scalar.activation(z[:], big[:, 2:4, :], ACT.Silu)
                act.wait_ge(ssm_up, g + 1)
                nc.scalar.copy(ssm[:], small[0:F, :]).then_inc(ssm_ready, 1)
                act.wait_ge(dt_up, g + 1)
                nc.scalar.activation(lam[:], out_ps[:].rearrange("p t d -> p (t d)"), ACT.Sigmoid).then_inc(lam_ready, 1)
                act.wait_ge(raw_ready, g + 1)
                nc.scalar.activation(soft[:], soft[:], ACT.Exp)
                act.drain()
                nc.scalar.activation(soft[:], soft[:], ACT.Ln, bias=1.0).then_inc(soft_ready, 1)
                act.wait_ge(mean_up, g + 1)
                nc.scalar.activation(vsq[:], small[0:BC, :], ACT.Sqrt, bias=RMS_EPS).then_inc(root_ready, 1)
                act.wait_ge(ang_ready, g + 1)
                nc.scalar.activation(turns[:], ang[:], ACT.Sin).then_inc(sin_ready, 1)
                act.wait_ge(cb_ready, g + 1)
                scan.act(act, g)

        @block.vector
        def _(dve):
            dve.wait_ge(loaded, 16 * n_loads)
            nc.vector.scalar_tensor_tensor(out=fsoft[:], in0=w["L2a_freq"][:], scalar=-1.0, in1=w["L2a_freq"][:],
                                           op0=ALU.mult, op1=ALU.min).then_inc(cleared, 1)
            dve.wait_ge(consts_exp, 1)
            nc.vector.tensor_scalar(a[:], a[:], -1.0, -A_FLOOR, ALU.mult, ALU.min)
            nc.vector.scalar_tensor_tensor(out=freq[:], in0=w["L2a_freq"][:], scalar=0.0, in1=fsoft[:], op0=ALU.max, op1=ALU.add)
            dve.drain()
            nc.vector.tensor_scalar(freq[:], freq[:], 1.0 / ED, None, ALU.mult).then_inc(consts_ready, 1)
            dve.drain()
            with dve.Fori(0, GROUPS) as g:
                dve.wait_ge(ssm_ready, g + 1)
                nc.vector.tensor_scalar(v[:], ssm[0:BC, :], w["L2a_bias"][:], None, ALU.add)
                dve.drain()
                nc.vector.tensor_tensor(vsq[:], v[:], v[:], ALU.mult).then_inc(vsq_ready, 1)
                dve.wait_ge(dt_up, g + 1)
                for i in range(CHH):
                    nc.vector.tensor_scalar(raw[:, i, :], y_ps[:, i, :], w["L2a_bdt"][:, i:i + 1], None, ALU.add)
                dve.drain()
                nc.vector.scalar_tensor_tensor(out=soft[:], in0=raw[:], scalar=-1.0, in1=raw[:], op0=ALU.mult, op1=ALU.min).then_inc(raw_ready, 1)
                dve.wait_ge(soft_ready, g + 1)
                nc.vector.scalar_tensor_tensor(out=delta[:], in0=raw[:], scalar=0.0, in1=soft[:], op0=ALU.max, op1=ALU.add).then_inc(delta_ready, 1)
                dve.drain()
                dve.wait_ge(lam_ready, g + 1)
                nc.vector.tensor_tensor(raw[:], delta[:], lam[:].rearrange("p (a t) -> p a t", a=1).to_broadcast([P, CHH, GROUP]), ALU.mult)
                dve.drain()
                by_seq = [b[:].rearrange("p i (b t) -> p i b t", b=BPG) for b in (delta, raw, xp)]
                for i in range(CHH):
                    nc.vector.tensor_tensor(ahead[:, i, :, 0:SEQ - 1], by_seq[0][:, i, :, 1:SEQ], by_seq[1][:, i, :, 1:SEQ], ALU.subtract)
                nc.vector.tensor_copy(by_seq[1][:, :, :, 0:1], by_seq[0][:, :, :, 0:1])
                dve.drain()
                ahead_x = ahead[:].rearrange("p i b t -> p i (b t)")
                nc.vector.tensor_tensor(dx[:], raw[:], ahead_x, ALU.add)
                dve.drain()
                nc.vector.tensor_tensor(dx[:], dx[:], xp[:], ALU.mult)
                nc.vector.tensor_tensor(soft[:], ahead_x, xp[:], ALU.mult)
                dve.wait_ge(root_ready, g + 1)
                nc.vector.reciprocal(vsq[:], vsq[:])
                dve.drain()
                nc.vector.scalar_tensor_tensor(out=v[:], in0=v[:], scalar=w["L2a_norm"][:], in1=vsq[:], op0=ALU.mult, op1=ALU.mult).then_inc(v_ready, 1)
                dve.wait_ge(turned, g + 1)
                nc.vector.tensor_tensor_scan(cum[:], w["c_not_first"][:], big[0:BC, 0, :], 0.0, ALU.mult, ALU.add)
                dve.drain()
                nc.vector.tensor_scalar(ang[:, 0, :], cum[:], freq[:], None, ALU.mult)
                nc.vector.tensor_scalar(ang[:, 1, :], cum[:], freq[:], HALF_TURN / 2, ALU.mult, ALU.add)
                dve.drain()
                nc.vector.tensor_scalar(turns[:], ang[:], 1.0 / TURN, ROUND, ALU.mult, ALU.add)
                dve.drain()
                nc.vector.tensor_scalar(turns[:], turns[:], -ROUND, None, ALU.add)
                dve.drain()
                nc.vector.scalar_tensor_tensor(out=ang[:], in0=turns[:], scalar=-TURN_HI, in1=ang[:], op0=ALU.mult, op1=ALU.add)
                dve.drain()
                nc.vector.scalar_tensor_tensor(out=ang[:], in0=turns[:], scalar=-TURN_LO, in1=ang[:], op0=ALU.mult, op1=ALU.add)
                dve.drain()
                nc.vector.tensor_scalar(ang[:], ang[:], 3.1415925, -3.1415925, ALU.min, ALU.max).then_inc(ang_ready, 1)
                dve.wait_ge(sin_ready, g + 1)
                nc.vector.tensor_tensor(cum[:], big[0:BC, 1, :], turns[:, 0, :], ALU.mult)
                nc.vector.tensor_tensor(v[:], v[:], turns[:, 1, :], ALU.mult)
                dve.drain()
                nc.vector.tensor_tensor(bc[:], v[:], cum[:], ALU.add).then_inc(bc_ready, 1)
                dve.wait_ge(c_up, g + 1)
                nc.vector.tensor_tensor(cb[:], bc[0:NST, :], small[0:NST, :], ALU.mult).then_inc(cb_ready, 1)
                dve.wait_ge(cb_up, g + 1)
                for i in range(CHH):
                    nc.vector.tensor_tensor(raw[:, i, :], soft[:, i, :], small[:], ALU.mult)
                dve.drain()
                for i in range(CHH):
                    nc.vector.scalar_tensor_tensor(out=y[:, i, :], in0=xp[:, i, :], scalar=w["L2a_d"][:, i:i + 1], in1=raw[:, i, :],
                                                   op0=ALU.mult, op1=ALU.subtract)
                dve.drain()
                scan.dve(dve, g)
                dve.wait_ge(scan.summed, g + 1)
                nc.vector.tensor_tensor(y[:], y[:], y_ps[:], ALU.add)
                dve.drain()
                nc.vector.tensor_tensor(y[:], y[:], z[:], ALU.mult).then_inc(y_ready, 1)
                dve.wait_ge(out_ready, g + 1)
                x = k.X[:, bass.ds(g * GT, GT), :]
                nc.vector.tensor_tensor(x, x, out_ps[:], ALU.add).then_inc(done, 1)


def l2_attn_b(nc, k, name):
    layer_norm(nc, k, name + "_ln")
    H, ROT = 8, 64
    AW = P + SEQ
    GN = D // 16
    with Scope(nc, name) as s:
        names = [("L2b_wQ", [P, H * D]), ("L2b_wK", [P, H * D]), ("L2b_wV", [P, H * D]), ("L2b_wQs", [P, H * ROT]), ("L2b_wKs", [P, H * ROT]),
                 ("L2b_g", [P, D]), ("L2b_be", [P, D]), ("c_cos", [ROT, GROUP]), ("c_sin", [ROT, GROUP]), ("c_decay", [P, AW])]
        w = {n: s.sb(n, shape) for n, shape in names}
        xg, v = s.sb("xg", [P, GROUP]), s.sb("v", [P, GT, H * D])
        rot, swap = s.sb("rot", [ROT, 2, GROUP]), s.sb("swap", [ROT, 2, GROUP])
        qk = [s.sb(f"qk{i}", [P, 2, GROUP]) for i in range(2)]
        a = [s.sb(f"a{i}", [P, BPG, AW]) for i in range(2)]
        rows, sq, mean, var = s.sb("rows", [P, GT * 16, GN]), s.sb("sq", [P, GT * 16, GN]), s.sb("mean", [P, GT * 16]), s.sb("var", [P, GT * 16])
        qk_ps, sw_ps = s.ps("qk_ps", [P, 2, GROUP]), s.ps("sw_ps", [ROT, 2, GROUP])
        a_ps, v_ps, o_ps = s.ps("a_ps", [P, BPG, 512]), s.ps("v_ps", [P, 512]), s.ps("o_ps", [P, GT, D])
        loaded, xg_ready, v_up, v_ready = s.sem("loaded"), s.sem("xg_ready"), s.sem("v_up"), s.sem("v_ready")
        projected, rot_ready, qk_ready = s.sem("projected"), s.sem("rot_ready"), s.sem("qk_ready")
        a_up, a_ready, o_ready, var_ready, root_ready, done = (s.sem(n) for n in ("a_up", "a_ready", "o_ready", "var_ready", "root_ready", "done"))
        block = s.block()

        @block.sync
        def _(sp):
            for n, _ in names:
                sp.dma_start(w[n][:], k.dram[n]).then_inc(loaded, 16)

        @block.tensor
        def _(pe):
            def project(g, h):
                if h > 0:
                    pe.wait_ge(qk_ready, g * H + h)
                for i, n in enumerate("QK"):
                    nc.tensor.matmul(qk_ps[:, i, :], w[f"L2b_w{n}"][:, h * D:(h + 1) * D], xg[:], start=True, stop=True)
                for i, n in enumerate("QK"):
                    last = nc.tensor.matmul(sw_ps[:, i, :], w[f"L2b_w{n}s"][:, h * ROT:(h + 1) * ROT], xg[:], start=True, stop=True)
                last.then_inc(projected, 1)

            def scores(g, h):
                pe.wait_ge(qk_ready, g * H + (h + 1))
                if h > 0:
                    pe.wait_ge(a_ready, g * H + h)
                for b in range(BPG):
                    q, kk = qk[h % 2][:, 0, :], qk[h % 2][:, 1, :]
                    c = b * SEQ
                    nc.tensor.matmul(a_ps[:, b, 0:P], q[:, c:c + P], kk[:, c:c + P], start=True, stop=True)
                    last = nc.tensor.matmul(a_ps[:, b, P:AW], q[:, c + P:c + SEQ], kk[:, c:c + SEQ], start=True, stop=True)
                last.then_inc(a_up, 1)

            def mix(g, h):
                pe.wait_ge(a_ready, g * H + (h + 1))
                for b in range(BPG):
                    for col, row_tile, key_tile in ((0, 0, 0), (P, 1, 0), (2 * P, 1, 1)):
                        last = nc.tensor.matmul(o_ps[:, b * TPB + key_tile, :], a[h % 2][:, b, col:col + P],
                                                v[:, b * TPB + row_tile, h * D:(h + 1) * D],
                                                start=(h == 0 and b == 0 and col == 0), stop=(h == H - 1), skip_group_check=True)
                return last

            pe.wait_ge(loaded, 16 * len(names))
            with pe.Fori(0, GROUPS) as g:
                pe.wait_ge(xg_ready, g + 1)
                project(g, 0)
                for n in range(2 * GT):
                    if n > 0:
                        pe.wait_ge(v_ready, g * 2 * GT + n)
                    t, half = divmod(n, 2)
                    nc.tensor.matmul(v_ps[:], xg[:, t * P:(t + 1) * P], w["L2b_wV"][:, half * 512:(half + 1) * 512], start=True, stop=True)\
                        .then_inc(v_up, 1)
                pe.wait_ge(v_ready, g * 2 * GT + 2 * GT)
                for h in range(H):
                    if h + 1 < H:
                        project(g, h + 1)
                    scores(g, h)
                    if h > 0:
                        mix(g, h - 1)
                mix(g, H - 1).then_inc(o_ready, 1)

        @block.scalar
        def _(act):
            with act.Fori(0, GROUPS) as g:
                act.wait_ge(done, g)
                nc.scalar.copy(xg[:], k.XNT[:, bass.ds(g * GROUP, GROUP)]).then_inc(xg_ready, 1)

                def activate(h):
                    act.wait_ge(projected, g * H + (h + 1))
                    nc.scalar.activation(qk[h % 2][ROT:P, :, :], qk_ps[ROT:P, :, :], ACT.Silu)
                    act.wait_ge(rot_ready, g * H + (h + 1))
                    nc.scalar.activation(qk[h % 2][0:ROT, :, :], rot[:], ACT.Silu).then_inc(qk_ready, 1)

                activate(0)
                for n in range(2 * GT):
                    t, half = divmod(n, 2)
                    act.wait_ge(v_up, g * 2 * GT + (n + 1))
                    nc.scalar.activation(v[:, t, half * 512:(half + 1) * 512], v_ps[:], ACT.Silu).then_inc(v_ready, 1)
                for h in range(1, H):
                    activate(h)
                act.wait_ge(var_ready, g + 1)
                nc.scalar.activation(var[:], var[:], ACT.Sqrt).then_inc(root_ready, 1)

        @block.vector
        def _(dve):
            def twice(ap):
                return ap[:].rearrange("p (a n) -> p a n", a=1).to_broadcast([ap.shape[0], 2, ap.shape[1]])

            def over_tiles(ap):
                return ap[:].rearrange("p (a n) -> p a n", a=1).to_broadcast([P, GT, D])

            def turn(g, h):
                dve.wait_ge(projected, g * H + (h + 1))
                nc.vector.tensor_tensor(swap[:], sw_ps[:], twice(w["c_sin"]), ALU.mult)
                if h > 0:
                    dve.wait_ge(qk_ready, g * H + h)
                nc.vector.tensor_tensor(rot[:], qk_ps[0:ROT, :, :], twice(w["c_cos"]), ALU.mult)
                dve.drain()
                nc.vector.tensor_tensor(rot[:], rot[:], swap[:], ALU.add).then_inc(rot_ready, 1)

            def decay(g, h):
                dve.wait_ge(a_up, g * H + (h + 1))
                nc.vector.tensor_tensor(a[h % 2][:], a_ps[:, :, 0:AW], twice(w["c_decay"]), ALU.mult).then_inc(a_ready, 1)

            dve.wait_ge(loaded, 16 * len(names))
            with dve.Fori(0, GROUPS) as g:
                turn(g, 0)
                for h in range(H):
                    if h + 1 < H:
                        turn(g, h + 1)
                    decay(g, h)
                dve.wait_ge(o_ready, g + 1)
                groups = o_ps[:].rearrange("p t (q d) -> p (t q) d", d=GN)
                nc.vector.tensor_reduce(mean[:], groups, AX.X, ALU.add)
                dve.drain()
                nc.vector.tensor_scalar(mean[:], mean[:], 1.0 / GN, None, ALU.mult)
                dve.drain()
                nc.vector.tensor_tensor(rows[:], groups, per_row(mean[:], GN), ALU.subtract)
                dve.drain()
                nc.vector.tensor_tensor(sq[:], rows[:], rows[:], ALU.mult)
                dve.drain()
                nc.vector.tensor_reduce(var[:], sq[:], AX.X, ALU.add)
                dve.drain()
                nc.vector.tensor_scalar(var[:], var[:], 1.0 / GN, 1e-5, ALU.mult, ALU.add).then_inc(var_ready, 1)
                dve.wait_ge(root_ready, g + 1)
                nc.vector.reciprocal(var[:], var[:])
                dve.drain()
                nc.vector.tensor_tensor(rows[:], rows[:], per_row(var[:], GN), ALU.mult)
                dve.drain()
                by_tile = rows[:].rearrange("p (t q) d -> p t (q d)", t=GT)
                nc.vector.tensor_tensor(by_tile, by_tile, over_tiles(w["L2b_g"]), ALU.mult)
                dve.drain()
                nc.vector.tensor_tensor(by_tile, by_tile, over_tiles(w["L2b_be"]), ALU.add)
                dve.drain()
                x = k.X[:, bass.ds(g * GT, GT), :]
                nc.vector.tensor_tensor(x, x, by_tile, ALU.add).then_inc(done, 1)


def l2_ffn(nc, k, name):
    NT, NC, KN = 64, 8, 8
    NS = NC + NT
    with Scope(nc, name + "_sig") as s:
        raw, q, low = s.sb("raw", [P, NT]), s.sb("q", [P, NT]), s.sb("low", [P, NT])
        loaded = s.sem("loaded")
        block = s.block()

        @block.sync
        def _(sp):
            sp.dma_start(raw[:], k.dram["L2f_sig"]).then_inc(loaded, 16)

        @block.vector
        def _(dve):
            dve.wait_ge(loaded, 16)
            nc.vector.tensor_scalar(q[:], raw[:], 0.3, None, ALU.is_gt)
            nc.vector.tensor_scalar(low[:], raw[:], -0.3, None, ALU.is_lt)
            dve.drain()
            nc.vector.tensor_tensor(q[:], q[:], low[:], ALU.subtract)
            dve.drain()
            nc.vector.tensor_tensor(q[:], q[:], raw[:], ALU.subtract)
            dve.drain()
            nc.vector.tensor_tensor(k.SIG[:, NC:NS], raw[:], q[:], ALU.add)
            dve.drain()
            nc.vector.tensor_reduce(low[:, 0:NC], k.SIG[:, NC:NS].rearrange("p (c t) -> p c t", t=8), AX.X, ALU.add)
            dve.drain()
            nc.vector.tensor_scalar(q[:, 0:NC], low[:, 0:NC], 0.0, None, ALU.is_gt)
            nc.vector.tensor_scalar(q[:, NC:2 * NC], low[:, 0:NC], 0.0, None, ALU.is_lt)
            dve.drain()
            nc.vector.tensor_tensor(k.SIG[:, 0:NC], q[:, 0:NC], q[:, NC:2 * NC], ALU.subtract)

    layer_norm(nc, k, name + "_ln", k.SIG, NS, keep_rows=True)

    with Scope(nc, name + "_pick") as s:
        names = [("L2f_temp", [P, 1]), ("L2f_knots", [P, KN]), ("c_first8", [P, NC]), ("c_first64", [P, NT]), ("c_minus_knot", [P, KN])]
        w = {n: s.sb(n, shape) for n, shape in names}
        temp, slope = s.sb("temp", [P, 1]), s.sb("slope", [P, KN])
        at = s.sb("at", [P, TILES * NS])
        over = [s.sb(f"over{i}", [P, TILES * NS]) for i in range(2)]
        gates = s.sb("gates", [P, TILES, NS])
        top, own, off = s.sb("top", [P, TILES]), s.sb("own", [P, TILES, NC]), s.sb("off", [P, TILES, NC])
        q = s.sb("q", [P, TILES, NT])
        loaded, temp_ready, over_ready, used = s.sem("loaded"), s.sem("temp_ready"), s.sem("over_ready"), s.sem("used")
        block = s.block()

        @block.sync
        def _(sp):
            for n, _ in names:
                sp.dma_start(w[n][:], k.dram[n]).then_inc(loaded, 16)

        @block.scalar
        def _(act):
            act.wait_ge(temp_ready, 1)
            nc.scalar.activation(at[:], k.LOG[:].rearrange("p t n -> p (t n)"), ACT.Sigmoid, scale=temp[:])
            act.drain()
            for j in range(KN - 1):
                if j >= 2:
                    act.wait_ge(used, j - 1)
                nc.scalar.activation(over[j % 2][:], at[:], ACT.Relu, scale=float(KN - 1), bias=w["c_minus_knot"][:, j:j + 1])\
                    .then_inc(over_ready, 1)

        @block.vector
        def _(dve):
            dve.wait_ge(loaded, 16 * len(names))
            nc.vector.tensor_scalar(temp[:], w["L2f_temp"][:], 1e-6, None, ALU.add)
            dve.drain()
            nc.vector.reciprocal(temp[:], temp[:]).then_inc(temp_ready, 1)
            nc.vector.tensor_tensor(slope[:, 0:KN - 1], w["L2f_knots"][:, 1:KN], w["L2f_knots"][:, 0:KN - 1], ALU.subtract)
            dve.drain()
            nc.vector.tensor_copy(off[:, 0, 0:KN - 1], slope[:, 0:KN - 1])
            dve.drain()
            nc.vector.tensor_tensor(slope[:, 1:KN - 1], off[:, 0, 1:KN - 1], off[:, 0, 0:KN - 2], ALU.subtract)
            dve.drain()
            g = gates[:].rearrange("p t n -> p (t n)")
            for j in range(KN - 1):
                dve.wait_ge(over_ready, j + 1)
                if j == 0:
                    nc.vector.tensor_scalar(g, over[0][:], slope[:, 0:1], w["L2f_knots"][:, 0:1], ALU.mult, ALU.add).then_inc(used, 1)
                else:
                    nc.vector.scalar_tensor_tensor(out=g, in0=over[j % 2][:], scalar=slope[:, j:j + 1], in1=g,
                                                   op0=ALU.mult, op1=ALU.add).then_inc(used, 1)
                dve.drain()

            def first_largest(vals, n, first, out):
                def spread(ap):
                    return ap.rearrange("p (t a) -> p t a", a=1).to_broadcast([P, TILES, n])
                nc.vector.tensor_reduce(top[:], vals, AX.X, ALU.max)
                dve.drain()
                nc.vector.tensor_tensor(out, vals, spread(top[:]), ALU.is_equal)
                dve.drain()
                nc.vector.tensor_tensor(out, out, first[:].rearrange("p (a n) -> p a n", a=1).to_broadcast([P, TILES, n]), ALU.mult)
                dve.drain()
                nc.vector.tensor_reduce(top[:], out, AX.X, ALU.max)
                dve.drain()
                nc.vector.tensor_tensor(out, out, spread(top[:]), ALU.is_equal)
                dve.drain()

            first_largest(gates[:, :, 0:NC], NC, w["c_first8"], own[:])
            nc.vector.tensor_scalar(off[:], own[:], 3e38, -3e38, ALU.mult, ALU.add)

            def over_cluster(ap):
                return ap.rearrange("p t (c a) -> p (t c) a", a=1).to_broadcast([P, TILES * NC, 8])
            gq = gates[:, :, NC:NS].rearrange("p t (c n) -> p t c n", n=8)
            qq = q[:].rearrange("p t (c n) -> p t c n", n=8)
            own4 = own[:].rearrange("p t (c a) -> p t c a", a=1).to_broadcast([P, TILES, NC, 8])
            nc.vector.tensor_tensor(qq, gq, own4, ALU.mult)
            dve.drain()
            qf = q[:].rearrange("p t (c n) -> p (t c) n", n=8)
            nc.vector.tensor_tensor(qf, qf, over_cluster(off[:]), ALU.add)
            dve.drain()
            first_largest(q[:], NT, w["c_first64"], k.PICK[:])

    CH, G2 = 32, 16
    W1, B1, W2, B2, DIR = 0, 2 * G2, 3 * G2, 4 * G2, 4 * G2 + 1
    TW = DIR + D
    with Scope(nc, name + "_mix") as s:
        names = [("L2f_scale", [P, 1]), ("L2f_cw1", [P, CH]), ("L2f_cb1", [CH, 1]), ("L2f_cw2", [CH, 2]), ("L2f_cb2", [1, 2 * GT]),
                 ("L2f_table", [P, TW]), ("L2f_gamma", [P, D]), ("L2f_beta", [P, D])]
        w = {n: s.sb(n, shape) for n, shape in names}
        picked, pt, hid = s.sb("picked", [P, GT * NT]), s.sb("pt", [P, 2, P]), s.sb("hid", [CH, GROUP])
        comp, sp1, sp2, mag = s.sb("comp", [P, GT, 2]), s.sb("sp1", [P, GT, G2]), s.sb("sp2", [P, GT, G2]), s.sb("mag", [P, GT])
        y = s.sb("y", [P, GT, D])
        stats, mv, rstd, minus = s.sb("stats", [P, GT, 6]), s.sb("mv", [P, GT, 2]), s.sb("rstd", [P, GT]), s.sb("minus", [P, GT])
        pt_ps, hid_ps, comp_ps, row_ps = s.ps("pt_ps", [P, 2, P]), s.ps("hid_ps", [CH, GROUP]), s.ps("comp_ps", [P, GT, 2]), s.ps("row_ps", [P, GT, 256])
        loaded, picked_ready, turned, pt_ready = s.sem("loaded"), s.sem("picked_ready"), s.sem("turned"), s.sem("pt_ready")
        hid_up, hid_ready, comp_up, comp_ready = s.sem("hid_up"), s.sem("hid_ready"), s.sem("comp_up"), s.sem("comp_ready")
        rows_up, var_ready, rstd_ready, done = s.sem("rows_up"), s.sem("var_ready"), s.sem("rstd_ready"), s.sem("done")
        block = s.block()

        @block.sync
        def _(sp):
            for n, _ in names:
                sp.dma_start(w[n][:], k.dram[n]).then_inc(loaded, 16)

        @block.tensor
        def _(pe):
            pe.wait_ge(loaded, 16 * len(names))
            with pe.Fori(0, GROUPS) as g:
                pe.wait_ge(picked_ready, g + 1)
                for i in range(2):
                    last = nc.tensor.transpose(pt_ps[:, i, :], picked[:, i * P:(i + 1) * P], k.ident[:])
                last.then_inc(turned, 1)
                nc.tensor.matmul(hid_ps[:], w["L2f_cw1"][:], k.XNT[:, bass.ds(g * GROUP, GROUP)], start=True, stop=True).then_inc(hid_up, 1)
                pe.wait_ge(pt_ready, g + 1)
                for t in range(GT):
                    r = t // 2 * NT
                    last = nc.tensor.matmul(row_ps[:, t, 0:TW], pt[r:r + NT, t % 2, :], w["L2f_table"][r:r + NT, :], start=True, stop=True)
                last.then_inc(rows_up, 1)
                nc.tensor.matmul(comp_ps[:], k.ones_row[0:1, 0:P], w["L2f_cb2"][:], start=True, stop=False, skip_group_check=True)
                pe.wait_ge(hid_ready, g + 1)
                for t in range(GT):
                    last = nc.tensor.matmul(comp_ps[:, t, :], hid[:, t * P:(t + 1) * P], w["L2f_cw2"][:], start=False, stop=True,
                                            skip_group_check=True)
                last.then_inc(comp_up, 1)

        @block.scalar
        def _(act):
            act.wait_ge(loaded, 16 * len(names))
            with act.Fori(0, GROUPS) as g:
                act.wait_ge(done, g)
                nc.scalar.copy(picked[:].rearrange("p (i r n) -> p r i n", i=2, r=2),
                               k.PICK[:, bass.ds(g * GT, GT), :].rearrange("p (r i) n -> p r i n", r=2)).then_inc(picked_ready, 1)
                act.wait_ge(turned, g + 1)
                nc.scalar.copy(pt[:], pt_ps[:]).then_inc(pt_ready, 1)
                act.wait_ge(hid_up, g + 1)
                nc.scalar.activation(hid[:], hid_ps[:], ACT.Gelu, bias=w["L2f_cb1"][:]).then_inc(hid_ready, 1)
                act.wait_ge(comp_up, g + 1)
                nc.scalar.activation(comp[:], comp_ps[:], ACT.Tanh).then_inc(comp_ready, 1)

        @block.gpsimd
        def _(pool):
            nc.gpsimd.memset(minus[:], -0.5)
            pool.drain()
            with pool.Fori(0, GROUPS) as g:
                pool.wait_ge(var_ready, g + 1)
                nc.gpsimd.tensor_tensor(rstd[:], rstd[:], minus[:], ALU.pow).then_inc(rstd_ready, 1)

        @block.vector
        def _(dve):
            def over_tiles(ap):
                return ap[:].rearrange("p (a n) -> p a n", a=1).to_broadcast([P, GT, D])

            dve.wait_ge(loaded, 16 * len(names))
            with dve.Fori(0, GROUPS) as g:
                dve.wait_ge(rows_up, g + 1)
                dve.wait_ge(comp_ready, g + 1)
                for j, out in enumerate((sp1, sp2)):
                    nc.vector.tensor_tensor(out[:], row_ps[:, :, W1 + j * G2:W1 + (j + 1) * G2], comp[:, :, j:j + 1].to_broadcast([P, GT, G2]), ALU.mult)
                dve.drain()
                nc.vector.tensor_tensor(sp1[:], sp1[:], sp2[:], ALU.add)
                dve.drain()
                nc.vector.tensor_tensor(sp1[:], sp1[:], row_ps[:, :, B1:B1 + G2], ALU.add)
                dve.drain()
                nc.vector.scalar_tensor_tensor(out=sp1[:], in0=sp1[:], scalar=0.0, in1=row_ps[:, :, W2:W2 + G2], op0=ALU.max, op1=ALU.mult)
                dve.drain()
                nc.vector.tensor_reduce(mag[:], sp1[:], AX.X, ALU.add)
                dve.drain()
                nc.vector.tensor_tensor(mag[:], mag[:], row_ps[:, :, B2], ALU.add)
                dve.drain()
                nc.vector.tensor_tensor(y[:], row_ps[:, :, DIR:DIR + D], per_row(mag[:], D), ALU.mult)
                dve.drain()
                nc.vector.scalar_tensor_tensor(out=y[:], in0=y[:], scalar=w["L2f_scale"][:], in1=k.XN[:, bass.ds(g * GT, GT), :],
                                               op0=ALU.mult, op1=ALU.add)
                dve.drain()
                group_norm_rows(nc, dve, y, stats, mv)
                nc.vector.tensor_scalar(rstd[:], mv[:, :, 1], 1e-5, None, ALU.add).then_inc(var_ready, 1)
                dve.wait_ge(rstd_ready, g + 1)
                for t in range(GT):
                    nc.vector.tensor_scalar(y[:, t, :], y[:, t, :], mv[:, t, 0:1], rstd[:, t:t + 1], ALU.subtract, ALU.mult)
                dve.drain()
                nc.vector.tensor_tensor(y[:], y[:], over_tiles(w["L2f_gamma"]), ALU.mult)
                dve.drain()
                nc.vector.tensor_tensor(y[:], y[:], over_tiles(w["L2f_beta"]), ALU.add)
                dve.drain()
                x = k.X[:, bass.ds(g * GT, GT), :]
                nc.vector.tensor_tensor(x, x, y[:], ALU.add).then_inc(done, 1)


def l1_attn_b(nc, k, name):
    layer_norm(nc, k, name + "_ln")
    H, HD, VD = 16, 4, 8
    FR, AR = H * HD, 96
    VC = 32
    LAMBDA_INIT = 0.8 - 0.6 * float(np.exp(-0.3 * 12))
    with Scope(nc, name) as s:
        names = [("L1b_wqk", [P, 2 * D]), ("L1b_wv", [P, D]), ("L1b_wo", [P, D]), ("L1b_bo", [1, TPB * D]), ("L1b_lam", [P, 4 * HD]),
                 ("L1b_sub", [P, VD]), ("c_head_rows", [AR, H])]
        w = {n: s.sb(n, shape) for n, shape in names}
        lam, sub = s.sb("lam", [P, 2]), s.sb("sub", [P, D])
        prod = s.sb("prod", [P, 2, HD])
        xg = s.sb("xg", [P, SEQ])
        qt, kt = s.sb("qt", [AR, 2, SEQ]), s.sb("kt", [AR, 2, SEQ])
        q0 = s.sb("q0", [AR, 2, SEQ])
        masked = s.sb("masked", [AR, 2, H, SEQ])
        vx = s.sb("vx", [P, TPB, H, VC])
        top = s.sb("top", [P, 2, TPB, AR])
        e = [s.sb(f"e{i}", [P, TPB, SEQ]) for i in range(3)]
        rden, att = s.sb("rden", [P, 2, TPB * H]), s.sb("att", [P, 2, TPB * H, VD])
        o, sq, ms, minus = s.sb("o", [P, TPB * H, VD]), s.sb("sq", [P, TPB * H, VD]), s.sb("ms", [P, TPB * H]), s.sb("minus", [P, TPB * H])
        ot, mixed = s.sb("ot", [P, SEQ]), s.sb("mixed", [P, 2, H // 4, SEQ])
        misc = s.ps("misc", [P, 2, SEQ])
        misc2 = s.ps("misc2", [P, 2, SEQ])
        score_ps = [s.ps(f"score_ps{i}", [P, TPB, SEQ]) for i in range(2)]
        o_ps = s.ps("o_ps", [P, 2, H // 4, SEQ])
        o_flat = o_ps[:].rearrange("p i s q -> p (i s q)")
        max_banks = [score_ps[0][:].rearrange("p t q -> p (t q)"), score_ps[1][:].rearrange("p t q -> p (t q)")] + \
            [o_flat[:, n * 512:(n + 1) * 512] for n in range(4)]
        NB = len(max_banks)
        sems = ("loaded", "exped", "consts_ready", "xg_ready", "projected", "copied", "v_ready", "masked_ready", "max_up", "max_ready",
                "top_ready", "turned", "turned_ready", "score_up", "e_ready", "o_up", "mixed_ready", "mixed_turned", "ms_ready", "rms_ready", "o_ready", "turned_o", "ot_ready",
                "y_ready", "done")
        (loaded, exped, consts_ready, xg_ready, projected, copied, v_ready, masked_ready, max_up, max_ready, top_ready, turned, turned_ready,
         score_up, e_ready, o_up, mixed_ready, mixed_turned, ms_ready, rms_ready, o_ready, turned_o, ot_ready, y_ready, done) = (s.sem(n) for n in sems)
        block = s.block()
        MAXES, SCORES = 2 * TPB * H // 2, 2 * H

        @block.sync
        def _(sp):
            for n, _ in names:
                sp.dma_start(w[n][:], k.dram[n]).then_inc(loaded, 16)

        @block.tensor
        def _(pe):
            pe.wait_ge(loaded, 16 * len(names))
            with pe.Fori(0, BATCH) as b:
                pe.wait_ge(xg_ready, b + 1)
                for j in range(2):
                    for i in range(2):
                        c = j * D + i * FR
                        last = nc.tensor.matmul((misc, misc2)[j][0:FR, i, :], w["L1b_wqk"][:, c:c + FR], xg[:], start=True, stop=True)
                for t in range(TPB):
                    last = nc.tensor.matmul(score_ps[0][:, t, 0:D], xg[:, t * P:(t + 1) * P], w["L1b_wv"][:], start=True, stop=True)
                last.then_inc(projected, 1)
                pe.wait_ge(v_ready, b + 1)
                pe.wait_ge(masked_ready, b + 1)
                for n in range(MAXES):
                    i, t, h = n // (TPB * H // 2), n // (H // 2) % TPB, n % (H // 2) * 2
                    if n >= NB:
                        pe.wait_ge(max_ready, b * MAXES + (n - NB + 1))
                    nc.tensor.matmul(max_banks[n % NB], q0[:, i, t * P:(t + 1) * P],
                                     masked[:, i, h:h + 2, :].rearrange("p h q -> p (h q)"), start=True, stop=True).then_inc(max_up, 1)
                pe.wait_ge(top_ready, b + 1)
                for i in range(2):
                    for t in range(TPB):
                        last = nc.tensor.transpose(misc[0:AR, i, t * P:(t + 1) * P], top[:, i, t, :], k.ident[:])
                last.then_inc(turned, 1)
                pe.wait_ge(turned_ready, b + 1)

                def score(n):
                    i, h = divmod(n, H)
                    for t in range(TPB):
                        last = nc.tensor.matmul(score_ps[n % 2][:, t, :], masked[:, i, h, t * P:(t + 1) * P], qt[:, i, :], start=True, stop=True)
                    last.then_inc(score_up, 1)

                def mix(n):
                    i, h = divmod(n, H)
                    pe.wait_ge(e_ready, b * SCORES + (n + 1))
                    r = h % 4 * VC
                    for t in range(TPB):
                        last = nc.tensor.matmul(o_ps[r:r + VC, i, h // 4, :], vx[:, t, h, :], e[n % 3][:, t, :],
                                                start=(t == 0), stop=(t == TPB - 1))
                    return last

                score(0)
                for n in range(SCORES):
                    if n + 1 < SCORES:
                        score(n + 1)
                    last = mix(n)
                    if n % H == H - 1:
                        last.then_inc(o_up, 1)
                pe.wait_ge(mixed_ready, b * 2 + 2)
                for i in range(2):
                    for t in range(TPB):
                        for c in range(H // 4):
                            last = nc.tensor.transpose(o_flat[:, ((i * TPB + t) * 4 + c) * P:((i * TPB + t) * 4 + c + 1) * P],
                                                       mixed[:, i, c, t * P:(t + 1) * P], k.ident[:])
                last.then_inc(mixed_turned, 1)
                nc.tensor.matmul(misc2[:, 0, :], k.ones_row[0:1, 0:P], w["L1b_bo"][:], start=True, stop=False, skip_group_check=True)
                pe.wait_ge(o_ready, b + 1)
                for t in range(TPB):
                    last = nc.tensor.transpose(misc[:, 0, t * P:(t + 1) * P], o[:, t * H:(t + 1) * H, :].rearrange("p h d -> p (h d)"), k.ident[:])
                last.then_inc(turned_o, 1)
                pe.wait_ge(ot_ready, b + 1)
                for t in range(TPB):
                    last = nc.tensor.matmul(misc2[:, 0, t * D:(t + 1) * D], ot[:, t * P:(t + 1) * P], w["L1b_wo"][:], start=False, stop=True,
                                            skip_group_check=True)
                last.then_inc(y_ready, 1)

        @block.scalar
        def _(act):
            act.wait_ge(consts_ready, 1)
            nc.scalar.activation(lam[:], lam[:], ACT.Exp).then_inc(exped, 1)
            act.wait_ge(consts_ready, 2)
            with act.Fori(0, BATCH) as b:
                act.wait_ge(done, b)
                nc.scalar.copy(xg[:], k.XNT[:, bass.ds(b * SEQ, SEQ)]).then_inc(xg_ready, 1)
                act.wait_ge(projected, b + 1)
                nc.scalar.copy(q0[0:FR, :, :], misc[0:FR, :, :])
                nc.scalar.copy(qt[0:FR, :, :], misc[0:FR, :, :])
                nc.scalar.copy(kt[0:FR, :, :], misc2[0:FR, :, :]).then_inc(copied, 1)
                act.wait_ge(turned, b + 1)
                nc.scalar.copy(qt[FR:AR, :, :], misc[FR:AR, :, :]).then_inc(turned_ready, 1)
                for n in range(SCORES):
                    act.wait_ge(score_up, b * SCORES + (n + 1))
                    nc.scalar.activation(e[n % 3][:], score_ps[n % 2][:], ACT.Exp, scale=HD ** -0.5).then_inc(e_ready, 1)
                    if n == H:
                        act.wait_ge(o_up, b * 2 + 1)
                        nc.scalar.copy(mixed[:, 0, :, :], o_ps[:, 0, :, :]).then_inc(mixed_ready, 1)
                act.wait_ge(o_up, b * 2 + 2)
                nc.scalar.copy(mixed[:, 1, :, :], o_ps[:, 1, :, :]).then_inc(mixed_ready, 1)
                act.wait_ge(turned_o, b + 1)
                nc.scalar.copy(ot[:], misc[:, 0, :]).then_inc(ot_ready, 1)

        @block.gpsimd
        def _(pool):
            nc.gpsimd.memset(minus[:], -0.5)
            pool.drain()
            with pool.Fori(0, BATCH) as b:
                pool.wait_ge(ms_ready, b + 1)
                nc.gpsimd.tensor_tensor(ms[:], ms[:], minus[:], ALU.pow).then_inc(rms_ready, 1)

        @block.vector
        def _(dve):
            dve.wait_ge(loaded, 16 * len(names))
            nc.vector.tensor_tensor(prod[:], w["L1b_lam"][:, 0:2 * HD].rearrange("p (i d) -> p i d", i=2),
                                    w["L1b_lam"][:, 2 * HD:4 * HD].rearrange("p (i d) -> p i d", i=2), ALU.mult)
            nc.vector.memset(kt[FR:AR, :, :], 1.0)
            nc.vector.memset(q0[FR:AR, :, :], 0.0)
            nc.vector.memset(top[:], 0.0)
            nc.vector.memset(vx[:], 0.0)
            dve.drain()
            nc.vector.memset(vx[:, :, :, VD:VD + 1], 1.0)
            nc.vector.tensor_scalar(sub[:].rearrange("p (h d) -> p h d", h=H),
                                    w["L1b_sub"][:].rearrange("p (a d) -> p a d", a=1).to_broadcast([P, H, VD]),
                                    1.0 - LAMBDA_INIT, None, ALU.mult)
            dve.drain()
            nc.vector.tensor_reduce(lam[:], prod[:], AX.X, ALU.add).then_inc(consts_ready, 1)
            dve.wait_ge(exped, 1)
            nc.vector.tensor_tensor(lam[:, 0:1], lam[:, 1:2], lam[:, 0:1], ALU.subtract)
            dve.drain()
            nc.vector.tensor_scalar(lam[:, 0:1], lam[:, 0:1], -LAMBDA_INIT, None, ALU.add).then_inc(consts_ready, 1)
            dve.drain()
            with dve.Fori(0, BATCH) as b:
                dve.wait_ge(projected, b + 1)
                nc.vector.tensor_copy(vx[:, :, :, 0:VD], score_ps[0][:, :, 0:D].rearrange("p t (h d) -> p t h d", d=VD)).then_inc(v_ready, 1)
                dve.wait_ge(copied, b + 1)
                for i in range(2):
                    last = nc.vector.tensor_tensor(masked[:, i, :, :], kt[:, i, :].rearrange("p (a q) -> p a q", a=1).to_broadcast([AR, H, SEQ]),
                                                   w["c_head_rows"][:].rearrange("p (h a) -> p h a", a=1).to_broadcast([AR, H, SEQ]), ALU.mult)
                last.then_inc(masked_ready, 1)
                for n in range(MAXES):
                    i, t, h = n // (TPB * H // 2), n // (H // 2) % TPB, n % (H // 2) * 2
                    dve.wait_ge(max_up, b * MAXES + (n + 1))
                    nc.vector.tensor_reduce(top[:, i, t, FR + h:FR + h + 2], max_banks[n % NB].rearrange("p (h q) -> p h q", h=2), AX.X, ALU.max).then_inc(max_ready, 1)
                dve.drain()
                tops = top[:].rearrange("p i t n -> p (i t) n")[:, :, FR:FR + H]
                nc.vector.tensor_scalar(tops, tops, -1.0, None, ALU.mult).then_inc(top_ready, 1)
                dve.wait_ge(mixed_turned, b + 1)
                heads = o_flat.rearrange("p (n c) -> p n c", c=VC)
                nc.vector.reciprocal(rden[:].rearrange("p i n -> p (i n)"), heads[:, :, VD])
                dve.drain()
                nc.vector.tensor_tensor(att[:].rearrange("p i n d -> p (i n) d"), heads[:, :, 0:VD],
                                        per_row(rden[:].rearrange("p i n -> p (i n)"), VD), ALU.mult)
                dve.drain()
                nc.vector.scalar_tensor_tensor(out=o[:], in0=att[:, 1, :, :], scalar=lam[:, 0:1], in1=att[:, 0, :, :], op0=ALU.mult, op1=ALU.add)
                dve.drain()
                nc.vector.tensor_tensor(sq[:], o[:], o[:], ALU.mult)
                dve.drain()
                nc.vector.tensor_reduce(ms[:], sq[:], AX.X, ALU.add)
                dve.drain()
                nc.vector.tensor_scalar(ms[:], ms[:], 1.0 / VD, 1e-5, ALU.mult, ALU.add).then_inc(ms_ready, 1)
                dve.wait_ge(rms_ready, b + 1)
                nc.vector.tensor_tensor(o[:], o[:], per_row(ms[:], VD), ALU.mult)
                dve.drain()
                by_tile = o[:].rearrange("p (t h) d -> p t (h d)", t=TPB)
                nc.vector.tensor_tensor(by_tile, by_tile, sub[:].rearrange("p (a n) -> p a n", a=1).to_broadcast([P, TPB, D]), ALU.mult).then_inc(o_ready, 1)
                dve.wait_ge(y_ready, b + 1)
                x = k.X[:, bass.ds(b * TPB, TPB), :]
                nc.vector.tensor_tensor(x, x, misc2[:, 0, :].rearrange("p (t d) -> p t d", d=D), ALU.add).then_inc(done, 1)


def rows128(a):
    n, m = a.shape[0] // P, a.shape[1]
    return a.reshape(n, P, m).transpose(1, 0, 2).reshape(P, n * m)


def layouts(inp):
    a = {n: np.asarray(v) for n, v in inp.items()}
    o = {"x": a["L0_attn_a_x"].reshape(TILES, P, D).transpose(1, 0, 2), "c_ident": np.eye(P, dtype=np.float32)}
    o["L0_ffn_router"] = a["L0_ffn_router_w"].T
    o["L0_ffn_w1"] = a["L0_ffn_w1"].transpose(2, 0, 1).reshape(D, -1)
    o["L0_ffn_w2"] = rows128(a["L0_ffn_w2"].transpose(0, 2, 1).reshape(-1, D))
    o["L3_ffn_router"] = a["L3_ffn_router_w"].T
    o["L3_ffn_rb"] = np.broadcast_to(a["L3_ffn_router_b"], (P, 8))
    o["L3_ffn_w1"] = a["L3_ffn_w1"].transpose(2, 0, 1).reshape(D, -1)
    o["L3_ffn_b1"] = a["L3_ffn_b1"].reshape(8 * 8, P).T
    o["L3_ffn_w2"] = rows128(a["L3_ffn_w2"].transpose(0, 2, 1).reshape(-1, D))
    o["L3_ffn_b2"] = np.tile(a["L3_ffn_b2"], (P // 8, 1))
    o["c_own_tile"] = np.repeat(np.eye(P // 8, dtype=np.float32), 8, axis=0)
    o["L1_ffn_router"] = a["L1_ffn_Wg"]
    o["L1_ffn_w1"] = a["L1_ffn_W1"].transpose(1, 0, 2).reshape(D, -1)
    o["L1_ffn_w2"] = rows128(a["L1_ffn_W2"].reshape(-1, D))
    o["c_before"] = np.triu(np.ones((P, P), np.float32), 1)
    o["c_not_first_tile"] = np.broadcast_to((np.arange(8 * TILES) % TILES > 0).astype(np.float32), (P, 8 * TILES))
    o["c_early_first"] = np.broadcast_to(np.repeat(8 - np.arange(8, dtype=np.float32), TILES), (P, 8 * TILES))
    row = lambda v: np.tile(v, GT).reshape(1, GROUP)
    spread = lambda v: np.broadcast_to(v, (P, v.shape[0]))
    col = lambda v: v.reshape(-1, P).T
    o["L0a_wqkv"] = np.concatenate([a["L0_attn_a_W" + n].T for n in "qkv"], axis=1)
    o["L0a_bqkv"] = spread(np.concatenate([a["L0_attn_a_b" + n] for n in "qkv"]))
    o["L0a_w1"], o["L0a_b1"] = a["L0_attn_a_W1"].T, col(a["L0_attn_a_b1"])
    o["L0a_w2"], o["L0a_b2"] = a["L0_attn_a_W2"].T, col(a["L0_attn_a_b2"])
    o["L0a_w3"], o["L0a_b3"] = rows128(a["L0_attn_a_W3"].T), row(a["L0_attn_a_b3"])
    o["L0b_w"] = np.concatenate([a["L0_attn_b_Wq"].T] + [a["L0_attn_b_W" + n][i].T for n in "kv" for i in range(2)], axis=1)
    o["L0b_b"] = spread(np.concatenate([a["L0_attn_b_bq"]] + [a["L0_attn_b_b" + n][i] for n in "kv" for i in range(2)]))
    o["L0b_wo"], o["L0b_bo"] = a["L0_attn_b_Wo"].T, row(a["L0_attn_b_bo"])
    o["L0b_g"], o["L0b_be"] = col(a["L0_attn_b_ln_g"]), col(a["L0_attn_b_ln_b"])
    o["L3b_w"] = np.concatenate([a["L3_attn_b_W" + n] for n in "qkv"], axis=1)
    o["L3b_b"] = spread(np.concatenate([a["L3_attn_b_b" + n] for n in "qkv"]))
    o["L3b_wo"], o["L3b_bo"] = a["L3_attn_b_Wo"], row(a["L3_attn_b_bo"])
    o["L3b_g1"], o["L3b_be1"] = col(a["L3_attn_b_g1"]), col(a["L3_attn_b_be1"])
    o["L3b_g2"], o["L3b_be2"] = spread(a["L3_attn_b_g2"]), spread(a["L3_attn_b_be2"])
    o["L3b_w1"], o["L3b_b1"] = a["L3_attn_b_W1"], col(a["L3_attn_b_b1"])
    o["L3b_w2"], o["L3b_b2"] = rows128(a["L3_attn_b_W2"]), row(a["L3_attn_b_b2"])
    o["L3a_wq"], o["L3a_wk"] = a["L3_attn_a_q_w"].T, np.tile(a["L3_attn_a_kv_w"][0:8].T, (1, 16))
    o["L3a_wv"] = np.tile(a["L3_attn_a_kv_w"][8:16].T, (1, 4))
    o["L3a_wo"], o["L3a_bo"] = a["L3_attn_a_proj_w"].T, row(a["L3_attn_a_proj_b"])
    o["c_head_of_row8"] = np.repeat(np.eye(16, dtype=np.float32), 8, axis=0)
    o["c_blocks32x8"] = np.kron(np.eye(4, dtype=np.float32), np.ones((32, 8), np.float32))
    o["L1a_win"] = a["L1_attn_a_in_proj_w"].T
    o["L1a_conv"] = a["L1_attn_a_conv_w"].reshape(2, P, 4).transpose(1, 0, 2).reshape(P, 8)
    o["L1a_wx"] = rows128(a["L1_attn_a_x_proj_w"].T)
    o["L1a_wdt"], o["L1a_bdt"] = a["L1_attn_a_dt_proj_w"].T, col(a["L1_attn_a_dt_proj_b"])
    o["L1a_alog"], o["L1a_d"] = rows128(a["L1_attn_a_A_log"]), col(a["L1_attn_a_D"])
    o["L1a_wout"] = rows128(a["L1_attn_a_out_proj_w"].T)
    even_odd = np.r_[0:16:2, 1:16:2]
    wx = np.zeros((65, 256), np.float32)
    wx[0:32], wx[32], wx[64] = a["L2_attn_a_W_x"][np.r_[even_odd, 16 + even_odd]], a["L2_attn_a_W_x"][32], a["L2_attn_a_W_x"][33]
    both = lambda n: np.concatenate([a[f"L2_attn_a_{c}_{n}"][even_odd] for c in "BC"]).reshape(32, 1)
    o["L2a_win"], o["L2a_wx"], o["L2a_wdt"] = a["L2_attn_a_W_in"].T, rows128(wx.T), a["L2_attn_a_W_dt"].T
    o["L2a_bdt"], o["L2a_d"] = col(a["L2_attn_a_b_dt"]), col(a["L2_attn_a_D"])
    o["L2a_alog"], o["L2a_wout"] = rows128(a["L2_attn_a_A_log"][:, even_odd]), rows128(a["L2_attn_a_W_out"].T)
    o["L2a_bias"], o["L2a_norm"] = both("bias"), both("norm_w")
    o["L2a_freq"] = np.tile(a["L2_attn_a_rope_freqs"], 4).reshape(32, 1)
    o["c_mean16"] = np.tile(np.kron(np.eye(2, dtype=np.float32), np.ones((16, 16), np.float32) / 16), (1, 4))
    quarter = np.kron(np.array([[0, 1], [-1, 0]], np.float32), np.eye(8, dtype=np.float32))
    o["c_quarter_turn"] = np.kron(np.eye(2, dtype=np.float32), quarter)
    o["c_not_first"] = np.broadcast_to((np.arange(GROUP) % SEQ > 0).astype(np.float32), (32, GROUP))
    swapped = np.arange(64) ^ 1
    heads = lambda v: v.reshape(D, 8, D)
    for n in "QK":
        o[f"L2b_w{n}"] = a[f"L2_attn_b_W_{n}"]
        o[f"L2b_w{n}s"] = heads(a[f"L2_attn_b_W_{n}"])[:, :, swapped].reshape(D, 512)
    o["L2b_wV"] = a["L2_attn_b_W_V"]
    o["L2b_g"], o["L2b_be"] = spread(a["L2_attn_b_gn_weight"]), spread(a["L2_attn_b_gn_bias"])
    inv_freq = 1.0 / 10000.0 ** (np.arange(0, 64, 2, dtype=np.float32) / 64)
    ang = np.repeat(np.arange(SEQ, dtype=np.float32)[:, None] * inv_freq[None, :], 2, axis=-1).astype(np.float32).T
    sign = np.where(np.arange(64) % 2 == 0, -1, 1).astype(np.float32)[:, None]
    o["c_cos"], o["c_sin"] = np.tile(np.cos(ang), (1, BPG)), np.tile(np.sin(ang) * sign, (1, BPG))
    diff = np.arange(SEQ)[:, None] - np.arange(SEQ)[None, :]
    decay = np.where(diff >= 0, np.float32(0.96875) ** np.maximum(diff, 0).astype(np.float32), 0).astype(np.float32)
    o["c_decay"] = np.concatenate([decay[0:P, 0:P], decay[P:, :]], axis=1)
    o["L2f_sig"] = a["L2_ffn_signatures_raw"].T
    o["L2f_temp"], o["L2f_knots"] = spread(a["L2_ffn_temperature"]), spread(a["L2_ffn_knot_values"])
    o["L2f_scale"] = spread(a["L2_ffn_output_scale"])
    o["L2f_cw1"], o["L2f_cb1"] = a["L2_ffn_compress_w1"], a["L2_ffn_compress_b1"].reshape(32, 1)
    o["L2f_cw2"], o["L2f_cb2"] = a["L2_ffn_compress_w2"], np.tile(a["L2_ffn_compress_b2"], GT).reshape(1, 2 * GT)
    table = np.concatenate([a["L2_ffn_spline_w1"].reshape(64, 32), a["L2_ffn_spline_b1"], a["L2_ffn_spline_w2"].reshape(64, 16),
                            a["L2_ffn_spline_b2"], a["L2_ffn_directions"]], axis=1)
    o["L2f_table"] = np.tile(table, (2, 1))
    o["L2f_gamma"], o["L2f_beta"] = spread(a["L2_ffn_norm_gamma"]), spread(a["L2_ffn_norm_beta"])
    o["c_first8"] = spread(8 - np.arange(8, dtype=np.float32))
    o["c_first64"] = spread(64 - np.arange(64, dtype=np.float32))
    o["c_minus_knot"] = spread(-np.arange(8, dtype=np.float32))
    o["L1b_wqk"], o["L1b_wv"] = a["L1_attn_b_W_qkv"][:, 0:2 * D], a["L1_attn_b_W_qkv"][:, 2 * D:]
    o["L1b_wo"], o["L1b_bo"] = a["L1_attn_b_W_proj"], np.tile(a["L1_attn_b_b_proj"], TPB).reshape(1, TPB * D)
    o["L1b_lam"] = spread(np.concatenate([a["L1_attn_b_lambda_" + n] for n in ("q1", "q2", "k1", "k2")]))
    o["L1b_sub"] = spread(a["L1_attn_b_subln_w"])
    o["c_head_rows"] = np.concatenate([np.repeat(np.eye(16, dtype=np.float32), 4, axis=0), np.eye(16, dtype=np.float32), np.zeros((16, 16), np.float32)])
    o["c_heads8"] = np.kron(np.eye(16, dtype=np.float32), np.ones((8, 8), np.float32))
    return o


RESIDENT = [("L0_ffn_router", "l0_ffn"),
            ("L1_ffn_router", "l1_ffn"),
            ("L3_ffn_router", "l3_ffn"), ("L3_ffn_rb", "l3_ffn"), ("L3_ffn_b1", "l3_ffn"),
            ("L3_ffn_b2", "l3_ffn"), ("c_own_tile", "l3_ffn")]
STEPS = {f.__name__: f for f in (l0_ffn, l3_ffn, l1_ffn, l0_attn_a, l0_attn_b,
                                l3_attn_a, l3_attn_b, l1_attn_a, l2_attn_a,
                                l1_attn_b, l2_attn_b, l2_ffn)}
PLAN = ["l0_attn_a",
        "l0_ffn",
        "l0_attn_b",
        "l0_ffn",
        "l1_attn_a",
        "l1_ffn",
        "l1_attn_b",
        "l1_ffn",
        "l2_attn_a",
        "l2_ffn",
        "l2_attn_b",
        "l2_ffn",
        "l3_attn_a",
        "l3_ffn",
        "l3_attn_b",
        "l3_ffn"]


def build(nc, dram, out, plan):
    k = Core(nc, dram)
    with k.stack:
        k.X = k.keep("X", [P, TILES, D])
        k.XN = k.keep("XN", [P, TILES, D])
        k.XNT = k.keep("XNT", [P, TOKENS])
        k.LOG = k.keep("LOG", [P, TILES, 72])
        k.PICK = k.keep("PICK", [P, TILES, 64])
        k.SIG = k.keep("SIG", [P, 72])
        k.neg_half = k.keep("neg_half", [P, TILES])
        k.ones = k.keep("ones", [P, P])
        k.ones_row = k.keep("ones_row", [1, GROUP])
        k.GATE = k.keep("GATE", [P, TILES, 8])
        k.ident = k.keep("c_ident", [P, P])
        k.up = k.keep("up", [P, max(dram[f"L{i}_ffn_w1"].shape[1] for i in (0, 1, 3))])
        k.down = k.keep("down", [P, max(dram[f"L{i}_ffn_w2"].shape[1] for i in (0, 1, 3))])
        k.weights_landed = k.stack.enter_context(nc.semaphore("weights_landed"))
        weights = ["c_ident"]
        for name, needed_by in RESIDENT:
            if any(p.startswith(needed_by) for p in plan):
                k.keep(name, list(dram[name].shape))
                weights.append(name)
        load_all(nc, k, weights)
        experts = [p for p in plan if p in ("l0_ffn", "l1_ffn", "l3_ffn")]
        landed = None
        if experts:
            start_expert_load(nc, k, experts[0])
        for n, step in enumerate(plan):
            if step in experts and landed != step:
                finish_expert_load(nc, k)
                landed = step
            STEPS[step](nc, k, f"s{n}_{step}")
            later = [p for p in plan[n + 1:] if p in experts]
            if step in experts and later and later[0] != step:
                start_expert_load(nc, k, later[0])
        store(nc, k, out)


def kernel(**inputs):
    import concourse.bacc as bacc
    from concourse.bass_utils import run_bass_kernel_spmd

    nc = bacc.Bacc("TRN2", target_bir_lowering=False, num_devices=1)
    arrays = {n: np.ascontiguousarray(a) for n, a in layouts(inputs).items()}
    dram = {n: nc.dram_tensor(f"in_{n}", a.shape, mybir.dt.from_np(a.dtype), kind="ExternalInput").ap()
            for n, a in arrays.items()}
    out = nc.dram_tensor("out_x", (BATCH, SEQ, D), F32, kind="ExternalOutput").ap()
    build(nc, dram, out.rearrange("b (t p) d -> p (b t) d", p=P), PLAN)
    r = run_bass_kernel_spmd(nc, [{f"in_{n}": a for n, a in arrays.items()}], core_ids=[0])
    return r.results[0]["out_x"]
```

```python
from contextlib import ExitStack

import numpy as np

import concourse.bass as bass
from concourse import mybir

F32 = mybir.dt.float32
BF16 = mybir.dt.bfloat16
U32 = mybir.dt.uint32
I32 = mybir.dt.int32
ALU = mybir.AluOpType
ACT = mybir.ActivationFunctionType
AX = mybir.AxisListType

P = 128
BATCH, SEQ, D = 16, 256, 128
TOKENS = BATCH * SEQ
TILES = TOKENS // P
GT = 4
GROUP = GT * P
GROUPS = TILES // GT
BPG = GROUP // SEQ
TPB = SEQ // P
LN_EPS = 1e-5


class Scope:

    def __init__(self, nc, name):
        self.nc, self.name, self.stack = nc, name, ExitStack()
        self.sems = []

    def __enter__(self):
        self.stack.__enter__()
        return self

    def __exit__(self, *a):
        return self.stack.__exit__(*a)

    def sb(self, name, shape, dt=F32):
        return self.stack.enter_context(self.nc.sbuf_tensor(f"{self.name}_{name}", shape, dt))

    def ps(self, name, shape, dt=F32):
        return self.stack.enter_context(self.nc.psum_tensor(f"{self.name}_{name}", shape, dt))

    def sem(self, name):
        self.sems.append(self.stack.enter_context(self.nc.semaphore(f"{self.name}_{name}")))
        return self.sems[-1]

    def clear(self):
        for sem in self.sems:
            self.nc.gpsimd.sem_clear(sem)

    def block(self):
        self.stack.callback(self.clear)
        return self.stack.enter_context(self.nc.Block())


class Core:

    def __init__(self, nc, dram):
        self.nc, self.dram = nc, dram
        self.stack = ExitStack()
        self.bufs = {}
        self.loads_started = 0

    def keep(self, name, shape, dt=F32):
        self.bufs[name] = self.stack.enter_context(self.nc.sbuf_tensor(name, shape, dt))
        return self.bufs[name]


def flat(ap):
    return ap.rearrange("p a n -> p (a n)")


def tile(buf, t):
    return flat(buf[:, bass.ds(t, 1), :])


def load_all(nc, k, weights):
    with Scope(nc, "load") as s:
        loaded = s.sem("loaded")
        block = s.block()

        @block.sync
        def _(sp):
            n = 0
            sp.dma_start(k.X[:], k.dram["x"]).then_inc(loaded, 16)
            for name in weights:
                sp.dma_start(k.bufs[name][:], k.dram[name]).then_inc(loaded, 16)
                n += 16
            sp.wait_ge(loaded, n + 16)

        @block.vector
        def _(dve):
            nc.vector.memset(k.ones[:], 1.0)
            nc.vector.memset(k.ones_row[:], 1.0)


def start_expert_load(nc, k, step):
    k.loads_started += 2
    layer = step[:2].upper()
    with Scope(nc, f"{step}_load{k.loads_started}") as s:
        block = s.block()

        @block.sync
        def _(sp):
            for buf, name in ((k.up, "w1"), (k.down, "w2")):
                src = k.dram[f"{layer}_ffn_{name}"]
                sp.dma_start(buf[:, 0:src.shape[1]], src).then_inc(k.weights_landed, 16)


def finish_expert_load(nc, k):
    with Scope(nc, f"landed{k.loads_started}") as s:
        block = s.block()

        @block.sync
        def _(sp):
            sp.wait_ge(k.weights_landed, 16 * k.loads_started)


def store(nc, k, out):
    with Scope(nc, "store") as s:
        stored = s.sem("stored")
        block = s.block()

        @block.sync
        def _(sp):
            sp.dma_start(out, k.X[:]).then_inc(stored, 16)
            sp.wait_ge(stored, 16)


def layer_norm(nc, k, name, project=None, n_out=0, keep_rows=False):
    with Scope(nc, name) as s:
        stats = s.sb("stats", [P, TILES, 6])
        meanvar = s.sb("meanvar", [P, TILES, 1])
        rstd = s.sb("rstd", [P, TILES])
        half_gap = s.sb("half_gap", [P, TILES])
        rows = [s.sb(f"rows{i}", [P, GT, D]) for i in range(2)]
        cols = [s.sb(f"cols{i}", [P, GROUP]) for i in range(2)]
        turned = [s.ps(f"turned{i}", [P, GROUP]) for i in range(2)]
        proj = [s.ps(f"proj{i}", [P, 512]) for i in range(2)]
        moments, ready = s.sem("moments"), s.sem("ready")
        rows_ready, rows_free = s.sem("rows_ready"), s.sem("rows_free")
        turned_ready = s.sem("turned_ready")
        turned_free, cols_ready = s.sem("turned_free"), s.sem("cols_ready")
        proj_ready, logits_kept = s.sem("proj_ready"), s.sem("logits_kept")
        rows_kept = s.sem("rows_kept")
        block = s.block()

        @block.vector
        def _(dve):
            for t in range(TILES):
                nc.vector.bn_stats(stats[:, t, :], k.X[:, t, :])
            dve.drain()
            nc.vector.tensor_tensor(meanvar[:, :, 0], stats[:, :, 1], stats[:, :, 4], ALU.add)
            nc.vector.tensor_tensor(half_gap[:], stats[:, :, 1], stats[:, :, 4], ALU.subtract)
            nc.vector.tensor_tensor(rstd[:], stats[:, :, 2], stats[:, :, 5], ALU.add)
            dve.drain()
            nc.vector.tensor_scalar(meanvar[:, :, 0], meanvar[:, :, 0], 0.5, None, ALU.mult)
            nc.vector.scalar_tensor_tensor(out=half_gap[:], in0=half_gap[:], scalar=0.25, in1=half_gap[:],
                                           op0=ALU.mult, op1=ALU.mult)
            nc.vector.tensor_scalar(rstd[:], rstd[:], 1.0 / D, LN_EPS, ALU.mult, ALU.add)
            dve.drain()
            nc.vector.tensor_tensor(rstd[:], rstd[:], half_gap[:], ALU.add).then_inc(moments, 1)
            dve.wait_ge(ready, 1)
            nc.vector.reciprocal(rstd[:], rstd[:])
            dve.drain()
            with dve.Fori(0, GROUPS // 2) as pair:
                g = pair * 2
                for i in range(2):
                    dve.wait_ge(rows_free, g + (i + 1))
                    if keep_rows:
                        dve.wait_ge(rows_kept, g + (i + 1))
                    for j in range(GT):
                        last = nc.vector.tensor_scalar(
                            rows[i][:, j, :], tile(k.X, g * GT + (i * GT + j)),
                            flat(meanvar[:, bass.ds(g * GT + (i * GT + j), 1), 0:1]),
                            rstd[:, bass.ds(g * GT + (i * GT + j), 1)], ALU.subtract, ALU.mult)
                    last.then_inc(rows_ready, 1)

        if keep_rows:
            @block.gpsimd
            def _(pool):
                pool.sem_inc(rows_kept, 2)
                with pool.Fori(0, GROUPS // 2) as pair:
                    for i in range(2):
                        pool.wait_ge(rows_ready, pair * 2 + (i + 1))
                        nc.gpsimd.tensor_copy(k.XN[:, bass.ds(pair * 2 * GT + i * GT, GT), :], rows[i][:]).then_inc(rows_kept, 1)

        @block.tensor
        def _(pe):
            pe.sem_inc(rows_free, 2)
            with pe.Fori(0, GROUPS // 2) as pair:
                g = pair * 2
                for i in range(2):
                    pe.wait_ge(rows_ready, g + (i + 1))
                    pe.wait_ge(turned_free, g + (i + 1))
                    for j in range(GT):
                        last = nc.tensor.transpose(turned[i][:, j * P:(j + 1) * P], rows[i][:, j, :], k.ident[:])
                    last.then_inc(turned_ready, 1)
                if project is not None:
                    for i in range(2):
                        pe.wait_ge(cols_ready, g + (i + 1))
                        for j in range(GT):
                            last = nc.tensor.matmul(proj[i][:, j * n_out:(j + 1) * n_out], cols[i][:, j * P:(j + 1) * P],
                                                    project[:, 0:n_out], start=True, stop=True)
                        last.then_inc(proj_ready, 1)

        @block.scalar
        def _(act):
            act.wait_ge(moments, 1)
            nc.scalar.activation(rstd[:], rstd[:], ACT.Sqrt).then_inc(ready, 1)
            act.sem_inc(turned_free, 2)
            with act.Fori(0, GROUPS // 2) as pair:
                g = pair * 2
                for i in range(2):
                    act.wait_ge(turned_ready, g + (i + 1))
                    act.sem_inc(rows_free, 1)
                    xnt = k.XNT[:, bass.ds(g * GROUP + i * GROUP, GROUP)]
                    if project is not None:
                        nc.scalar.copy(cols[i][:], turned[i][:]).then_inc(cols_ready, 1)
                    nc.scalar.copy(xnt, turned[i][:]).then_inc(turned_free, 1)
                if project is not None:
                    for i in range(2):
                        act.wait_ge(proj_ready, g + (i + 1))
                        nc.scalar.copy(k.LOG[:, bass.ds(g * GT + i * GT, GT), 0:n_out],
                                       proj[i][:, 0:GT * n_out].rearrange("p (t n) -> p t n", n=n_out)).then_inc(logits_kept, 1)


def rank_below_two(nc, dve, s, probs, keep):
    ahead = s.sb("ahead", [P, TILES, 8])
    cmp = s.sb("cmp", [P, TILES, 8])
    nc.vector.memset(ahead[:], 0.0)
    for j in range(8):
        pj = probs[:, :, j:j + 1]
        dve.drain()
        if j > 0:
            nc.vector.tensor_tensor(cmp[:, :, 0:j], pj.to_broadcast([P, TILES, j]), probs[:, :, 0:j], ALU.is_gt)
        if j < 7:
            nc.vector.tensor_tensor(cmp[:, :, j + 1:8], pj.to_broadcast([P, TILES, 7 - j]), probs[:, :, j + 1:8], ALU.is_ge)
        nc.vector.memset(cmp[:, :, j:j + 1], 0.0)
        dve.drain()
        nc.vector.tensor_tensor(ahead[:], ahead[:], cmp[:], ALU.add)
    dve.drain()
    nc.vector.tensor_scalar(keep[:], ahead[:], 2.0, None, ALU.is_lt)
    dve.drain()


def softmax8(nc, k, name, top2_first, bias=None):
    with Scope(nc, name) as s:
        shifted = s.sb("shifted", [P, TILES, 8])
        e = s.sb("e", [P, TILES, 8])
        keep = s.sb("keep", [P, TILES, 8])
        top = s.sb("top", [P, TILES])
        total = s.sb("total", [P, TILES])
        shift_ready, exp_ready = s.sem("shift_ready"), s.sem("exp_ready")
        block = s.block()
        logits = k.LOG[:, :, 0:8]

        def per_tile(ap):
            return ap.rearrange("p (t a) -> p t a", a=1).to_broadcast([P, TILES, 8])

        @block.vector
        def _(dve):
            if bias is not None:
                nc.vector.tensor_tensor(logits, logits, bias[:].rearrange("p (a e) -> p a e", a=1)
                                        .to_broadcast([P, TILES, 8]), ALU.add)
                dve.drain()
            nc.vector.tensor_reduce(top[:], logits, AX.X, ALU.max)
            if top2_first:
                rank_below_two(nc, dve, s, k.LOG[:, :, 0:8], keep)
            dve.drain()
            nc.vector.tensor_tensor(shifted[:], logits, per_tile(top[:]), ALU.subtract).then_inc(shift_ready, 1)
            dve.wait_ge(exp_ready, 1)
            if top2_first:
                nc.vector.tensor_tensor(e[:], e[:], keep[:], ALU.mult)
                dve.drain()
            nc.vector.tensor_reduce(total[:], e[:], AX.X, ALU.add)
            dve.drain()
            nc.vector.reciprocal(total[:], total[:])
            dve.drain()
            nc.vector.tensor_tensor(k.GATE[:], e[:], per_tile(total[:]), ALU.mult)
            if top2_first is False:
                dve.drain()
                rank_below_two(nc, dve, s, k.GATE, keep)
                nc.vector.tensor_tensor(k.GATE[:], k.GATE[:], keep[:], ALU.mult)

        @block.scalar
        def _(act):
            act.wait_ge(shift_ready, 1)
            nc.scalar.activation(e[:], shifted[:], ACT.Exp).then_inc(exp_ready, 1)


def gelu_experts(nc, k, name, w1, w2, chunks):
    with Scope(nc, name) as s:
        up = [s.ps(f"up{i}", [P, GROUP]) for i in range(2)]
        down = [s.ps(f"down{i}", [P, GT, D]) for i in range(2)]
        hid = [s.sb(f"hid{i}", [P, GROUP]) for i in range(2)]
        up_ready, hid_ready = s.sem("up_ready"), s.sem("hid_ready")
        down_ready, down_free = s.sem("down_ready"), s.sem("down_free")
        block = s.block()
        steps = 8 * chunks

        @block.tensor
        def _(pe):
            def go_up(g, c):
                nc.tensor.matmul(up[c % 2][:], w1[:, c * P:(c + 1) * P], k.XNT[:, bass.ds(g * GROUP, GROUP)],
                                 start=True, stop=True).then_inc(up_ready, 1)

            def go_down(g, c):
                e, j = divmod(c, chunks)
                pe.wait_ge(hid_ready, g * steps + (c + 1))
                if j == 0:
                    pe.wait_ge(down_free, g * 8 + (e + 1))
                for t in range(GT):
                    last = nc.tensor.matmul(down[e % 2][:, t, :], hid[c % 2][:, t * P:(t + 1) * P],
                                            w2[:, c * D:(c + 1) * D], start=(j == 0 and t == 0),
                                            stop=(j == chunks - 1), skip_group_check=True)
                if j == chunks - 1:
                    last.then_inc(down_ready, 1)

            with pe.Fori(0, GROUPS) as g:
                go_up(g, 0)
                for c in range(steps):
                    if c + 1 < steps:
                        go_up(g, c + 1)
                    go_down(g, c)

        @block.scalar
        def _(act):
            with act.Fori(0, GROUPS) as g:
                for c in range(steps):
                    act.wait_ge(up_ready, g * steps + (c + 1))
                    nc.scalar.activation(hid[c % 2][:], up[c % 2][:], ACT.Gelu).then_inc(hid_ready, 1)

        @block.vector
        def _(dve):
            dve.sem_inc(down_free, 2)
            with dve.Fori(0, GROUPS) as g:
                for e in range(8):
                    dve.wait_ge(down_ready, g * 8 + (e + 1))
                    for t in range(GT):
                        xt = tile(k.X, g * GT + t)
                        last = nc.vector.scalar_tensor_tensor(
                            out=xt, in0=down[e % 2][:, t, :], scalar=flat(k.GATE[:, bass.ds(g * GT + t, 1), e:e + 1]),
                            in1=xt, op0=ALU.mult, op1=ALU.add)
                    last.then_inc(down_free, 1)
                    dve.drain()


def l0_ffn(nc, k, name):
    layer_norm(nc, k, name + "_ln", k.bufs["L0_ffn_router"], 8)
    softmax8(nc, k, name + "_gate", False)
    gelu_experts(nc, k, name + "_ffn", k.up, k.down, 4)


def silu_experts(nc, k, name):
    w1, b1, w2 = k.up, k.bufs["L3_ffn_b1"], k.down
    chunks = 4
    steps = 8 * chunks
    with Scope(nc, name) as s:
        up_a = [s.ps(f"up_a{i}", [P, GROUP]) for i in range(2)]
        up_b = [s.ps(f"up_b{i}", [P, GROUP]) for i in range(2)]
        down = [s.ps(f"down{i}", [P, GT, D]) for i in range(2)]
        gated = [s.sb(f"gated{i}", [P, GROUP]) for i in range(2)]
        hid = [s.sb(f"hid{i}", [P, GROUP]) for i in range(2)]
        up_ready, gated_ready, hid_ready = s.sem("up_ready"), s.sem("gated_ready"), s.sem("hid_ready")
        down_ready, down_free = s.sem("down_ready"), s.sem("down_free")
        block = s.block()

        @block.tensor
        def _(pe):
            def go_up(g, c):
                e, j = divmod(c, chunks)
                xn = k.XNT[:, bass.ds(g * GROUP, GROUP)]
                a, b = (2 * e * chunks + j) * P, ((2 * e + 1) * chunks + j) * P
                nc.tensor.matmul(up_a[c % 2][:], w1[:, a:a + P], xn, start=True, stop=True)
                nc.tensor.matmul(up_b[c % 2][:], w1[:, b:b + P], xn, start=True, stop=True).then_inc(up_ready, 1)

            def go_down(g, c):
                e, j = divmod(c, chunks)
                pe.wait_ge(hid_ready, g * steps + (c + 1))
                if j == 0:
                    pe.wait_ge(down_free, g * 8 + (e + 1))
                for t in range(GT):
                    last = nc.tensor.matmul(down[e % 2][:, t, :], hid[c % 2][:, t * P:(t + 1) * P],
                                            w2[:, c * D:(c + 1) * D], start=(j == 0 and t == 0),
                                            stop=(j == chunks - 1), skip_group_check=True)
                if j == chunks - 1:
                    last.then_inc(down_ready, 1)

            with pe.Fori(0, GROUPS) as g:
                go_up(g, 0)
                for c in range(steps):
                    if c + 1 < steps:
                        go_up(g, c + 1)
                    go_down(g, c)

        @block.scalar
        def _(act):
            with act.Fori(0, GROUPS) as g:
                for c in range(steps):
                    e, j = divmod(c, chunks)
                    act.wait_ge(up_ready, g * steps + (c + 1))
                    nc.scalar.activation(gated[c % 2][:], up_a[c % 2][:], ACT.Silu,
                                         bias=b1[:, 2 * e * chunks + j:2 * e * chunks + j + 1]).then_inc(gated_ready, 1)

        @block.vector
        def _(dve):
            dve.sem_inc(down_free, 2)

            def add_expert(g, e):
                dve.wait_ge(down_ready, g * 8 + (e + 1))
                for t in range(GT):
                    xt = tile(k.X, g * GT + t)
                    last = nc.vector.scalar_tensor_tensor(
                        out=xt, in0=down[e % 2][:, t, :], scalar=flat(k.GATE[:, bass.ds(g * GT + t, 1), e:e + 1]),
                        in1=xt, op0=ALU.mult, op1=ALU.add)
                last.then_inc(down_free, 1)
                dve.drain()

            with dve.Fori(0, GROUPS) as g:
                for c in range(steps):
                    e, j = divmod(c, chunks)
                    b = (2 * e + 1) * chunks + j
                    dve.wait_ge(gated_ready, g * steps + (c + 1))
                    nc.vector.scalar_tensor_tensor(out=hid[c % 2][:], in0=up_b[c % 2][:], scalar=b1[:, b:b + 1],
                                                   in1=gated[c % 2][:], op0=ALU.add, op1=ALU.mult).then_inc(hid_ready, 1)
                    if j == 1 and e > 0:
                        add_expert(g, e - 1)
                add_expert(g, 7)


def expert_bias(nc, k, name):
    half = TILES // 2
    with Scope(nc, name) as s:
        turned = s.ps("turned", [P, 2, P])
        gates = s.sb("gates", [P, 2, P])
        spread = s.sb("spread", [P, half, D])
        added = [s.ps(f"added{i}", [P, GT, D]) for i in range(4)]
        turned_ready, gates_ready = s.sem("turned_ready"), s.sem("gates_ready")
        spread_ready, added_ready, added_free = s.sem("spread_ready"), s.sem("added_ready"), s.sem("added_free")
        block = s.block()

        @block.gpsimd
        def _(pool):
            nc.gpsimd.tensor_tensor(spread[:],
                                    k.bufs["L3_ffn_b2"][:].rearrange("p (a d) -> p a d", a=1).to_broadcast([P, half, D]),
                                    k.bufs["c_own_tile"][:].rearrange("p (t a) -> p t a", a=1).to_broadcast([P, half, D]),
                                    ALU.mult).then_inc(spread_ready, 1)

        @block.tensor
        def _(pe):
            for h in range(2):
                nc.tensor.transpose(turned[:, h, :], k.GATE[:, h * half:(h + 1) * half, :].rearrange("p t e -> p (t e)"),
                                    k.ident[:]).then_inc(turned_ready, 1)
            pe.wait_ge(gates_ready, 1)
            pe.wait_ge(spread_ready, 1)
            for g in range(GROUPS):
                if g >= 4:
                    pe.wait_ge(added_free, g - 3)
                h, q = divmod(g * GT, half)
                nc.tensor.matmul(added[g % 4][:], gates[:, h, :], spread[:, q:q + GT, :], start=True, stop=True)\
                    .then_inc(added_ready, 1)

        @block.scalar
        def _(act):
            act.wait_ge(turned_ready, 2)
            nc.scalar.copy(gates[:], turned[:]).then_inc(gates_ready, 1)

        @block.vector
        def _(dve):
            for g in range(GROUPS):
                dve.wait_ge(added_ready, g + 1)
                xg = k.X[:, g * GT:(g + 1) * GT, :]
                nc.vector.tensor_tensor(xg, xg, added[g % 4][:], ALU.add).then_inc(added_free, 1)


def l3_ffn(nc, k, name):
    layer_norm(nc, k, name + "_ln", k.bufs["L3_ffn_router"], 8)
    softmax8(nc, k, name + "_gate", True, k.bufs["L3_ffn_rb"])
    expert_bias(nc, k, name + "_bias")
    silu_experts(nc, k, name + "_ffn")


def claim_by_capacity(nc, k, name):
    cap = TOKENS // 8
    with Scope(nc, name) as s:
        before, carry, weight = s.sb("before", [P, P]), s.sb("carry", [P, 8 * TILES]), s.sb("weight", [P, 8, TILES])
        p = s.sb("p", [P, 8, TILES])
        floor, cand, bit = s.sb("floor", [P, 8], U32), s.sb("cand", [P, 8], U32), s.sb("bit", [P, 8], U32)
        take = s.sb("take", [P, 8], U32)
        cmp, tie = s.sb("cmp", [P, 8, TILES]), s.sb("tie", [P, 8, TILES])
        rank, claim, q = s.sb("rank", [P, 8, TILES]), s.sb("claim", [P, 8, TILES]), s.sb("q", [P, 8, TILES])
        some, count, room = s.sb("some", [P, TILES]), s.sb("count", [P, 8]), s.sb("room", [P, 8])
        total = s.ps("total", [P, 8])
        ties_before, ties_tile = s.ps("ties_before", [P, 8 * TILES]), s.ps("ties_tile", [P, 8 * TILES])
        loaded, counted, totalled = s.sem("loaded"), s.sem("counted"), s.sem("totalled")
        tied, ranked = s.sem("tied"), s.sem("ranked")
        block = s.block()
        BITS = 30

        def over_tiles(ap):
            return ap.rearrange("p (e a) -> p e a", a=1).to_broadcast([P, 8, TILES])

        def over_experts(ap):
            return ap.rearrange("p (a t) -> p a t", a=1).to_broadcast([P, 8, TILES])

        def by_token(ap):
            return ap.rearrange("p e t -> p t e")

        @block.sync
        def _(sp):
            sp.dma_start(before[:], k.dram["c_before"]).then_inc(loaded, 16)
            sp.dma_start(carry[:], k.dram["c_not_first_tile"]).then_inc(loaded, 16)
            sp.dma_start(weight[:].rearrange("p e t -> p (e t)"), k.dram["c_early_first"]).then_inc(loaded, 16)

        @block.vector
        def _(dve):
            nc.vector.tensor_copy(by_token(p[:]), k.GATE[:])
            nc.vector.memset(floor[:], 0)
            nc.vector.memset(bit[:], 1 << (BITS - 1))
            dve.drain()
            with dve.Fori(0, BITS) as b:
                nc.vector.tensor_tensor(cand[:], floor[:], bit[:], ALU.bitwise_or)
                dve.drain()
                nc.vector.tensor_tensor(cmp[:], p[:], over_tiles(cand[:].bitcast(F32)), ALU.is_ge)
                nc.vector.tensor_scalar(bit[:], bit[:], 1, None, ALU.logical_shift_right)
                dve.drain()
                nc.vector.tensor_reduce(count[:], cmp[:], AX.X, ALU.add).then_inc(counted, 1)
                dve.wait_ge(totalled, b + 1)
                nc.vector.tensor_scalar(take[:], total[:], float(cap), None, ALU.is_ge)
                dve.drain()
                nc.vector.copy_predicated(floor[:], take[:], cand[:])
                dve.drain()
            nc.vector.tensor_tensor(claim[:], p[:], over_tiles(floor[:].bitcast(F32)), ALU.is_gt)
            nc.vector.tensor_tensor(tie[:], p[:], over_tiles(floor[:].bitcast(F32)), ALU.is_equal)
            dve.drain()
            nc.vector.tensor_reduce(count[:], claim[:], AX.X, ALU.add).then_inc(tied, 1)
            dve.wait_ge(loaded, 48)
            dve.wait_ge(ranked, 1)
            nc.vector.tensor_scalar(room[:], total[:], -1.0, float(cap), ALU.mult, ALU.add)
            nc.vector.tensor_tensor_scan(rank[:].rearrange("p e t -> p (e t)"), carry[:], ties_tile[:], 0.0, ALU.mult, ALU.add)
            dve.drain()
            nc.vector.tensor_tensor(rank[:].rearrange("p e t -> p (e t)"), rank[:].rearrange("p e t -> p (e t)"), ties_tile[:], ALU.subtract)
            dve.drain()
            nc.vector.tensor_tensor(rank[:].rearrange("p e t -> p (e t)"), rank[:].rearrange("p e t -> p (e t)"), ties_before[:], ALU.add)
            dve.drain()
            nc.vector.tensor_tensor(cmp[:], rank[:], over_tiles(room[:]), ALU.is_lt)
            dve.drain()
            nc.vector.tensor_tensor(cmp[:], cmp[:], tie[:], ALU.mult)
            dve.drain()
            nc.vector.tensor_tensor(claim[:], claim[:], cmp[:], ALU.add)
            dve.drain()
            nc.vector.tensor_reduce(some[:], by_token(claim[:]), AX.X, ALU.max)
            dve.drain()
            nc.vector.tensor_scalar(some[:], some[:], -1.0, 1.0, ALU.mult, ALU.add)
            dve.drain()
            nc.vector.tensor_tensor(claim[:], claim[:], over_experts(some[:]), ALU.max)
            dve.drain()
            nc.vector.tensor_tensor(q[:], p[:], claim[:], ALU.mult)
            dve.drain()
            nc.vector.scalar_tensor_tensor(out=q[:].rearrange("p e t -> p (e t)"), in0=claim[:].rearrange("p e t -> p (e t)"),
                                           scalar=-1.0, in1=q[:].rearrange("p e t -> p (e t)"), op0=ALU.add, op1=ALU.add)
            dve.drain()
            nc.vector.tensor_reduce(some[:], by_token(q[:]), AX.X, ALU.max)
            dve.drain()
            nc.vector.tensor_tensor(cmp[:], q[:], over_experts(some[:]), ALU.is_equal)
            dve.drain()
            nc.vector.tensor_tensor(cmp[:], cmp[:], weight[:], ALU.mult)
            dve.drain()
            nc.vector.tensor_reduce(some[:], by_token(cmp[:]), AX.X, ALU.max)
            dve.drain()
            nc.vector.tensor_tensor(cmp[:], cmp[:], over_experts(some[:]), ALU.is_equal)
            dve.drain()
            nc.vector.tensor_tensor(k.GATE[:], by_token(cmp[:]), by_token(p[:]), ALU.mult)

        @block.tensor
        def _(pe):
            with pe.Fori(0, BITS) as b:
                pe.wait_ge(counted, b + 1)
                nc.tensor.matmul(total[:], k.ones[:], count[:], start=True, stop=True).then_inc(totalled, 1)
            pe.wait_ge(tied, 1)
            pe.wait_ge(loaded, 48)
            ties = tie[:].rearrange("p e t -> p (e t)")
            nc.tensor.matmul(total[:], k.ones[:], count[:], start=True, stop=True)
            nc.tensor.matmul(ties_before[:], before[:], ties, start=True, stop=True)
            nc.tensor.matmul(ties_tile[:], k.ones[:], ties, start=True, stop=True).then_inc(ranked, 1)


def l1_ffn(nc, k, name):
    layer_norm(nc, k, name + "_ln", k.bufs["L1_ffn_router"], 8)
    softmax8(nc, k, name + "_probs", None)
    claim_by_capacity(nc, k, name + "_claim")
    gelu_experts(nc, k, name + "_ffn", k.up, k.down, 2)


def group_norm_rows(nc, dve, rows_ps, stats, mv):
    for t in range(GT):
        nc.vector.bn_stats(stats[:, t, :], rows_ps[:, t, :])
    dve.drain()
    for t in range(GT):
        nc.vector.bn_aggr(mv[:, t, :], stats[:, t, :])
    dve.drain()


def per_row(ap, n):
    return ap.rearrange("p (m a) -> p m a", a=1).to_broadcast([P, ap.shape[1], n])


def l0_attn_a(nc, k, name):
    layer_norm(nc, k, name + "_ln")
    with Scope(nc, name) as s:
        names = [("L0a_wqkv", [P, 3 * D]), ("L0a_bqkv", [P, 3 * D]), ("L0a_w1", [P, D]), ("L0a_b1", [P, 1]), ("L0a_w2", [P, 512]), ("L0a_b2", [P, 4]),
                 ("L0a_w3", [P, 512]), ("L0a_b3", [1, GROUP])]
        w = {n: s.sb(n, shape) for n, shape in names}
        xg, qkv = s.sb("xg", [P, GROUP]), s.sb("qkv", [P, GT, 3 * D])
        sq, norm = s.sb("sq", [P, GT, 2 * D]), s.sb("norm", [P, GT * 2])
        qk = s.sb("qk", [P, 2, GROUP])
        e = s.sb("e", [P, BPG, TPB, SEQ])
        rden, o, h1, h2 = s.sb("rden", [P, GROUP]), s.sb("o", [P, GROUP]), s.sb("h1", [P, GROUP]), s.sb("h2", [P, 4, GROUP])
        proj = s.ps("proj", [P, GT, 512])
        qkt_ps, s_ps = proj[:, 0:2, :], proj[:, 2:4, :]
        den_ps, o_ps = s.ps("den_ps", [P, GROUP]), s.ps("o_ps", [P, GROUP])
        y_ps, h1_ps = s.ps("y_ps", [P, GT, D]), s.ps("h1_ps", [P, GROUP])
        loaded, xg_ready, projected, squared = s.sem("loaded"), s.sem("xg_ready"), s.sem("projected"), s.sem("squared")
        rooted, unit, turned, qk_ready = s.sem("rooted"), s.sem("unit"), s.sem("turned"), s.sem("qk_ready")
        scored, exped, summed, mixed = s.sem("scored"), s.sem("exped"), s.sem("summed"), s.sem("mixed")
        h1_up, h1_ready, h2_up, h2_ready = s.sem("h1_up"), s.sem("h1_ready"), s.sem("h2_up"), s.sem("h2_ready")
        y_ready, done = s.sem("y_ready"), s.sem("done")
        block = s.block()

        @block.sync
        def _(sp):
            for n, _ in names:
                sp.dma_start(w[n][:], k.dram[n]).then_inc(loaded, 16)

        @block.tensor
        def _(pe):
            pe.wait_ge(loaded, 16 * len(names))
            with pe.Fori(0, GROUPS) as g:
                pe.wait_ge(xg_ready, g + 1)
                for t in range(GT):
                    last = nc.tensor.matmul(proj[:, t, 0:3 * D], xg[:, t * P:(t + 1) * P], w["L0a_wqkv"][:], start=True, stop=True)
                last.then_inc(projected, 1)
                pe.wait_ge(unit, g + 1)
                for i in range(2):
                    for t in range(GT):
                        last = nc.tensor.transpose(qkt_ps[:, i, t * P:(t + 1) * P], qkv[:, t, i * D:(i + 1) * D], k.ident[:])
                last.then_inc(turned, 1)
                pe.wait_ge(qk_ready, g + 1)
                for b in range(BPG):
                    for kt in range(TPB):
                        c = b * SEQ + kt * P
                        last = nc.tensor.matmul(s_ps[:, b, kt * SEQ:(kt + 1) * SEQ], qk[:, 1, c:c + P],
                                                qk[:, 0, b * SEQ:(b + 1) * SEQ], start=True, stop=True)
                    last.then_inc(scored, 1)
                for b in range(BPG):
                    pe.wait_ge(exped, g * BPG + (b + 1))
                    for kt in range(TPB):
                        nc.tensor.matmul(den_ps[:, b * SEQ:(b + 1) * SEQ], k.ones[:], e[:, b, kt, :],
                                         start=(kt == 0), stop=(kt == TPB - 1))
                    for kt in range(TPB):
                        last = nc.tensor.matmul(o_ps[:, b * SEQ:(b + 1) * SEQ], qkv[:, b * TPB + kt, 2 * D:3 * D], e[:, b, kt, :],
                                                start=(kt == 0), stop=(kt == TPB - 1))
                last.then_inc(summed, 1)
                nc.tensor.matmul(y_ps[:], k.ones_row[0:1, 0:P], w["L0a_b3"][:], start=True, stop=False, skip_group_check=True)
                pe.wait_ge(mixed, g + 1)
                nc.tensor.matmul(h1_ps[:], w["L0a_w1"][:], o[:], start=True, stop=True).then_inc(h1_up, 1)
                pe.wait_ge(h1_ready, g + 1)
                for j in range(4):
                    nc.tensor.matmul(proj[:, j, :], w["L0a_w2"][:, j * P:(j + 1) * P], h1[:], start=True, stop=True)\
                        .then_inc(h2_up, 1)
                for j in range(4):
                    pe.wait_ge(h2_ready, g * 4 + (j + 1))
                    for t in range(GT):
                        last = nc.tensor.matmul(y_ps[:, t, :], h2[:, j, t * P:(t + 1) * P], w["L0a_w3"][:, j * D:(j + 1) * D],
                                                start=False, stop=(j == 3), skip_group_check=True)
                last.then_inc(y_ready, 1)

        @block.scalar
        def _(act):
            act.wait_ge(loaded, 16 * len(names))
            with act.Fori(0, GROUPS) as g:
                act.wait_ge(done, g)
                nc.scalar.copy(xg[:], k.XNT[:, bass.ds(g * GROUP, GROUP)]).then_inc(xg_ready, 1)
                act.wait_ge(squared, g + 1)
                nc.scalar.activation(norm[:], norm[:], ACT.Sqrt).then_inc(rooted, 1)
                act.wait_ge(turned, g + 1)
                nc.scalar.copy(qk[:], qkt_ps).then_inc(qk_ready, 1)
                for b in range(BPG):
                    act.wait_ge(scored, g * BPG + (b + 1))
                    nc.scalar.activation(e[:, b, :, :], s_ps[:, b, :], ACT.Exp).then_inc(exped, 1)
                act.wait_ge(h1_up, g + 1)
                nc.scalar.activation(h1[:], h1_ps[:], ACT.Relu, bias=w["L0a_b1"][:]).then_inc(h1_ready, 1)
                for j in range(4):
                    act.wait_ge(h2_up, g * 4 + (j + 1))
                    nc.scalar.activation(h2[:, j, :], proj[:, j, :], ACT.Relu, bias=w["L0a_b2"][:, j:j + 1]).then_inc(h2_ready, 1)

        @block.vector
        def _(dve):
            dve.wait_ge(loaded, 16 * len(names))
            with dve.Fori(0, GROUPS) as g:
                dve.wait_ge(projected, g + 1)
                nc.vector.tensor_tensor(qkv[:], proj[:, :, 0:3 * D],
                                        w["L0a_bqkv"][:].rearrange("p (a n) -> p a n", a=1).to_broadcast([P, GT, 3 * D]), ALU.add)
                dve.drain()
                nc.vector.tensor_tensor(sq[:], qkv[:, :, 0:2 * D], qkv[:, :, 0:2 * D], ALU.mult)
                dve.drain()
                nc.vector.tensor_reduce(norm[:], sq[:].rearrange("p t (i d) -> p (t i) d", d=D), AX.X, ALU.add).then_inc(squared, 1)
                dve.wait_ge(rooted, g + 1)
                nc.vector.tensor_scalar(norm[:], norm[:], 1e-12, None, ALU.max)
                dve.drain()
                nc.vector.reciprocal(norm[:], norm[:])
                dve.drain()
                for t in range(GT):
                    rows = qkv[:, t, 0:2 * D].rearrange("p (i d) -> p i d", d=D)
                    last = nc.vector.tensor_tensor(rows, rows, per_row(norm[:, 2 * t:2 * t + 2], D), ALU.mult)
                last.then_inc(unit, 1)
                dve.wait_ge(summed, g + 1)
                nc.vector.reciprocal(rden[:], den_ps[:])
                dve.drain()
                nc.vector.tensor_tensor(o[:], o_ps[:], rden[:], ALU.mult).then_inc(mixed, 1)
                dve.wait_ge(y_ready, g + 1)
                x = k.X[:, bass.ds(g * GT, GT), :]
                nc.vector.tensor_tensor(x, x, y_ps[:], ALU.add).then_inc(done, 1)


def l0_attn_b(nc, k, name):
    layer_norm(nc, k, name + "_ln")
    QK = 3 * D
    HD = 8
    with Scope(nc, name) as s:
        names = [("L0b_w", [P, 5 * D]), ("L0b_b", [P, 5 * D]), ("L0b_wo", [P, D]), ("L0b_bo", [1, GROUP]),
                 ("L0b_g", [P, 1]), ("L0b_be", [P, 1]), ("c_heads8", [P, P])]
        w = {n: s.sb(n, shape) for n, shape in names}
        xg, z = s.sb("xg", [P, GROUP]), s.sb("z", [P, GT, 5 * D])
        a, sq = s.sb("a", [P, GT, QK]), s.sb("sq", [P, GT, QK])
        norm = s.sb("norm", [P, GT * QK // HD])
        minus = s.sb("minus", [P, GT])
        qt, state, half_state = s.sb("qt", [P, GROUP]), s.sb("state", [P, BPG, P]), s.sb("half_state", [P, BPG, P])
        stats, mv, rstd = s.sb("stats", [P, GT, 6]), s.sb("mv", [P, GT, 2]), s.sb("rstd", [P, GT])
        on, ont = s.sb("on", [P, GT, D]), s.sb("ont", [P, GROUP])
        proj = s.ps("proj", [P, GT, 4 * D])
        proj_v = s.ps("proj_v", [P, GT, D])
        turned, st_ps, o_ps = s.ps("turned", [P, GROUP]), s.ps("st_ps", [P, BPG, 2, P]), s.ps("o_ps", [P, GT, D])
        loaded, w_ready, xg_ready, projected = s.sem("loaded"), s.sem("w_ready"), s.sem("xg_ready"), s.sem("projected")
        biased, activated, squared, rooted, unit = s.sem("biased"), s.sem("activated"), s.sem("squared"), s.sem("rooted"), s.sem("unit")
        turned_q, qt_ready, stated, state_ready = s.sem("turned_q"), s.sem("qt_ready"), s.sem("stated"), s.sem("state_ready")
        o_ready, var_ready, rstd_ready, on_ready = s.sem("o_ready"), s.sem("var_ready"), s.sem("rstd_ready"), s.sem("on_ready")
        turned_o, ont_ready, y_ready, done = s.sem("turned_o"), s.sem("ont_ready"), s.sem("y_ready"), s.sem("done")
        block = s.block()

        @block.sync
        def _(sp):
            for n, _ in names:
                sp.dma_start(w[n][:], k.dram[n]).then_inc(loaded, 16)

        @block.gpsimd
        def _(pool):
            nc.gpsimd.memset(minus[:], -0.5)
            pool.drain()
            with pool.Fori(0, GROUPS) as g:
                pool.wait_ge(var_ready, g + 1)
                nc.gpsimd.tensor_tensor(rstd[:], rstd[:], minus[:], ALU.pow).then_inc(rstd_ready, 1)

        @block.tensor
        def _(pe):
            pe.wait_ge(w_ready, 1)
            with pe.Fori(0, GROUPS) as g:
                pe.wait_ge(xg_ready, g + 1)
                for t in range(GT):
                    xt = xg[:, t * P:(t + 1) * P]
                    nc.tensor.matmul(proj[:, t, :], xt, w["L0b_w"][:, 0:4 * D], start=True, stop=True)
                    last = nc.tensor.matmul(proj_v[:, t, :], xt, w["L0b_w"][:, 4 * D:5 * D], start=True, stop=True)
                last.then_inc(projected, 1)
                pe.wait_ge(unit, g + 1)
                for t in range(GT):
                    last = nc.tensor.transpose(turned[:, t * P:(t + 1) * P], a[:, t, 0:D], k.ident[:])
                last.then_inc(turned_q, 1)
                for b in range(BPG):
                    for i in range(2):
                        for t in range(TPB):
                            last = nc.tensor.matmul(st_ps[:, b, i, :], a[:, b * TPB + t, (1 + i) * D:(2 + i) * D],
                                                    z[:, b * TPB + t, (3 + i) * D:(4 + i) * D], start=(t == 0), stop=(t == TPB - 1))
                last.then_inc(stated, 1)
                pe.wait_ge(state_ready, g + 1)
                pe.wait_ge(qt_ready, g + 1)
                for t in range(GT):
                    last = nc.tensor.matmul(o_ps[:, t, :], qt[:, t * P:(t + 1) * P], state[:, t // TPB, :], start=True, stop=True)
                last.then_inc(o_ready, 1)
                pe.wait_ge(on_ready, g + 1)
                for t in range(GT):
                    last = nc.tensor.transpose(turned[:, t * P:(t + 1) * P], on[:, t, :], k.ident[:])
                last.then_inc(turned_o, 1)
                nc.tensor.matmul(proj_v[:], k.ones_row[0:1, 0:P], w["L0b_bo"][:], start=True, stop=False, skip_group_check=True)
                pe.wait_ge(ont_ready, g + 1)
                for t in range(GT):
                    last = nc.tensor.matmul(proj_v[:, t, :], ont[:, t * P:(t + 1) * P], w["L0b_wo"][:], start=False, stop=True,
                                            skip_group_check=True)
                last.then_inc(y_ready, 1)

        @block.scalar
        def _(act):
            act.wait_ge(loaded, 16 * len(names))
            with act.Fori(0, GROUPS) as g:
                act.wait_ge(done, g)
                nc.scalar.copy(xg[:], k.XNT[:, bass.ds(g * GROUP, GROUP)]).then_inc(xg_ready, 1)
                act.wait_ge(biased, g + 1)
                nc.scalar.activation(a[:], z[:, :, 0:QK], ACT.Silu).then_inc(activated, 1)
                act.wait_ge(squared, g + 1)
                nc.scalar.activation(norm[:], norm[:], ACT.Sqrt).then_inc(rooted, 1)
                act.wait_ge(turned_q, g + 1)
                nc.scalar.copy(qt[:], turned[:]).then_inc(qt_ready, 1)
                act.wait_ge(turned_o, g + 1)
                nc.scalar.activation(ont[:], turned[:], ACT.Identity, bias=w["L0b_be"][:], scale=w["L0b_g"][:]).then_inc(ont_ready, 1)

        @block.vector
        def _(dve):
            dve.wait_ge(loaded, 16 * len(names))
            for i in range(5):
                last = nc.vector.tensor_tensor(w["L0b_w"][:, i * D:(i + 1) * D], w["L0b_w"][:, i * D:(i + 1) * D], k.ident[:], ALU.add)
            last.then_inc(w_ready, 1)
            with dve.Fori(0, GROUPS) as g:
                dve.wait_ge(projected, g + 1)
                for t in range(GT):
                    nc.vector.tensor_tensor(z[:, t, 0:4 * D], proj[:, t, :], w["L0b_b"][:, 0:4 * D], ALU.add)
                nc.vector.tensor_tensor(z[:, :, 4 * D:5 * D], proj_v[:],
                                        w["L0b_b"][:, 4 * D:5 * D].rearrange("p (a d) -> p a d", a=1).to_broadcast([P, GT, D]),
                                        ALU.add).then_inc(biased, 1)
                dve.wait_ge(activated, g + 1)
                nc.vector.tensor_scalar(a[:], a[:], 0.5, None, ALU.add)
                dve.drain()
                nc.vector.tensor_tensor(sq[:], a[:], a[:], ALU.mult)
                dve.drain()
                nc.vector.tensor_reduce(norm[:], sq[:].rearrange("p t (h d) -> p (t h) d", d=HD), AX.X, ALU.add).then_inc(squared, 1)
                dve.wait_ge(rooted, g + 1)
                nc.vector.tensor_scalar(norm[:], norm[:], 1e-6, None, ALU.add)
                dve.drain()
                nc.vector.reciprocal(norm[:], norm[:])
                dve.drain()
                heads = a[:].rearrange("p t (h d) -> p (t h) d", d=HD)
                nc.vector.tensor_tensor(heads, heads, per_row(norm[:], HD), ALU.mult).then_inc(unit, 1)
                dve.wait_ge(stated, g + 1)
                for b in range(BPG):
                    nc.vector.scalar_tensor_tensor(out=half_state[:, b, :], in0=st_ps[:, b, 0, :], scalar=1.0 / SEQ ** 2,
                                                   in1=w["c_heads8"][:], op0=ALU.mult, op1=ALU.mult)
                dve.drain()
                for b in range(BPG):
                    last = nc.vector.tensor_tensor(state[:, b, :], half_state[:, b, :], st_ps[:, b, 1, :], ALU.mult)
                last.then_inc(state_ready, 1)
                dve.wait_ge(o_ready, g + 1)
                group_norm_rows(nc, dve, o_ps, stats, mv)
                nc.vector.tensor_scalar(rstd[:], mv[:, :, 1], 1e-5, None, ALU.add).then_inc(var_ready, 1)
                dve.wait_ge(rstd_ready, g + 1)
                for t in range(GT):
                    last = nc.vector.tensor_scalar(on[:, t, :], o_ps[:, t, :], mv[:, t, 0:1], rstd[:, t:t + 1], ALU.subtract, ALU.mult)
                last.then_inc(on_ready, 1)
                dve.wait_ge(y_ready, g + 1)
                x = k.X[:, bass.ds(g * GT, GT), :]
                nc.vector.tensor_tensor(x, x, proj_v[:], ALU.add).then_inc(done, 1)


def l3_attn_b(nc, k, name):
    layer_norm(nc, k, name + "_ln")
    HD, CH = 8, 4
    with Scope(nc, name) as s:
        names = [("L3b_w", [P, 3 * D]), ("L3b_b", [P, 3 * D]), ("L3b_wo", [P, D]), ("L3b_bo", [1, GROUP]),
                 ("L3b_g1", [P, 1]), ("L3b_be1", [P, 1]), ("L3b_g2", [P, D]), ("L3b_be2", [P, D]),
                 ("L3b_w1", [P, CH * P]), ("L3b_b1", [P, CH]), ("L3b_w2", [P, CH * D]), ("L3b_b2", [1, GROUP]),
                 ("c_heads8", [P, P])]
        w = {n: s.sb(n, shape) for n, shape in names}
        xg, z = s.sb("xg", [P, GROUP]), s.sb("z", [P, GT, 3 * D])
        low, sq = s.sb("low", [P, GT, 2 * D]), s.sb("sq", [P, GT, 2 * D])
        norm, minus = s.sb("norm", [P, GT * 2 * D // HD]), s.sb("minus", [P, GT])
        qt, state, ctxt = s.sb("qt", [P, GROUP]), s.sb("state", [P, BPG, P]), s.sb("ctxt", [P, GROUP])
        stats, mv, rstd = s.sb("stats", [P, GT, 6]), s.sb("mv", [P, GT, 2]), s.sb("rstd", [P, GT])
        rows, at, hid = s.sb("rows", [P, GT, D]), s.sb("at", [P, GROUP]), s.sb("hid", [P, CH, GROUP])
        proj = s.ps("proj", [P, GT, 512])
        turned, st_ps, ctx_ps, y_ps = s.ps("turned", [P, GROUP]), s.ps("st_ps", [P, BPG, P]), s.ps("ctx_ps", [P, GROUP]), s.ps("y_ps", [P, GT, D])
        loaded, xg_ready, projected, clipped = s.sem("loaded"), s.sem("xg_ready"), s.sem("projected"), s.sem("clipped")
        exped, squared, rooted, unit = s.sem("exped"), s.sem("squared"), s.sem("rooted"), s.sem("unit")
        turned_q, qt_ready, stated, state_ready = s.sem("turned_q"), s.sem("qt_ready"), s.sem("stated"), s.sem("state_ready")
        ctx_up, ctx_ready, y1_ready, var_ready = s.sem("ctx_up"), s.sem("ctx_ready"), s.sem("y1_ready"), s.sem("var_ready")
        rstd_ready, rows_ready, turned_a, at_ready = s.sem("rstd_ready"), s.sem("rows_ready"), s.sem("turned_a"), s.sem("at_ready")
        hid_up, hid_ready, y2_ready, done = s.sem("hid_up"), s.sem("hid_ready"), s.sem("y2_ready"), s.sem("done")
        block = s.block()

        @block.sync
        def _(sp):
            for n, _ in names:
                sp.dma_start(w[n][:], k.dram[n]).then_inc(loaded, 16)

        @block.gpsimd
        def _(pool):
            nc.gpsimd.memset(minus[:], -0.5)
            pool.drain()
            with pool.Fori(0, GROUPS) as g:
                for i in range(2):
                    pool.wait_ge(var_ready, g * 2 + (i + 1))
                    nc.gpsimd.tensor_tensor(rstd[:], rstd[:], minus[:], ALU.pow).then_inc(rstd_ready, 1)

        @block.tensor
        def _(pe):
            pe.wait_ge(loaded, 16 * len(names))
            with pe.Fori(0, GROUPS) as g:
                pe.wait_ge(xg_ready, g + 1)
                for t in range(GT):
                    last = nc.tensor.matmul(proj[:, t, 0:3 * D], xg[:, t * P:(t + 1) * P], w["L3b_w"][:], start=True, stop=True)
                last.then_inc(projected, 1)
                pe.wait_ge(unit, g + 1)
                for t in range(GT):
                    last = nc.tensor.transpose(turned[:, t * P:(t + 1) * P], low[:, t, 0:D], k.ident[:])
                last.then_inc(turned_q, 1)
                for b in range(BPG):
                    for t in range(TPB):
                        r = b * TPB + t
                        last = nc.tensor.matmul(st_ps[:, b, :], low[:, r, D:2 * D], z[:, r, 2 * D:3 * D], start=(t == 0), stop=(t == TPB - 1))
                last.then_inc(stated, 1)
                pe.wait_ge(state_ready, g + 1)
                pe.wait_ge(qt_ready, g + 1)
                for b in range(BPG):
                    last = nc.tensor.matmul(ctx_ps[:, b * SEQ:(b + 1) * SEQ], state[:, b, :], qt[:, b * SEQ:(b + 1) * SEQ], start=True, stop=True)
                last.then_inc(ctx_up, 1)
                nc.tensor.matmul(y_ps[:], k.ones_row[0:1, 0:P], w["L3b_bo"][:], start=True, stop=False, skip_group_check=True)
                for t in range(GT):
                    nc.tensor.matmul(y_ps[:, t, :], xg[:, t * P:(t + 1) * P], k.ident[:], start=False, stop=False, skip_group_check=True)
                pe.wait_ge(ctx_ready, g + 1)
                for t in range(GT):
                    last = nc.tensor.matmul(y_ps[:, t, :], ctxt[:, t * P:(t + 1) * P], w["L3b_wo"][:], start=False, stop=True,
                                            skip_group_check=True)
                last.then_inc(y1_ready, 1)
                pe.wait_ge(rows_ready, g + 1)
                for t in range(GT):
                    last = nc.tensor.transpose(turned[:, t * P:(t + 1) * P], rows[:, t, :], k.ident[:])
                last.then_inc(turned_a, 1)
                pe.wait_ge(at_ready, g + 1)
                for j in range(CH):
                    nc.tensor.matmul(proj[:, j, :], w["L3b_w1"][:, j * P:(j + 1) * P], at[:], start=True, stop=True).then_inc(hid_up, 1)
                nc.tensor.matmul(y_ps[:], k.ones_row[0:1, 0:P], w["L3b_b2"][:], start=True, stop=False, skip_group_check=True)
                for t in range(GT):
                    nc.tensor.matmul(y_ps[:, t, :], at[:, t * P:(t + 1) * P], k.ident[:], start=False, stop=False, skip_group_check=True)
                for j in range(CH):
                    pe.wait_ge(hid_ready, g * CH + (j + 1))
                    for t in range(GT):
                        last = nc.tensor.matmul(y_ps[:, t, :], hid[:, j, t * P:(t + 1) * P], w["L3b_w2"][:, j * D:(j + 1) * D],
                                                start=False, stop=(j == CH - 1), skip_group_check=True)
                last.then_inc(y2_ready, 1)

        @block.scalar
        def _(act):
            act.wait_ge(loaded, 16 * len(names))
            with act.Fori(0, GROUPS) as g:
                act.wait_ge(done, g)
                nc.scalar.copy(xg[:], k.XNT[:, bass.ds(g * GROUP, GROUP)]).then_inc(xg_ready, 1)
                act.wait_ge(clipped, g + 1)
                nc.scalar.activation(low[:], low[:], ACT.Exp).then_inc(exped, 1)
                act.wait_ge(squared, g + 1)
                nc.scalar.activation(norm[:], norm[:], ACT.Sqrt).then_inc(rooted, 1)
                act.wait_ge(turned_q, g + 1)
                nc.scalar.copy(qt[:], turned[:]).then_inc(qt_ready, 1)
                act.wait_ge(ctx_up, g + 1)
                nc.scalar.copy(ctxt[:], ctx_ps[:]).then_inc(ctx_ready, 1)
                act.wait_ge(turned_a, g + 1)
                nc.scalar.activation(at[:], turned[:], ACT.Identity, bias=w["L3b_be1"][:], scale=w["L3b_g1"][:]).then_inc(at_ready, 1)
                for j in range(CH):
                    act.wait_ge(hid_up, g * CH + (j + 1))
                    nc.scalar.activation(hid[:, j, :], proj[:, j, :], ACT.Gelu, bias=w["L3b_b1"][:, j:j + 1]).then_inc(hid_ready, 1)

        @block.vector
        def _(dve):
            def normalise(g, i):
                group_norm_rows(nc, dve, y_ps, stats, mv)
                nc.vector.tensor_scalar(rstd[:], mv[:, :, 1], 1e-12, None, ALU.add).then_inc(var_ready, 1)
                dve.wait_ge(rstd_ready, g * 2 + (i + 1))
                for t in range(GT):
                    last = nc.vector.tensor_scalar(rows[:, t, :], y_ps[:, t, :], mv[:, t, 0:1], rstd[:, t:t + 1], ALU.subtract, ALU.mult)
                return last

            def over_tiles(ap):
                return ap.rearrange("p (a n) -> p a n", a=1).to_broadcast([P, GT, ap.shape[1]])

            dve.wait_ge(loaded, 16 * len(names))
            with dve.Fori(0, GROUPS) as g:
                dve.wait_ge(projected, g + 1)
                nc.vector.tensor_tensor(z[:], proj[:, :, 0:3 * D], over_tiles(w["L3b_b"][:]), ALU.add)
                dve.drain()
                nc.vector.tensor_scalar(low[:], z[:, :, 0:2 * D], 0.0, None, ALU.min).then_inc(clipped, 1)
                nc.vector.tensor_scalar(z[:, :, 0:2 * D], z[:, :, 0:2 * D], 0.0, None, ALU.max)
                dve.drain()
                dve.wait_ge(exped, g + 1)
                nc.vector.scalar_tensor_tensor(out=low[:], in0=low[:], scalar=-1.0, in1=z[:, :, 0:2 * D], op0=ALU.add, op1=ALU.add)
                dve.drain()
                nc.vector.tensor_tensor(sq[:], low[:], low[:], ALU.mult)
                dve.drain()
                nc.vector.tensor_reduce(norm[:], sq[:].rearrange("p t (h d) -> p (t h) d", d=HD), AX.X, ALU.add).then_inc(squared, 1)
                dve.wait_ge(rooted, g + 1)
                nc.vector.reciprocal(norm[:], norm[:])
                dve.drain()
                heads = low[:].rearrange("p t (h d) -> p (t h) d", d=HD)
                nc.vector.tensor_tensor(heads, heads, per_row(norm[:], HD), ALU.mult).then_inc(unit, 1)
                dve.wait_ge(stated, g + 1)
                for b in range(BPG):
                    last = nc.vector.scalar_tensor_tensor(out=state[:, b, :], in0=st_ps[:, b, :], scalar=HD ** -0.5, in1=w["c_heads8"][:],
                                                          op0=ALU.mult, op1=ALU.mult)
                last.then_inc(state_ready, 1)
                dve.wait_ge(y1_ready, g + 1)
                normalise(g, 0).then_inc(rows_ready, 1)
                dve.wait_ge(y2_ready, g + 1)
                normalise(g, 1)
                dve.drain()
                nc.vector.tensor_tensor(rows[:], rows[:], over_tiles(w["L3b_g2"][:]), ALU.mult)
                dve.drain()
                nc.vector.tensor_tensor(rows[:], rows[:], over_tiles(w["L3b_be2"][:]), ALU.add)
                dve.drain()
                x = k.X[:, bass.ds(g * GT, GT), :]
                nc.vector.tensor_tensor(x, x, rows[:], ALU.add).then_inc(done, 1)


def l3_attn_a(nc, k, name):
    layer_norm(nc, k, name + "_ln")
    H, HD, WIN = 16, 8, 32
    WPT, WPG = P // WIN, GROUP // WIN
    HB = P // WIN
    with Scope(nc, name) as s:
        names = [("L3a_wq", [P, D]), ("L3a_wk", [P, D]), ("L3a_wv", [P, HB * HD]), ("L3a_wo", [P, D]), ("L3a_bo", [1, GROUP]),
                 ("c_head_of_row8", [P, H]), ("c_blocks32x8", [P, HB * HD])]
        w = {n: s.sb(n, shape) for n, shape in names}
        xg, q, kk = s.sb("xg", [P, GROUP]), s.sb("q", [P, GROUP]), s.sb("kk", [P, GROUP])
        xrep = s.sb("xrep", [P, WPG, HB, WIN])
        keys, vals = s.sb("keys", [P, WPG, H, WIN]), s.sb("vals", [P, WPG, HB * HD])
        p, top, den = s.sb("p", [P, GT * H, WIN]), s.sb("top", [P, GT * H]), s.sb("den", [P, GT * H])
        pt, o, ot = s.sb("pt", [P, GT, H // HB, P]), s.sb("o", [P, GT, D]), s.sb("ot", [P, GROUP])
        big_a, big_b = s.ps("big_a", [P, GT, 512]), s.ps("big_b", [P, GT, 512])
        q_ps, k_ps, v_ps, y_ps = (big_a[:, i, :] for i in range(4))
        loaded, xg_ready, xrep_ready, projected = s.sem("loaded"), s.sem("xg_ready"), s.sem("xrep_ready"), s.sem("projected")
        k_ready, qv_ready, keys_ready, scored = s.sem("k_ready"), s.sem("qv_ready"), s.sem("keys_ready"), s.sem("scored")
        shifted, exped, probs_ready, turned = s.sem("shifted"), s.sem("exped"), s.sem("probs_ready"), s.sem("turned")
        pt_ready, o_up, o_ready, turned_o, ot_ready = s.sem("pt_ready"), s.sem("o_up"), s.sem("o_ready"), s.sem("turned_o"), s.sem("ot_ready")
        v_ready, y_ready, done = s.sem("v_ready"), s.sem("y_ready"), s.sem("done")
        block = s.block()

        @block.sync
        def _(sp):
            for n, _ in names:
                sp.dma_start(w[n][:], k.dram[n]).then_inc(loaded, 16)

        @block.tensor
        def _(pe):
            pe.wait_ge(loaded, 16 * len(names))
            with pe.Fori(0, GROUPS) as g:
                pe.wait_ge(xg_ready, g + 1)
                nc.tensor.matmul(k_ps, w["L3a_wk"][:], xg[:], start=True, stop=True)
                nc.tensor.matmul(q_ps, w["L3a_wq"][:], xg[:], start=True, stop=True)
                pe.wait_ge(xrep_ready, g + 1)
                for n in range(WPG):
                    last = nc.tensor.matmul(v_ps[:, n * HB * HD:(n + 1) * HB * HD], xrep[:, n, :, :].rearrange("p h u -> p (h u)"),
                                            w["L3a_wv"][:], start=True, stop=True)
                last.then_inc(projected, 1)
                pe.wait_ge(qv_ready, g + 1)
                pe.wait_ge(v_ready, g + 1)
                pe.wait_ge(keys_ready, g + 1)
                for t in range(GT):
                    for i in range(WPT):
                        n = t * WPT + i
                        last = nc.tensor.matmul(big_a[i * WIN:(i + 1) * WIN, t, :], q[:, n * WIN:(n + 1) * WIN],
                                                keys[:, n, :, :].rearrange("p h u -> p (h u)"), start=True, stop=True)
                last.then_inc(scored, 1)
                pe.wait_ge(probs_ready, g + 1)
                for t in range(GT):
                    for c in range(H // HB):
                        last = nc.tensor.transpose(big_b[:, t, c * P:(c + 1) * P],
                                                   p[:, t * H + c * HB:t * H + (c + 1) * HB, :].rearrange("p h u -> p (h u)"), k.ident[:])
                last.then_inc(turned, 1)
                pe.wait_ge(pt_ready, g + 1)
                for t in range(GT):
                    for c in range(H // HB):
                        for i in range(WPT):
                            last = nc.tensor.matmul(big_a[i * WIN:(i + 1) * WIN, 0, t * D + c * HB * HD:t * D + (c + 1) * HB * HD],
                                                    pt[:, t, c, i * WIN:(i + 1) * WIN], vals[:, t * WPT + i, :], start=True, stop=True)
                last.then_inc(o_up, 1)
                pe.wait_ge(o_ready, g + 1)
                for t in range(GT):
                    last = nc.tensor.transpose(big_a[:, 1, t * P:(t + 1) * P], o[:, t, :], k.ident[:])
                last.then_inc(turned_o, 1)
                nc.tensor.matmul(y_ps, k.ones_row[0:1, 0:P], w["L3a_bo"][:], start=True, stop=False, skip_group_check=True)
                pe.wait_ge(ot_ready, g + 1)
                for t in range(GT):
                    last = nc.tensor.matmul(y_ps[:, t * D:(t + 1) * D], ot[:, t * P:(t + 1) * P], w["L3a_wo"][:], start=False, stop=True,
                                            skip_group_check=True)
                last.then_inc(y_ready, 1)

        @block.scalar
        def _(act):
            with act.Fori(0, GROUPS) as g:
                act.wait_ge(done, g)
                xnt = k.XNT[:, bass.ds(g * GROUP, GROUP)]
                nc.scalar.copy(xg[:], xnt).then_inc(xg_ready, 1)
                act.wait_ge(projected, g + 1)
                nc.scalar.copy(kk[:], k_ps).then_inc(k_ready, 1)
                nc.scalar.copy(q[:], q_ps).then_inc(qv_ready, 1)
                act.wait_ge(shifted, g + 1)
                nc.scalar.activation(p[:], p[:], ACT.Exp, scale=HD ** -0.5).then_inc(exped, 1)
                act.wait_ge(turned, g + 1)
                nc.scalar.copy(pt[:].rearrange("p t c n -> p t (c n)"), big_b[:]).then_inc(pt_ready, 1)
                act.wait_ge(o_up, g + 1)
                nc.scalar.copy(o[:].rearrange("p t d -> p (t d)"), big_a[:, 0, :]).then_inc(o_ready, 1)
                act.wait_ge(turned_o, g + 1)
                nc.scalar.copy(ot[:], big_a[:, 1, :]).then_inc(ot_ready, 1)

        @block.vector
        def _(dve):
            dve.wait_ge(loaded, 16 * len(names))
            with dve.Fori(0, GROUPS) as g:
                dve.wait_ge(xg_ready, g + 1)
                for h in range(HB):
                    last = nc.vector.tensor_copy(xrep[:, :, h, :], xg[:].rearrange("p (n u) -> p n u", u=WIN))
                last.then_inc(xrep_ready, 1)
                dve.wait_ge(projected, g + 1)
                blocks = w["c_blocks32x8"][:].rearrange("p (a n) -> p a n", a=1).to_broadcast([P, WPG, HB * HD])
                nc.vector.tensor_tensor(vals[:], v_ps.rearrange("p (w n) -> p w n", w=WPG), blocks, ALU.mult).then_inc(v_ready, 1)
                dve.wait_ge(k_ready, g + 1)
                for h in range(H):
                    last = nc.vector.tensor_scalar(keys[:, :, h, :], kk[:].rearrange("p (n u) -> p n u", u=WIN),
                                                   w["c_head_of_row8"][:, h:h + 1], None, ALU.mult)
                last.then_inc(keys_ready, 1)
                dve.wait_ge(scored, g + 1)
                scores = big_a[:].rearrange("p t (h u) -> p (t h) u", u=WIN)
                nc.vector.tensor_reduce(top[:], scores, AX.X, ALU.max)
                dve.drain()
                nc.vector.tensor_tensor(p[:], scores, per_row(top[:], WIN), ALU.subtract).then_inc(shifted, 1)
                dve.wait_ge(exped, g + 1)
                nc.vector.tensor_reduce(den[:], p[:], AX.X, ALU.add)
                dve.drain()
                nc.vector.reciprocal(den[:], den[:])
                dve.drain()
                nc.vector.tensor_tensor(p[:], p[:], per_row(den[:], WIN), ALU.mult).then_inc(probs_ready, 1)
                dve.wait_ge(y_ready, g + 1)
                x = k.X[:, bass.ds(g * GT, GT), :]
                nc.vector.tensor_tensor(x, x, y_ps.rearrange("p (t d) -> p t d", d=D), ALU.add).then_inc(done, 1)

ED, CHH, NST = 256, 2, 16


class StateScan:

    def __init__(self, nc, k, s, delta, dx, a):
        self.nc, self.k, self.delta, self.dx, self.a = nc, k, delta, dx, a
        self.pick32 = s.sb("pick32", [96, 32])
        self.pick = s.sb("pick", [96, 32], BF16)
        self.parts = [s.sb(f"parts{i}", [96, GROUP], BF16) for i in range(2)]
        self.rest = s.sb("rest", [96, GROUP])
        self.spread, self.y_ps = s.ps("spread", [P, 4, GROUP]), s.ps("y_ps", [P, CHH, GROUP])
        self.da = [s.sb(f"da{i}", [P, CHH, BPG, SEQ]) for i in range(2)]
        spare = [k.XN[:, i * CHH * GT:(i + 1) * CHH * GT, :].rearrange("p (i t) d -> p i (t d)", i=CHH) for i in range(4)]
        self.u, self.hc = spare[0:2], spare[2:4]
        self.h = [s.sb(f"h{i}", [P, CHH, GROUP]) for i in range(2)]
        self.zeros = s.sb("zeros", [P, CHH, BPG])
        self.split_ready, self.y_ready = s.sem("split_ready"), s.sem("y_ready")
        self.spread_ready, self.da_ready, self.reset = s.sem("spread_ready"), s.sem("da_ready"), s.sem("reset")
        self.hc_ready, self.added_up = s.sem("hc_ready"), s.sem("added_up")

    def pe_spread(self, pe, g, par, n):
        if n == 0:
            pe.wait_ge(self.split_ready, g + 1)
        for i in range(2):
            last = self.nc.tensor.matmul(self.spread[:, 2 * (n % 2) + i, :], self.pick[:, i * NST + n:i * NST + n + 1].to_broadcast([96, P]),
                                         self.parts[par][:], start=True, stop=True)
        last.then_inc(self.spread_ready, 1)

    def pe_state(self, pe, g, par, n, first, last_group):
        pe.wait_ge(self.hc_ready, g * NST + (n + 1))
        if n + 2 < NST:
            self.pe_spread(pe, g, par, n + 2)
        elif not last_group:
            self.pe_spread(pe, g + 1, 1 - par, n + 2 - NST)
        if n == 0 and not first:
            pe.wait_ge(self.y_ready, g)
        for i in range(CHH):
            last = self.nc.tensor.matmul(self.y_ps[:, i, :], self.k.ident[:], self.hc[n % 2][:, i, :], start=(n == 0), stop=(n == NST - 1))
        last.then_inc(self.added_up, 1)

    def act_state(self, act, g, par, n, first):
        if n >= 2 or not first:
            act.wait_ge(self.hc_ready, g * NST + (n - 1))
        for i in range(CHH):
            last = self.nc.scalar.activation(self.da[n % 2][:, i, :, :].rearrange("p b t -> p (b t)"), self.delta[par][:, i, :], ACT.Exp,
                                             scale=self.a[:, i * NST + n:i * NST + n + 1])
        last.then_inc(self.da_ready, 1)

    def pool_state(self, pool, g, n):
        pool.wait_ge(self.da_ready, g * NST + (n + 1))
        starts = self.da[n % 2][:, :, :, 0]
        self.nc.gpsimd.tensor_tensor(starts, starts, self.zeros[:], ALU.mult).then_inc(self.reset, 1)

    def pool_split(self, pool, par, part):
        nc = self.nc
        source, rows = self.rest[32 * part:32 * part + 32, :], self.parts[par][32 * part:32 * part + 32, :]
        pool.drain()
        copy = nc.gpsimd.tensor_copy(rows, source)
        if part == 2:
            copy.then_inc(self.split_ready, 1)
        else:
            pool.drain()
            nc.gpsimd.tensor_tensor(self.rest[32 * part + 32:32 * part + 64, :], source, rows, ALU.subtract)
        pool.drain()

    def dve_input(self, dve, g, par, n):
        dve.wait_ge(self.spread_ready, g * NST + (n + 1))
        self.nc.vector.tensor_tensor(self.u[n % 2], self.dx[par][:], self.over_halves(n, 0), ALU.mult)

    def over_halves(self, n, i):
        return self.spread[:, 2 * (n % 2) + i, :].rearrange("p (a t) -> p a t", a=1).to_broadcast([P, CHH, GROUP])

    def dve_state(self, dve, g, par, n, first):
        nc = self.nc
        dve.drain()
        dve.wait_ge(self.reset, g * NST + (n + 1))
        nc.vector.tensor_tensor_scan(self.h[n % 2][:].rearrange("p i t -> p (i t)"), self.da[n % 2][:].rearrange("p i b t -> p (i b t)"),
                                     self.u[n % 2].rearrange("p i t -> p (i t)"), 0.0, ALU.mult, ALU.add)
        if n + 1 < NST:
            self.dve_input(dve, g, par, n + 1)
        dve.drain()
        if n >= 2 or not first:
            dve.wait_ge(self.added_up, g * NST + (n - 1))
        nc.vector.tensor_tensor(self.hc[n % 2], self.h[n % 2][:], self.over_halves(n, 1), ALU.mult).then_inc(self.hc_ready, 1)


def over_pairs(engine, count, step):
    step(0, 0, True, False)
    with engine.Fori(0, count // 2 - 1) as pair:
        step(pair * 2 + 1, 1, False, False)
        step(pair * 2 + 2, 0, False, False)
    step(count - 1, 1, False, True)


def l1_attn_a(nc, k, name):
    layer_norm(nc, k, name + "_ln")
    R, TAPS = 64, 4
    with Scope(nc, name) as s:
        names = [("L1a_win", [P, 4 * P]), ("L1a_conv", [P, CHH * TAPS]), ("L1a_wx", [P, CHH * (R + 2 * NST)]), ("L1a_wdt", [R, ED]),
                 ("L1a_bdt", [P, CHH]), ("L1a_alog", [P, CHH * NST]), ("L1a_d", [P, CHH]), ("L1a_wout", [P, CHH * D])]
        w = {n: s.sb(n, shape) for n, shape in names}
        F = R + 2 * NST
        a = s.sb("a", [P, CHH * NST])
        padded = s.sb("padded", [P, CHH, BPG, TAPS - 1 + SEQ])
        xc, z = [s.sb(f"xc{i}", [P, CHH, BPG, SEQ]) for i in range(2)], [s.sb(f"z{i}", [P, CHH, GROUP]) for i in range(2)]
        delta, dx = [s.sb(f"delta{i}", [P, CHH, GROUP]) for i in range(2)], [s.sb(f"dx{i}", [P, CHH, GROUP]) for i in range(2)]
        dt, conv = s.sb("dt", [R, GROUP]), s.sb("conv", [P, CHH, GROUP])
        raw, soft, y = s.sb("raw", [P, CHH, GROUP]), s.sb("soft", [P, CHH, GROUP]), s.sb("y", [P, CHH, GROUP])
        aux = s.ps("aux", [P, 2, GROUP])
        scan = StateScan(nc, k, s, delta, dx, a)
        loaded, a_exp, a_ready, cleared = s.sem("loaded"), s.sem("a_exp"), s.sem("a_ready"), s.sem("cleared")
        x_up, padded_ready, z_up, conv_ready, xc_ready = s.sem("x_up"), s.sem("padded_ready"), s.sem("z_up"), s.sem("conv_ready"), s.sem("xc_ready")
        bc_up, bc_ready, dt_up, raw_ready = s.sem("bc_up"), s.sem("bc_ready"), s.sem("dt_up"), s.sem("raw_ready")
        soft_ready, delta_ready, out_ready, added = s.sem("soft_ready"), s.sem("delta_ready"), s.sem("out_ready"), s.sem("added")
        block = s.block()

        @block.sync
        def _(sp):
            for n, _ in names:
                sp.dma_start(w[n][:], k.dram[n]).then_inc(loaded, 16)
            sp.dma_start(scan.pick32[:], k.dram["c_pick"]).then_inc(loaded, 16)

        @block.tensor
        def _(pe):
            def project_in(q, j, ready):
                xn = k.XNT[:, bass.ds(q * GROUP, GROUP)]
                for i in range(CHH):
                    last = nc.tensor.matmul(aux[:, i, :], w["L1a_win"][:, (j + i) * P:(j + i + 1) * P], xn, start=True, stop=True)
                last.then_inc(ready, 1)

            def project_z(q):
                pe.wait_ge(padded_ready, q + 1)
                project_in(q, 2, z_up)

            def project_bc(q, par):
                pe.wait_ge(xc_ready, q + 1)
                for i in range(CHH):
                    last = nc.tensor.matmul(aux[0:F, 0, :], w["L1a_wx"][:, i * F:(i + 1) * F], xc[par][:, i, :, :].rearrange("p b t -> p (b t)"),
                                            start=(i == 0), stop=(i == 1))
                last.then_inc(bc_up, 1)

            def project_dt(q):
                pe.wait_ge(bc_ready, q + 1)
                for i in range(CHH):
                    last = nc.tensor.matmul(aux[:, i, :], w["L1a_wdt"][:, i * P:(i + 1) * P], dt[:], start=True, stop=True)
                last.then_inc(dt_up, 1)

            def project_out(q):
                pe.wait_ge(scan.y_ready, q + 1)
                for i in range(CHH):
                    for t in range(GT):
                        last = nc.tensor.matmul(aux[:, 0, t * P:(t + 1) * P], y[:, i, t * P:(t + 1) * P], w["L1a_wout"][:, i * D:(i + 1) * D],
                                                start=(i == 0 and t == 0), stop=(i == 1), skip_group_check=True)
                last.then_inc(out_ready, 1)

            def step(g, par, first, last_group):
                for n in range(NST):
                    scan.pe_state(pe, g, par, n, first, last_group)
                    if n == 1 and not first:
                        project_out(g - 1)
                    if n == 3 and not last_group:
                        if not first:
                            pe.wait_ge(added, g)
                        project_in(g + 1, 0, x_up)
                    if n == 5 and not last_group:
                        project_z(g + 1)
                    if n == 8 and not last_group:
                        project_bc(g + 1, 1 - par)
                    if n == 10 and not last_group:
                        project_dt(g + 1)

            pe.wait_ge(loaded, 16 * (len(names) + 1))
            project_in(0, 0, x_up)
            project_z(0)
            project_bc(0, 0)
            project_dt(0)
            scan.pe_spread(pe, 0, 0, 0)
            scan.pe_spread(pe, 0, 0, 1)
            over_pairs(pe, GROUPS, step)
            project_out(GROUPS - 1)

        @block.gpsimd
        def _(pool):
            nc.gpsimd.memset(padded[:, :, :, 0:TAPS - 1], 0.0).then_inc(cleared, 1)
            nc.gpsimd.memset(scan.zeros[:], 0.0)
            pool.wait_ge(loaded, 16 * (len(names) + 1))
            nc.gpsimd.tensor_copy(scan.pick[:], scan.pick32[:])
            pool.drain()

            def step(g, par, first, last_group):
                for n in range(NST):
                    if n == 12 and not last_group:
                        pool.wait_ge(bc_ready, g + 2)
                    scan.pool_state(pool, g, n)
                    if n in (12, 13, 14) and not last_group:
                        scan.pool_split(pool, 1 - par, n - 12)

            pool.wait_ge(bc_ready, 1)
            for part in range(3):
                scan.pool_split(pool, 0, part)
            over_pairs(pool, GROUPS, step)

        @block.scalar
        def _(act):
            def pad(q):
                act.wait_ge(x_up, q + 1)
                nc.scalar.copy(padded[:, :, :, TAPS - 1:], aux[:].rearrange("p i (b t) -> p i b t", b=BPG)).then_inc(padded_ready, 1)

            def gates(q, par):
                act.wait_ge(conv_ready, q + 1)
                act.wait_ge(z_up, q + 1)
                nc.scalar.activation(z[par][:], aux[:], ACT.Silu)
                nc.scalar.activation(xc[par][:], conv[:].rearrange("p i (b t) -> p i b t", b=BPG), ACT.Silu).then_inc(xc_ready, 1)

            def keep_bc(q):
                act.wait_ge(bc_up, q + 1)
                nc.scalar.copy(dt[:], aux[0:R, 0, :])
                nc.scalar.copy(scan.rest[0:2 * NST, :], aux[R:F, 0, :]).then_inc(bc_ready, 1)

            def log_term(q):
                act.wait_ge(raw_ready, q + 1)
                nc.scalar.activation(soft[:], soft[:], ACT.Exp)
                act.drain()
                nc.scalar.activation(soft[:], soft[:], ACT.Ln, bias=1.0).then_inc(soft_ready, 1)

            def step(g, par, first, last_group):
                for n in range(NST):
                    if n == 0:
                        act.wait_ge(delta_ready, g + 1)
                    scan.act_state(act, g, par, n, first)
                    if n == 4 and not last_group:
                        pad(g + 1)
                    if n == 8 and not last_group:
                        gates(g + 1, 1 - par)
                    if n == 10 and not last_group:
                        keep_bc(g + 1)
                    if n == 13 and not last_group:
                        log_term(g + 1)

            act.wait_ge(loaded, 16 * (len(names) + 1))
            nc.scalar.activation(a[:], w["L1a_alog"][:], ACT.Exp).then_inc(a_exp, 1)
            act.wait_ge(a_ready, 1)
            pad(0)
            gates(0, 0)
            keep_bc(0)
            log_term(0)
            over_pairs(act, GROUPS, step)

        @block.vector
        def _(dve):
            def convolve(q):
                dve.wait_ge(padded_ready, q + 1)
                for j in range(TAPS):
                    for i in range(CHH):
                        out = conv[:, i, :].rearrange("p (b t) -> p b t", b=BPG)
                        tap = w["L1a_conv"][:, i * TAPS + j:i * TAPS + j + 1]
                        if j == 0:
                            last = nc.vector.tensor_scalar(out, padded[:, i, :, j:j + SEQ], tap, None, ALU.mult)
                        else:
                            last = nc.vector.scalar_tensor_tensor(out=out, in0=padded[:, i, :, j:j + SEQ], scalar=tap, in1=out,
                                                                  op0=ALU.mult, op1=ALU.add)
                    if j < TAPS - 1:
                        dve.drain()
                last.then_inc(conv_ready, 1)

            def raw_delta(q):
                dve.wait_ge(dt_up, q + 1)
                for i in range(CHH):
                    nc.vector.tensor_scalar(raw[:, i, :], aux[:, i, :], w["L1a_bdt"][:, i:i + 1], None, ALU.add)
                dve.drain()
                nc.vector.scalar_tensor_tensor(out=soft[:], in0=raw[:], scalar=-1.0, in1=raw[:], op0=ALU.mult, op1=ALU.min).then_inc(raw_ready, 1)

            def make_delta(q, par):
                dve.wait_ge(soft_ready, q + 1)
                nc.vector.scalar_tensor_tensor(out=delta[par][:], in0=raw[:], scalar=0.0, in1=soft[:], op0=ALU.max, op1=ALU.add)\
                    .then_inc(delta_ready, 1)
                dve.drain()
                nc.vector.tensor_tensor(dx[par][:], delta[par][:], xc[par][:].rearrange("p i b t -> p i (b t)"), ALU.mult)
                dve.drain()

            def gate_y(q, par):
                dve.wait_ge(scan.added_up, (q + 1) * NST)
                for i in range(CHH):
                    nc.vector.scalar_tensor_tensor(out=y[:, i, :], in0=xc[par][:, i, :, :].rearrange("p b t -> p (b t)"), scalar=w["L1a_d"][:, i:i + 1],
                                                   in1=scan.y_ps[:, i, :], op0=ALU.mult, op1=ALU.add)
                dve.drain()
                nc.vector.tensor_tensor(y[:], y[:], z[par][:], ALU.mult).then_inc(scan.y_ready, 1)

            def add_out(q):
                dve.wait_ge(out_ready, q + 1)
                x = k.X[:, bass.ds(q * GT, GT), :]
                nc.vector.tensor_tensor(x, x, aux[:, 0, :].rearrange("p (t d) -> p t d", d=D), ALU.add).then_inc(added, 1)

            def step(g, par, first, last_group):
                scan.dve_input(dve, g, par, 0)
                for n in range(NST):
                    scan.dve_state(dve, g, par, n, first)
                    if n == 0 and not first:
                        gate_y(g - 1, 1 - par)
                    if n == 3 and not first:
                        add_out(g - 1)
                    if n == 6 and not last_group:
                        convolve(g + 1)
                    if n == 12 and not last_group:
                        raw_delta(g + 1)
                    if n == 14 and not last_group:
                        make_delta(g + 1, 1 - par)

            dve.wait_ge(a_exp, 1)
            nc.vector.tensor_scalar(a[:], a[:], -1.0, None, ALU.mult).then_inc(a_ready, 1)
            dve.wait_ge(loaded, 16 * (len(names) + 1))
            dve.wait_ge(cleared, 1)
            convolve(0)
            raw_delta(0)
            make_delta(0, 0)
            over_pairs(dve, GROUPS, step)
            gate_y(GROUPS - 1, 1)
            add_out(GROUPS - 1)


def l2_attn_a(nc, k, name):
    layer_norm(nc, k, name + "_ln")
    RMS_EPS, A_FLOOR = float(np.finfo(np.float32).eps), 1e-4
    HALF_TURN, TURN = float(np.pi), 2 * float(np.pi)
    TURN_HI = 6.28125
    TURN_LO = TURN - TURN_HI
    ROUND = 1.5 * 2.0 ** 23
    BC, DT, LAM = 2 * NST, 32, 64
    F = LAM + 1
    with Scope(nc, name) as s:
        names = [("L2a_win", [P, 4 * P]), ("L2a_wx", [P, CHH * F]), ("L2a_bdt", [P, CHH]), ("L2a_alog", [P, CHH * NST]),
                 ("L2a_d", [P, CHH]), ("L2a_wout", [P, CHH * D]), ("L2a_bias", [BC, 1]), ("L2a_norm", [BC, 1]), ("L2a_freq", [BC, 1]),
                 ("c_mean16", [BC, P]), ("c_quarter_turn", [BC, BC]), ("c_not_first", [BC, GROUP])]
        w = {n: s.sb(n, shape) for n, shape in names}
        wdt = s.sb("wdt", [DT + 1, ED])
        a, freq, fsoft = s.sb("a", [P, CHH * NST]), s.sb("freq", [BC, 1]), s.sb("fsoft", [BC, 1])
        xp, ssm = s.sb("xp", [P, CHH, GROUP]), s.sb("ssm", [F, GROUP])
        z, delta, dx = [[s.sb(f"{n}{i}", [P, CHH, GROUP]) for i in range(2)] for n in ("z", "delta", "dx")]
        v, vsq = s.sb("v", [BC, GROUP]), s.sb("vsq", [BC, GROUP])
        cum, turns = s.sb("cum", [BC, GROUP]), s.sb("turns", [BC, 2, GROUP])
        raw, soft, lam = s.sb("raw", [P, CHH, GROUP]), s.sb("soft", [P, CHH, GROUP]), s.sb("lam", [P, GROUP])
        ang, cb = raw[0:BC, :, :], cum[0:NST, :]
        ahead = s.sb("ahead", [P, CHH, BPG, SEQ])
        y = s.sb("y", [P, CHH, GROUP])
        aux = s.ps("aux", [P, 2, GROUP])
        scan = StateScan(nc, k, s, delta, dx, a)
        bc = scan.rest[0:BC, :]
        loaded, consts_exp, consts_ready, cleared = s.sem("loaded"), s.sem("consts_exp"), s.sem("consts_ready"), s.sem("cleared")
        x_up, xp_ready, z_up, z_ready = s.sem("x_up"), s.sem("xp_ready"), s.sem("z_up"), s.sem("z_ready")
        ssm_up, ssm_ready, dt_up, raw_ready = s.sem("ssm_up"), s.sem("ssm_ready"), s.sem("dt_up"), s.sem("raw_ready")
        soft_ready, vsq_ready, mean_up, root_ready = s.sem("soft_ready"), s.sem("vsq_ready"), s.sem("mean_up"), s.sem("root_ready")
        delta_ready, sum_up, v_ready, turned = s.sem("delta_ready"), s.sem("sum_up"), s.sem("v_ready"), s.sem("turned")
        ang_ready, sin_ready, bc_ready = s.sem("ang_ready"), s.sem("sin_ready"), s.sem("bc_ready")
        c_up, cb_ready, cb_up, corrected, out_ready = s.sem("c_up"), s.sem("cb_ready"), s.sem("cb_up"), s.sem("corrected"), s.sem("out_ready")
        block = s.block()
        n_loads = len(names) + 2

        @block.sync
        def _(sp):
            for n, _ in names:
                sp.dma_start(w[n][:], k.dram[n]).then_inc(loaded, 16)
            sp.dma_start(wdt[DT:DT + 1, :], k.dram["L2a_wdt"]).then_inc(loaded, 16)
            sp.dma_start(scan.pick32[:], k.dram["c_pick"]).then_inc(loaded, 16)

        @block.tensor
        def _(pe):
            def project_in(q, j, ready):
                xn = k.XNT[:, bass.ds(q * GROUP, GROUP)]
                for i in range(CHH):
                    last = nc.tensor.matmul(aux[:, i, :], w["L2a_win"][:, (j + i) * P:(j + i + 1) * P], xn, start=True, stop=True)
                last.then_inc(ready, 1)

            def project_z(q):
                pe.wait_ge(xp_ready, q + 1)
                project_in(q, 2, z_up)

            def project_ssm(q):
                pe.wait_ge(z_ready, q + 1)
                for i in range(CHH):
                    last = nc.tensor.matmul(aux[0:F, 0, :], w["L2a_wx"][:, i * F:(i + 1) * F], xp[:, i, :], start=(i == 0), stop=(i == 1))
                last.then_inc(ssm_up, 1)

            def project_dt(q):
                pe.wait_ge(ssm_ready, q + 1)
                for i in range(CHH):
                    last = nc.tensor.matmul(aux[:, i, :], wdt[DT:DT + 1, i * P:(i + 1) * P], ssm[DT:DT + 1, :], start=True, stop=True)
                last.then_inc(dt_up, 1)

            def spread_lam_mean(q):
                pe.wait_ge(vsq_ready, q + 1)
                pe.wait_ge(raw_ready, q + 1)
                nc.tensor.matmul(aux[:, 0, :], k.ones[LAM:LAM + 1, :], ssm[LAM:LAM + 1, :], start=True, stop=True)
                nc.tensor.matmul(aux[:, 1, :], w["c_mean16"][:], vsq[:], start=True, stop=True).then_inc(mean_up, 1)

            def sum_delta_turn(q, par):
                pe.wait_ge(delta_ready, q + 1)
                pe.wait_ge(v_ready, q + 1)
                for i in range(CHH):
                    last = nc.tensor.matmul(aux[0:BC, 0, :], k.ones[:, 0:BC], delta[par][:, i, :], start=(i == 0), stop=(i == 1))
                last.then_inc(sum_up, 1)
                nc.tensor.matmul(aux[0:BC, 1, :], w["c_quarter_turn"][:], v[:], start=True, stop=True).then_inc(turned, 1)

            def move_c(q):
                nc.tensor.matmul(aux[0:P - NST, 1, :], k.ident[0:BC, NST:P], bc, start=True, stop=True).then_inc(c_up, 1)

            def sum_cb(q):
                pe.wait_ge(cb_ready, q + 1)
                nc.tensor.matmul(aux[:, 1, :], k.ones[0:NST, :], cb, start=True, stop=True).then_inc(cb_up, 1)

            def project_out(q):
                pe.wait_ge(scan.y_ready, q + 1)
                for i in range(CHH):
                    for t in range(GT):
                        last = nc.tensor.matmul(aux[:, 0, t * P:(t + 1) * P], y[:, i, t * P:(t + 1) * P], w["L2a_wout"][:, i * D:(i + 1) * D],
                                                start=(i == 0 and t == 0), stop=(i == 1), skip_group_check=True)
                last.then_inc(out_ready, 1)

            def step(g, par, first, last_group):
                for n in range(NST):
                    scan.pe_state(pe, g, par, n, first, last_group)
                    if n == 0:
                        move_c(g)
                    if n == 1 and not first:
                        project_out(g - 1)
                    if n == 2:
                        sum_cb(g)
                    if not last_group:
                        if n == 3:
                            pe.wait_ge(corrected, g + 1)
                            project_in(g + 1, 0, x_up)
                        if n == 4:
                            project_z(g + 1)
                        if n == 5:
                            project_ssm(g + 1)
                        if n == 6:
                            project_dt(g + 1)
                        if n == 7:
                            spread_lam_mean(g + 1)
                        if n == 10:
                            sum_delta_turn(g + 1, 1 - par)

            pe.wait_ge(loaded, 16 * n_loads)
            project_in(0, 0, x_up)
            project_z(0)
            project_ssm(0)
            project_dt(0)
            spread_lam_mean(0)
            sum_delta_turn(0, 0)
            scan.pe_spread(pe, 0, 0, 0)
            scan.pe_spread(pe, 0, 0, 1)
            over_pairs(pe, GROUPS, step)
            project_out(GROUPS - 1)

        @block.gpsimd
        def _(pool):
            nc.gpsimd.memset(ahead[:, :, :, SEQ - 1:SEQ], 0.0).then_inc(cleared, 1)
            nc.gpsimd.memset(scan.zeros[:], 0.0)
            pool.wait_ge(loaded, 16 * n_loads)
            nc.gpsimd.tensor_copy(scan.pick[:], scan.pick32[:])
            pool.drain()

            def step(g, par, first, last_group):
                for n in range(NST):
                    if n == 13 and not last_group:
                        pool.wait_ge(bc_ready, g + 2)
                    scan.pool_state(pool, g, n)
                    if n in (13, 14, 15) and not last_group:
                        scan.pool_split(pool, 1 - par, n - 13)

            pool.wait_ge(bc_ready, 1)
            for part in range(3):
                scan.pool_split(pool, 0, part)
            over_pairs(pool, GROUPS, step)

        @block.scalar
        def _(act):
            def gate_x(q):
                act.wait_ge(x_up, q + 1)
                nc.scalar.activation(xp[:], aux[:], ACT.Silu).then_inc(xp_ready, 1)

            def gate_z(q, par):
                act.wait_ge(z_up, q + 1)
                nc.scalar.activation(z[par][:], aux[:], ACT.Silu).then_inc(z_ready, 1)

            def keep_ssm(q):
                act.wait_ge(ssm_up, q + 1)
                nc.scalar.copy(ssm[:], aux[0:F, 0, :]).then_inc(ssm_ready, 1)

            def log_term(q):
                act.wait_ge(raw_ready, q + 1)
                nc.scalar.activation(soft[:], soft[:], ACT.Exp)
                act.drain()
                nc.scalar.activation(soft[:], soft[:], ACT.Ln, bias=1.0).then_inc(soft_ready, 1)

            def lam_root(q):
                act.wait_ge(mean_up, q + 1)
                nc.scalar.activation(lam[:], aux[:, 0, :], ACT.Sigmoid)
                nc.scalar.activation(vsq[:], aux[0:BC, 1, :], ACT.Sqrt, bias=RMS_EPS).then_inc(root_ready, 1)

            def sine(q):
                act.wait_ge(ang_ready, q + 1)
                nc.scalar.activation(turns[:], ang, ACT.Sin).then_inc(sin_ready, 1)

            def step(g, par, first, last_group):
                for n in range(NST):
                    scan.act_state(act, g, par, n, first)
                    if not last_group:
                        if n == 4:
                            gate_x(g + 1)
                        if n == 5:
                            gate_z(g + 1, 1 - par)
                        if n == 6:
                            keep_ssm(g + 1)
                        if n == 8:
                            log_term(g + 1)
                            lam_root(g + 1)
                        if n == 12:
                            sine(g + 1)

            act.wait_ge(loaded, 16 * n_loads)
            nc.scalar.activation(a[:], w["L2a_alog"][:], ACT.Exp)
            act.wait_ge(cleared, 2)
            nc.scalar.activation(fsoft[:], fsoft[:], ACT.Exp)
            act.drain()
            nc.scalar.activation(fsoft[:], fsoft[:], ACT.Ln, bias=1.0).then_inc(consts_exp, 1)
            act.wait_ge(consts_ready, 1)
            gate_x(0)
            gate_z(0, 0)
            keep_ssm(0)
            log_term(0)
            lam_root(0)
            sine(0)
            over_pairs(act, GROUPS, step)

        @block.vector
        def _(dve):
            def square_v(q):
                dve.wait_ge(ssm_ready, q + 1)
                nc.vector.tensor_scalar(v[:], ssm[0:BC, :], w["L2a_bias"][:], None, ALU.add)
                dve.drain()
                nc.vector.tensor_tensor(vsq[:], v[:], v[:], ALU.mult).then_inc(vsq_ready, 1)

            def raw_delta(q):
                dve.wait_ge(dt_up, q + 1)
                for i in range(CHH):
                    nc.vector.tensor_scalar(raw[:, i, :], aux[:, i, :], w["L2a_bdt"][:, i:i + 1], None, ALU.add)
                dve.drain()
                nc.vector.scalar_tensor_tensor(out=soft[:], in0=raw[:], scalar=-1.0, in1=raw[:], op0=ALU.mult, op1=ALU.min).then_inc(raw_ready, 1)

            def make_delta(q, par):
                dve.wait_ge(soft_ready, q + 1)
                nc.vector.scalar_tensor_tensor(out=delta[par][:], in0=raw[:], scalar=0.0, in1=soft[:], op0=ALU.max, op1=ALU.add)\
                    .then_inc(delta_ready, 1)
                dve.drain()
                dve.wait_ge(root_ready, q + 1)
                nc.vector.tensor_tensor(raw[:], delta[par][:], lam[:].rearrange("p (a t) -> p a t", a=1).to_broadcast([P, CHH, GROUP]), ALU.mult)
                dve.drain()
                by_seq = [b[:].rearrange("p i (b t) -> p i b t", b=BPG) for b in (delta[par], raw)]
                for i in range(CHH):
                    nc.vector.tensor_tensor(ahead[:, i, :, 0:SEQ - 1], by_seq[0][:, i, :, 1:SEQ], by_seq[1][:, i, :, 1:SEQ], ALU.subtract)
                nc.vector.tensor_copy(by_seq[1][:, :, :, 0:1], by_seq[0][:, :, :, 0:1])
                dve.drain()

            def make_dx(par):
                ahead_x = ahead[:].rearrange("p i b t -> p i (b t)")
                nc.vector.tensor_tensor(dx[par][:], raw[:], ahead_x, ALU.add)
                dve.drain()
                nc.vector.tensor_tensor(dx[par][:], dx[par][:], xp[:], ALU.mult)
                nc.vector.tensor_tensor(soft[:], ahead_x, xp[:], ALU.mult)

            def normalise_v(q):
                nc.vector.reciprocal(vsq[:], vsq[:])
                dve.drain()
                nc.vector.scalar_tensor_tensor(out=v[:], in0=v[:], scalar=w["L2a_norm"][:], in1=vsq[:], op0=ALU.mult, op1=ALU.mult).then_inc(v_ready, 1)

            def angles(q):
                dve.wait_ge(sum_up, q + 1)
                nc.vector.tensor_tensor_scan(cum[:], w["c_not_first"][:], aux[0:BC, 0, :], 0.0, ALU.mult, ALU.add)
                dve.drain()
                nc.vector.tensor_scalar(ang[:, 0, :], cum[:], freq[:], None, ALU.mult)
                nc.vector.tensor_scalar(ang[:, 1, :], cum[:], freq[:], HALF_TURN / 2, ALU.mult, ALU.add)
                dve.drain()
                nc.vector.tensor_scalar(turns[:], ang, 1.0 / TURN, ROUND, ALU.mult, ALU.add)
                dve.drain()
                nc.vector.tensor_scalar(turns[:], turns[:], -ROUND, None, ALU.add)
                dve.drain()
                nc.vector.scalar_tensor_tensor(out=ang, in0=turns[:], scalar=-TURN_HI, in1=ang, op0=ALU.mult, op1=ALU.add)
                dve.drain()
                nc.vector.scalar_tensor_tensor(out=ang, in0=turns[:], scalar=-TURN_LO, in1=ang, op0=ALU.mult, op1=ALU.add)
                dve.drain()
                nc.vector.tensor_scalar(ang, ang, 3.1415925, -3.1415925, ALU.min, ALU.max).then_inc(ang_ready, 1)

            def turn_bc(q):
                dve.wait_ge(turned, q + 1)
                dve.wait_ge(sin_ready, q + 1)
                nc.vector.tensor_tensor(cum[:], aux[0:BC, 1, :], turns[:, 0, :], ALU.mult)
                nc.vector.tensor_tensor(v[:], v[:], turns[:, 1, :], ALU.mult)
                dve.drain()
                nc.vector.tensor_tensor(bc, v[:], cum[:], ALU.add).then_inc(bc_ready, 1)

            def multiply_cb(q):
                dve.wait_ge(c_up, q + 1)
                nc.vector.tensor_tensor(cb, scan.rest[0:NST, :], aux[0:NST, 1, :], ALU.mult).then_inc(cb_ready, 1)

            def correct(q):
                dve.wait_ge(cb_up, q + 1)
                cb_sum = aux[:, 1, :].rearrange("p (a t) -> p a t", a=1).to_broadcast([P, CHH, GROUP])
                nc.vector.tensor_tensor(raw[:], soft[:], cb_sum, ALU.mult)
                dve.drain()
                for i in range(CHH):
                    last = nc.vector.scalar_tensor_tensor(out=y[:, i, :], in0=xp[:, i, :], scalar=w["L2a_d"][:, i:i + 1], in1=raw[:, i, :],
                                                          op0=ALU.mult, op1=ALU.subtract)
                last.then_inc(corrected, 1)

            def gate_y(q, par):
                dve.wait_ge(scan.added_up, (q + 1) * NST)
                nc.vector.tensor_tensor(y[:], y[:], scan.y_ps[:], ALU.add)
                dve.drain()
                nc.vector.tensor_tensor(y[:], y[:], z[par][:], ALU.mult).then_inc(scan.y_ready, 1)

            def add_out(q):
                dve.wait_ge(out_ready, q + 1)
                x = k.X[:, bass.ds(q * GT, GT), :]
                nc.vector.tensor_tensor(x, x, aux[:, 0, :].rearrange("p (t d) -> p t d", d=D), ALU.add)

            def step(g, par, first, last_group):
                scan.dve_input(dve, g, par, 0)
                for n in range(NST):
                    scan.dve_state(dve, g, par, n, first)
                    if n == 0 and not first:
                        gate_y(g - 1, 1 - par)
                    if n == 1:
                        multiply_cb(g)
                    if n == 2 and not first:
                        add_out(g - 1)
                    if n == 3:
                        correct(g)
                    if not last_group:
                        if n == 6:
                            square_v(g + 1)
                        if n == 7:
                            raw_delta(g + 1)
                        if n == 9:
                            make_delta(g + 1, 1 - par)
                        if n == 10:
                            make_dx(1 - par)
                            normalise_v(g + 1)
                        if n == 11:
                            angles(g + 1)
                        if n == 12:
                            turn_bc(g + 1)

            dve.wait_ge(loaded, 16 * n_loads)
            nc.vector.scalar_tensor_tensor(out=fsoft[:], in0=w["L2a_freq"][:], scalar=-1.0, in1=w["L2a_freq"][:],
                                           op0=ALU.mult, op1=ALU.min).then_inc(cleared, 1)
            dve.wait_ge(consts_exp, 1)
            nc.vector.tensor_scalar(a[:], a[:], -1.0, -A_FLOOR, ALU.mult, ALU.min)
            nc.vector.scalar_tensor_tensor(out=freq[:], in0=w["L2a_freq"][:], scalar=0.0, in1=fsoft[:], op0=ALU.max, op1=ALU.add)
            dve.drain()
            nc.vector.tensor_scalar(freq[:], freq[:], 1.0 / ED, None, ALU.mult).then_inc(consts_ready, 1)
            dve.drain()
            square_v(0)
            raw_delta(0)
            make_delta(0, 0)
            make_dx(0)
            normalise_v(0)
            angles(0)
            turn_bc(0)
            dve.drain()
            over_pairs(dve, GROUPS, step)
            gate_y(GROUPS - 1, 1)
            add_out(GROUPS - 1)


def l2_attn_b(nc, k, name):
    layer_norm(nc, k, name + "_ln")
    H, ROT = 8, 64
    AW = P + SEQ
    GN = D // 16
    with Scope(nc, name) as s:
        names = [("L2b_wQ", [P, H * D]), ("L2b_wK", [P, H * D]), ("L2b_wV", [P, H * D]), ("L2b_wQs", [P, H * ROT]), ("L2b_wKs", [P, H * ROT]),
                 ("L2b_g", [P, D]), ("L2b_be", [P, D]), ("c_cos", [ROT, GROUP]), ("c_sin", [ROT, GROUP]), ("c_decay", [P, AW])]
        w = {n: s.sb(n, shape) for n, shape in names}
        xg, v = s.sb("xg", [P, GROUP]), s.sb("v", [P, GT, H * D])
        rot, swap = s.sb("rot", [ROT, 2, GROUP]), [s.sb(f"swap{i}", [ROT, 2, GROUP]) for i in range(2)]
        qk = [s.sb(f"qk{i}", [P, 2, GROUP]) for i in range(2)]
        a = [s.sb(f"a{i}", [P, BPG, AW]) for i in range(2)]
        rows, sq, mean, var = s.sb("rows", [P, GT * 16, GN]), s.sb("sq", [P, GT * 16, GN]), s.sb("mean", [P, GT * 16]), s.sb("var", [P, GT * 16])
        qk_ps, sw_ps = s.ps("qk_ps", [P, 2, GROUP]), s.ps("sw_ps", [ROT, 2, GROUP])
        a_ps, v_ps, o_ps = s.ps("a_ps", [P, BPG, 512]), s.ps("v_ps", [P, 512]), s.ps("o_ps", [P, GT, D])
        loaded, xg_ready, v_up, v_ready = s.sem("loaded"), s.sem("xg_ready"), s.sem("v_up"), s.sem("v_ready")
        projected, rot_ready, qk_ready = s.sem("projected"), s.sem("rot_ready"), s.sem("qk_ready")
        high_ready, low_read = s.sem("high_ready"), s.sem("low_read")
        a_up, a_ready, o_ready, var_ready, root_ready, done = (s.sem(n) for n in ("a_up", "a_ready", "o_ready", "var_ready", "root_ready", "done"))
        block = s.block()

        @block.sync
        def _(sp):
            for n, _ in names:
                sp.dma_start(w[n][:], k.dram[n]).then_inc(loaded, 16)

        @block.tensor
        def _(pe):
            def project(g, h, first=False):
                if h > 0 or not first:
                    pe.wait_ge(high_ready, g * H + h)
                    pe.wait_ge(low_read, g * H + h)
                for i, n in enumerate("QK"):
                    nc.tensor.matmul(qk_ps[:, i, :], w[f"L2b_w{n}"][:, h * D:(h + 1) * D], xg[:], start=True, stop=True)
                for i, n in enumerate("QK"):
                    last = nc.tensor.matmul(sw_ps[:, i, :], w[f"L2b_w{n}s"][:, h * ROT:(h + 1) * ROT], xg[:], start=True, stop=True)
                last.then_inc(projected, 1)

            def scores(g, h):
                pe.wait_ge(qk_ready, g * H + (h + 1))
                if h > 0:
                    pe.wait_ge(a_ready, g * H + h)
                for b in range(BPG):
                    q, kk = qk[h % 2][:, 0, :], qk[h % 2][:, 1, :]
                    c = b * SEQ
                    nc.tensor.matmul(a_ps[:, b, 0:P], q[:, c:c + P], kk[:, c:c + P], start=True, stop=True)
                    last = nc.tensor.matmul(a_ps[:, b, P:AW], q[:, c + P:c + SEQ], kk[:, c:c + SEQ], start=True, stop=True)
                last.then_inc(a_up, 1)

            def mix(g, h):
                pe.wait_ge(a_ready, g * H + (h + 1))
                for b in range(BPG):
                    for col, row_tile, key_tile in ((0, 0, 0), (P, 1, 0), (2 * P, 1, 1)):
                        last = nc.tensor.matmul(o_ps[:, b * TPB + key_tile, :], a[h % 2][:, b, col:col + P],
                                                v[:, b * TPB + row_tile, h * D:(h + 1) * D],
                                                start=(h == 0 and b == 0 and col == 0), stop=(h == H - 1), skip_group_check=True)
                return last

            pe.wait_ge(loaded, 16 * len(names))

            def step(g, par, first, last_group):
                pe.wait_ge(xg_ready, g + 1)
                project(g, 0, first)
                for n in range(2 * GT):
                    if n > 0:
                        pe.wait_ge(v_ready, g * 2 * GT + n)
                    t, half = divmod(n, 2)
                    nc.tensor.matmul(v_ps[:], xg[:, t * P:(t + 1) * P], w["L2b_wV"][:, half * 512:(half + 1) * 512], start=True, stop=True)\
                        .then_inc(v_up, 1)
                pe.wait_ge(v_ready, g * 2 * GT + 2 * GT)
                for h in range(H):
                    if h + 1 < H:
                        project(g, h + 1)
                    scores(g, h)
                    if h == 1 and not first:
                        pe.wait_ge(done, g)
                    if h > 0:
                        mix(g, h - 1)
                mix(g, H - 1).then_inc(o_ready, 1)

            over_pairs(pe, GROUPS, step)

        @block.scalar
        def _(act):
            def high(g, h):
                act.wait_ge(projected, g * H + (h + 1))
                nc.scalar.activation(qk[h % 2][ROT:P, :, :], qk_ps[ROT:P, :, :], ACT.Silu).then_inc(high_ready, 1)

            def low(g, h):
                act.wait_ge(rot_ready, g * H + (h + 1))
                nc.scalar.activation(qk[h % 2][0:ROT, :, :], rot[:], ACT.Silu).then_inc(qk_ready, 1)

            def root(g):
                act.wait_ge(var_ready, g + 1)
                nc.scalar.activation(var[:], var[:], ACT.Sqrt).then_inc(root_ready, 1)

            def step(g, par, first, last_group):
                nc.scalar.copy(xg[:], k.XNT[:, bass.ds(g * GROUP, GROUP)]).then_inc(xg_ready, 1)
                high(g, 0)
                for n in range(2 * GT):
                    t, half = divmod(n, 2)
                    act.wait_ge(v_up, g * 2 * GT + (n + 1))
                    nc.scalar.activation(v[:, t, half * 512:(half + 1) * 512], v_ps[:], ACT.Silu).then_inc(v_ready, 1)
                    if n == 4 and not first:
                        root(g - 1)
                low(g, 0)
                for h in range(1, H):
                    high(g, h)
                    low(g, h)

            over_pairs(act, GROUPS, step)
            root(GROUPS - 1)

        @block.vector
        def _(dve):
            def twice(ap):
                return ap[:].rearrange("p (a n) -> p a n", a=1).to_broadcast([ap.shape[0], 2, ap.shape[1]])

            def over_tiles(ap):
                return ap[:].rearrange("p (a n) -> p a n", a=1).to_broadcast([P, GT, D])

            def turn(g, h, first=False):
                dve.wait_ge(projected, g * H + (h + 1))
                nc.vector.tensor_tensor(swap[h % 2][:], sw_ps[:], twice(w["c_sin"]), ALU.mult)
                if h > 0 or not first:
                    dve.wait_ge(qk_ready, g * H + h)
                nc.vector.tensor_tensor(rot[:], qk_ps[0:ROT, :, :], twice(w["c_cos"]), ALU.mult).then_inc(low_read, 1)
                dve.drain()
                nc.vector.tensor_tensor(rot[:], rot[:], swap[h % 2][:], ALU.add).then_inc(rot_ready, 1)

            def decay(g, h):
                dve.wait_ge(a_up, g * H + (h + 1))
                nc.vector.tensor_tensor(a[h % 2][:], a_ps[:, :, 0:AW], twice(w["c_decay"]), ALU.mult).then_inc(a_ready, 1)

            dve.wait_ge(loaded, 16 * len(names))

            def normalise(g):
                dve.wait_ge(o_ready, g + 1)
                groups = o_ps[:].rearrange("p t (q d) -> p (t q) d", d=GN)
                nc.vector.tensor_reduce(mean[:], groups, AX.X, ALU.add)
                dve.drain()
                nc.vector.tensor_scalar(mean[:], mean[:], 1.0 / GN, None, ALU.mult)
                dve.drain()
                nc.vector.tensor_tensor(rows[:], groups, per_row(mean[:], GN), ALU.subtract)
                dve.drain()
                nc.vector.tensor_tensor(sq[:], rows[:], rows[:], ALU.mult)
                dve.drain()
                nc.vector.tensor_reduce(var[:], sq[:], AX.X, ALU.add)
                dve.drain()
                nc.vector.tensor_scalar(var[:], var[:], 1.0 / GN, 1e-5, ALU.mult, ALU.add).then_inc(var_ready, 1)
                dve.wait_ge(root_ready, g + 1)
                nc.vector.reciprocal(var[:], var[:])
                dve.drain()
                nc.vector.tensor_tensor(rows[:], rows[:], per_row(var[:], GN), ALU.mult)
                dve.drain()
                by_tile = rows[:].rearrange("p (t q) d -> p t (q d)", t=GT)
                nc.vector.tensor_tensor(by_tile, by_tile, over_tiles(w["L2b_g"]), ALU.mult)
                dve.drain()
                nc.vector.tensor_tensor(by_tile, by_tile, over_tiles(w["L2b_be"]), ALU.add)
                dve.drain()
                x = k.X[:, bass.ds(g * GT, GT), :]
                nc.vector.tensor_tensor(x, x, by_tile, ALU.add).then_inc(done, 1)

            def step(g, par, first, last_group):
                if not first:
                    normalise(g - 1)
                turn(g, 0, first)
                for h in range(H):
                    if h + 1 < H:
                        turn(g, h + 1)
                    decay(g, h)

            over_pairs(dve, GROUPS, step)
            normalise(GROUPS - 1)


def l2_ffn(nc, k, name):
    NT, NC, KN = 64, 8, 8
    NS = NC + NT
    with Scope(nc, name + "_sig") as s:
        raw, q, low = s.sb("raw", [P, NT]), s.sb("q", [P, NT]), s.sb("low", [P, NT])
        loaded = s.sem("loaded")
        block = s.block()

        @block.sync
        def _(sp):
            sp.dma_start(raw[:], k.dram["L2f_sig"]).then_inc(loaded, 16)

        @block.vector
        def _(dve):
            dve.wait_ge(loaded, 16)
            nc.vector.tensor_scalar(q[:], raw[:], 0.3, None, ALU.is_gt)
            nc.vector.tensor_scalar(low[:], raw[:], -0.3, None, ALU.is_lt)
            dve.drain()
            nc.vector.tensor_tensor(q[:], q[:], low[:], ALU.subtract)
            dve.drain()
            nc.vector.tensor_tensor(q[:], q[:], raw[:], ALU.subtract)
            dve.drain()
            nc.vector.tensor_tensor(k.SIG[:, NC:NS], raw[:], q[:], ALU.add)
            dve.drain()
            nc.vector.tensor_reduce(low[:, 0:NC], k.SIG[:, NC:NS].rearrange("p (c t) -> p c t", t=8), AX.X, ALU.add)
            dve.drain()
            nc.vector.tensor_scalar(q[:, 0:NC], low[:, 0:NC], 0.0, None, ALU.is_gt)
            nc.vector.tensor_scalar(q[:, NC:2 * NC], low[:, 0:NC], 0.0, None, ALU.is_lt)
            dve.drain()
            nc.vector.tensor_tensor(k.SIG[:, 0:NC], q[:, 0:NC], q[:, NC:2 * NC], ALU.subtract)

    layer_norm(nc, k, name + "_ln", k.SIG, NS, keep_rows=True)

    with Scope(nc, name + "_pick") as s:
        names = [("L2f_temp", [P, 1]), ("L2f_knots", [P, KN]), ("c_first8", [P, NC]), ("c_first64", [P, NT]), ("c_minus_knot", [P, KN])]
        w = {n: s.sb(n, shape) for n, shape in names}
        temp, slope = s.sb("temp", [P, 1]), s.sb("slope", [P, KN])
        at = s.sb("at", [P, TILES * NS])
        over = [s.sb(f"over{i}", [P, TILES * NS]) for i in range(2)]
        gates = s.sb("gates", [P, TILES, NS])
        top, own, off = s.sb("top", [P, TILES]), s.sb("own", [P, TILES, NC]), s.sb("off", [P, TILES, NC])
        q = s.sb("q", [P, TILES, NT])
        loaded, temp_ready, over_ready, used = s.sem("loaded"), s.sem("temp_ready"), s.sem("over_ready"), s.sem("used")
        block = s.block()

        @block.sync
        def _(sp):
            for n, _ in names:
                sp.dma_start(w[n][:], k.dram[n]).then_inc(loaded, 16)

        @block.scalar
        def _(act):
            act.wait_ge(temp_ready, 1)
            nc.scalar.activation(at[:], k.LOG[:].rearrange("p t n -> p (t n)"), ACT.Sigmoid, scale=temp[:])
            act.drain()
            for j in range(KN - 1):
                if j >= 2:
                    act.wait_ge(used, j - 1)
                nc.scalar.activation(over[j % 2][:], at[:], ACT.Relu, scale=float(KN - 1), bias=w["c_minus_knot"][:, j:j + 1])\
                    .then_inc(over_ready, 1)

        @block.vector
        def _(dve):
            dve.wait_ge(loaded, 16 * len(names))
            nc.vector.tensor_scalar(temp[:], w["L2f_temp"][:], 1e-6, None, ALU.add)
            dve.drain()
            nc.vector.reciprocal(temp[:], temp[:]).then_inc(temp_ready, 1)
            nc.vector.tensor_tensor(slope[:, 0:KN - 1], w["L2f_knots"][:, 1:KN], w["L2f_knots"][:, 0:KN - 1], ALU.subtract)
            dve.drain()
            nc.vector.tensor_copy(off[:, 0, 0:KN - 1], slope[:, 0:KN - 1])
            dve.drain()
            nc.vector.tensor_tensor(slope[:, 1:KN - 1], off[:, 0, 1:KN - 1], off[:, 0, 0:KN - 2], ALU.subtract)
            dve.drain()
            g = gates[:].rearrange("p t n -> p (t n)")
            for j in range(KN - 1):
                dve.wait_ge(over_ready, j + 1)
                if j == 0:
                    nc.vector.tensor_scalar(g, over[0][:], slope[:, 0:1], w["L2f_knots"][:, 0:1], ALU.mult, ALU.add).then_inc(used, 1)
                else:
                    nc.vector.scalar_tensor_tensor(out=g, in0=over[j % 2][:], scalar=slope[:, j:j + 1], in1=g,
                                                   op0=ALU.mult, op1=ALU.add).then_inc(used, 1)
                dve.drain()

            def first_largest(vals, n, first, out):
                def spread(ap):
                    return ap.rearrange("p (t a) -> p t a", a=1).to_broadcast([P, TILES, n])
                nc.vector.tensor_reduce(top[:], vals, AX.X, ALU.max)
                dve.drain()
                nc.vector.tensor_tensor(out, vals, spread(top[:]), ALU.is_equal)
                dve.drain()
                nc.vector.tensor_tensor(out, out, first[:].rearrange("p (a n) -> p a n", a=1).to_broadcast([P, TILES, n]), ALU.mult)
                dve.drain()
                nc.vector.tensor_reduce(top[:], out, AX.X, ALU.max)
                dve.drain()
                nc.vector.tensor_tensor(out, out, spread(top[:]), ALU.is_equal)
                dve.drain()

            first_largest(gates[:, :, 0:NC], NC, w["c_first8"], own[:])
            nc.vector.tensor_scalar(off[:], own[:], 3e38, -3e38, ALU.mult, ALU.add)

            def over_cluster(ap):
                return ap.rearrange("p t (c a) -> p (t c) a", a=1).to_broadcast([P, TILES * NC, 8])
            gq = gates[:, :, NC:NS].rearrange("p t (c n) -> p t c n", n=8)
            qq = q[:].rearrange("p t (c n) -> p t c n", n=8)
            own4 = own[:].rearrange("p t (c a) -> p t c a", a=1).to_broadcast([P, TILES, NC, 8])
            nc.vector.tensor_tensor(qq, gq, own4, ALU.mult)
            dve.drain()
            qf = q[:].rearrange("p t (c n) -> p (t c) n", n=8)
            nc.vector.tensor_tensor(qf, qf, over_cluster(off[:]), ALU.add)
            dve.drain()
            first_largest(q[:], NT, w["c_first64"], k.PICK[:])

    CH, G2 = 32, 16
    W1, B1, W2, B2, DIR = 0, 2 * G2, 3 * G2, 4 * G2, 4 * G2 + 1
    TW = DIR + D
    with Scope(nc, name + "_mix") as s:
        names = [("L2f_scale", [P, 1]), ("L2f_cw1", [P, CH]), ("L2f_cb1", [CH, 1]), ("L2f_cw2", [CH, 2]), ("L2f_cb2", [1, 2 * GT]),
                 ("L2f_table", [P, TW]), ("L2f_gamma", [P, D]), ("L2f_beta", [P, D])]
        w = {n: s.sb(n, shape) for n, shape in names}
        picked, pt, hid = s.sb("picked", [P, GT * NT]), s.sb("pt", [P, 2, P]), s.sb("hid", [CH, GROUP])
        comp, sp1, sp2, mag = s.sb("comp", [P, GT, 2]), s.sb("sp1", [P, GT, G2]), s.sb("sp2", [P, GT, G2]), s.sb("mag", [P, GT])
        y = s.sb("y", [P, GT, D])
        stats, mv, rstd, minus = s.sb("stats", [P, GT, 6]), s.sb("mv", [P, GT, 2]), s.sb("rstd", [P, GT]), s.sb("minus", [P, GT])
        pt_ps, hid_ps, comp_ps, row_ps = s.ps("pt_ps", [P, 2, P]), s.ps("hid_ps", [CH, GROUP]), s.ps("comp_ps", [P, GT, 2]), s.ps("row_ps", [P, GT, 256])
        loaded, picked_ready, turned, pt_ready = s.sem("loaded"), s.sem("picked_ready"), s.sem("turned"), s.sem("pt_ready")
        hid_up, hid_ready, comp_up, comp_ready = s.sem("hid_up"), s.sem("hid_ready"), s.sem("comp_up"), s.sem("comp_ready")
        rows_up, var_ready, rstd_ready, done = s.sem("rows_up"), s.sem("var_ready"), s.sem("rstd_ready"), s.sem("done")
        block = s.block()

        @block.sync
        def _(sp):
            for n, _ in names:
                sp.dma_start(w[n][:], k.dram[n]).then_inc(loaded, 16)

        @block.tensor
        def _(pe):
            pe.wait_ge(loaded, 16 * len(names))
            with pe.Fori(0, GROUPS) as g:
                pe.wait_ge(picked_ready, g + 1)
                for i in range(2):
                    last = nc.tensor.transpose(pt_ps[:, i, :], picked[:, i * P:(i + 1) * P], k.ident[:])
                last.then_inc(turned, 1)
                nc.tensor.matmul(hid_ps[:], w["L2f_cw1"][:], k.XNT[:, bass.ds(g * GROUP, GROUP)], start=True, stop=True).then_inc(hid_up, 1)
                pe.wait_ge(pt_ready, g + 1)
                for t in range(GT):
                    r = t // 2 * NT
                    last = nc.tensor.matmul(row_ps[:, t, 0:TW], pt[r:r + NT, t % 2, :], w["L2f_table"][r:r + NT, :], start=True, stop=True)
                last.then_inc(rows_up, 1)
                nc.tensor.matmul(comp_ps[:], k.ones_row[0:1, 0:P], w["L2f_cb2"][:], start=True, stop=False, skip_group_check=True)
                pe.wait_ge(hid_ready, g + 1)
                for t in range(GT):
                    last = nc.tensor.matmul(comp_ps[:, t, :], hid[:, t * P:(t + 1) * P], w["L2f_cw2"][:], start=False, stop=True,
                                            skip_group_check=True)
                last.then_inc(comp_up, 1)

        @block.scalar
        def _(act):
            act.wait_ge(loaded, 16 * len(names))
            with act.Fori(0, GROUPS) as g:
                act.wait_ge(done, g)
                nc.scalar.copy(picked[:].rearrange("p (i r n) -> p r i n", i=2, r=2),
                               k.PICK[:, bass.ds(g * GT, GT), :].rearrange("p (r i) n -> p r i n", r=2)).then_inc(picked_ready, 1)
                act.wait_ge(turned, g + 1)
                nc.scalar.copy(pt[:], pt_ps[:]).then_inc(pt_ready, 1)
                act.wait_ge(hid_up, g + 1)
                nc.scalar.activation(hid[:], hid_ps[:], ACT.Gelu, bias=w["L2f_cb1"][:]).then_inc(hid_ready, 1)
                act.wait_ge(comp_up, g + 1)
                nc.scalar.activation(comp[:], comp_ps[:], ACT.Tanh).then_inc(comp_ready, 1)

        @block.gpsimd
        def _(pool):
            nc.gpsimd.memset(minus[:], -0.5)
            pool.drain()
            with pool.Fori(0, GROUPS) as g:
                pool.wait_ge(var_ready, g + 1)
                nc.gpsimd.tensor_tensor(rstd[:], rstd[:], minus[:], ALU.pow).then_inc(rstd_ready, 1)

        @block.vector
        def _(dve):
            def over_tiles(ap):
                return ap[:].rearrange("p (a n) -> p a n", a=1).to_broadcast([P, GT, D])

            dve.wait_ge(loaded, 16 * len(names))
            with dve.Fori(0, GROUPS) as g:
                dve.wait_ge(rows_up, g + 1)
                dve.wait_ge(comp_ready, g + 1)
                for j, out in enumerate((sp1, sp2)):
                    nc.vector.tensor_tensor(out[:], row_ps[:, :, W1 + j * G2:W1 + (j + 1) * G2], comp[:, :, j:j + 1].to_broadcast([P, GT, G2]), ALU.mult)
                dve.drain()
                nc.vector.tensor_tensor(sp1[:], sp1[:], sp2[:], ALU.add)
                dve.drain()
                nc.vector.tensor_tensor(sp1[:], sp1[:], row_ps[:, :, B1:B1 + G2], ALU.add)
                dve.drain()
                nc.vector.scalar_tensor_tensor(out=sp1[:], in0=sp1[:], scalar=0.0, in1=row_ps[:, :, W2:W2 + G2], op0=ALU.max, op1=ALU.mult)
                dve.drain()
                nc.vector.tensor_reduce(mag[:], sp1[:], AX.X, ALU.add)
                dve.drain()
                nc.vector.tensor_tensor(mag[:], mag[:], row_ps[:, :, B2], ALU.add)
                dve.drain()
                nc.vector.tensor_tensor(y[:], row_ps[:, :, DIR:DIR + D], per_row(mag[:], D), ALU.mult)
                dve.drain()
                nc.vector.scalar_tensor_tensor(out=y[:], in0=y[:], scalar=w["L2f_scale"][:], in1=k.XN[:, bass.ds(g * GT, GT), :],
                                               op0=ALU.mult, op1=ALU.add)
                dve.drain()
                group_norm_rows(nc, dve, y, stats, mv)
                nc.vector.tensor_scalar(rstd[:], mv[:, :, 1], 1e-5, None, ALU.add).then_inc(var_ready, 1)
                dve.wait_ge(rstd_ready, g + 1)
                for t in range(GT):
                    nc.vector.tensor_scalar(y[:, t, :], y[:, t, :], mv[:, t, 0:1], rstd[:, t:t + 1], ALU.subtract, ALU.mult)
                dve.drain()
                nc.vector.tensor_tensor(y[:], y[:], over_tiles(w["L2f_gamma"]), ALU.mult)
                dve.drain()
                nc.vector.tensor_tensor(y[:], y[:], over_tiles(w["L2f_beta"]), ALU.add)
                dve.drain()
                x = k.X[:, bass.ds(g * GT, GT), :]
                nc.vector.tensor_tensor(x, x, y[:], ALU.add).then_inc(done, 1)


def l1_attn_b(nc, k, name):
    layer_norm(nc, k, name + "_ln")
    H, HD, VD = 16, 4, 8
    FR, AR = H * HD, 96
    VC = 32
    LAMBDA_INIT = 0.8 - 0.6 * float(np.exp(-0.3 * 12))
    with Scope(nc, name) as s:
        names = [("L1b_wqk", [P, 2 * D]), ("L1b_wv", [P, D]), ("L1b_wo", [P, D]), ("L1b_bo", [1, TPB * D]), ("L1b_lam", [P, 4 * HD]),
                 ("L1b_sub", [P, VD]), ("c_head_rows", [AR, H])]
        w = {n: s.sb(n, shape) for n, shape in names}
        lam, sub = s.sb("lam", [P, 2]), s.sb("sub", [P, D])
        prod = s.sb("prod", [P, 2, HD])
        xg = s.sb("xg", [P, SEQ])
        qt, kt = [s.sb(f"qt{i}", [AR, 2, SEQ]) for i in range(2)], s.sb("kt", [AR, 2, SEQ])
        q0 = s.sb("q0", [AR, 2, SEQ])
        masked = [s.sb(f"masked{i}", [AR, 2, H, SEQ]) for i in range(2)]
        spare = [k.XN[:, i * 8:(i + 1) * 8, :].rearrange("p t d -> p (t d)") for i in range(2)]
        vx = [spare[i].rearrange("p (t h d) -> p t h d", t=TPB, h=H) for i in range(2)]
        e = [k.PICK[:, i * 8:(i + 1) * 8, :].rearrange("p t n -> p (t n)").rearrange("p (t q) -> p t q", t=TPB) for i in range(3)]
        mixed = k.XN[:, 16:32, :].rearrange("p t d -> p (t d)").rearrange("p (i c q) -> p i c q", i=2, c=H // 4)
        top = s.sb("top", [P, 2, TPB, AR])
        rden, att = s.sb("rden", [P, 2, TPB * H]), s.sb("att", [P, 2, TPB * H, VD])
        o, sq, ms, minus = s.sb("o", [P, TPB * H, VD]), s.sb("sq", [P, TPB * H, VD]), s.sb("ms", [P, TPB * H]), s.sb("minus", [P, TPB * H])
        ot = s.sb("ot", [P, SEQ])
        misc = s.ps("misc", [P, 2, SEQ])
        misc2 = s.ps("misc2", [P, 2, SEQ])
        score_ps = [s.ps(f"score_ps{i}", [P, TPB, SEQ]) for i in range(2)]
        o_ps = s.ps("o_ps", [P, 2, H // 4, SEQ])
        o_flat = o_ps[:].rearrange("p i s q -> p (i s q)")
        max_banks = [b[:].rearrange("p t q -> p (t q)") for b in (*score_ps, misc)]
        NB = len(max_banks)
        sems = ("loaded", "exped", "consts_ready", "xg_ready", "projected", "copied", "copied_k", "v_up", "v_ready", "masked_ready", "max_up", "max_ready",
                "top_ready", "turned", "turned_ready", "score_up", "e_ready", "o_up", "mixed_ready", "mixed_turned", "ms_ready", "rms_ready", "o_ready", "turned_o", "ot_ready",
                "y_ready", "done")
        (loaded, exped, consts_ready, xg_ready, projected, copied, copied_k, v_up, v_ready, masked_ready, max_up, max_ready, top_ready, turned, turned_ready,
         score_up, e_ready, o_up, mixed_ready, mixed_turned, ms_ready, rms_ready, o_ready, turned_o, ot_ready, y_ready, done) = (s.sem(n) for n in sems)
        block = s.block()
        MAXES, SCORES = 2 * TPB * H // 2, 2 * H

        @block.sync
        def _(sp):
            for n, _ in names:
                sp.dma_start(w[n][:], k.dram[n]).then_inc(loaded, 16)

        @block.tensor
        def _(pe):
            pe.wait_ge(loaded, 16 * len(names))

            def project_qk(b):
                pe.wait_ge(xg_ready, b + 1)
                for j in range(2):
                    for i in range(2):
                        c = j * D + i * FR
                        last = nc.tensor.matmul((misc, misc2)[j][0:FR, i, :], w["L1b_wqk"][:, c:c + FR], xg[:], start=True, stop=True)
                last.then_inc(projected, 1)

            def project_v(b):
                pe.wait_ge(copied, b + 1)
                for t in range(TPB):
                    last = nc.tensor.matmul(misc[:, t, 0:D], xg[:, t * P:(t + 1) * P], w["L1b_wv"][:], start=True, stop=True)
                last.then_inc(v_up, 1)

            def turn_mixed(b):
                pe.wait_ge(mixed_ready, b * 2 + 2)
                for i in range(2):
                    for t in range(TPB):
                        for c in range(H // 4):
                            last = nc.tensor.transpose(o_flat[:, ((i * TPB + t) * 4 + c) * P:((i * TPB + t) * 4 + c + 1) * P],
                                                       mixed[:, i, c, t * P:(t + 1) * P], k.ident[:])
                last.then_inc(mixed_turned, 1)

            def turn_o(b):
                pe.wait_ge(o_ready, b + 1)
                for t in range(TPB):
                    last = nc.tensor.transpose(misc2[:, 0, t * P:(t + 1) * P], o[:, t * H:(t + 1) * H, :].rearrange("p h d -> p (h d)"), k.ident[:])
                last.then_inc(turned_o, 1)

            def project_o(b):
                pe.wait_ge(ot_ready, b + 1)
                nc.tensor.matmul(misc2[:, 1, :], k.ones_row[0:1, 0:P], w["L1b_bo"][:], start=True, stop=False, skip_group_check=True)
                for t in range(TPB):
                    last = nc.tensor.matmul(misc2[:, 1, t * D:(t + 1) * D], ot[:, t * P:(t + 1) * P], w["L1b_wo"][:], start=False, stop=True,
                                            skip_group_check=True)
                last.then_inc(y_ready, 1)

            def step(b, par, first, last_batch):
                pe.wait_ge(v_ready, b + 1)
                pe.wait_ge(masked_ready, b + 1)
                for n in range(MAXES):
                    i, t, h = n // (TPB * H // 2), n // (H // 2) % TPB, n % (H // 2) * 2
                    if n >= NB:
                        pe.wait_ge(max_ready, b * MAXES + (n - NB + 1))
                    nc.tensor.matmul(max_banks[n % NB], q0[:, i, t * P:(t + 1) * P],
                                     masked[par][:, i, h:h + 2, :].rearrange("p h q -> p (h q)"), start=True, stop=True).then_inc(max_up, 1)
                    if not first:
                        if n == 2:
                            turn_mixed(b - 1)
                        if n == 18:
                            turn_o(b - 1)
                        if n == 21:
                            project_o(b - 1)
                pe.wait_ge(top_ready, b + 1)
                for i in range(2):
                    for t in range(TPB):
                        last = nc.tensor.transpose(misc[0:AR, i, t * P:(t + 1) * P], top[:, i, t, :], k.ident[:])
                last.then_inc(turned, 1)
                pe.wait_ge(turned_ready, b + 1)

                def score(n):
                    i, h = divmod(n, H)
                    for t in range(TPB):
                        last = nc.tensor.matmul(score_ps[n % 2][:, t, :], masked[par][:, i, h, t * P:(t + 1) * P], qt[par][:, i, :], start=True, stop=True)
                    last.then_inc(score_up, 1)

                def mix(n):
                    i, h = divmod(n, H)
                    pe.wait_ge(e_ready, b * SCORES + (n + 1))
                    r = h % 4 * VC
                    for t in range(TPB):
                        last = nc.tensor.matmul(o_ps[r:r + VC, i, h // 4, :], vx[par][:, t, h, :], e[n % 3][:, t, :],
                                                start=(t == 0), stop=(t == TPB - 1))
                    return last

                score(0)
                for n in range(SCORES):
                    if n + 1 < SCORES:
                        score(n + 1)
                    last = mix(n)
                    if n % H == H - 1:
                        last.then_inc(o_up, 1)
                    if n == 2 and not last_batch:
                        if not first:
                            pe.wait_ge(done, b)
                        project_qk(b + 1)
                    if n == 9 and not last_batch:
                        project_v(b + 1)

            project_qk(0)
            project_v(0)
            over_pairs(pe, BATCH, step)
            turn_mixed(BATCH - 1)
            turn_o(BATCH - 1)
            project_o(BATCH - 1)

        @block.scalar
        def _(act):
            act.wait_ge(consts_ready, 1)
            nc.scalar.activation(lam[:], lam[:], ACT.Exp).then_inc(exped, 1)
            act.wait_ge(consts_ready, 2)

            def copy_x(b):
                nc.scalar.copy(xg[:], k.XNT[:, bass.ds(b * SEQ, SEQ)]).then_inc(xg_ready, 1)

            def keep_qk(b, par, part):
                if part == 0:
                    act.wait_ge(projected, b + 1)
                    nc.scalar.copy(kt[0:FR, :, :], misc2[0:FR, :, :]).then_inc(copied_k, 1)
                if part == 1:
                    nc.scalar.copy(q0[0:FR, :, :], misc[0:FR, :, :])
                if part == 2:
                    nc.scalar.copy(qt[par][0:FR, :, :], misc[0:FR, :, :]).then_inc(copied, 1)

            def keep_o(b):
                act.wait_ge(turned_o, b + 1)
                nc.scalar.copy(ot[:], misc2[:, 0, :]).then_inc(ot_ready, 1)

            def step(b, par, first, last_batch):
                if not first:
                    keep_o(b - 1)
                act.wait_ge(turned, b + 1)
                nc.scalar.copy(qt[par][FR:AR, :, :], misc[FR:AR, :, :]).then_inc(turned_ready, 1)
                for n in range(SCORES):
                    act.wait_ge(score_up, b * SCORES + (n + 1))
                    nc.scalar.activation(e[n % 3], score_ps[n % 2][:], ACT.Exp, scale=HD ** -0.5).then_inc(e_ready, 1)
                    if n == H:
                        act.wait_ge(o_up, b * 2 + 1)
                        nc.scalar.copy(mixed[:, 0, :, :], o_ps[:, 0, :, :]).then_inc(mixed_ready, 1)
                    if not last_batch:
                        if n == 0:
                            copy_x(b + 1)
                        if n in (4, 5, 6):
                            keep_qk(b + 1, 1 - par, n - 4)
                act.wait_ge(o_up, b * 2 + 2)
                nc.scalar.copy(mixed[:, 1, :, :], o_ps[:, 1, :, :]).then_inc(mixed_ready, 1)

            copy_x(0)
            for part in range(3):
                keep_qk(0, 0, part)
            over_pairs(act, BATCH, step)
            keep_o(BATCH - 1)

        @block.gpsimd
        def _(pool):
            nc.gpsimd.memset(minus[:], -0.5)
            pool.drain()
            with pool.Fori(0, BATCH) as b:
                pool.wait_ge(ms_ready, b + 1)
                nc.gpsimd.tensor_tensor(ms[:], ms[:], minus[:], ALU.pow).then_inc(rms_ready, 1)

        @block.vector
        def _(dve):
            dve.wait_ge(loaded, 16 * len(names))
            nc.vector.tensor_tensor(prod[:], w["L1b_lam"][:, 0:2 * HD].rearrange("p (i d) -> p i d", i=2),
                                    w["L1b_lam"][:, 2 * HD:4 * HD].rearrange("p (i d) -> p i d", i=2), ALU.mult)
            nc.vector.memset(kt[FR:AR, :, :], 1.0)
            nc.vector.memset(q0[FR:AR, :, :], 0.0)
            nc.vector.memset(top[:], 0.0)
            for buf in vx:
                nc.vector.memset(buf, 0.0)
            dve.drain()
            for buf in vx:
                nc.vector.memset(buf[:, :, :, VD:VD + 1], 1.0)
            nc.vector.tensor_scalar(sub[:].rearrange("p (h d) -> p h d", h=H),
                                    w["L1b_sub"][:].rearrange("p (a d) -> p a d", a=1).to_broadcast([P, H, VD]),
                                    1.0 - LAMBDA_INIT, None, ALU.mult)
            dve.drain()
            nc.vector.tensor_reduce(lam[:], prod[:], AX.X, ALU.add).then_inc(consts_ready, 1)
            dve.wait_ge(exped, 1)
            nc.vector.tensor_tensor(lam[:, 0:1], lam[:, 1:2], lam[:, 0:1], ALU.subtract)
            dve.drain()
            nc.vector.tensor_scalar(lam[:, 0:1], lam[:, 0:1], -LAMBDA_INIT, None, ALU.add).then_inc(consts_ready, 1)
            dve.drain()

            def mask_keys(b, par):
                dve.wait_ge(copied_k, b + 1)
                for i in range(2):
                    last = nc.vector.tensor_tensor(masked[par][:, i, :, :], kt[:, i, :].rearrange("p (a q) -> p a q", a=1).to_broadcast([AR, H, SEQ]),
                                                   w["c_head_rows"][:].rearrange("p (h a) -> p h a", a=1).to_broadcast([AR, H, SEQ]), ALU.mult)
                last.then_inc(masked_ready, 1)

            def keep_v(b, par):
                dve.wait_ge(v_up, b + 1)
                nc.vector.tensor_copy(vx[par][:, :, :, 0:VD], misc[:, :, 0:D].rearrange("p t (h d) -> p t h d", d=VD)).then_inc(v_ready, 1)

            def subtract_sets(b):
                dve.wait_ge(mixed_turned, b + 1)
                heads = o_flat.rearrange("p (n c) -> p n c", c=VC)
                nc.vector.reciprocal(rden[:].rearrange("p i n -> p (i n)"), heads[:, :, VD])
                dve.drain()
                nc.vector.tensor_tensor(att[:].rearrange("p i n d -> p (i n) d"), heads[:, :, 0:VD],
                                        per_row(rden[:].rearrange("p i n -> p (i n)"), VD), ALU.mult)
                dve.drain()
                nc.vector.scalar_tensor_tensor(out=o[:], in0=att[:, 1, :, :], scalar=lam[:, 0:1], in1=att[:, 0, :, :], op0=ALU.mult, op1=ALU.add)
                dve.drain()
                nc.vector.tensor_tensor(sq[:], o[:], o[:], ALU.mult)
                dve.drain()
                nc.vector.tensor_reduce(ms[:], sq[:], AX.X, ALU.add)
                dve.drain()
                nc.vector.tensor_scalar(ms[:], ms[:], 1.0 / VD, 1e-5, ALU.mult, ALU.add).then_inc(ms_ready, 1)

            def normalise_o(b):
                dve.wait_ge(rms_ready, b + 1)
                nc.vector.tensor_tensor(o[:], o[:], per_row(ms[:], VD), ALU.mult)
                dve.drain()
                by_tile = o[:].rearrange("p (t h) d -> p t (h d)", t=TPB)
                nc.vector.tensor_tensor(by_tile, by_tile, sub[:].rearrange("p (a n) -> p a n", a=1).to_broadcast([P, TPB, D]), ALU.mult).then_inc(o_ready, 1)

            def add_out(b):
                dve.wait_ge(y_ready, b + 1)
                x = k.X[:, bass.ds(b * TPB, TPB), :]
                nc.vector.tensor_tensor(x, x, misc2[:, 1, :].rearrange("p (t d) -> p t d", d=D), ALU.add).then_inc(done, 1)

            def step(b, par, first, last_batch):
                for n in range(MAXES):
                    i, t, h = n // (TPB * H // 2), n // (H // 2) % TPB, n % (H // 2) * 2
                    dve.wait_ge(max_up, b * MAXES + (n + 1))
                    nc.vector.tensor_reduce(top[:, i, t, FR + h:FR + h + 2], max_banks[n % NB].rearrange("p (h q) -> p h q", h=2), AX.X, ALU.max).then_inc(max_ready, 1)
                    if not first:
                        if n == 4:
                            subtract_sets(b - 1)
                        if n == 16:
                            normalise_o(b - 1)
                        if n == 25:
                            add_out(b - 1)
                dve.drain()
                tops = top[:].rearrange("p i t n -> p (i t) n")[:, :, FR:FR + H]
                nc.vector.tensor_scalar(tops, tops, -1.0, None, ALU.mult).then_inc(top_ready, 1)
                if not last_batch:
                    mask_keys(b + 1, 1 - par)
                    keep_v(b + 1, 1 - par)

            mask_keys(0, 0)
            keep_v(0, 0)
            over_pairs(dve, BATCH, step)
            subtract_sets(BATCH - 1)
            normalise_o(BATCH - 1)
            add_out(BATCH - 1)


def rows128(a):
    n, m = a.shape[0] // P, a.shape[1]
    return a.reshape(n, P, m).transpose(1, 0, 2).reshape(P, n * m)


def layouts(inp):
    a = {n: np.asarray(v) for n, v in inp.items()}
    o = {"x": a["L0_attn_a_x"].reshape(TILES, P, D).transpose(1, 0, 2), "c_ident": np.eye(P, dtype=np.float32)}
    o["L0_ffn_router"] = a["L0_ffn_router_w"].T
    o["L0_ffn_w1"] = a["L0_ffn_w1"].transpose(2, 0, 1).reshape(D, -1)
    o["L0_ffn_w2"] = rows128(a["L0_ffn_w2"].transpose(0, 2, 1).reshape(-1, D))
    o["L3_ffn_router"] = a["L3_ffn_router_w"].T
    o["L3_ffn_rb"] = np.broadcast_to(a["L3_ffn_router_b"], (P, 8))
    o["L3_ffn_w1"] = a["L3_ffn_w1"].transpose(2, 0, 1).reshape(D, -1)
    o["L3_ffn_b1"] = a["L3_ffn_b1"].reshape(8 * 8, P).T
    o["L3_ffn_w2"] = rows128(a["L3_ffn_w2"].transpose(0, 2, 1).reshape(-1, D))
    o["L3_ffn_b2"] = np.tile(a["L3_ffn_b2"], (P // 8, 1))
    o["c_own_tile"] = np.repeat(np.eye(P // 8, dtype=np.float32), 8, axis=0)
    o["L1_ffn_router"] = a["L1_ffn_Wg"]
    o["L1_ffn_w1"] = a["L1_ffn_W1"].transpose(1, 0, 2).reshape(D, -1)
    o["L1_ffn_w2"] = rows128(a["L1_ffn_W2"].reshape(-1, D))
    o["c_before"] = np.triu(np.ones((P, P), np.float32), 1)
    o["c_not_first_tile"] = np.broadcast_to((np.arange(8 * TILES) % TILES > 0).astype(np.float32), (P, 8 * TILES))
    o["c_early_first"] = np.broadcast_to(np.repeat(8 - np.arange(8, dtype=np.float32), TILES), (P, 8 * TILES))
    row = lambda v: np.tile(v, GT).reshape(1, GROUP)
    spread = lambda v: np.broadcast_to(v, (P, v.shape[0]))
    col = lambda v: v.reshape(-1, P).T
    o["L0a_wqkv"] = np.concatenate([a["L0_attn_a_W" + n].T for n in "qkv"], axis=1)
    o["L0a_bqkv"] = spread(np.concatenate([a["L0_attn_a_b" + n] for n in "qkv"]))
    o["L0a_w1"], o["L0a_b1"] = a["L0_attn_a_W1"].T, col(a["L0_attn_a_b1"])
    o["L0a_w2"], o["L0a_b2"] = a["L0_attn_a_W2"].T, col(a["L0_attn_a_b2"])
    o["L0a_w3"], o["L0a_b3"] = rows128(a["L0_attn_a_W3"].T), row(a["L0_attn_a_b3"])
    o["L0b_w"] = np.concatenate([a["L0_attn_b_Wq"].T] + [a["L0_attn_b_W" + n][i].T for n in "kv" for i in range(2)], axis=1)
    o["L0b_b"] = spread(np.concatenate([a["L0_attn_b_bq"]] + [a["L0_attn_b_b" + n][i] for n in "kv" for i in range(2)]))
    o["L0b_wo"], o["L0b_bo"] = a["L0_attn_b_Wo"].T, row(a["L0_attn_b_bo"])
    o["L0b_g"], o["L0b_be"] = col(a["L0_attn_b_ln_g"]), col(a["L0_attn_b_ln_b"])
    o["L3b_w"] = np.concatenate([a["L3_attn_b_W" + n] for n in "qkv"], axis=1)
    o["L3b_b"] = spread(np.concatenate([a["L3_attn_b_b" + n] for n in "qkv"]))
    o["L3b_wo"], o["L3b_bo"] = a["L3_attn_b_Wo"], row(a["L3_attn_b_bo"])
    o["L3b_g1"], o["L3b_be1"] = col(a["L3_attn_b_g1"]), col(a["L3_attn_b_be1"])
    o["L3b_g2"], o["L3b_be2"] = spread(a["L3_attn_b_g2"]), spread(a["L3_attn_b_be2"])
    o["L3b_w1"], o["L3b_b1"] = a["L3_attn_b_W1"], col(a["L3_attn_b_b1"])
    o["L3b_w2"], o["L3b_b2"] = rows128(a["L3_attn_b_W2"]), row(a["L3_attn_b_b2"])
    o["L3a_wq"], o["L3a_wk"] = a["L3_attn_a_q_w"].T, np.tile(a["L3_attn_a_kv_w"][0:8].T, (1, 16))
    o["L3a_wv"] = np.tile(a["L3_attn_a_kv_w"][8:16].T, (1, 4))
    o["L3a_wo"], o["L3a_bo"] = a["L3_attn_a_proj_w"].T, row(a["L3_attn_a_proj_b"])
    o["c_head_of_row8"] = np.repeat(np.eye(16, dtype=np.float32), 8, axis=0)
    o["c_blocks32x8"] = np.kron(np.eye(4, dtype=np.float32), np.ones((32, 8), np.float32))
    o["c_pick"] = np.tile(np.eye(32, dtype=np.float32), (3, 1))
    o["L1a_win"] = a["L1_attn_a_in_proj_w"].T
    o["L1a_conv"] = a["L1_attn_a_conv_w"].reshape(2, P, 4).transpose(1, 0, 2).reshape(P, 8)
    o["L1a_wx"] = rows128(a["L1_attn_a_x_proj_w"].T)
    o["L1a_wdt"], o["L1a_bdt"] = a["L1_attn_a_dt_proj_w"].T, col(a["L1_attn_a_dt_proj_b"])
    o["L1a_alog"], o["L1a_d"] = rows128(a["L1_attn_a_A_log"]), col(a["L1_attn_a_D"])
    o["L1a_wout"] = rows128(a["L1_attn_a_out_proj_w"].T)
    even_odd = np.r_[0:16:2, 1:16:2]
    wx = np.zeros((65, 256), np.float32)
    wx[0:32], wx[32], wx[64] = a["L2_attn_a_W_x"][np.r_[even_odd, 16 + even_odd]], a["L2_attn_a_W_x"][32], a["L2_attn_a_W_x"][33]
    both = lambda n: np.concatenate([a[f"L2_attn_a_{c}_{n}"][even_odd] for c in "BC"]).reshape(32, 1)
    o["L2a_win"], o["L2a_wx"], o["L2a_wdt"] = a["L2_attn_a_W_in"].T, rows128(wx.T), a["L2_attn_a_W_dt"].T
    o["L2a_bdt"], o["L2a_d"] = col(a["L2_attn_a_b_dt"]), col(a["L2_attn_a_D"])
    o["L2a_alog"], o["L2a_wout"] = rows128(a["L2_attn_a_A_log"][:, even_odd]), rows128(a["L2_attn_a_W_out"].T)
    o["L2a_bias"], o["L2a_norm"] = both("bias"), both("norm_w")
    o["L2a_freq"] = np.tile(a["L2_attn_a_rope_freqs"], 4).reshape(32, 1)
    o["c_mean16"] = np.tile(np.kron(np.eye(2, dtype=np.float32), np.ones((16, 16), np.float32) / 16), (1, 4))
    quarter = np.kron(np.array([[0, 1], [-1, 0]], np.float32), np.eye(8, dtype=np.float32))
    o["c_quarter_turn"] = np.kron(np.eye(2, dtype=np.float32), quarter)
    o["c_not_first"] = np.broadcast_to((np.arange(GROUP) % SEQ > 0).astype(np.float32), (32, GROUP))
    swapped = np.arange(64) ^ 1
    heads = lambda v: v.reshape(D, 8, D)
    for n in "QK":
        o[f"L2b_w{n}"] = a[f"L2_attn_b_W_{n}"]
        o[f"L2b_w{n}s"] = heads(a[f"L2_attn_b_W_{n}"])[:, :, swapped].reshape(D, 512)
    o["L2b_wV"] = a["L2_attn_b_W_V"]
    o["L2b_g"], o["L2b_be"] = spread(a["L2_attn_b_gn_weight"]), spread(a["L2_attn_b_gn_bias"])
    inv_freq = 1.0 / 10000.0 ** (np.arange(0, 64, 2, dtype=np.float32) / 64)
    ang = np.repeat(np.arange(SEQ, dtype=np.float32)[:, None] * inv_freq[None, :], 2, axis=-1).astype(np.float32).T
    sign = np.where(np.arange(64) % 2 == 0, -1, 1).astype(np.float32)[:, None]
    o["c_cos"], o["c_sin"] = np.tile(np.cos(ang), (1, BPG)), np.tile(np.sin(ang) * sign, (1, BPG))
    diff = np.arange(SEQ)[:, None] - np.arange(SEQ)[None, :]
    decay = np.where(diff >= 0, np.float32(0.96875) ** np.maximum(diff, 0).astype(np.float32), 0).astype(np.float32)
    o["c_decay"] = np.concatenate([decay[0:P, 0:P], decay[P:, :]], axis=1)
    o["L2f_sig"] = a["L2_ffn_signatures_raw"].T
    o["L2f_temp"], o["L2f_knots"] = spread(a["L2_ffn_temperature"]), spread(a["L2_ffn_knot_values"])
    o["L2f_scale"] = spread(a["L2_ffn_output_scale"])
    o["L2f_cw1"], o["L2f_cb1"] = a["L2_ffn_compress_w1"], a["L2_ffn_compress_b1"].reshape(32, 1)
    o["L2f_cw2"], o["L2f_cb2"] = a["L2_ffn_compress_w2"], np.tile(a["L2_ffn_compress_b2"], GT).reshape(1, 2 * GT)
    table = np.concatenate([a["L2_ffn_spline_w1"].reshape(64, 32), a["L2_ffn_spline_b1"], a["L2_ffn_spline_w2"].reshape(64, 16),
                            a["L2_ffn_spline_b2"], a["L2_ffn_directions"]], axis=1)
    o["L2f_table"] = np.tile(table, (2, 1))
    o["L2f_gamma"], o["L2f_beta"] = spread(a["L2_ffn_norm_gamma"]), spread(a["L2_ffn_norm_beta"])
    o["c_first8"] = spread(8 - np.arange(8, dtype=np.float32))
    o["c_first64"] = spread(64 - np.arange(64, dtype=np.float32))
    o["c_minus_knot"] = spread(-np.arange(8, dtype=np.float32))
    o["L1b_wqk"], o["L1b_wv"] = a["L1_attn_b_W_qkv"][:, 0:2 * D], a["L1_attn_b_W_qkv"][:, 2 * D:]
    o["L1b_wo"], o["L1b_bo"] = a["L1_attn_b_W_proj"], np.tile(a["L1_attn_b_b_proj"], TPB).reshape(1, TPB * D)
    o["L1b_lam"] = spread(np.concatenate([a["L1_attn_b_lambda_" + n] for n in ("q1", "q2", "k1", "k2")]))
    o["L1b_sub"] = spread(a["L1_attn_b_subln_w"])
    o["c_head_rows"] = np.concatenate([np.repeat(np.eye(16, dtype=np.float32), 4, axis=0), np.eye(16, dtype=np.float32), np.zeros((16, 16), np.float32)])
    o["c_heads8"] = np.kron(np.eye(16, dtype=np.float32), np.ones((8, 8), np.float32))
    return o


RESIDENT = [("L0_ffn_router", "l0_ffn"),
            ("L1_ffn_router", "l1_ffn"),
            ("L3_ffn_router", "l3_ffn"), ("L3_ffn_rb", "l3_ffn"), ("L3_ffn_b1", "l3_ffn"),
            ("L3_ffn_b2", "l3_ffn"), ("c_own_tile", "l3_ffn")]
STEPS = {f.__name__: f for f in (l0_ffn, l3_ffn, l1_ffn, l0_attn_a, l0_attn_b,
                                l3_attn_a, l3_attn_b, l1_attn_a, l2_attn_a,
                                l1_attn_b, l2_attn_b, l2_ffn)}
PLAN = ["l0_attn_a",
        "l0_ffn",
        "l0_attn_b",
        "l0_ffn",
        "l1_attn_a",
        "l1_ffn",
        "l1_attn_b",
        "l1_ffn",
        "l2_attn_a",
        "l2_ffn",
        "l2_attn_b",
        "l2_ffn",
        "l3_attn_a",
        "l3_ffn",
        "l3_attn_b",
        "l3_ffn"]


def build(nc, dram, out, plan):
    k = Core(nc, dram)
    with k.stack:
        k.X = k.keep("X", [P, TILES, D])
        k.XN = k.keep("XN", [P, TILES, D])
        k.XNT = k.keep("XNT", [P, TOKENS])
        k.LOG = k.keep("LOG", [P, TILES, 72])
        k.PICK = k.keep("PICK", [P, TILES, 64])
        k.SIG = k.keep("SIG", [P, 72])
        k.ones = k.keep("ones", [P, P])
        k.ones_row = k.keep("ones_row", [1, GROUP])
        k.GATE = k.keep("GATE", [P, TILES, 8])
        k.ident = k.keep("c_ident", [P, P])
        k.up = k.keep("up", [P, max(dram[f"L{i}_ffn_w1"].shape[1] for i in (0, 1, 3))])
        k.down = k.keep("down", [P, max(dram[f"L{i}_ffn_w2"].shape[1] for i in (0, 1, 3))])
        k.weights_landed = k.stack.enter_context(nc.semaphore("weights_landed"))
        weights = ["c_ident"]
        for name, needed_by in RESIDENT:
            if any(p.startswith(needed_by) for p in plan):
                k.keep(name, list(dram[name].shape))
                weights.append(name)
        load_all(nc, k, weights)
        experts = [p for p in plan if p in ("l0_ffn", "l1_ffn", "l3_ffn")]
        landed = None
        if experts:
            start_expert_load(nc, k, experts[0])
        for n, step in enumerate(plan):
            if step in experts and landed != step:
                finish_expert_load(nc, k)
                landed = step
            STEPS[step](nc, k, f"s{n}_{step}")
            later = [p for p in plan[n + 1:] if p in experts]
            if step in experts and later and later[0] != step:
                start_expert_load(nc, k, later[0])
        store(nc, k, out)


def kernel(**inputs):
    import concourse.bacc as bacc
    from concourse.bass_utils import run_bass_kernel_spmd

    nc = bacc.Bacc("TRN2", target_bir_lowering=False, num_devices=1)
    arrays = {n: np.ascontiguousarray(a) for n, a in layouts(inputs).items()}
    dram = {n: nc.dram_tensor(f"in_{n}", a.shape, mybir.dt.from_np(a.dtype), kind="ExternalInput").ap()
            for n, a in arrays.items()}
    out = nc.dram_tensor("out_x", (BATCH, SEQ, D), F32, kind="ExternalOutput").ap()
    build(nc, dram, out.rearrange("b (t p) d -> p (b t) d", p=P), PLAN)
    r = run_bass_kernel_spmd(nc, [{f"in_{n}": a for n, a in arrays.items()}], core_ids=[0])
    return r.results[0]["out_x"]
```

```python
from contextlib import ExitStack

import numpy as np

import concourse.bass as bass
from concourse import mybir

F32 = mybir.dt.float32
BF16 = mybir.dt.bfloat16
U32 = mybir.dt.uint32
I32 = mybir.dt.int32
ALU = mybir.AluOpType
ACT = mybir.ActivationFunctionType
AX = mybir.AxisListType

P = 128
BATCH, SEQ, D = 16, 256, 128
TOKENS = BATCH * SEQ
TILES = TOKENS // P
GT = 4
GROUP = GT * P
GROUPS = TILES // GT
BPG = GROUP // SEQ
TPB = SEQ // P
LN_EPS = 1e-5


class Scope:

    def __init__(self, nc, name):
        self.nc, self.name, self.stack = nc, name, ExitStack()
        self.sems = []

    def __enter__(self):
        self.stack.__enter__()
        return self

    def __exit__(self, *a):
        return self.stack.__exit__(*a)

    def sb(self, name, shape, dt=F32):
        return self.stack.enter_context(self.nc.sbuf_tensor(f"{self.name}_{name}", shape, dt))

    def ps(self, name, shape, dt=F32):
        return self.stack.enter_context(self.nc.psum_tensor(f"{self.name}_{name}", shape, dt))

    def two(self, name, shape):
        return [self.sb(f"{name}{m}", shape) for m in range(2)]

    def two_ps(self, name, shape):
        return [self.ps(f"{name}{m}", shape) for m in range(2)]

    def sem(self, name):
        self.sems.append(self.stack.enter_context(self.nc.semaphore(f"{self.name}_{name}")))
        return self.sems[-1]

    def clear(self):
        for sem in self.sems:
            self.nc.gpsimd.sem_clear(sem)

    def block(self):
        self.stack.callback(self.clear)
        return self.stack.enter_context(self.nc.Block())


class Core:

    def __init__(self, nc, dram):
        self.nc, self.dram = nc, dram
        self.stack = ExitStack()
        self.bufs = {}
        self.loads_started = 0

    def keep(self, name, shape, dt=F32):
        self.bufs[name] = self.stack.enter_context(self.nc.sbuf_tensor(name, shape, dt))
        return self.bufs[name]


def flat(ap):
    return ap.rearrange("p a n -> p (a n)")


def tile(buf, t):
    return flat(buf[:, bass.ds(t, 1), :])


def load_all(nc, k, weights):
    with Scope(nc, "load") as s:
        loaded = s.sem("loaded")
        block = s.block()

        @block.sync
        def _(sp):
            n = 0
            sp.dma_start(k.X[:], k.dram["x"]).then_inc(loaded, 16)
            for name in weights:
                sp.dma_start(k.bufs[name][:], k.dram[name]).then_inc(loaded, 16)
                n += 16
            sp.wait_ge(loaded, n + 16)

        @block.vector
        def _(dve):
            nc.vector.memset(k.ones[:], 1.0)
            nc.vector.memset(k.ones_row[:], 1.0)


def start_expert_load(nc, k, step):
    k.loads_started += 2
    layer = step[:2].upper()
    with Scope(nc, f"{step}_load{k.loads_started}") as s:
        block = s.block()

        @block.sync
        def _(sp):
            for buf, name in ((k.up, "w1"), (k.down, "w2")):
                src = k.dram[f"{layer}_ffn_{name}"]
                sp.dma_start(buf[:, 0:src.shape[1]], src).then_inc(k.weights_landed, 16)


def finish_expert_load(nc, k):
    with Scope(nc, f"landed{k.loads_started}") as s:
        block = s.block()

        @block.sync
        def _(sp):
            sp.wait_ge(k.weights_landed, 16 * k.loads_started)


def store(nc, k, out):
    with Scope(nc, "store") as s:
        stored = s.sem("stored")
        block = s.block()

        @block.sync
        def _(sp):
            sp.dma_start(out, k.X[:]).then_inc(stored, 16)
            sp.wait_ge(stored, 16)


def layer_norm(nc, k, name, project=None, n_out=0, keep_rows=False, loads=()):
    with Scope(nc, name) as s:
        stats = s.sb("stats", [P, TILES, 6])
        meanvar = s.sb("meanvar", [P, TILES, 1])
        rstd = s.sb("rstd", [P, TILES])
        half_gap = s.sb("half_gap", [P, TILES])
        rows = [s.sb(f"rows{i}", [P, GT, D]) for i in range(2)]
        cols = [s.sb(f"cols{i}", [P, GROUP]) for i in range(2)]
        turned = [s.ps(f"turned{i}", [P, GROUP]) for i in range(2)]
        proj = [s.ps(f"proj{i}", [P, 512]) for i in range(2)]
        moments, ready = s.sem("moments"), s.sem("ready")
        rows_ready, rows_free = s.sem("rows_ready"), s.sem("rows_free")
        turned_ready = s.sem("turned_ready")
        turned_free, cols_ready = s.sem("turned_free"), s.sem("cols_ready")
        proj_ready, logits_kept = s.sem("proj_ready"), s.sem("logits_kept")
        rows_kept = s.sem("rows_kept")
        block = s.block()

        @block.sync
        def _(sp):
            for buf, src, loaded in loads:
                sp.dma_start(buf, src).then_inc(loaded, 16)

        @block.vector
        def _(dve):
            for t in range(TILES):
                nc.vector.bn_stats(stats[:, t, :], k.X[:, t, :])
            dve.drain()
            nc.vector.tensor_tensor(meanvar[:, :, 0], stats[:, :, 1], stats[:, :, 4], ALU.add)
            nc.vector.tensor_tensor(half_gap[:], stats[:, :, 1], stats[:, :, 4], ALU.subtract)
            nc.vector.tensor_tensor(rstd[:], stats[:, :, 2], stats[:, :, 5], ALU.add)
            dve.drain()
            nc.vector.tensor_scalar(meanvar[:, :, 0], meanvar[:, :, 0], 0.5, None, ALU.mult)
            nc.vector.scalar_tensor_tensor(out=half_gap[:], in0=half_gap[:], scalar=0.25, in1=half_gap[:],
                                           op0=ALU.mult, op1=ALU.mult)
            nc.vector.tensor_scalar(rstd[:], rstd[:], 1.0 / D, LN_EPS, ALU.mult, ALU.add)
            dve.drain()
            nc.vector.tensor_tensor(rstd[:], rstd[:], half_gap[:], ALU.add).then_inc(moments, 1)
            dve.wait_ge(ready, 1)
            nc.vector.reciprocal(rstd[:], rstd[:])
            dve.drain()
            with dve.Fori(0, GROUPS // 2) as pair:
                g = pair * 2
                for i in range(2):
                    dve.wait_ge(rows_free, g + (i + 1))
                    if keep_rows:
                        dve.wait_ge(rows_kept, g + (i + 1))
                    for j in range(GT):
                        last = nc.vector.tensor_scalar(
                            rows[i][:, j, :], tile(k.X, g * GT + (i * GT + j)),
                            flat(meanvar[:, bass.ds(g * GT + (i * GT + j), 1), 0:1]),
                            rstd[:, bass.ds(g * GT + (i * GT + j), 1)], ALU.subtract, ALU.mult)
                    last.then_inc(rows_ready, 1)

        if keep_rows:
            @block.gpsimd
            def _(pool):
                pool.sem_inc(rows_kept, 2)
                with pool.Fori(0, GROUPS // 2) as pair:
                    for i in range(2):
                        pool.wait_ge(rows_ready, pair * 2 + (i + 1))
                        nc.gpsimd.tensor_copy(k.XN[:, bass.ds(pair * 2 * GT + i * GT, GT), :], rows[i][:]).then_inc(rows_kept, 1)

        @block.tensor
        def _(pe):
            pe.sem_inc(rows_free, 2)
            with pe.Fori(0, GROUPS // 2) as pair:
                g = pair * 2
                for i in range(2):
                    pe.wait_ge(rows_ready, g + (i + 1))
                    pe.wait_ge(turned_free, g + (i + 1))
                    for j in range(GT):
                        last = nc.tensor.transpose(turned[i][:, j * P:(j + 1) * P], rows[i][:, j, :], k.ident[:])
                    last.then_inc(turned_ready, 1)
                if project is not None:
                    for i in range(2):
                        pe.wait_ge(cols_ready, g + (i + 1))
                        for j in range(GT):
                            last = nc.tensor.matmul(proj[i][:, j * n_out:(j + 1) * n_out], cols[i][:, j * P:(j + 1) * P],
                                                    project[:, 0:n_out], start=True, stop=True)
                        last.then_inc(proj_ready, 1)

        @block.scalar
        def _(act):
            act.wait_ge(moments, 1)
            nc.scalar.activation(rstd[:], rstd[:], ACT.Sqrt).then_inc(ready, 1)
            act.sem_inc(turned_free, 2)
            with act.Fori(0, GROUPS // 2) as pair:
                g = pair * 2
                for i in range(2):
                    act.wait_ge(turned_ready, g + (i + 1))
                    act.sem_inc(rows_free, 1)
                    xnt = k.XNT[:, bass.ds(g * GROUP + i * GROUP, GROUP)]
                    if project is not None:
                        nc.scalar.copy(cols[i][:], turned[i][:]).then_inc(cols_ready, 1)
                    nc.scalar.copy(xnt, turned[i][:]).then_inc(turned_free, 1)
                if project is not None:
                    for i in range(2):
                        act.wait_ge(proj_ready, g + (i + 1))
                        nc.scalar.copy(k.LOG[:, bass.ds(g * GT + i * GT, GT), 0:n_out],
                                       proj[i][:, 0:GT * n_out].rearrange("p (t n) -> p t n", n=n_out)).then_inc(logits_kept, 1)


def rank_below_two(nc, dve, s, probs, keep):
    ahead = s.sb("ahead", [P, TILES, 8])
    cmp = s.sb("cmp", [P, TILES, 8])
    nc.vector.memset(ahead[:], 0.0)
    for j in range(8):
        pj = probs[:, :, j:j + 1]
        dve.drain()
        if j > 0:
            nc.vector.tensor_tensor(cmp[:, :, 0:j], pj.to_broadcast([P, TILES, j]), probs[:, :, 0:j], ALU.is_gt)
        if j < 7:
            nc.vector.tensor_tensor(cmp[:, :, j + 1:8], pj.to_broadcast([P, TILES, 7 - j]), probs[:, :, j + 1:8], ALU.is_ge)
        nc.vector.memset(cmp[:, :, j:j + 1], 0.0)
        dve.drain()
        nc.vector.tensor_tensor(ahead[:], ahead[:], cmp[:], ALU.add)
    dve.drain()
    nc.vector.tensor_scalar(keep[:], ahead[:], 2.0, None, ALU.is_lt)
    dve.drain()


def softmax8(nc, k, name, top2_first, bias=None):
    with Scope(nc, name) as s:
        shifted = s.sb("shifted", [P, TILES, 8])
        e = s.sb("e", [P, TILES, 8])
        keep = s.sb("keep", [P, TILES, 8])
        top = s.sb("top", [P, TILES])
        total = s.sb("total", [P, TILES])
        shift_ready, exp_ready = s.sem("shift_ready"), s.sem("exp_ready")
        block = s.block()
        logits = k.LOG[:, :, 0:8]

        def per_tile(ap):
            return ap.rearrange("p (t a) -> p t a", a=1).to_broadcast([P, TILES, 8])

        @block.vector
        def _(dve):
            if bias is not None:
                nc.vector.tensor_tensor(logits, logits, bias[:].rearrange("p (a e) -> p a e", a=1)
                                        .to_broadcast([P, TILES, 8]), ALU.add)
                dve.drain()
            nc.vector.tensor_reduce(top[:], logits, AX.X, ALU.max)
            if top2_first:
                rank_below_two(nc, dve, s, k.LOG[:, :, 0:8], keep)
            dve.drain()
            nc.vector.tensor_tensor(shifted[:], logits, per_tile(top[:]), ALU.subtract).then_inc(shift_ready, 1)
            dve.wait_ge(exp_ready, 1)
            if top2_first:
                nc.vector.tensor_tensor(e[:], e[:], keep[:], ALU.mult)
                dve.drain()
            nc.vector.tensor_reduce(total[:], e[:], AX.X, ALU.add)
            dve.drain()
            nc.vector.reciprocal(total[:], total[:])
            dve.drain()
            nc.vector.tensor_tensor(k.GATE[:], e[:], per_tile(total[:]), ALU.mult)
            if top2_first is False:
                dve.drain()
                rank_below_two(nc, dve, s, k.GATE, keep)
                nc.vector.tensor_tensor(k.GATE[:], k.GATE[:], keep[:], ALU.mult)

        @block.scalar
        def _(act):
            act.wait_ge(shift_ready, 1)
            nc.scalar.activation(e[:], shifted[:], ACT.Exp).then_inc(exp_ready, 1)


def gelu_experts(nc, k, name, w1, w2, chunks):
    with Scope(nc, name) as s:
        up = [s.ps(f"up{i}", [P, GROUP]) for i in range(2)]
        down = [s.ps(f"down{i}", [P, GT, D]) for i in range(2)]
        hid = [s.sb(f"hid{i}", [P, GROUP]) for i in range(2)]
        up_ready, hid_ready = s.sem("up_ready"), s.sem("hid_ready")
        down_ready, down_free = s.sem("down_ready"), s.sem("down_free")
        block = s.block()
        steps = 8 * chunks

        @block.tensor
        def _(pe):
            def go_up(g, c):
                nc.tensor.matmul(up[c % 2][:], w1[:, c * P:(c + 1) * P], k.XNT[:, bass.ds(g * GROUP, GROUP)],
                                 start=True, stop=True).then_inc(up_ready, 1)

            def go_down(g, c):
                e, j = divmod(c, chunks)
                pe.wait_ge(hid_ready, g * steps + (c + 1))
                if j == 0:
                    pe.wait_ge(down_free, g * 8 + (e + 1))
                for t in range(GT):
                    last = nc.tensor.matmul(down[e % 2][:, t, :], hid[c % 2][:, t * P:(t + 1) * P],
                                            w2[:, c * D:(c + 1) * D], start=(j == 0 and t == 0),
                                            stop=(j == chunks - 1), skip_group_check=True)
                if j == chunks - 1:
                    last.then_inc(down_ready, 1)

            with pe.Fori(0, GROUPS) as g:
                go_up(g, 0)
                for c in range(steps):
                    if c + 1 < steps:
                        go_up(g, c + 1)
                    go_down(g, c)

        @block.scalar
        def _(act):
            with act.Fori(0, GROUPS) as g:
                for c in range(steps):
                    act.wait_ge(up_ready, g * steps + (c + 1))
                    nc.scalar.activation(hid[c % 2][:], up[c % 2][:], ACT.Gelu).then_inc(hid_ready, 1)

        @block.vector
        def _(dve):
            dve.sem_inc(down_free, 2)
            with dve.Fori(0, GROUPS) as g:
                for e in range(8):
                    dve.wait_ge(down_ready, g * 8 + (e + 1))
                    for t in range(GT):
                        xt = tile(k.X, g * GT + t)
                        last = nc.vector.scalar_tensor_tensor(
                            out=xt, in0=down[e % 2][:, t, :], scalar=flat(k.GATE[:, bass.ds(g * GT + t, 1), e:e + 1]),
                            in1=xt, op0=ALU.mult, op1=ALU.add)
                    last.then_inc(down_free, 1)
                    dve.drain()


def l0_ffn(nc, k, name):
    layer_norm(nc, k, name + "_ln", k.bufs["L0_ffn_router"], 8)
    softmax8(nc, k, name + "_gate", False)
    gelu_experts(nc, k, name + "_ffn", k.up, k.down, 4)


def silu_experts(nc, k, name):
    w1, b1, w2 = k.up, k.bufs["L3_ffn_b1"], k.down
    chunks = 4
    steps = 8 * chunks
    with Scope(nc, name) as s:
        up_a = [s.ps(f"up_a{i}", [P, GROUP]) for i in range(2)]
        up_b = [s.ps(f"up_b{i}", [P, GROUP]) for i in range(2)]
        down = [s.ps(f"down{i}", [P, GT, D]) for i in range(2)]
        gated = [s.sb(f"gated{i}", [P, GROUP]) for i in range(2)]
        hid = [s.sb(f"hid{i}", [P, GROUP]) for i in range(2)]
        up_ready, gated_ready, hid_ready = s.sem("up_ready"), s.sem("gated_ready"), s.sem("hid_ready")
        down_ready, down_free = s.sem("down_ready"), s.sem("down_free")
        block = s.block()

        @block.tensor
        def _(pe):
            def go_up(g, c):
                e, j = divmod(c, chunks)
                xn = k.XNT[:, bass.ds(g * GROUP, GROUP)]
                a, b = (2 * e * chunks + j) * P, ((2 * e + 1) * chunks + j) * P
                nc.tensor.matmul(up_a[c % 2][:], w1[:, a:a + P], xn, start=True, stop=True)
                nc.tensor.matmul(up_b[c % 2][:], w1[:, b:b + P], xn, start=True, stop=True).then_inc(up_ready, 1)

            def go_down(g, c):
                e, j = divmod(c, chunks)
                pe.wait_ge(hid_ready, g * steps + (c + 1))
                if j == 0:
                    pe.wait_ge(down_free, g * 8 + (e + 1))
                for t in range(GT):
                    last = nc.tensor.matmul(down[e % 2][:, t, :], hid[c % 2][:, t * P:(t + 1) * P],
                                            w2[:, c * D:(c + 1) * D], start=(j == 0 and t == 0),
                                            stop=(j == chunks - 1), skip_group_check=True)
                if j == chunks - 1:
                    last.then_inc(down_ready, 1)

            with pe.Fori(0, GROUPS) as g:
                go_up(g, 0)
                for c in range(steps):
                    if c + 1 < steps:
                        go_up(g, c + 1)
                    go_down(g, c)

        @block.scalar
        def _(act):
            with act.Fori(0, GROUPS) as g:
                for c in range(steps):
                    e, j = divmod(c, chunks)
                    act.wait_ge(up_ready, g * steps + (c + 1))
                    nc.scalar.activation(gated[c % 2][:], up_a[c % 2][:], ACT.Silu,
                                         bias=b1[:, 2 * e * chunks + j:2 * e * chunks + j + 1]).then_inc(gated_ready, 1)

        @block.vector
        def _(dve):
            dve.sem_inc(down_free, 2)

            def add_expert(g, e):
                dve.wait_ge(down_ready, g * 8 + (e + 1))
                for t in range(GT):
                    xt = tile(k.X, g * GT + t)
                    last = nc.vector.scalar_tensor_tensor(
                        out=xt, in0=down[e % 2][:, t, :], scalar=flat(k.GATE[:, bass.ds(g * GT + t, 1), e:e + 1]),
                        in1=xt, op0=ALU.mult, op1=ALU.add)
                last.then_inc(down_free, 1)
                dve.drain()

            with dve.Fori(0, GROUPS) as g:
                for c in range(steps):
                    e, j = divmod(c, chunks)
                    b = (2 * e + 1) * chunks + j
                    dve.wait_ge(gated_ready, g * steps + (c + 1))
                    nc.vector.scalar_tensor_tensor(out=hid[c % 2][:], in0=up_b[c % 2][:], scalar=b1[:, b:b + 1],
                                                   in1=gated[c % 2][:], op0=ALU.add, op1=ALU.mult).then_inc(hid_ready, 1)
                    if j == 1 and e > 0:
                        add_expert(g, e - 1)
                add_expert(g, 7)


def expert_bias(nc, k, name):
    half = TILES // 2
    with Scope(nc, name) as s:
        turned = s.ps("turned", [P, 2, P])
        gates = s.sb("gates", [P, 2, P])
        spread = s.sb("spread", [P, half, D])
        added = [s.ps(f"added{i}", [P, GT, D]) for i in range(4)]
        turned_ready, gates_ready = s.sem("turned_ready"), s.sem("gates_ready")
        spread_ready, added_ready, added_free = s.sem("spread_ready"), s.sem("added_ready"), s.sem("added_free")
        block = s.block()

        @block.gpsimd
        def _(pool):
            nc.gpsimd.tensor_tensor(spread[:],
                                    k.bufs["L3_ffn_b2"][:].rearrange("p (a d) -> p a d", a=1).to_broadcast([P, half, D]),
                                    k.bufs["c_own_tile"][:].rearrange("p (t a) -> p t a", a=1).to_broadcast([P, half, D]),
                                    ALU.mult).then_inc(spread_ready, 1)

        @block.tensor
        def _(pe):
            for h in range(2):
                nc.tensor.transpose(turned[:, h, :], k.GATE[:, h * half:(h + 1) * half, :].rearrange("p t e -> p (t e)"),
                                    k.ident[:]).then_inc(turned_ready, 1)
            pe.wait_ge(gates_ready, 1)
            pe.wait_ge(spread_ready, 1)
            for g in range(GROUPS):
                if g >= 4:
                    pe.wait_ge(added_free, g - 3)
                h, q = divmod(g * GT, half)
                nc.tensor.matmul(added[g % 4][:], gates[:, h, :], spread[:, q:q + GT, :], start=True, stop=True)\
                    .then_inc(added_ready, 1)

        @block.scalar
        def _(act):
            act.wait_ge(turned_ready, 2)
            nc.scalar.copy(gates[:], turned[:]).then_inc(gates_ready, 1)

        @block.vector
        def _(dve):
            for g in range(GROUPS):
                dve.wait_ge(added_ready, g + 1)
                xg = k.X[:, g * GT:(g + 1) * GT, :]
                nc.vector.tensor_tensor(xg, xg, added[g % 4][:], ALU.add).then_inc(added_free, 1)


def l3_ffn(nc, k, name):
    layer_norm(nc, k, name + "_ln", k.bufs["L3_ffn_router"], 8)
    softmax8(nc, k, name + "_gate", True, k.bufs["L3_ffn_rb"])
    expert_bias(nc, k, name + "_bias")
    silu_experts(nc, k, name + "_ffn")


def claim_by_capacity(nc, k, name):
    cap = TOKENS // 8
    with Scope(nc, name) as s:
        before, carry, weight = s.sb("before", [P, P]), s.sb("carry", [P, 8 * TILES]), s.sb("weight", [P, 8, TILES])
        p = s.sb("p", [P, 8, TILES])
        floor, cand, bits = s.sb("floor", [P, 8], U32), s.sb("cand", [P, 3, 8], U32), s.sb("bits", [P, 3, 8], U32)
        take, reach, counts = s.sb("take", [P, 3, 8], U32), s.sb("reach", [P, 3, 8, TILES]), s.sb("counts", [P, 3, 8])
        cmp, tie = s.sb("cmp", [P, 8, TILES]), s.sb("tie", [P, 8, TILES])
        rank, claim, q = s.sb("rank", [P, 8, TILES]), s.sb("claim", [P, 8, TILES]), s.sb("q", [P, 8, TILES])
        some, count, room = s.sb("some", [P, TILES]), s.sb("count", [P, 8]), s.sb("room", [P, 8])
        totals, total = s.ps("totals", [P, 3, 8]), s.ps("total", [P, 8])
        ties_before, ties_tile = s.ps("ties_before", [P, 8 * TILES]), s.ps("ties_tile", [P, 8 * TILES])
        loaded, counted, totalled = s.sem("loaded"), s.sem("counted"), s.sem("totalled")
        tied, ranked = s.sem("tied"), s.sem("ranked")
        block = s.block()
        BITS = 30

        def over_tiles(ap):
            return ap.rearrange("p (e a) -> p e a", a=1).to_broadcast([P, 8, TILES])

        def over_experts(ap):
            return ap.rearrange("p (a t) -> p a t", a=1).to_broadcast([P, 8, TILES])

        def by_token(ap):
            return ap.rearrange("p e t -> p t e")

        @block.sync
        def _(sp):
            sp.dma_start(before[:], k.dram["c_before"]).then_inc(loaded, 16)
            sp.dma_start(carry[:], k.dram["c_not_first_tile"]).then_inc(loaded, 16)
            sp.dma_start(weight[:].rearrange("p e t -> p (e t)"), k.dram["c_early_first"]).then_inc(loaded, 16)

        @block.vector
        def _(dve):
            nc.vector.tensor_copy(by_token(p[:]), k.GATE[:])
            nc.vector.memset(floor[:], 0)
            for j in range(3):
                nc.vector.memset(bits[:, j, :], (j + 1) << (BITS - 2))
            dve.drain()
            p3 = p[:].rearrange("p (a e) t -> p a e t", a=1).to_broadcast([P, 3, 8, TILES])
            with dve.Fori(0, BITS // 2) as b:
                nc.vector.tensor_tensor(cand[:], floor[:].rearrange("p (a e) -> p a e", a=1).to_broadcast([P, 3, 8]), bits[:], ALU.bitwise_or)
                dve.drain()
                nc.vector.tensor_tensor(reach[:], p3, cand[:].bitcast(F32).rearrange("p j (e a) -> p j e a", a=1).to_broadcast([P, 3, 8, TILES]), ALU.is_ge)
                nc.vector.tensor_scalar(bits[:], bits[:], 2, None, ALU.logical_shift_right)
                dve.drain()
                nc.vector.tensor_reduce(counts[:], reach[:], AX.X, ALU.add).then_inc(counted, 1)
                dve.wait_ge(totalled, b + 1)
                nc.vector.tensor_scalar(take[:], totals[:], float(cap), None, ALU.is_ge)
                dve.drain()
                for j in range(3):
                    nc.vector.copy_predicated(floor[:], take[:, j, :], cand[:, j, :])
                    dve.drain()
            nc.vector.tensor_tensor(claim[:], p[:], over_tiles(floor[:].bitcast(F32)), ALU.is_gt)
            nc.vector.tensor_tensor(tie[:], p[:], over_tiles(floor[:].bitcast(F32)), ALU.is_equal)
            dve.drain()
            nc.vector.tensor_reduce(count[:], claim[:], AX.X, ALU.add).then_inc(tied, 1)
            dve.wait_ge(loaded, 48)
            dve.wait_ge(ranked, 1)
            nc.vector.tensor_scalar(room[:], total[:], -1.0, float(cap), ALU.mult, ALU.add)
            nc.vector.tensor_tensor_scan(rank[:].rearrange("p e t -> p (e t)"), carry[:], ties_tile[:], 0.0, ALU.mult, ALU.add)
            dve.drain()
            nc.vector.tensor_tensor(rank[:].rearrange("p e t -> p (e t)"), rank[:].rearrange("p e t -> p (e t)"), ties_tile[:], ALU.subtract)
            dve.drain()
            nc.vector.tensor_tensor(rank[:].rearrange("p e t -> p (e t)"), rank[:].rearrange("p e t -> p (e t)"), ties_before[:], ALU.add)
            dve.drain()
            nc.vector.tensor_tensor(cmp[:], rank[:], over_tiles(room[:]), ALU.is_lt)
            dve.drain()
            nc.vector.tensor_tensor(cmp[:], cmp[:], tie[:], ALU.mult)
            dve.drain()
            nc.vector.tensor_tensor(claim[:], claim[:], cmp[:], ALU.add)
            dve.drain()
            nc.vector.tensor_reduce(some[:], by_token(claim[:]), AX.X, ALU.max)
            dve.drain()
            nc.vector.tensor_scalar(some[:], some[:], -1.0, 1.0, ALU.mult, ALU.add)
            dve.drain()
            nc.vector.tensor_tensor(claim[:], claim[:], over_experts(some[:]), ALU.max)
            dve.drain()
            nc.vector.tensor_tensor(q[:], p[:], claim[:], ALU.mult)
            dve.drain()
            nc.vector.scalar_tensor_tensor(out=q[:].rearrange("p e t -> p (e t)"), in0=claim[:].rearrange("p e t -> p (e t)"),
                                           scalar=-1.0, in1=q[:].rearrange("p e t -> p (e t)"), op0=ALU.add, op1=ALU.add)
            dve.drain()
            nc.vector.tensor_reduce(some[:], by_token(q[:]), AX.X, ALU.max)
            dve.drain()
            nc.vector.tensor_tensor(cmp[:], q[:], over_experts(some[:]), ALU.is_equal)
            dve.drain()
            nc.vector.tensor_tensor(cmp[:], cmp[:], weight[:], ALU.mult)
            dve.drain()
            nc.vector.tensor_reduce(some[:], by_token(cmp[:]), AX.X, ALU.max)
            dve.drain()
            nc.vector.tensor_tensor(cmp[:], cmp[:], over_experts(some[:]), ALU.is_equal)
            dve.drain()
            nc.vector.tensor_tensor(k.GATE[:], by_token(cmp[:]), by_token(p[:]), ALU.mult)

        @block.tensor
        def _(pe):
            with pe.Fori(0, BITS // 2) as b:
                pe.wait_ge(counted, b + 1)
                nc.tensor.matmul(totals[:], k.ones[:], counts[:], start=True, stop=True).then_inc(totalled, 1)
            pe.wait_ge(tied, 1)
            pe.wait_ge(loaded, 48)
            ties = tie[:].rearrange("p e t -> p (e t)")
            nc.tensor.matmul(total[:], k.ones[:], count[:], start=True, stop=True)
            nc.tensor.matmul(ties_before[:], before[:], ties, start=True, stop=True)
            nc.tensor.matmul(ties_tile[:], k.ones[:], ties, start=True, stop=True).then_inc(ranked, 1)


def l1_ffn(nc, k, name):
    layer_norm(nc, k, name + "_ln", k.bufs["L1_ffn_router"], 8)
    softmax8(nc, k, name + "_probs", None)
    claim_by_capacity(nc, k, name + "_claim")
    gelu_experts(nc, k, name + "_ffn", k.up, k.down, 2)


def group_norm_rows(nc, dve, rows_ps, stats, mv):
    for t in range(stats.shape[1]):
        nc.vector.bn_stats(stats[:, t, :], rows_ps[:, t, :])
    dve.drain()
    for t in range(stats.shape[1]):
        nc.vector.bn_aggr(mv[:, t, :], stats[:, t, :])
    dve.drain()


def per_row(ap, n):
    return ap.rearrange("p (m a) -> p m a", a=1).to_broadcast([P, ap.shape[1], n])


def l0_attn_a(nc, k, name):
    BPG = 1
    with Scope(nc, name) as s:
        names = [("L0a_wqkv", [P, 3 * D]), ("L0a_bqkv", [P, 3 * D]), ("L0a_w1", [P, D]), ("L0a_b1", [P, 1]), ("L0a_w2", [P, 512]), ("L0a_b2", [P, 4]),
                 ("L0a_w3", [P, 512]), ("L0a_b3", [1, SEQ])]
        w = {n: s.sb(n, shape) for n, shape in names}
        loaded = s.sem("loaded")
        layer_norm(nc, k, name + "_ln", loads=[(w[n][:], k.dram[n], loaded) for n, _ in names])
        xg, qkv = s.two("xg", [P, SEQ]), s.two("qkv", [P, TPB, 3 * D])
        sq, norm = s.two("sq", [P, TPB, 2 * D]), s.two("norm", [P, TPB * 2])
        qk = s.two("qk", [P, 2, SEQ])
        e = s.two("e", [P, BPG, TPB, SEQ])
        rden, o, h1, h2 = s.two("rden", [P, SEQ]), s.two("o", [P, SEQ]), s.two("h1", [P, SEQ]), s.two("h2", [P, 4, SEQ])
        proj = s.two_ps("proj", [P, TPB, 512])
        qkt_ps = [b[:, 0, :].rearrange("p (i q) -> p i q", i=2) for b in proj]
        s_ps = [b[:, 1:2, :] for b in proj]
        h2_ps = [b[:].rearrange("p j (i q) -> p (j i) q", i=2) for b in proj]
        mid, late = s.ps("mid", [P, 2, 2, SEQ]), s.ps("late", [P, 2, 2, SEQ])
        den_ps, o_ps = ([mid[:, m, j, :] for m in range(2)] for j in range(2))
        y_ps = [late[:, m, 0, :].rearrange("p (t d) -> p t d", d=D) for m in range(2)]
        h1_ps = [late[:, m, 1, :] for m in range(2)]

        xg_ready, projected, squared = s.sem("xg_ready"), s.sem("projected"), s.sem("squared")
        rooted, unit, turned, qk_ready = s.sem("rooted"), s.sem("unit"), s.sem("turned"), s.sem("qk_ready")
        scored, exped, summed, mixed = s.sem("scored"), s.sem("exped"), s.sem("summed"), s.sem("mixed")
        h1_up, h1_ready, h2_up, h2_ready = s.sem("h1_up"), s.sem("h1_ready"), s.sem("h2_up"), s.sem("h2_ready")
        y_ready = s.sem("y_ready")
        block = s.block()

        @block.tensor
        def _(pe):
            pe.wait_ge(loaded, 16 * len(names))
            with pe.Fori(0, BATCH // 2) as pair:
                for m in range(2):
                    u = pair * 2 + m
                    pe.wait_ge(xg_ready, u + 1)
                    for t in range(TPB):
                        last = nc.tensor.matmul(proj[m][:, t, 0:3 * D], xg[m][:, t * P:(t + 1) * P], w["L0a_wqkv"][:], start=True, stop=True)
                    last.then_inc(projected, 1)
                for m in range(2):
                    u = pair * 2 + m
                    pe.wait_ge(unit, u + 1)
                    for i in range(2):
                        for t in range(TPB):
                            last = nc.tensor.transpose(qkt_ps[m][:, i, t * P:(t + 1) * P], qkv[m][:, t, i * D:(i + 1) * D], k.ident[:])
                    last.then_inc(turned, 1)
                for m in range(2):
                    u = pair * 2 + m
                    pe.wait_ge(qk_ready, u + 1)
                    for b in range(BPG):
                        for kt in range(TPB):
                            c = b * SEQ + kt * P
                            last = nc.tensor.matmul(s_ps[m][:, b, kt * SEQ:(kt + 1) * SEQ], qk[m][:, 1, c:c + P],
                                                    qk[m][:, 0, b * SEQ:(b + 1) * SEQ], start=True, stop=True)
                        last.then_inc(scored, 1)
                    for b in range(BPG):
                        pe.wait_ge(exped, u * BPG + (b + 1))
                        for kt in range(TPB):
                            nc.tensor.matmul(den_ps[m][:, b * SEQ:(b + 1) * SEQ], k.ones[:], e[m][:, b, kt, :],
                                             start=(kt == 0), stop=(kt == TPB - 1))
                        for kt in range(TPB):
                            last = nc.tensor.matmul(o_ps[m][:, b * SEQ:(b + 1) * SEQ], qkv[m][:, b * TPB + kt, 2 * D:3 * D], e[m][:, b, kt, :],
                                                    start=(kt == 0), stop=(kt == TPB - 1))
                    last.then_inc(summed, 1)
                for m in range(2):
                    u = pair * 2 + m
                    pe.wait_ge(mixed, u + 1)
                    nc.tensor.matmul(h1_ps[m][:], w["L0a_w1"][:], o[m][:], start=True, stop=True).then_inc(h1_up, 1)
                for m in range(2):
                    u = pair * 2 + m
                    pe.wait_ge(h1_ready, u + 1)
                    for j in range(4):
                        last = nc.tensor.matmul(h2_ps[m][:, j, :], w["L0a_w2"][:, j * P:(j + 1) * P], h1[m][:], start=True, stop=True)
                        if j % 2 == 1:
                            last.then_inc(h2_up, 1)
                    nc.tensor.matmul(y_ps[m][:], k.ones_row[0:1, 0:P], w["L0a_b3"][:], start=True, stop=False, skip_group_check=True)
                    for j in range(4):
                        pe.wait_ge(h2_ready, u * 4 + (j + 1))
                        for t in range(TPB):
                            last = nc.tensor.matmul(y_ps[m][:, t, :], h2[m][:, j, t * P:(t + 1) * P], w["L0a_w3"][:, j * D:(j + 1) * D],
                                                    start=False, stop=(j == 3), skip_group_check=True)
                    last.then_inc(y_ready, 1)

        @block.scalar
        def _(act):
            act.wait_ge(loaded, 16 * len(names))
            with act.Fori(0, BATCH // 2) as pair:
                for m in range(2):
                    u = pair * 2 + m
                    nc.scalar.copy(xg[m][:], k.XNT[:, bass.ds(u * SEQ, SEQ)]).then_inc(xg_ready, 1)
                for m in range(2):
                    u = pair * 2 + m
                    act.wait_ge(squared, u + 1)
                    nc.scalar.activation(norm[m][:], norm[m][:], ACT.Sqrt).then_inc(rooted, 1)
                for m in range(2):
                    u = pair * 2 + m
                    act.wait_ge(turned, u + 1)
                    nc.scalar.copy(qk[m][:], qkt_ps[m]).then_inc(qk_ready, 1)
                    for b in range(BPG):
                        act.wait_ge(scored, u * BPG + (b + 1))
                        nc.scalar.activation(e[m][:, b, :, :], s_ps[m][:, b, :], ACT.Exp).then_inc(exped, 1)
                for m in range(2):
                    u = pair * 2 + m
                    act.wait_ge(h1_up, u + 1)
                    nc.scalar.activation(h1[m][:], h1_ps[m][:], ACT.Relu, bias=w["L0a_b1"][:]).then_inc(h1_ready, 1)
                    for j in range(4):
                        if j % 2 == 0:
                            act.wait_ge(h2_up, u * 2 + (j // 2 + 1))
                        nc.scalar.activation(h2[m][:, j, :], h2_ps[m][:, j, :], ACT.Relu, bias=w["L0a_b2"][:, j:j + 1]).then_inc(h2_ready, 1)

        @block.vector
        def _(dve):
            dve.wait_ge(loaded, 16 * len(names))
            with dve.Fori(0, BATCH // 2) as pair:
                for m in range(2):
                    u = pair * 2 + m
                    dve.wait_ge(projected, u + 1)
                    nc.vector.tensor_tensor(qkv[m][:], proj[m][:, :, 0:3 * D],
                                            w["L0a_bqkv"][:].rearrange("p (a n) -> p a n", a=1).to_broadcast([P, TPB, 3 * D]), ALU.add)
                    dve.drain()
                    nc.vector.tensor_tensor(sq[m][:], qkv[m][:, :, 0:2 * D], qkv[m][:, :, 0:2 * D], ALU.mult)
                    dve.drain()
                    nc.vector.tensor_reduce(norm[m][:], sq[m][:].rearrange("p t (i d) -> p (t i) d", d=D), AX.X, ALU.add).then_inc(squared, 1)
                for m in range(2):
                    u = pair * 2 + m
                    dve.wait_ge(rooted, u + 1)
                    nc.vector.tensor_scalar(norm[m][:], norm[m][:], 1e-12, None, ALU.max)
                    dve.drain()
                    nc.vector.reciprocal(norm[m][:], norm[m][:])
                    dve.drain()
                    for t in range(TPB):
                        rows = qkv[m][:, t, 0:2 * D].rearrange("p (i d) -> p i d", d=D)
                        last = nc.vector.tensor_tensor(rows, rows, per_row(norm[m][:, 2 * t:2 * t + 2], D), ALU.mult)
                    last.then_inc(unit, 1)
                for m in range(2):
                    u = pair * 2 + m
                    dve.wait_ge(summed, u + 1)
                    nc.vector.reciprocal(rden[m][:], den_ps[m][:])
                    dve.drain()
                    nc.vector.tensor_tensor(o[m][:], o_ps[m][:], rden[m][:], ALU.mult).then_inc(mixed, 1)
                for m in range(2):
                    u = pair * 2 + m
                    dve.wait_ge(y_ready, u + 1)
                    x = k.X[:, bass.ds(u * TPB, TPB), :]
                    nc.vector.tensor_tensor(x, x, y_ps[m][:], ALU.add)


def l0_attn_b(nc, k, name):
    QK = 3 * D
    HD = 8
    BPG = 1
    with Scope(nc, name) as s:
        names = [("L0b_w", [P, 5 * D]), ("L0b_b", [P, 5 * D]), ("L0b_wo", [P, D]), ("L0b_bo", [1, SEQ]),
                 ("L0b_g", [P, 1]), ("L0b_be", [P, 1]), ("c_heads8", [P, P])]
        w = {n: s.sb(n, shape) for n, shape in names}
        loaded = s.sem("loaded")
        layer_norm(nc, k, name + "_ln", loads=[(w[n][:], k.dram[n], loaded) for n, _ in names])
        xg, z = s.two("xg", [P, SEQ]), s.two("z", [P, TPB, 5 * D])
        a, sq = s.two("a", [P, TPB, QK]), s.two("sq", [P, TPB, QK])
        norm = s.two("norm", [P, TPB * QK // HD])
        minus = s.sb("minus", [P, TPB])
        qt, state, half_state = s.two("qt", [P, SEQ]), s.two("state", [P, BPG, P]), s.two("half_state", [P, BPG, P])
        stats, mv, rstd = s.two("stats", [P, TPB, 6]), s.two("mv", [P, TPB, 2]), s.two("rstd", [P, TPB])
        on, ont = s.two("on", [P, TPB, D]), s.two("ont", [P, SEQ])
        proj = s.two_ps("proj", [P, TPB, 4 * D])
        mid, late = s.ps("mid", [P, 2, 2, SEQ]), s.ps("late", [P, 2, 2, SEQ])
        proj_v = [mid[:, m, 0, :].rearrange("p (t d) -> p t d", d=D) for m in range(2)]
        st_ps = [mid[:, m, 1:2, :].rearrange("p b (i d) -> p b i d", i=2) for m in range(2)]
        turned = [late[:, m, 0, :] for m in range(2)]
        o_ps = [late[:, m, 1, :].rearrange("p (t d) -> p t d", d=D) for m in range(2)]
        w_ready, xg_ready, projected = s.sem("w_ready"), s.sem("xg_ready"), s.sem("projected")
        biased, activated, squared, rooted, unit = s.sem("biased"), s.sem("activated"), s.sem("squared"), s.sem("rooted"), s.sem("unit")
        turned_q, qt_ready, stated, state_ready = s.sem("turned_q"), s.sem("qt_ready"), s.sem("stated"), s.sem("state_ready")
        o_ready, var_ready, rstd_ready, on_ready = s.sem("o_ready"), s.sem("var_ready"), s.sem("rstd_ready"), s.sem("on_ready")
        turned_o, ont_ready, y_ready, done = s.sem("turned_o"), s.sem("ont_ready"), s.sem("y_ready"), s.sem("done")
        block = s.block()

        @block.gpsimd
        def _(pool):
            nc.gpsimd.memset(minus[:], -0.5)
            pool.drain()
            with pool.Fori(0, BATCH // 2) as pair:
                for m in range(2):
                    u = pair * 2 + m
                    pool.wait_ge(var_ready, u + 1)
                    nc.gpsimd.tensor_tensor(rstd[m][:], rstd[m][:], minus[:], ALU.pow).then_inc(rstd_ready, 1)

        @block.tensor
        def _(pe):
            pe.wait_ge(w_ready, 1)
            with pe.Fori(0, BATCH // 2) as pair:
                for m in range(2):
                    u = pair * 2 + m
                    pe.wait_ge(xg_ready, u + 1)
                    pe.wait_ge(done, u + 1)
                    for t in range(TPB):
                        xt = xg[m][:, t * P:(t + 1) * P]
                        nc.tensor.matmul(proj[m][:, t, :], xt, w["L0b_w"][:, 0:4 * D], start=True, stop=True)
                        last = nc.tensor.matmul(proj_v[m][:, t, :], xt, w["L0b_w"][:, 4 * D:5 * D], start=True, stop=True)
                    last.then_inc(projected, 1)
                for m in range(2):
                    u = pair * 2 + m
                    pe.wait_ge(unit, u + 1)
                    for t in range(TPB):
                        last = nc.tensor.transpose(turned[m][:, t * P:(t + 1) * P], a[m][:, t, 0:D], k.ident[:])
                    last.then_inc(turned_q, 1)
                    for b in range(BPG):
                        for i in range(2):
                            for t in range(TPB):
                                last = nc.tensor.matmul(st_ps[m][:, b, i, :], a[m][:, b * TPB + t, (1 + i) * D:(2 + i) * D],
                                                        z[m][:, b * TPB + t, (3 + i) * D:(4 + i) * D], start=(t == 0), stop=(t == TPB - 1))
                    last.then_inc(stated, 1)
                for m in range(2):
                    u = pair * 2 + m
                    pe.wait_ge(state_ready, u + 1)
                    pe.wait_ge(qt_ready, u + 1)
                    for t in range(TPB):
                        last = nc.tensor.matmul(o_ps[m][:, t, :], qt[m][:, t * P:(t + 1) * P], state[m][:, t // TPB, :], start=True, stop=True)
                    last.then_inc(o_ready, 1)
                for m in range(2):
                    u = pair * 2 + m
                    pe.wait_ge(on_ready, u + 1)
                    for t in range(TPB):
                        last = nc.tensor.transpose(turned[m][:, t * P:(t + 1) * P], on[m][:, t, :], k.ident[:])
                    last.then_inc(turned_o, 1)
                    nc.tensor.matmul(proj_v[m][:], k.ones_row[0:1, 0:P], w["L0b_bo"][:], start=True, stop=False, skip_group_check=True)
                for m in range(2):
                    u = pair * 2 + m
                    pe.wait_ge(ont_ready, u + 1)
                    for t in range(TPB):
                        last = nc.tensor.matmul(proj_v[m][:, t, :], ont[m][:, t * P:(t + 1) * P], w["L0b_wo"][:], start=False, stop=True,
                                                skip_group_check=True)
                    last.then_inc(y_ready, 1)

        @block.scalar
        def _(act):
            act.wait_ge(loaded, 16 * len(names))
            act.sem_inc(done, 2)
            with act.Fori(0, BATCH // 2) as pair:
                for m in range(2):
                    u = pair * 2 + m
                    nc.scalar.copy(xg[m][:], k.XNT[:, bass.ds(u * SEQ, SEQ)]).then_inc(xg_ready, 1)
                for m in range(2):
                    u = pair * 2 + m
                    act.wait_ge(biased, u + 1)
                    nc.scalar.activation(a[m][:], z[m][:, :, 0:QK], ACT.Silu).then_inc(activated, 1)
                for m in range(2):
                    u = pair * 2 + m
                    act.wait_ge(squared, u + 1)
                    nc.scalar.activation(norm[m][:], norm[m][:], ACT.Sqrt).then_inc(rooted, 1)
                for m in range(2):
                    u = pair * 2 + m
                    act.wait_ge(turned_q, u + 1)
                    nc.scalar.copy(qt[m][:], turned[m][:]).then_inc(qt_ready, 1)
                for m in range(2):
                    u = pair * 2 + m
                    act.wait_ge(turned_o, u + 1)
                    nc.scalar.activation(ont[m][:], turned[m][:], ACT.Identity, bias=w["L0b_be"][:], scale=w["L0b_g"][:]).then_inc(ont_ready, 1)

        @block.vector
        def _(dve):
            dve.wait_ge(loaded, 16 * len(names))
            for i in range(5):
                last = nc.vector.tensor_tensor(w["L0b_w"][:, i * D:(i + 1) * D], w["L0b_w"][:, i * D:(i + 1) * D], k.ident[:], ALU.add)
            last.then_inc(w_ready, 1)
            with dve.Fori(0, BATCH // 2) as pair:
                for m in range(2):
                    u = pair * 2 + m
                    dve.wait_ge(projected, u + 1)
                    for t in range(TPB):
                        nc.vector.tensor_tensor(z[m][:, t, 0:4 * D], proj[m][:, t, :], w["L0b_b"][:, 0:4 * D], ALU.add)
                    nc.vector.tensor_tensor(z[m][:, :, 4 * D:5 * D], proj_v[m][:],
                                            w["L0b_b"][:, 4 * D:5 * D].rearrange("p (a d) -> p a d", a=1).to_broadcast([P, TPB, D]),
                                            ALU.add).then_inc(biased, 1)
                for m in range(2):
                    u = pair * 2 + m
                    dve.wait_ge(activated, u + 1)
                    nc.vector.tensor_scalar(a[m][:], a[m][:], 0.5, None, ALU.add)
                    dve.drain()
                    nc.vector.tensor_tensor(sq[m][:], a[m][:], a[m][:], ALU.mult)
                    dve.drain()
                    nc.vector.tensor_reduce(norm[m][:], sq[m][:].rearrange("p t (h d) -> p (t h) d", d=HD), AX.X, ALU.add).then_inc(squared, 1)
                for m in range(2):
                    u = pair * 2 + m
                    dve.wait_ge(rooted, u + 1)
                    nc.vector.tensor_scalar(norm[m][:], norm[m][:], 1e-6, None, ALU.add)
                    dve.drain()
                    nc.vector.reciprocal(norm[m][:], norm[m][:])
                    dve.drain()
                    heads = a[m][:].rearrange("p t (h d) -> p (t h) d", d=HD)
                    nc.vector.tensor_tensor(heads, heads, per_row(norm[m][:], HD), ALU.mult).then_inc(unit, 1)
                for m in range(2):
                    u = pair * 2 + m
                    dve.wait_ge(stated, u + 1)
                    for b in range(BPG):
                        nc.vector.scalar_tensor_tensor(out=half_state[m][:, b, :], in0=st_ps[m][:, b, 0, :], scalar=1.0 / SEQ ** 2,
                                                       in1=w["c_heads8"][:], op0=ALU.mult, op1=ALU.mult)
                    dve.drain()
                    for b in range(BPG):
                        last = nc.vector.tensor_tensor(state[m][:, b, :], half_state[m][:, b, :], st_ps[m][:, b, 1, :], ALU.mult)
                    last.then_inc(state_ready, 1)
                for m in range(2):
                    u = pair * 2 + m
                    dve.wait_ge(o_ready, u + 1)
                    group_norm_rows(nc, dve, o_ps[m], stats[m], mv[m])
                    nc.vector.tensor_scalar(rstd[m][:], mv[m][:, :, 1], 1e-5, None, ALU.add).then_inc(var_ready, 1)
                for m in range(2):
                    u = pair * 2 + m
                    dve.wait_ge(rstd_ready, u + 1)
                    for t in range(TPB):
                        last = nc.vector.tensor_scalar(on[m][:, t, :], o_ps[m][:, t, :], mv[m][:, t, 0:1], rstd[m][:, t:t + 1], ALU.subtract, ALU.mult)
                    last.then_inc(on_ready, 1)
                for m in range(2):
                    u = pair * 2 + m
                    dve.wait_ge(y_ready, u + 1)
                    x = k.X[:, bass.ds(u * TPB, TPB), :]
                    nc.vector.tensor_tensor(x, x, proj_v[m][:], ALU.add).then_inc(done, 1)


def l3_attn_b(nc, k, name):
    HD, CH = 8, 4
    BPG = 1
    with Scope(nc, name) as s:
        names = [("L3b_w", [P, 3 * D]), ("L3b_b", [P, 3 * D]), ("L3b_wo", [P, D]), ("L3b_bo", [1, SEQ]),
                 ("L3b_g1", [P, 1]), ("L3b_be1", [P, 1]), ("L3b_g2", [P, D]), ("L3b_be2", [P, D]),
                 ("L3b_w1", [P, CH * P]), ("L3b_b1", [P, CH]), ("L3b_w2", [P, CH * D]), ("L3b_b2", [1, SEQ]),
                 ("c_heads8", [P, P])]
        w = {n: s.sb(n, shape) for n, shape in names}
        loaded = s.sem("loaded")
        layer_norm(nc, k, name + "_ln", loads=[(w[n][:], k.dram[n], loaded) for n, _ in names])
        xg, z = s.two("xg", [P, SEQ]), s.two("z", [P, TPB, 3 * D])
        low, sq = s.two("low", [P, TPB, 2 * D]), s.two("sq", [P, TPB, 2 * D])
        norm, minus = s.two("norm", [P, TPB * 2 * D // HD]), s.sb("minus", [P, TPB])
        qt, state, ctxt = s.two("qt", [P, SEQ]), s.two("state", [P, BPG, P]), s.two("ctxt", [P, SEQ])
        stats, mv, rstd = s.two("stats", [P, TPB, 6]), s.two("mv", [P, TPB, 2]), s.two("rstd", [P, TPB])
        rows, at, hid = s.two("rows", [P, TPB, D]), s.two("at", [P, SEQ]), s.two("hid", [P, CH, SEQ])
        proj = s.two_ps("proj", [P, TPB, 512])
        hid_ps = [b[:].rearrange("p j (i q) -> p (j i) q", i=2) for b in proj]
        mid, late = s.ps("mid", [P, 2, 2, SEQ]), s.ps("late", [P, 2, 2, SEQ])
        st_ps = [mid[:, m, 0:1, 0:P] for m in range(2)]
        ctx_ps = [mid[:, m, 1, :] for m in range(2)]
        turned = [late[:, m, 0, :] for m in range(2)]
        y_ps = [late[:, m, 1, :].rearrange("p (t d) -> p t d", d=D) for m in range(2)]
        xg_ready, projected, clipped = s.sem("xg_ready"), s.sem("projected"), s.sem("clipped")
        exped, squared, rooted, unit = s.sem("exped"), s.sem("squared"), s.sem("rooted"), s.sem("unit")
        turned_q, qt_ready, stated, state_ready = s.sem("turned_q"), s.sem("qt_ready"), s.sem("stated"), s.sem("state_ready")
        ctx_up, ctx_ready, y1_ready = s.sem("ctx_up"), s.sem("ctx_ready"), s.sem("y1_ready")
        var_ready, rstd_ready = ([s.sem(f"{n}_ready{i}") for i in range(2)] for n in ("var", "rstd"))
        rows_ready, turned_a, at_ready = s.sem("rows_ready"), s.sem("turned_a"), s.sem("at_ready")
        hid_up, hid_ready, y2_ready = s.sem("hid_up"), s.sem("hid_ready"), s.sem("y2_ready")
        block = s.block()

        @block.gpsimd
        def _(pool):
            nc.gpsimd.memset(minus[:], -0.5)
            pool.drain()
            with pool.Fori(0, BATCH // 2) as pair:
                for m in range(2):
                    u = pair * 2 + m
                    pool.wait_ge(var_ready[0], u + 1)
                    nc.gpsimd.tensor_tensor(rstd[m][:], rstd[m][:], minus[:], ALU.pow).then_inc(rstd_ready[0], 1)
                for m in range(2):
                    u = pair * 2 + m
                    pool.wait_ge(var_ready[1], u + 1)
                    nc.gpsimd.tensor_tensor(rstd[m][:], rstd[m][:], minus[:], ALU.pow).then_inc(rstd_ready[1], 1)

        @block.tensor
        def _(pe):
            pe.wait_ge(loaded, 16 * len(names))
            with pe.Fori(0, BATCH // 2) as pair:
                for m in range(2):
                    u = pair * 2 + m
                    pe.wait_ge(xg_ready, u + 1)
                    for t in range(TPB):
                        last = nc.tensor.matmul(proj[m][:, t, 0:3 * D], xg[m][:, t * P:(t + 1) * P], w["L3b_w"][:], start=True, stop=True)
                    last.then_inc(projected, 1)
                for m in range(2):
                    u = pair * 2 + m
                    pe.wait_ge(unit, u + 1)
                    for t in range(TPB):
                        last = nc.tensor.transpose(turned[m][:, t * P:(t + 1) * P], low[m][:, t, 0:D], k.ident[:])
                    last.then_inc(turned_q, 1)
                    for b in range(BPG):
                        for t in range(TPB):
                            r = b * TPB + t
                            last = nc.tensor.matmul(st_ps[m][:, b, :], low[m][:, r, D:2 * D], z[m][:, r, 2 * D:3 * D], start=(t == 0), stop=(t == TPB - 1))
                    last.then_inc(stated, 1)
                for m in range(2):
                    u = pair * 2 + m
                    pe.wait_ge(state_ready, u + 1)
                    pe.wait_ge(qt_ready, u + 1)
                    for b in range(BPG):
                        last = nc.tensor.matmul(ctx_ps[m][:, b * SEQ:(b + 1) * SEQ], state[m][:, b, :], qt[m][:, b * SEQ:(b + 1) * SEQ], start=True, stop=True)
                    last.then_inc(ctx_up, 1)
                    nc.tensor.matmul(y_ps[m][:], k.ones_row[0:1, 0:P], w["L3b_bo"][:], start=True, stop=False, skip_group_check=True)
                    for t in range(TPB):
                        nc.tensor.matmul(y_ps[m][:, t, :], xg[m][:, t * P:(t + 1) * P], k.ident[:], start=False, stop=False, skip_group_check=True)
                for m in range(2):
                    u = pair * 2 + m
                    pe.wait_ge(ctx_ready, u + 1)
                    for t in range(TPB):
                        last = nc.tensor.matmul(y_ps[m][:, t, :], ctxt[m][:, t * P:(t + 1) * P], w["L3b_wo"][:], start=False, stop=True,
                                                skip_group_check=True)
                    last.then_inc(y1_ready, 1)
                for m in range(2):
                    u = pair * 2 + m
                    pe.wait_ge(rows_ready, u + 1)
                    for t in range(TPB):
                        last = nc.tensor.transpose(turned[m][:, t * P:(t + 1) * P], rows[m][:, t, :], k.ident[:])
                    last.then_inc(turned_a, 1)
                for m in range(2):
                    u = pair * 2 + m
                    pe.wait_ge(at_ready, u + 1)
                    for j in range(CH):
                        last = nc.tensor.matmul(hid_ps[m][:, j, :], w["L3b_w1"][:, j * P:(j + 1) * P], at[m][:], start=True, stop=True)
                        if j % 2 == 1:
                            last.then_inc(hid_up, 1)
                    nc.tensor.matmul(y_ps[m][:], k.ones_row[0:1, 0:P], w["L3b_b2"][:], start=True, stop=False, skip_group_check=True)
                    for t in range(TPB):
                        nc.tensor.matmul(y_ps[m][:, t, :], at[m][:, t * P:(t + 1) * P], k.ident[:], start=False, stop=False, skip_group_check=True)
                    for j in range(CH):
                        pe.wait_ge(hid_ready, u * CH + (j + 1))
                        for t in range(TPB):
                            last = nc.tensor.matmul(y_ps[m][:, t, :], hid[m][:, j, t * P:(t + 1) * P], w["L3b_w2"][:, j * D:(j + 1) * D],
                                                    start=False, stop=(j == CH - 1), skip_group_check=True)
                    last.then_inc(y2_ready, 1)

        @block.scalar
        def _(act):
            act.wait_ge(loaded, 16 * len(names))
            with act.Fori(0, BATCH // 2) as pair:
                for m in range(2):
                    u = pair * 2 + m
                    nc.scalar.copy(xg[m][:], k.XNT[:, bass.ds(u * SEQ, SEQ)]).then_inc(xg_ready, 1)
                for m in range(2):
                    u = pair * 2 + m
                    act.wait_ge(clipped, u + 1)
                    nc.scalar.activation(low[m][:], low[m][:], ACT.Exp).then_inc(exped, 1)
                for m in range(2):
                    u = pair * 2 + m
                    act.wait_ge(squared, u + 1)
                    nc.scalar.activation(norm[m][:], norm[m][:], ACT.Sqrt).then_inc(rooted, 1)
                for m in range(2):
                    u = pair * 2 + m
                    act.wait_ge(turned_q, u + 1)
                    nc.scalar.copy(qt[m][:], turned[m][:]).then_inc(qt_ready, 1)
                for m in range(2):
                    u = pair * 2 + m
                    act.wait_ge(ctx_up, u + 1)
                    nc.scalar.copy(ctxt[m][:], ctx_ps[m][:]).then_inc(ctx_ready, 1)
                for m in range(2):
                    u = pair * 2 + m
                    act.wait_ge(turned_a, u + 1)
                    nc.scalar.activation(at[m][:], turned[m][:], ACT.Identity, bias=w["L3b_be1"][:], scale=w["L3b_g1"][:]).then_inc(at_ready, 1)
                    for j in range(CH):
                        if j % 2 == 0:
                            act.wait_ge(hid_up, u * (CH // 2) + (j // 2 + 1))
                        nc.scalar.activation(hid[m][:, j, :], hid_ps[m][:, j, :], ACT.Gelu, bias=w["L3b_b1"][:, j:j + 1]).then_inc(hid_ready, 1)

        @block.vector
        def _(dve):
            def variance(m, i):
                group_norm_rows(nc, dve, y_ps[m], stats[m], mv[m])
                nc.vector.tensor_scalar(rstd[m][:], mv[m][:, :, 1], 1e-12, None, ALU.add).then_inc(var_ready[i], 1)

            def normalise(m):
                for t in range(TPB):
                    last = nc.vector.tensor_scalar(rows[m][:, t, :], y_ps[m][:, t, :], mv[m][:, t, 0:1], rstd[m][:, t:t + 1], ALU.subtract, ALU.mult)
                return last

            def over_tiles(ap):
                return ap.rearrange("p (a n) -> p a n", a=1).to_broadcast([P, TPB, ap.shape[1]])

            dve.wait_ge(loaded, 16 * len(names))
            with dve.Fori(0, BATCH // 2) as pair:
                for m in range(2):
                    u = pair * 2 + m
                    dve.wait_ge(projected, u + 1)
                    nc.vector.tensor_tensor(z[m][:], proj[m][:, :, 0:3 * D], over_tiles(w["L3b_b"][:]), ALU.add)
                    dve.drain()
                    nc.vector.tensor_scalar(low[m][:], z[m][:, :, 0:2 * D], 0.0, None, ALU.min).then_inc(clipped, 1)
                    nc.vector.tensor_scalar(z[m][:, :, 0:2 * D], z[m][:, :, 0:2 * D], 0.0, None, ALU.max)
                    dve.drain()
                for m in range(2):
                    u = pair * 2 + m
                    dve.wait_ge(exped, u + 1)
                    nc.vector.scalar_tensor_tensor(out=low[m][:], in0=low[m][:], scalar=-1.0, in1=z[m][:, :, 0:2 * D], op0=ALU.add, op1=ALU.add)
                    dve.drain()
                    nc.vector.tensor_tensor(sq[m][:], low[m][:], low[m][:], ALU.mult)
                    dve.drain()
                    nc.vector.tensor_reduce(norm[m][:], sq[m][:].rearrange("p t (h d) -> p (t h) d", d=HD), AX.X, ALU.add).then_inc(squared, 1)
                for m in range(2):
                    u = pair * 2 + m
                    dve.wait_ge(rooted, u + 1)
                    nc.vector.reciprocal(norm[m][:], norm[m][:])
                    dve.drain()
                    heads = low[m][:].rearrange("p t (h d) -> p (t h) d", d=HD)
                    nc.vector.tensor_tensor(heads, heads, per_row(norm[m][:], HD), ALU.mult).then_inc(unit, 1)
                for m in range(2):
                    u = pair * 2 + m
                    dve.wait_ge(stated, u + 1)
                    for b in range(BPG):
                        last = nc.vector.scalar_tensor_tensor(out=state[m][:, b, :], in0=st_ps[m][:, b, :], scalar=HD ** -0.5, in1=w["c_heads8"][:],
                                                              op0=ALU.mult, op1=ALU.mult)
                    last.then_inc(state_ready, 1)
                for m in range(2):
                    u = pair * 2 + m
                    dve.wait_ge(y1_ready, u + 1)
                    variance(m, 0)
                for m in range(2):
                    u = pair * 2 + m
                    dve.wait_ge(rstd_ready[0], u + 1)
                    normalise(m).then_inc(rows_ready, 1)
                for m in range(2):
                    u = pair * 2 + m
                    dve.wait_ge(y2_ready, u + 1)
                    variance(m, 1)
                for m in range(2):
                    u = pair * 2 + m
                    dve.wait_ge(rstd_ready[1], u + 1)
                    normalise(m)
                    dve.drain()
                    nc.vector.tensor_tensor(rows[m][:], rows[m][:], over_tiles(w["L3b_g2"][:]), ALU.mult)
                    dve.drain()
                    nc.vector.tensor_tensor(rows[m][:], rows[m][:], over_tiles(w["L3b_be2"][:]), ALU.add)
                    dve.drain()
                    x = k.X[:, bass.ds(u * TPB, TPB), :]
                    nc.vector.tensor_tensor(x, x, rows[m][:], ALU.add)


def l3_attn_a(nc, k, name):
    H, HD, WIN = 16, 8, 32
    WPT, WPG = P // WIN, SEQ // WIN
    HB = P // WIN
    BPG = 1
    with Scope(nc, name) as s:
        names = [("L3a_wq", [P, D]), ("L3a_wk", [P, D]), ("L3a_wv", [P, HB * HD]), ("L3a_wo", [P, D]), ("L3a_bo", [1, SEQ]),
                 ("c_head_of_row8", [P, H]), ("c_blocks32x8", [P, HB * HD])]
        w = {n: s.sb(n, shape) for n, shape in names}
        loaded = s.sem("loaded")
        layer_norm(nc, k, name + "_ln", loads=[(w[n][:], k.dram[n], loaded) for n, _ in names])
        xg, q, kk = s.two("xg", [P, SEQ]), s.two("q", [P, SEQ]), s.two("kk", [P, SEQ])
        xrep = s.two("xrep", [P, WPG, HB, WIN])
        keys, vals = s.two("keys", [P, WPG, H, WIN]), s.two("vals", [P, WPG, HB * HD])
        p, top, den = s.two("p", [P, TPB * H, WIN]), s.two("top", [P, TPB * H]), s.two("den", [P, TPB * H])
        pt, o, ot = s.two("pt", [P, TPB, H // HB, P]), s.two("o", [P, TPB, D]), s.two("ot", [P, SEQ])
        big_a, big_b = s.two_ps("big_a", [P, TPB, 512]), s.two_ps("big_b", [P, TPB, 512])
        k_ps, q_ps = ([b[:, 0, i * SEQ:(i + 1) * SEQ] for b in big_a] for i in range(2))
        v_ps, y_ps = [b[:, 1, 0:SEQ] for b in big_a], [b[:, 0, 0:SEQ] for b in big_b]


        xg_ready, xrep_ready, projected = s.sem("xg_ready"), s.sem("xrep_ready"), s.sem("projected")
        k_ready, qv_ready, keys_ready, scored = s.sem("k_ready"), s.sem("qv_ready"), s.sem("keys_ready"), s.sem("scored")
        shifted, exped, probs_ready, turned = s.sem("shifted"), s.sem("exped"), s.sem("probs_ready"), s.sem("turned")
        pt_ready, o_up, o_ready, turned_o, ot_ready = s.sem("pt_ready"), s.sem("o_up"), s.sem("o_ready"), s.sem("turned_o"), s.sem("ot_ready")
        v_ready, y_ready = s.sem("v_ready"), s.sem("y_ready")
        block = s.block()

        @block.tensor
        def _(pe):
            pe.wait_ge(loaded, 16 * len(names))
            with pe.Fori(0, BATCH // 2) as pair:
                for m in range(2):
                    u = pair * 2 + m
                    pe.wait_ge(xg_ready, u + 1)
                    nc.tensor.matmul(k_ps[m], w["L3a_wk"][:], xg[m][:], start=True, stop=True)
                    nc.tensor.matmul(q_ps[m], w["L3a_wq"][:], xg[m][:], start=True, stop=True)
                for m in range(2):
                    u = pair * 2 + m
                    pe.wait_ge(xrep_ready, u + 1)
                    for n in range(WPG):
                        last = nc.tensor.matmul(v_ps[m][:, n * HB * HD:(n + 1) * HB * HD], xrep[m][:, n, :, :].rearrange("p h u -> p (h u)"),
                                                w["L3a_wv"][:], start=True, stop=True)
                    last.then_inc(projected, 1)
                for m in range(2):
                    u = pair * 2 + m
                    pe.wait_ge(qv_ready, u + 1)
                    pe.wait_ge(v_ready, u + 1)
                    pe.wait_ge(keys_ready, u + 1)
                    for t in range(TPB):
                        for i in range(WPT):
                            n = t * WPT + i
                            last = nc.tensor.matmul(big_a[m][i * WIN:(i + 1) * WIN, t, :], q[m][:, n * WIN:(n + 1) * WIN],
                                                    keys[m][:, n, :, :].rearrange("p h u -> p (h u)"), start=True, stop=True)
                    last.then_inc(scored, 1)
                for m in range(2):
                    u = pair * 2 + m
                    pe.wait_ge(probs_ready, u + 1)
                    for t in range(TPB):
                        for c in range(H // HB):
                            last = nc.tensor.transpose(big_b[m][:, t, c * P:(c + 1) * P],
                                                       p[m][:, t * H + c * HB:t * H + (c + 1) * HB, :].rearrange("p h u -> p (h u)"), k.ident[:])
                    last.then_inc(turned, 1)
                for m in range(2):
                    u = pair * 2 + m
                    pe.wait_ge(pt_ready, u + 1)
                    for t in range(TPB):
                        for c in range(H // HB):
                            for i in range(WPT):
                                last = nc.tensor.matmul(big_a[m][i * WIN:(i + 1) * WIN, 0, t * D + c * HB * HD:t * D + (c + 1) * HB * HD],
                                                        pt[m][:, t, c, i * WIN:(i + 1) * WIN], vals[m][:, t * WPT + i, :], start=True, stop=True)
                    last.then_inc(o_up, 1)
                for m in range(2):
                    u = pair * 2 + m
                    pe.wait_ge(o_ready, u + 1)
                    for t in range(TPB):
                        last = nc.tensor.transpose(big_a[m][:, 1, t * P:(t + 1) * P], o[m][:, t, :], k.ident[:])
                    last.then_inc(turned_o, 1)
                    nc.tensor.matmul(y_ps[m], k.ones_row[0:1, 0:P], w["L3a_bo"][:], start=True, stop=False, skip_group_check=True)
                for m in range(2):
                    u = pair * 2 + m
                    pe.wait_ge(ot_ready, u + 1)
                    for t in range(TPB):
                        last = nc.tensor.matmul(y_ps[m][:, t * D:(t + 1) * D], ot[m][:, t * P:(t + 1) * P], w["L3a_wo"][:], start=False, stop=True,
                                                skip_group_check=True)
                    last.then_inc(y_ready, 1)

        @block.scalar
        def _(act):
            with act.Fori(0, BATCH // 2) as pair:
                for m in range(2):
                    u = pair * 2 + m
                    xnt = k.XNT[:, bass.ds(u * SEQ, SEQ)]
                    nc.scalar.copy(xg[m][:], xnt).then_inc(xg_ready, 1)
                for m in range(2):
                    u = pair * 2 + m
                    act.wait_ge(projected, u + 1)
                    nc.scalar.copy(kk[m][:], k_ps[m]).then_inc(k_ready, 1)
                    nc.scalar.copy(q[m][:], q_ps[m]).then_inc(qv_ready, 1)
                for m in range(2):
                    u = pair * 2 + m
                    act.wait_ge(shifted, u + 1)
                    nc.scalar.activation(p[m][:], p[m][:], ACT.Exp, scale=HD ** -0.5).then_inc(exped, 1)
                for m in range(2):
                    u = pair * 2 + m
                    act.wait_ge(turned, u + 1)
                    nc.scalar.copy(pt[m][:].rearrange("p t c n -> p t (c n)"), big_b[m][:]).then_inc(pt_ready, 1)
                for m in range(2):
                    u = pair * 2 + m
                    act.wait_ge(o_up, u + 1)
                    nc.scalar.copy(o[m][:].rearrange("p t d -> p (t d)"), big_a[m][:, 0, 0:SEQ]).then_inc(o_ready, 1)
                for m in range(2):
                    u = pair * 2 + m
                    act.wait_ge(turned_o, u + 1)
                    nc.scalar.copy(ot[m][:], big_a[m][:, 1, 0:SEQ]).then_inc(ot_ready, 1)

        @block.vector
        def _(dve):
            dve.wait_ge(loaded, 16 * len(names))
            with dve.Fori(0, BATCH // 2) as pair:
                for m in range(2):
                    u = pair * 2 + m
                    dve.wait_ge(xg_ready, u + 1)
                    for h in range(HB):
                        last = nc.vector.tensor_copy(xrep[m][:, :, h, :], xg[m][:].rearrange("p (n u) -> p n u", u=WIN))
                    last.then_inc(xrep_ready, 1)
                for m in range(2):
                    u = pair * 2 + m
                    dve.wait_ge(projected, u + 1)
                    blocks = w["c_blocks32x8"][:].rearrange("p (a n) -> p a n", a=1).to_broadcast([P, WPG, HB * HD])
                    nc.vector.tensor_tensor(vals[m][:], v_ps[m].rearrange("p (w n) -> p w n", w=WPG), blocks, ALU.mult).then_inc(v_ready, 1)
                for m in range(2):
                    u = pair * 2 + m
                    dve.wait_ge(k_ready, u + 1)
                    for h in range(H):
                        last = nc.vector.tensor_scalar(keys[m][:, :, h, :], kk[m][:].rearrange("p (n u) -> p n u", u=WIN),
                                                       w["c_head_of_row8"][:, h:h + 1], None, ALU.mult)
                    last.then_inc(keys_ready, 1)
                for m in range(2):
                    u = pair * 2 + m
                    dve.wait_ge(scored, u + 1)
                    scores = big_a[m][:].rearrange("p t (h u) -> p (t h) u", u=WIN)
                    nc.vector.tensor_reduce(top[m][:], scores, AX.X, ALU.max)
                    dve.drain()
                    nc.vector.tensor_tensor(p[m][:], scores, per_row(top[m][:], WIN), ALU.subtract).then_inc(shifted, 1)
                for m in range(2):
                    u = pair * 2 + m
                    dve.wait_ge(exped, u + 1)
                    nc.vector.tensor_reduce(den[m][:], p[m][:], AX.X, ALU.add)
                    dve.drain()
                    nc.vector.reciprocal(den[m][:], den[m][:])
                    dve.drain()
                    nc.vector.tensor_tensor(p[m][:], p[m][:], per_row(den[m][:], WIN), ALU.mult).then_inc(probs_ready, 1)
                for m in range(2):
                    u = pair * 2 + m
                    dve.wait_ge(y_ready, u + 1)
                    x = k.X[:, bass.ds(u * TPB, TPB), :]
                    nc.vector.tensor_tensor(x, x, y_ps[m].rearrange("p (t d) -> p t d", d=D), ALU.add)

ED, CHH, NST = 256, 2, 16


class StateScan:

    def __init__(self, nc, k, s, delta, dx, a):
        self.nc, self.k, self.delta, self.dx, self.a = nc, k, delta, dx, a
        self.pick = s.sb("pick", [96, 32], BF16)
        self.parts = [s.sb(f"parts{i}", [96, GROUP], BF16) for i in range(2)]
        self.rest = s.sb("rest", [96, GROUP])
        self.spread, self.y_ps = s.ps("spread", [P, 4, GROUP]), s.ps("y_ps", [P, CHH, GROUP])
        self.da = [s.sb(f"da{i}", [P, CHH, BPG, SEQ]) for i in range(2)]
        spare = [k.XN[:, i * CHH * GT:(i + 1) * CHH * GT, :].rearrange("p (i t) d -> p i (t d)", i=CHH) for i in range(4)]
        self.u, self.hc = spare[0:2], spare[2:4]
        self.h = [s.sb(f"h{i}", [P, CHH, GROUP]) for i in range(2)]
        self.zeros = s.sb("zeros", [P, CHH, BPG])
        self.split_ready, self.y_ready = s.sem("split_ready"), s.sem("y_ready")
        self.spread_ready, self.da_ready, self.reset = s.sem("spread_ready"), s.sem("da_ready"), s.sem("reset")
        self.hc_ready, self.added_up = s.sem("hc_ready"), s.sem("added_up")

    def pe_spread(self, pe, g, par, n):
        if n == 0:
            pe.wait_ge(self.split_ready, g + 1)
        for i in range(2):
            last = self.nc.tensor.matmul(self.spread[:, 2 * (n % 2) + i, :], self.pick[:, i * NST + n:i * NST + n + 1].to_broadcast([96, P]),
                                         self.parts[par][:], start=True, stop=True)
        last.then_inc(self.spread_ready, 1)

    def pe_state(self, pe, g, par, n, first, last_group):
        pe.wait_ge(self.hc_ready, g * NST + (n + 1))
        if n + 2 < NST:
            self.pe_spread(pe, g, par, n + 2)
        elif not last_group:
            self.pe_spread(pe, g + 1, 1 - par, n + 2 - NST)
        if n == 0 and not first:
            pe.wait_ge(self.y_ready, g)
        for i in range(CHH):
            last = self.nc.tensor.matmul(self.y_ps[:, i, :], self.k.ident[:], self.hc[n % 2][:, i, :], start=(n == 0), stop=(n == NST - 1))
        last.then_inc(self.added_up, 1)

    def act_state(self, act, g, par, n, first):
        if n >= 2 or not first:
            act.wait_ge(self.hc_ready, g * NST + (n - 1))
        for i in range(CHH):
            last = self.nc.scalar.activation(self.da[n % 2][:, i, :, :].rearrange("p b t -> p (b t)"), self.delta[par][:, i, :], ACT.Exp,
                                             scale=self.a[:, i * NST + n:i * NST + n + 1])
        last.then_inc(self.da_ready, 1)

    def pool_state(self, pool, g, n):
        pool.wait_ge(self.da_ready, g * NST + (n + 1))
        starts = self.da[n % 2][:, :, :, 0]
        self.nc.gpsimd.tensor_tensor(starts, starts, self.zeros[:], ALU.mult).then_inc(self.reset, 1)

    def pool_split(self, pool, par, part):
        nc = self.nc
        source, rows = self.rest[32 * part:32 * part + 32, :], self.parts[par][32 * part:32 * part + 32, :]
        pool.drain()
        copy = nc.gpsimd.tensor_copy(rows, source)
        if part == 2:
            copy.then_inc(self.split_ready, 1)
        else:
            pool.drain()
            nc.gpsimd.tensor_tensor(self.rest[32 * part + 32:32 * part + 64, :], source, rows, ALU.subtract)
        pool.drain()

    def dve_input(self, dve, g, par, n):
        dve.wait_ge(self.spread_ready, g * NST + (n + 1))
        self.nc.vector.tensor_tensor(self.u[n % 2], self.dx[par][:], self.over_halves(n, 0), ALU.mult)

    def over_halves(self, n, i):
        return self.spread[:, 2 * (n % 2) + i, :].rearrange("p (a t) -> p a t", a=1).to_broadcast([P, CHH, GROUP])

    def dve_state(self, dve, g, par, n, first):
        nc = self.nc
        dve.drain()
        dve.wait_ge(self.reset, g * NST + (n + 1))
        nc.vector.tensor_tensor_scan(self.h[n % 2][:].rearrange("p i t -> p (i t)"), self.da[n % 2][:].rearrange("p i b t -> p (i b t)"),
                                     self.u[n % 2].rearrange("p i t -> p (i t)"), 0.0, ALU.mult, ALU.add)
        if n + 1 < NST:
            self.dve_input(dve, g, par, n + 1)
        dve.drain()
        if n >= 2 or not first:
            dve.wait_ge(self.added_up, g * NST + (n - 1))
        nc.vector.tensor_tensor(self.hc[n % 2], self.h[n % 2][:], self.over_halves(n, 1), ALU.mult).then_inc(self.hc_ready, 1)


def over_pairs(engine, count, step):
    step(0, 0, True, False)
    with engine.Fori(0, count // 2 - 1) as pair:
        step(pair * 2 + 1, 1, False, False)
        step(pair * 2 + 2, 0, False, False)
    step(count - 1, 1, False, True)


def l1_attn_a(nc, k, name):
    R, TAPS = 64, 4
    with Scope(nc, name) as s:
        names = [("L1a_win", [P, 4 * P]), ("L1a_conv", [P, CHH * TAPS]), ("L1a_wx", [P, CHH * (R + 2 * NST)]), ("L1a_wdt", [R, ED]),
                 ("L1a_bdt", [P, CHH]), ("L1a_alog", [P, CHH * NST]), ("L1a_d", [P, CHH]), ("L1a_wout", [P, CHH * D]),
                 ("c_pick", [96, 2 * NST])]
        w = {n: s.sb(n, shape) for n, shape in names}
        loaded = s.sem("loaded")
        layer_norm(nc, k, name + "_ln", loads=[(w[n][:], k.dram[n], loaded) for n, _ in names])
        F = R + 2 * NST
        a = s.sb("a", [P, CHH * NST])
        padded = s.sb("padded", [P, CHH, BPG, TAPS - 1 + SEQ])
        xc, z = [s.sb(f"xc{i}", [P, CHH, BPG, SEQ]) for i in range(2)], [s.sb(f"z{i}", [P, CHH, GROUP]) for i in range(2)]
        delta, dx = [s.sb(f"delta{i}", [P, CHH, GROUP]) for i in range(2)], [s.sb(f"dx{i}", [P, CHH, GROUP]) for i in range(2)]
        dt, conv = s.sb("dt", [R, GROUP]), s.sb("conv", [P, CHH, GROUP])
        raw, soft, y = s.sb("raw", [P, CHH, GROUP]), s.sb("soft", [P, CHH, GROUP]), s.sb("y", [P, CHH, GROUP])
        aux = s.ps("aux", [P, 2, GROUP])
        scan = StateScan(nc, k, s, delta, dx, a)
        a_exp, a_ready, cleared = s.sem("a_exp"), s.sem("a_ready"), s.sem("cleared")
        x_up, padded_ready, z_up, conv_ready, xc_ready = s.sem("x_up"), s.sem("padded_ready"), s.sem("z_up"), s.sem("conv_ready"), s.sem("xc_ready")
        bc_up, bc_ready, dt_up, raw_ready = s.sem("bc_up"), s.sem("bc_ready"), s.sem("dt_up"), s.sem("raw_ready")
        soft_ready, delta_ready, out_ready, added = s.sem("soft_ready"), s.sem("delta_ready"), s.sem("out_ready"), s.sem("added")
        block = s.block()

        @block.tensor
        def _(pe):
            def project_in(q, j, ready):
                xn = k.XNT[:, bass.ds(q * GROUP, GROUP)]
                for i in range(CHH):
                    last = nc.tensor.matmul(aux[:, i, :], w["L1a_win"][:, (j + i) * P:(j + i + 1) * P], xn, start=True, stop=True)
                last.then_inc(ready, 1)

            def project_z(q):
                pe.wait_ge(padded_ready, q + 1)
                project_in(q, 2, z_up)

            def project_bc(q, par):
                pe.wait_ge(xc_ready, q + 1)
                for i in range(CHH):
                    last = nc.tensor.matmul(aux[0:F, 0, :], w["L1a_wx"][:, i * F:(i + 1) * F], xc[par][:, i, :, :].rearrange("p b t -> p (b t)"),
                                            start=(i == 0), stop=(i == 1))
                last.then_inc(bc_up, 1)

            def project_dt(q):
                pe.wait_ge(bc_ready, q + 1)
                for i in range(CHH):
                    last = nc.tensor.matmul(aux[:, i, :], w["L1a_wdt"][:, i * P:(i + 1) * P], dt[:], start=True, stop=True)
                last.then_inc(dt_up, 1)

            def project_out(q):
                pe.wait_ge(scan.y_ready, q + 1)
                for i in range(CHH):
                    for t in range(GT):
                        last = nc.tensor.matmul(aux[:, 0, t * P:(t + 1) * P], y[:, i, t * P:(t + 1) * P], w["L1a_wout"][:, i * D:(i + 1) * D],
                                                start=(i == 0 and t == 0), stop=(i == 1), skip_group_check=True)
                last.then_inc(out_ready, 1)

            def step(g, par, first, last_group):
                for n in range(NST):
                    scan.pe_state(pe, g, par, n, first, last_group)
                    if n == 1 and not first:
                        project_out(g - 1)
                    if n == 3 and not last_group:
                        if not first:
                            pe.wait_ge(added, g)
                        project_in(g + 1, 0, x_up)
                    if n == 5 and not last_group:
                        project_z(g + 1)
                    if n == 8 and not last_group:
                        project_bc(g + 1, 1 - par)
                    if n == 10 and not last_group:
                        project_dt(g + 1)

            pe.wait_ge(loaded, 16 * len(names))
            project_in(0, 0, x_up)
            project_z(0)
            project_bc(0, 0)
            project_dt(0)
            scan.pe_spread(pe, 0, 0, 0)
            scan.pe_spread(pe, 0, 0, 1)
            over_pairs(pe, GROUPS, step)
            project_out(GROUPS - 1)

        @block.gpsimd
        def _(pool):
            nc.gpsimd.memset(padded[:, :, :, 0:TAPS - 1], 0.0).then_inc(cleared, 1)
            nc.gpsimd.memset(scan.zeros[:], 0.0)
            pool.wait_ge(loaded, 16 * len(names))
            nc.gpsimd.tensor_copy(scan.pick[:], w["c_pick"][:])
            pool.drain()

            def step(g, par, first, last_group):
                for n in range(NST):
                    if n == 12 and not last_group:
                        pool.wait_ge(bc_ready, g + 2)
                    scan.pool_state(pool, g, n)
                    if n in (12, 13, 14) and not last_group:
                        scan.pool_split(pool, 1 - par, n - 12)

            pool.wait_ge(bc_ready, 1)
            for part in range(3):
                scan.pool_split(pool, 0, part)
            over_pairs(pool, GROUPS, step)

        @block.scalar
        def _(act):
            def pad(q):
                act.wait_ge(x_up, q + 1)
                nc.scalar.copy(padded[:, :, :, TAPS - 1:], aux[:].rearrange("p i (b t) -> p i b t", b=BPG)).then_inc(padded_ready, 1)

            def gates(q, par):
                act.wait_ge(conv_ready, q + 1)
                act.wait_ge(z_up, q + 1)
                nc.scalar.activation(z[par][:], aux[:], ACT.Silu)
                nc.scalar.activation(xc[par][:], conv[:].rearrange("p i (b t) -> p i b t", b=BPG), ACT.Silu).then_inc(xc_ready, 1)

            def keep_bc(q):
                act.wait_ge(bc_up, q + 1)
                nc.scalar.copy(dt[:], aux[0:R, 0, :])
                nc.scalar.copy(scan.rest[0:2 * NST, :], aux[R:F, 0, :]).then_inc(bc_ready, 1)

            def log_term(q):
                act.wait_ge(raw_ready, q + 1)
                nc.scalar.activation(soft[:], soft[:], ACT.Exp)
                act.drain()
                nc.scalar.activation(soft[:], soft[:], ACT.Ln, bias=1.0).then_inc(soft_ready, 1)

            def step(g, par, first, last_group):
                for n in range(NST):
                    if n == 0:
                        act.wait_ge(delta_ready, g + 1)
                    scan.act_state(act, g, par, n, first)
                    if n == 4 and not last_group:
                        pad(g + 1)
                    if n == 8 and not last_group:
                        gates(g + 1, 1 - par)
                    if n == 10 and not last_group:
                        keep_bc(g + 1)
                    if n == 13 and not last_group:
                        log_term(g + 1)

            act.wait_ge(loaded, 16 * len(names))
            nc.scalar.activation(a[:], w["L1a_alog"][:], ACT.Exp).then_inc(a_exp, 1)
            act.wait_ge(a_ready, 1)
            pad(0)
            gates(0, 0)
            keep_bc(0)
            log_term(0)
            over_pairs(act, GROUPS, step)

        @block.vector
        def _(dve):
            def convolve(q):
                dve.wait_ge(padded_ready, q + 1)
                for j in range(TAPS):
                    for i in range(CHH):
                        out = conv[:, i, :].rearrange("p (b t) -> p b t", b=BPG)
                        tap = w["L1a_conv"][:, i * TAPS + j:i * TAPS + j + 1]
                        if j == 0:
                            last = nc.vector.tensor_scalar(out, padded[:, i, :, j:j + SEQ], tap, None, ALU.mult)
                        else:
                            last = nc.vector.scalar_tensor_tensor(out=out, in0=padded[:, i, :, j:j + SEQ], scalar=tap, in1=out,
                                                                  op0=ALU.mult, op1=ALU.add)
                    if j < TAPS - 1:
                        dve.drain()
                last.then_inc(conv_ready, 1)

            def raw_delta(q):
                dve.wait_ge(dt_up, q + 1)
                for i in range(CHH):
                    nc.vector.tensor_scalar(raw[:, i, :], aux[:, i, :], w["L1a_bdt"][:, i:i + 1], None, ALU.add)
                dve.drain()
                nc.vector.scalar_tensor_tensor(out=soft[:], in0=raw[:], scalar=-1.0, in1=raw[:], op0=ALU.mult, op1=ALU.min).then_inc(raw_ready, 1)

            def make_delta(q, par):
                dve.wait_ge(soft_ready, q + 1)
                nc.vector.scalar_tensor_tensor(out=delta[par][:], in0=raw[:], scalar=0.0, in1=soft[:], op0=ALU.max, op1=ALU.add)\
                    .then_inc(delta_ready, 1)
                dve.drain()
                nc.vector.tensor_tensor(dx[par][:], delta[par][:], xc[par][:].rearrange("p i b t -> p i (b t)"), ALU.mult)
                dve.drain()

            def gate_y(q, par):
                dve.wait_ge(scan.added_up, (q + 1) * NST)
                for i in range(CHH):
                    nc.vector.scalar_tensor_tensor(out=y[:, i, :], in0=xc[par][:, i, :, :].rearrange("p b t -> p (b t)"), scalar=w["L1a_d"][:, i:i + 1],
                                                   in1=scan.y_ps[:, i, :], op0=ALU.mult, op1=ALU.add)
                dve.drain()
                nc.vector.tensor_tensor(y[:], y[:], z[par][:], ALU.mult).then_inc(scan.y_ready, 1)

            def add_out(q):
                dve.wait_ge(out_ready, q + 1)
                x = k.X[:, bass.ds(q * GT, GT), :]
                nc.vector.tensor_tensor(x, x, aux[:, 0, :].rearrange("p (t d) -> p t d", d=D), ALU.add).then_inc(added, 1)

            def step(g, par, first, last_group):
                scan.dve_input(dve, g, par, 0)
                for n in range(NST):
                    scan.dve_state(dve, g, par, n, first)
                    if n == 0 and not first:
                        gate_y(g - 1, 1 - par)
                    if n == 3 and not first:
                        add_out(g - 1)
                    if n == 6 and not last_group:
                        convolve(g + 1)
                    if n == 12 and not last_group:
                        raw_delta(g + 1)
                    if n == 14 and not last_group:
                        make_delta(g + 1, 1 - par)

            dve.wait_ge(a_exp, 1)
            nc.vector.tensor_scalar(a[:], a[:], -1.0, None, ALU.mult).then_inc(a_ready, 1)
            dve.wait_ge(loaded, 16 * len(names))
            dve.wait_ge(cleared, 1)
            convolve(0)
            raw_delta(0)
            make_delta(0, 0)
            over_pairs(dve, GROUPS, step)
            gate_y(GROUPS - 1, 1)
            add_out(GROUPS - 1)


def l2_attn_a(nc, k, name):
    RMS_EPS, A_FLOOR = float(np.finfo(np.float32).eps), 1e-4
    HALF_TURN, TURN = float(np.pi), 2 * float(np.pi)
    TURN_HI = 6.28125
    TURN_LO = TURN - TURN_HI
    ROUND = 1.5 * 2.0 ** 23
    BC, DT, LAM = 2 * NST, 32, 64
    F = LAM + 1
    with Scope(nc, name) as s:
        names = [("L2a_win", [P, 4 * P]), ("L2a_wx", [P, CHH * F]), ("L2a_bdt", [P, CHH]), ("L2a_alog", [P, CHH * NST]),
                 ("L2a_d", [P, CHH]), ("L2a_wout", [P, CHH * D]), ("L2a_bias", [BC, 1]), ("L2a_norm", [BC, 1]), ("L2a_freq", [BC, 1]),
                 ("c_mean16", [BC, P]), ("c_quarter_turn", [BC, BC]), ("c_not_first", [BC, GROUP]), ("c_pick", [96, 2 * NST])]
        w = {n: s.sb(n, shape) for n, shape in names}
        wdt = s.sb("wdt", [DT + 1, ED])
        loaded = s.sem("loaded")
        layer_norm(nc, k, name + "_ln", loads=[(w[n][:], k.dram[n], loaded) for n, _ in names] + \
            [(wdt[DT:DT + 1, :], k.dram["L2a_wdt"], loaded)])
        a, freq, fsoft = s.sb("a", [P, CHH * NST]), s.sb("freq", [BC, 1]), s.sb("fsoft", [BC, 1])
        xp, ssm = s.sb("xp", [P, CHH, GROUP]), s.sb("ssm", [F, GROUP])
        z, delta, dx = [[s.sb(f"{n}{i}", [P, CHH, GROUP]) for i in range(2)] for n in ("z", "delta", "dx")]
        v, vsq = s.sb("v", [BC, GROUP]), s.sb("vsq", [BC, GROUP])
        cum, turns = s.sb("cum", [BC, GROUP]), s.sb("turns", [BC, 2, GROUP])
        raw, soft, lam = s.sb("raw", [P, CHH, GROUP]), s.sb("soft", [P, CHH, GROUP]), s.sb("lam", [P, GROUP])
        ang, cb = raw[0:BC, :, :], cum[0:NST, :]
        ahead = s.sb("ahead", [P, CHH, BPG, SEQ])
        y = s.sb("y", [P, CHH, GROUP])
        aux = s.ps("aux", [P, 2, GROUP])
        scan = StateScan(nc, k, s, delta, dx, a)
        bc = scan.rest[0:BC, :]
        consts_exp, consts_ready, cleared = s.sem("consts_exp"), s.sem("consts_ready"), s.sem("cleared")
        x_up, xp_ready, z_up, z_ready = s.sem("x_up"), s.sem("xp_ready"), s.sem("z_up"), s.sem("z_ready")
        ssm_up, ssm_ready, dt_up, raw_ready = s.sem("ssm_up"), s.sem("ssm_ready"), s.sem("dt_up"), s.sem("raw_ready")
        soft_ready, vsq_ready, mean_up, root_ready = s.sem("soft_ready"), s.sem("vsq_ready"), s.sem("mean_up"), s.sem("root_ready")
        delta_ready, sum_up, v_ready, turned = s.sem("delta_ready"), s.sem("sum_up"), s.sem("v_ready"), s.sem("turned")
        ang_ready, sin_ready, bc_ready = s.sem("ang_ready"), s.sem("sin_ready"), s.sem("bc_ready")
        c_up, cb_ready, cb_up, corrected, out_ready = s.sem("c_up"), s.sem("cb_ready"), s.sem("cb_up"), s.sem("corrected"), s.sem("out_ready")
        block = s.block()
        n_loads = len(names) + 1

        @block.tensor
        def _(pe):
            def project_in(q, j, ready):
                xn = k.XNT[:, bass.ds(q * GROUP, GROUP)]
                for i in range(CHH):
                    last = nc.tensor.matmul(aux[:, i, :], w["L2a_win"][:, (j + i) * P:(j + i + 1) * P], xn, start=True, stop=True)
                last.then_inc(ready, 1)

            def project_z(q):
                pe.wait_ge(xp_ready, q + 1)
                project_in(q, 2, z_up)

            def project_ssm(q):
                pe.wait_ge(z_ready, q + 1)
                for i in range(CHH):
                    last = nc.tensor.matmul(aux[0:F, 0, :], w["L2a_wx"][:, i * F:(i + 1) * F], xp[:, i, :], start=(i == 0), stop=(i == 1))
                last.then_inc(ssm_up, 1)

            def project_dt(q):
                pe.wait_ge(ssm_ready, q + 1)
                for i in range(CHH):
                    last = nc.tensor.matmul(aux[:, i, :], wdt[DT:DT + 1, i * P:(i + 1) * P], ssm[DT:DT + 1, :], start=True, stop=True)
                last.then_inc(dt_up, 1)

            def spread_lam_mean(q):
                pe.wait_ge(vsq_ready, q + 1)
                pe.wait_ge(raw_ready, q + 1)
                nc.tensor.matmul(aux[:, 0, :], k.ones[LAM:LAM + 1, :], ssm[LAM:LAM + 1, :], start=True, stop=True)
                nc.tensor.matmul(aux[:, 1, :], w["c_mean16"][:], vsq[:], start=True, stop=True).then_inc(mean_up, 1)

            def sum_delta_turn(q, par):
                pe.wait_ge(delta_ready, q + 1)
                pe.wait_ge(v_ready, q + 1)
                for i in range(CHH):
                    last = nc.tensor.matmul(aux[0:BC, 0, :], k.ones[:, 0:BC], delta[par][:, i, :], start=(i == 0), stop=(i == 1))
                last.then_inc(sum_up, 1)
                nc.tensor.matmul(aux[0:BC, 1, :], w["c_quarter_turn"][:], v[:], start=True, stop=True).then_inc(turned, 1)

            def move_c(q):
                nc.tensor.matmul(aux[0:P - NST, 1, :], k.ident[0:BC, NST:P], bc, start=True, stop=True).then_inc(c_up, 1)

            def sum_cb(q):
                pe.wait_ge(cb_ready, q + 1)
                nc.tensor.matmul(aux[:, 1, :], k.ones[0:NST, :], cb, start=True, stop=True).then_inc(cb_up, 1)

            def project_out(q):
                pe.wait_ge(scan.y_ready, q + 1)
                for i in range(CHH):
                    for t in range(GT):
                        last = nc.tensor.matmul(aux[:, 0, t * P:(t + 1) * P], y[:, i, t * P:(t + 1) * P], w["L2a_wout"][:, i * D:(i + 1) * D],
                                                start=(i == 0 and t == 0), stop=(i == 1), skip_group_check=True)
                last.then_inc(out_ready, 1)

            def step(g, par, first, last_group):
                for n in range(NST):
                    scan.pe_state(pe, g, par, n, first, last_group)
                    if n == 0:
                        move_c(g)
                    if n == 1 and not first:
                        project_out(g - 1)
                    if n == 2:
                        sum_cb(g)
                    if not last_group:
                        if n == 3:
                            pe.wait_ge(corrected, g + 1)
                            project_in(g + 1, 0, x_up)
                        if n == 4:
                            project_z(g + 1)
                        if n == 5:
                            project_ssm(g + 1)
                        if n == 6:
                            project_dt(g + 1)
                        if n == 7:
                            spread_lam_mean(g + 1)
                        if n == 10:
                            sum_delta_turn(g + 1, 1 - par)

            pe.wait_ge(loaded, 16 * n_loads)
            project_in(0, 0, x_up)
            project_z(0)
            project_ssm(0)
            project_dt(0)
            spread_lam_mean(0)
            sum_delta_turn(0, 0)
            scan.pe_spread(pe, 0, 0, 0)
            scan.pe_spread(pe, 0, 0, 1)
            over_pairs(pe, GROUPS, step)
            project_out(GROUPS - 1)

        @block.gpsimd
        def _(pool):
            nc.gpsimd.memset(ahead[:, :, :, SEQ - 1:SEQ], 0.0).then_inc(cleared, 1)
            nc.gpsimd.memset(scan.zeros[:], 0.0)
            pool.wait_ge(loaded, 16 * n_loads)
            nc.gpsimd.tensor_copy(scan.pick[:], w["c_pick"][:])
            pool.drain()

            def step(g, par, first, last_group):
                for n in range(NST):
                    if n == 13 and not last_group:
                        pool.wait_ge(bc_ready, g + 2)
                    scan.pool_state(pool, g, n)
                    if n in (13, 14, 15) and not last_group:
                        scan.pool_split(pool, 1 - par, n - 13)

            pool.wait_ge(bc_ready, 1)
            for part in range(3):
                scan.pool_split(pool, 0, part)
            over_pairs(pool, GROUPS, step)

        @block.scalar
        def _(act):
            def gate_x(q):
                act.wait_ge(x_up, q + 1)
                nc.scalar.activation(xp[:], aux[:], ACT.Silu).then_inc(xp_ready, 1)

            def gate_z(q, par):
                act.wait_ge(z_up, q + 1)
                nc.scalar.activation(z[par][:], aux[:], ACT.Silu).then_inc(z_ready, 1)

            def keep_ssm(q):
                act.wait_ge(ssm_up, q + 1)
                nc.scalar.copy(ssm[:], aux[0:F, 0, :]).then_inc(ssm_ready, 1)

            def log_term(q):
                act.wait_ge(raw_ready, q + 1)
                nc.scalar.activation(soft[:], soft[:], ACT.Exp)
                act.drain()
                nc.scalar.activation(soft[:], soft[:], ACT.Ln, bias=1.0).then_inc(soft_ready, 1)

            def lam_root(q):
                act.wait_ge(mean_up, q + 1)
                nc.scalar.activation(lam[:], aux[:, 0, :], ACT.Sigmoid)
                nc.scalar.activation(vsq[:], aux[0:BC, 1, :], ACT.Sqrt, bias=RMS_EPS).then_inc(root_ready, 1)

            def sine(q):
                act.wait_ge(ang_ready, q + 1)
                nc.scalar.activation(turns[:], ang, ACT.Sin).then_inc(sin_ready, 1)

            def step(g, par, first, last_group):
                for n in range(NST):
                    scan.act_state(act, g, par, n, first)
                    if not last_group:
                        if n == 4:
                            gate_x(g + 1)
                        if n == 5:
                            gate_z(g + 1, 1 - par)
                        if n == 6:
                            keep_ssm(g + 1)
                        if n == 8:
                            log_term(g + 1)
                            lam_root(g + 1)
                        if n == 12:
                            sine(g + 1)

            act.wait_ge(loaded, 16 * n_loads)
            nc.scalar.activation(a[:], w["L2a_alog"][:], ACT.Exp)
            act.wait_ge(cleared, 2)
            nc.scalar.activation(fsoft[:], fsoft[:], ACT.Exp)
            act.drain()
            nc.scalar.activation(fsoft[:], fsoft[:], ACT.Ln, bias=1.0).then_inc(consts_exp, 1)
            act.wait_ge(consts_ready, 1)
            gate_x(0)
            gate_z(0, 0)
            keep_ssm(0)
            log_term(0)
            lam_root(0)
            sine(0)
            over_pairs(act, GROUPS, step)

        @block.vector
        def _(dve):
            def square_v(q):
                dve.wait_ge(ssm_ready, q + 1)
                nc.vector.tensor_scalar(v[:], ssm[0:BC, :], w["L2a_bias"][:], None, ALU.add)
                dve.drain()
                nc.vector.tensor_tensor(vsq[:], v[:], v[:], ALU.mult).then_inc(vsq_ready, 1)

            def raw_delta(q):
                dve.wait_ge(dt_up, q + 1)
                for i in range(CHH):
                    nc.vector.tensor_scalar(raw[:, i, :], aux[:, i, :], w["L2a_bdt"][:, i:i + 1], None, ALU.add)
                dve.drain()
                nc.vector.scalar_tensor_tensor(out=soft[:], in0=raw[:], scalar=-1.0, in1=raw[:], op0=ALU.mult, op1=ALU.min).then_inc(raw_ready, 1)

            def make_delta(q, par):
                dve.wait_ge(soft_ready, q + 1)
                nc.vector.scalar_tensor_tensor(out=delta[par][:], in0=raw[:], scalar=0.0, in1=soft[:], op0=ALU.max, op1=ALU.add)\
                    .then_inc(delta_ready, 1)
                dve.drain()
                dve.wait_ge(root_ready, q + 1)
                nc.vector.tensor_tensor(raw[:], delta[par][:], lam[:].rearrange("p (a t) -> p a t", a=1).to_broadcast([P, CHH, GROUP]), ALU.mult)
                dve.drain()
                by_seq = [b[:].rearrange("p i (b t) -> p i b t", b=BPG) for b in (delta[par], raw)]
                for i in range(CHH):
                    nc.vector.tensor_tensor(ahead[:, i, :, 0:SEQ - 1], by_seq[0][:, i, :, 1:SEQ], by_seq[1][:, i, :, 1:SEQ], ALU.subtract)
                nc.vector.tensor_copy(by_seq[1][:, :, :, 0:1], by_seq[0][:, :, :, 0:1])
                dve.drain()

            def make_dx(par):
                ahead_x = ahead[:].rearrange("p i b t -> p i (b t)")
                nc.vector.tensor_tensor(dx[par][:], raw[:], ahead_x, ALU.add)
                dve.drain()
                nc.vector.tensor_tensor(dx[par][:], dx[par][:], xp[:], ALU.mult)
                nc.vector.tensor_tensor(soft[:], ahead_x, xp[:], ALU.mult)

            def normalise_v(q):
                nc.vector.reciprocal(vsq[:], vsq[:])
                dve.drain()
                nc.vector.scalar_tensor_tensor(out=v[:], in0=v[:], scalar=w["L2a_norm"][:], in1=vsq[:], op0=ALU.mult, op1=ALU.mult).then_inc(v_ready, 1)

            def angles(q):
                dve.wait_ge(sum_up, q + 1)
                nc.vector.tensor_tensor_scan(cum[:], w["c_not_first"][:], aux[0:BC, 0, :], 0.0, ALU.mult, ALU.add)
                dve.drain()
                nc.vector.tensor_scalar(ang[:, 0, :], cum[:], freq[:], None, ALU.mult)
                nc.vector.tensor_scalar(ang[:, 1, :], cum[:], freq[:], HALF_TURN / 2, ALU.mult, ALU.add)
                dve.drain()
                nc.vector.tensor_scalar(turns[:], ang, 1.0 / TURN, ROUND, ALU.mult, ALU.add)
                dve.drain()
                nc.vector.tensor_scalar(turns[:], turns[:], -ROUND, None, ALU.add)
                dve.drain()
                nc.vector.scalar_tensor_tensor(out=ang, in0=turns[:], scalar=-TURN_HI, in1=ang, op0=ALU.mult, op1=ALU.add)
                dve.drain()
                nc.vector.scalar_tensor_tensor(out=ang, in0=turns[:], scalar=-TURN_LO, in1=ang, op0=ALU.mult, op1=ALU.add)
                dve.drain()
                nc.vector.tensor_scalar(ang, ang, 3.1415925, -3.1415925, ALU.min, ALU.max).then_inc(ang_ready, 1)

            def turn_bc(q):
                dve.wait_ge(turned, q + 1)
                dve.wait_ge(sin_ready, q + 1)
                nc.vector.tensor_tensor(cum[:], aux[0:BC, 1, :], turns[:, 0, :], ALU.mult)
                nc.vector.tensor_tensor(v[:], v[:], turns[:, 1, :], ALU.mult)
                dve.drain()
                nc.vector.tensor_tensor(bc, v[:], cum[:], ALU.add).then_inc(bc_ready, 1)

            def multiply_cb(q):
                dve.wait_ge(c_up, q + 1)
                nc.vector.tensor_tensor(cb, scan.rest[0:NST, :], aux[0:NST, 1, :], ALU.mult).then_inc(cb_ready, 1)

            def correct(q):
                dve.wait_ge(cb_up, q + 1)
                cb_sum = aux[:, 1, :].rearrange("p (a t) -> p a t", a=1).to_broadcast([P, CHH, GROUP])
                nc.vector.tensor_tensor(raw[:], soft[:], cb_sum, ALU.mult)
                dve.drain()
                for i in range(CHH):
                    last = nc.vector.scalar_tensor_tensor(out=y[:, i, :], in0=xp[:, i, :], scalar=w["L2a_d"][:, i:i + 1], in1=raw[:, i, :],
                                                          op0=ALU.mult, op1=ALU.subtract)
                last.then_inc(corrected, 1)

            def gate_y(q, par):
                dve.wait_ge(scan.added_up, (q + 1) * NST)
                nc.vector.tensor_tensor(y[:], y[:], scan.y_ps[:], ALU.add)
                dve.drain()
                nc.vector.tensor_tensor(y[:], y[:], z[par][:], ALU.mult).then_inc(scan.y_ready, 1)

            def add_out(q):
                dve.wait_ge(out_ready, q + 1)
                x = k.X[:, bass.ds(q * GT, GT), :]
                nc.vector.tensor_tensor(x, x, aux[:, 0, :].rearrange("p (t d) -> p t d", d=D), ALU.add)

            def step(g, par, first, last_group):
                scan.dve_input(dve, g, par, 0)
                for n in range(NST):
                    scan.dve_state(dve, g, par, n, first)
                    if n == 0 and not first:
                        gate_y(g - 1, 1 - par)
                    if n == 1:
                        multiply_cb(g)
                    if n == 2 and not first:
                        add_out(g - 1)
                    if n == 3:
                        correct(g)
                    if not last_group:
                        if n == 6:
                            square_v(g + 1)
                        if n == 7:
                            raw_delta(g + 1)
                        if n == 9:
                            make_delta(g + 1, 1 - par)
                        if n == 10:
                            make_dx(1 - par)
                            normalise_v(g + 1)
                        if n == 11:
                            angles(g + 1)
                        if n == 12:
                            turn_bc(g + 1)

            dve.wait_ge(loaded, 16 * n_loads)
            nc.vector.scalar_tensor_tensor(out=fsoft[:], in0=w["L2a_freq"][:], scalar=-1.0, in1=w["L2a_freq"][:],
                                           op0=ALU.mult, op1=ALU.min).then_inc(cleared, 1)
            dve.wait_ge(consts_exp, 1)
            nc.vector.tensor_scalar(a[:], a[:], -1.0, -A_FLOOR, ALU.mult, ALU.min)
            nc.vector.scalar_tensor_tensor(out=freq[:], in0=w["L2a_freq"][:], scalar=0.0, in1=fsoft[:], op0=ALU.max, op1=ALU.add)
            dve.drain()
            nc.vector.tensor_scalar(freq[:], freq[:], 1.0 / ED, None, ALU.mult).then_inc(consts_ready, 1)
            dve.drain()
            square_v(0)
            raw_delta(0)
            make_delta(0, 0)
            make_dx(0)
            normalise_v(0)
            angles(0)
            turn_bc(0)
            dve.drain()
            over_pairs(dve, GROUPS, step)
            gate_y(GROUPS - 1, 1)
            add_out(GROUPS - 1)


def l2_attn_b(nc, k, name):
    H, ROT = 8, 64
    AW = P + SEQ
    GN = D // 16
    with Scope(nc, name) as s:
        names = [("L2b_wQ", [P, H * D]), ("L2b_wK", [P, H * D]), ("L2b_wV", [P, H * D]), ("L2b_wQs", [P, H * ROT]), ("L2b_wKs", [P, H * ROT]),
                 ("L2b_g", [P, D]), ("L2b_be", [P, D]), ("c_cos", [ROT, GROUP]), ("c_sin", [ROT, GROUP]), ("c_decay", [P, AW])]
        w = {n: s.sb(n, shape) for n, shape in names}
        loaded = s.sem("loaded")
        layer_norm(nc, k, name + "_ln", loads=[(w[n][:], k.dram[n], loaded) for n, _ in names])
        xg, v = s.sb("xg", [P, GROUP]), s.sb("v", [P, GT, H * D])
        rot, swap = s.sb("rot", [ROT, 2, GROUP]), [s.sb(f"swap{i}", [ROT, 2, GROUP]) for i in range(2)]
        qk = [s.sb(f"qk{i}", [P, 2, GROUP]) for i in range(2)]
        a = [s.sb(f"a{i}", [P, BPG, AW]) for i in range(2)]
        rows, sq, mean, var = s.sb("rows", [P, GT * 16, GN]), s.sb("sq", [P, GT * 16, GN]), s.sb("mean", [P, GT * 16]), s.sb("var", [P, GT * 16])
        qk_ps, sw_ps = s.ps("qk_ps", [P, 2, GROUP]), s.ps("sw_ps", [ROT, 2, GROUP])
        a_ps, v_ps, o_ps = s.ps("a_ps", [P, BPG, 512]), s.ps("v_ps", [P, 512]), s.ps("o_ps", [P, GT, D])
        xg_ready, v_up, v_ready = s.sem("xg_ready"), s.sem("v_up"), s.sem("v_ready")
        projected, rot_ready, qk_ready = s.sem("projected"), s.sem("rot_ready"), s.sem("qk_ready")
        high_ready, low_read = s.sem("high_ready"), s.sem("low_read")
        a_up, a_ready, o_ready, var_ready, root_ready, done = (s.sem(n) for n in ("a_up", "a_ready", "o_ready", "var_ready", "root_ready", "done"))
        block = s.block()

        @block.tensor
        def _(pe):
            def project(g, h, first=False):
                if h > 0 or not first:
                    pe.wait_ge(high_ready, g * H + h)
                    pe.wait_ge(low_read, g * H + h)
                for i, n in enumerate("QK"):
                    nc.tensor.matmul(qk_ps[:, i, :], w[f"L2b_w{n}"][:, h * D:(h + 1) * D], xg[:], start=True, stop=True)
                for i, n in enumerate("QK"):
                    last = nc.tensor.matmul(sw_ps[:, i, :], w[f"L2b_w{n}s"][:, h * ROT:(h + 1) * ROT], xg[:], start=True, stop=True)
                last.then_inc(projected, 1)

            def scores(g, h):
                pe.wait_ge(qk_ready, g * H + (h + 1))
                if h > 0:
                    pe.wait_ge(a_ready, g * H + h)
                for b in range(BPG):
                    q, kk = qk[h % 2][:, 0, :], qk[h % 2][:, 1, :]
                    c = b * SEQ
                    nc.tensor.matmul(a_ps[:, b, 0:P], q[:, c:c + P], kk[:, c:c + P], start=True, stop=True)
                    last = nc.tensor.matmul(a_ps[:, b, P:AW], q[:, c + P:c + SEQ], kk[:, c:c + SEQ], start=True, stop=True)
                last.then_inc(a_up, 1)

            def mix(g, h):
                pe.wait_ge(a_ready, g * H + (h + 1))
                for b in range(BPG):
                    for col, row_tile, key_tile in ((0, 0, 0), (P, 1, 0), (2 * P, 1, 1)):
                        last = nc.tensor.matmul(o_ps[:, b * TPB + key_tile, :], a[h % 2][:, b, col:col + P],
                                                v[:, b * TPB + row_tile, h * D:(h + 1) * D],
                                                start=(h == 0 and b == 0 and col == 0), stop=(h == H - 1), skip_group_check=True)
                return last

            pe.wait_ge(loaded, 16 * len(names))

            def step(g, par, first, last_group):
                pe.wait_ge(xg_ready, g + 1)
                project(g, 0, first)
                for n in range(2 * GT):
                    if n > 0:
                        pe.wait_ge(v_ready, g * 2 * GT + n)
                    t, half = divmod(n, 2)
                    nc.tensor.matmul(v_ps[:], xg[:, t * P:(t + 1) * P], w["L2b_wV"][:, half * 512:(half + 1) * 512], start=True, stop=True)\
                        .then_inc(v_up, 1)
                pe.wait_ge(v_ready, g * 2 * GT + 2 * GT)
                for h in range(H):
                    if h + 1 < H:
                        project(g, h + 1)
                    scores(g, h)
                    if h == 1 and not first:
                        pe.wait_ge(done, g)
                    if h > 0:
                        mix(g, h - 1)
                mix(g, H - 1).then_inc(o_ready, 1)

            over_pairs(pe, GROUPS, step)

        @block.scalar
        def _(act):
            def high(g, h):
                act.wait_ge(projected, g * H + (h + 1))
                nc.scalar.activation(qk[h % 2][ROT:P, :, :], qk_ps[ROT:P, :, :], ACT.Silu).then_inc(high_ready, 1)

            def low(g, h):
                act.wait_ge(rot_ready, g * H + (h + 1))
                nc.scalar.activation(qk[h % 2][0:ROT, :, :], rot[:], ACT.Silu).then_inc(qk_ready, 1)

            def root(g):
                act.wait_ge(var_ready, g + 1)
                nc.scalar.activation(var[:], var[:], ACT.Sqrt).then_inc(root_ready, 1)

            def step(g, par, first, last_group):
                nc.scalar.copy(xg[:], k.XNT[:, bass.ds(g * GROUP, GROUP)]).then_inc(xg_ready, 1)
                high(g, 0)
                for n in range(2 * GT):
                    t, half = divmod(n, 2)
                    act.wait_ge(v_up, g * 2 * GT + (n + 1))
                    nc.scalar.activation(v[:, t, half * 512:(half + 1) * 512], v_ps[:], ACT.Silu).then_inc(v_ready, 1)
                    if n == 4 and not first:
                        root(g - 1)
                low(g, 0)
                for h in range(1, H):
                    high(g, h)
                    low(g, h)

            over_pairs(act, GROUPS, step)
            root(GROUPS - 1)

        @block.vector
        def _(dve):
            def twice(ap):
                return ap[:].rearrange("p (a n) -> p a n", a=1).to_broadcast([ap.shape[0], 2, ap.shape[1]])

            def over_tiles(ap):
                return ap[:].rearrange("p (a n) -> p a n", a=1).to_broadcast([P, GT, D])

            def turn(g, h, first=False):
                dve.wait_ge(projected, g * H + (h + 1))
                nc.vector.tensor_tensor(swap[h % 2][:], sw_ps[:], twice(w["c_sin"]), ALU.mult)
                if h > 0 or not first:
                    dve.wait_ge(qk_ready, g * H + h)
                nc.vector.tensor_tensor(rot[:], qk_ps[0:ROT, :, :], twice(w["c_cos"]), ALU.mult).then_inc(low_read, 1)
                dve.drain()
                nc.vector.tensor_tensor(rot[:], rot[:], swap[h % 2][:], ALU.add).then_inc(rot_ready, 1)

            def decay(g, h):
                dve.wait_ge(a_up, g * H + (h + 1))
                nc.vector.tensor_tensor(a[h % 2][:], a_ps[:, :, 0:AW], twice(w["c_decay"]), ALU.mult).then_inc(a_ready, 1)

            dve.wait_ge(loaded, 16 * len(names))

            def normalise(g):
                dve.wait_ge(o_ready, g + 1)
                groups = o_ps[:].rearrange("p t (q d) -> p (t q) d", d=GN)
                nc.vector.tensor_reduce(mean[:], groups, AX.X, ALU.add)
                dve.drain()
                nc.vector.tensor_scalar(mean[:], mean[:], 1.0 / GN, None, ALU.mult)
                dve.drain()
                nc.vector.tensor_tensor(rows[:], groups, per_row(mean[:], GN), ALU.subtract)
                dve.drain()
                nc.vector.tensor_tensor(sq[:], rows[:], rows[:], ALU.mult)
                dve.drain()
                nc.vector.tensor_reduce(var[:], sq[:], AX.X, ALU.add)
                dve.drain()
                nc.vector.tensor_scalar(var[:], var[:], 1.0 / GN, 1e-5, ALU.mult, ALU.add).then_inc(var_ready, 1)
                dve.wait_ge(root_ready, g + 1)
                nc.vector.reciprocal(var[:], var[:])
                dve.drain()
                nc.vector.tensor_tensor(rows[:], rows[:], per_row(var[:], GN), ALU.mult)
                dve.drain()
                by_tile = rows[:].rearrange("p (t q) d -> p t (q d)", t=GT)
                nc.vector.tensor_tensor(by_tile, by_tile, over_tiles(w["L2b_g"]), ALU.mult)
                dve.drain()
                nc.vector.tensor_tensor(by_tile, by_tile, over_tiles(w["L2b_be"]), ALU.add)
                dve.drain()
                x = k.X[:, bass.ds(g * GT, GT), :]
                nc.vector.tensor_tensor(x, x, by_tile, ALU.add).then_inc(done, 1)

            def step(g, par, first, last_group):
                if not first:
                    normalise(g - 1)
                turn(g, 0, first)
                for h in range(H):
                    if h + 1 < H:
                        turn(g, h + 1)
                    decay(g, h)

            over_pairs(dve, GROUPS, step)
            normalise(GROUPS - 1)


def l2_ffn(nc, k, name):
    NT, NC, KN = 64, 8, 8
    NS = NC + NT
    with Scope(nc, name + "_sig") as s:
        raw, q, low = s.sb("raw", [P, NT]), s.sb("q", [P, NT]), s.sb("low", [P, NT])
        loaded = s.sem("loaded")
        block = s.block()

        @block.sync
        def _(sp):
            sp.dma_start(raw[:], k.dram["L2f_sig"]).then_inc(loaded, 16)

        @block.vector
        def _(dve):
            dve.wait_ge(loaded, 16)
            nc.vector.tensor_scalar(q[:], raw[:], 0.3, None, ALU.is_gt)
            nc.vector.tensor_scalar(low[:], raw[:], -0.3, None, ALU.is_lt)
            dve.drain()
            nc.vector.tensor_tensor(q[:], q[:], low[:], ALU.subtract)
            dve.drain()
            nc.vector.tensor_tensor(q[:], q[:], raw[:], ALU.subtract)
            dve.drain()
            nc.vector.tensor_tensor(k.SIG[:, NC:NS], raw[:], q[:], ALU.add)
            dve.drain()
            nc.vector.tensor_reduce(low[:, 0:NC], k.SIG[:, NC:NS].rearrange("p (c t) -> p c t", t=8), AX.X, ALU.add)
            dve.drain()
            nc.vector.tensor_scalar(q[:, 0:NC], low[:, 0:NC], 0.0, None, ALU.is_gt)
            nc.vector.tensor_scalar(q[:, NC:2 * NC], low[:, 0:NC], 0.0, None, ALU.is_lt)
            dve.drain()
            nc.vector.tensor_tensor(k.SIG[:, 0:NC], q[:, 0:NC], q[:, NC:2 * NC], ALU.subtract)

    layer_norm(nc, k, name + "_ln", k.SIG, NS, keep_rows=True)

    with Scope(nc, name + "_pick") as s:
        names = [("L2f_temp", [P, 1]), ("L2f_knots", [P, KN]), ("c_first8", [P, NC]), ("c_first64", [P, NT]), ("c_minus_knot", [P, KN])]
        w = {n: s.sb(n, shape) for n, shape in names}
        temp, slope = s.sb("temp", [P, 1]), s.sb("slope", [P, KN])
        at = s.sb("at", [P, TILES * NS])
        over = [s.sb(f"over{i}", [P, TILES * NS]) for i in range(2)]
        gates = s.sb("gates", [P, TILES, NS])
        top, own, off = s.sb("top", [P, TILES]), s.sb("own", [P, TILES, NC]), s.sb("off", [P, TILES, NC])
        q = s.sb("q", [P, TILES, NT])
        loaded, temp_ready, over_ready, used = s.sem("loaded"), s.sem("temp_ready"), s.sem("over_ready"), s.sem("used")
        block = s.block()

        @block.sync
        def _(sp):
            for n, _ in names:
                sp.dma_start(w[n][:], k.dram[n]).then_inc(loaded, 16)

        @block.scalar
        def _(act):
            act.wait_ge(temp_ready, 1)
            nc.scalar.activation(at[:], k.LOG[:].rearrange("p t n -> p (t n)"), ACT.Sigmoid, scale=temp[:])
            act.drain()
            for j in range(KN - 1):
                if j >= 2:
                    act.wait_ge(used, j - 1)
                nc.scalar.activation(over[j % 2][:], at[:], ACT.Relu, scale=float(KN - 1), bias=w["c_minus_knot"][:, j:j + 1])\
                    .then_inc(over_ready, 1)

        @block.vector
        def _(dve):
            dve.wait_ge(loaded, 16 * len(names))
            nc.vector.tensor_scalar(temp[:], w["L2f_temp"][:], 1e-6, None, ALU.add)
            dve.drain()
            nc.vector.reciprocal(temp[:], temp[:]).then_inc(temp_ready, 1)
            nc.vector.tensor_tensor(slope[:, 0:KN - 1], w["L2f_knots"][:, 1:KN], w["L2f_knots"][:, 0:KN - 1], ALU.subtract)
            dve.drain()
            nc.vector.tensor_copy(off[:, 0, 0:KN - 1], slope[:, 0:KN - 1])
            dve.drain()
            nc.vector.tensor_tensor(slope[:, 1:KN - 1], off[:, 0, 1:KN - 1], off[:, 0, 0:KN - 2], ALU.subtract)
            dve.drain()
            g = gates[:].rearrange("p t n -> p (t n)")
            for j in range(KN - 1):
                dve.wait_ge(over_ready, j + 1)
                if j == 0:
                    nc.vector.tensor_scalar(g, over[0][:], slope[:, 0:1], w["L2f_knots"][:, 0:1], ALU.mult, ALU.add).then_inc(used, 1)
                else:
                    nc.vector.scalar_tensor_tensor(out=g, in0=over[j % 2][:], scalar=slope[:, j:j + 1], in1=g,
                                                   op0=ALU.mult, op1=ALU.add).then_inc(used, 1)
                dve.drain()

            def first_largest(vals, n, first, out):
                def spread(ap):
                    return ap.rearrange("p (t a) -> p t a", a=1).to_broadcast([P, TILES, n])
                nc.vector.tensor_reduce(top[:], vals, AX.X, ALU.max)
                dve.drain()
                nc.vector.tensor_tensor(out, vals, spread(top[:]), ALU.is_equal)
                dve.drain()
                nc.vector.tensor_tensor(out, out, first[:].rearrange("p (a n) -> p a n", a=1).to_broadcast([P, TILES, n]), ALU.mult)
                dve.drain()
                nc.vector.tensor_reduce(top[:], out, AX.X, ALU.max)
                dve.drain()
                nc.vector.tensor_tensor(out, out, spread(top[:]), ALU.is_equal)
                dve.drain()

            first_largest(gates[:, :, 0:NC], NC, w["c_first8"], own[:])
            nc.vector.tensor_scalar(off[:], own[:], 3e38, -3e38, ALU.mult, ALU.add)

            def over_cluster(ap):
                return ap.rearrange("p t (c a) -> p (t c) a", a=1).to_broadcast([P, TILES * NC, 8])
            gq = gates[:, :, NC:NS].rearrange("p t (c n) -> p t c n", n=8)
            qq = q[:].rearrange("p t (c n) -> p t c n", n=8)
            own4 = own[:].rearrange("p t (c a) -> p t c a", a=1).to_broadcast([P, TILES, NC, 8])
            nc.vector.tensor_tensor(qq, gq, own4, ALU.mult)
            dve.drain()
            qf = q[:].rearrange("p t (c n) -> p (t c) n", n=8)
            nc.vector.tensor_tensor(qf, qf, over_cluster(off[:]), ALU.add)
            dve.drain()
            first_largest(q[:], NT, w["c_first64"], k.PICK[:])

    CH, G2 = 32, 16
    W1, B1, W2, B2, DIR = 0, 2 * G2, 3 * G2, 4 * G2, 4 * G2 + 1
    TW = DIR + D
    BPG = 1
    with Scope(nc, name + "_mix") as s:
        names = [("L2f_scale", [P, 1]), ("L2f_cw1", [P, CH]), ("L2f_cb1", [CH, 1]), ("L2f_cw2", [CH, 2]), ("L2f_cb2", [1, 2 * TPB]),
                 ("L2f_table", [P, TW]), ("L2f_gamma", [P, D]), ("L2f_beta", [P, D])]
        w = {n: s.sb(n, shape) for n, shape in names}
        picked, pt, hid = s.two("picked", [P, TPB * NT]), s.two("pt", [P, P]), s.two("hid", [CH, SEQ])
        comp, sp1, sp2, mag = s.two("comp", [P, TPB, 2]), s.two("sp1", [P, TPB, G2]), s.two("sp2", [P, TPB, G2]), s.two("mag", [P, TPB])
        y = s.two("y", [P, TPB, D])
        stats, mv, rstd, minus = s.two("stats", [P, TPB, 6]), s.two("mv", [P, TPB, 2]), s.two("rstd", [P, TPB]), s.sb("minus", [P, TPB])
        turns, hid_ps, row_ps = s.two_ps("turns", [P, 512]), s.two_ps("hid_ps", [CH, 512]), s.two_ps("row_ps", [P, TPB, 512])
        pt_ps, comp_ps = [b[:, 0:P] for b in turns], [b[:, P:2 * P] for b in turns]
        loaded, picked_ready, turned, pt_ready = s.sem("loaded"), s.sem("picked_ready"), s.sem("turned"), s.sem("pt_ready")
        hid_up, hid_ready, comp_up, comp_ready = s.sem("hid_up"), s.sem("hid_ready"), s.sem("comp_up"), s.sem("comp_ready")
        rows_up, var_ready, rstd_ready, done = s.sem("rows_up"), s.sem("var_ready"), s.sem("rstd_ready"), s.sem("done")
        block = s.block()

        @block.sync
        def _(sp):
            for n, _ in names:
                sp.dma_start(w[n][:], k.dram[n]).then_inc(loaded, 16)

        @block.tensor
        def _(pe):
            pe.wait_ge(loaded, 16 * len(names))
            with pe.Fori(0, BATCH // 2) as pair:
                for m in range(2):
                    u = pair * 2 + m
                    pe.wait_ge(picked_ready, u + 1)
                    nc.tensor.transpose(pt_ps[m][:, 0:P], picked[m][:], k.ident[:]).then_inc(turned, 1)
                    nc.tensor.matmul(hid_ps[m][:, 0:SEQ], w["L2f_cw1"][:], k.XNT[:, bass.ds(u * SEQ, SEQ)], start=True, stop=True).then_inc(hid_up, 1)
                for m in range(2):
                    u = pair * 2 + m
                    pe.wait_ge(pt_ready, u + 1)
                    for t in range(TPB):
                        r = t * NT
                        last = nc.tensor.matmul(row_ps[m][:, t, 0:TW], pt[m][r:r + NT, :], w["L2f_table"][r:r + NT, :], start=True, stop=True)
                    last.then_inc(rows_up, 1)
                    nc.tensor.matmul(comp_ps[m][:, 0:2 * TPB], k.ones_row[0:1, 0:P], w["L2f_cb2"][:], start=True, stop=False, skip_group_check=True)
                for m in range(2):
                    u = pair * 2 + m
                    pe.wait_ge(hid_ready, u + 1)
                    for t in range(TPB):
                        last = nc.tensor.matmul(comp_ps[m][:, 2 * t:2 * t + 2], hid[m][:, t * P:(t + 1) * P], w["L2f_cw2"][:], start=False, stop=True,
                                                skip_group_check=True)
                    last.then_inc(comp_up, 1)

        @block.scalar
        def _(act):
            act.wait_ge(loaded, 16 * len(names))
            act.sem_inc(done, 2)
            with act.Fori(0, BATCH // 2) as pair:
                for m in range(2):
                    u = pair * 2 + m
                    act.wait_ge(done, u + 1)
                    nc.scalar.copy(picked[m][:].rearrange("p (t n) -> p t n", n=NT), k.PICK[:, bass.ds(u * TPB, TPB), :]).then_inc(picked_ready, 1)
                for m in range(2):
                    u = pair * 2 + m
                    act.wait_ge(turned, u + 1)
                    nc.scalar.copy(pt[m][:], pt_ps[m][:, 0:P]).then_inc(pt_ready, 1)
                for m in range(2):
                    u = pair * 2 + m
                    act.wait_ge(hid_up, u + 1)
                    nc.scalar.activation(hid[m][:], hid_ps[m][:, 0:SEQ], ACT.Gelu, bias=w["L2f_cb1"][:]).then_inc(hid_ready, 1)
                for m in range(2):
                    u = pair * 2 + m
                    act.wait_ge(comp_up, u + 1)
                    nc.scalar.activation(comp[m][:], comp_ps[m][:, 0:2 * TPB].rearrange("p (t n) -> p t n", n=2), ACT.Tanh).then_inc(comp_ready, 1)

        @block.gpsimd
        def _(pool):
            nc.gpsimd.memset(minus[:], -0.5)
            pool.drain()
            with pool.Fori(0, BATCH // 2) as pair:
                for m in range(2):
                    u = pair * 2 + m
                    pool.wait_ge(var_ready, u + 1)
                    nc.gpsimd.tensor_tensor(rstd[m][:], rstd[m][:], minus[:], ALU.pow).then_inc(rstd_ready, 1)

        @block.vector
        def _(dve):
            def over_tiles(ap):
                return ap[:].rearrange("p (a n) -> p a n", a=1).to_broadcast([P, TPB, D])

            dve.wait_ge(loaded, 16 * len(names))
            with dve.Fori(0, BATCH // 2) as pair:
                for m in range(2):
                    u = pair * 2 + m
                    dve.wait_ge(rows_up, u + 1)
                    dve.wait_ge(comp_ready, u + 1)
                    for j, out in enumerate((sp1[m], sp2[m])):
                        nc.vector.tensor_tensor(out[:], row_ps[m][:, :, W1 + j * G2:W1 + (j + 1) * G2], comp[m][:, :, j:j + 1].to_broadcast([P, TPB, G2]), ALU.mult)
                    dve.drain()
                    nc.vector.tensor_tensor(sp1[m][:], sp1[m][:], sp2[m][:], ALU.add)
                    dve.drain()
                    nc.vector.tensor_tensor(sp1[m][:], sp1[m][:], row_ps[m][:, :, B1:B1 + G2], ALU.add)
                    dve.drain()
                    nc.vector.scalar_tensor_tensor(out=sp1[m][:], in0=sp1[m][:], scalar=0.0, in1=row_ps[m][:, :, W2:W2 + G2], op0=ALU.max, op1=ALU.mult)
                    dve.drain()
                    nc.vector.tensor_reduce(mag[m][:], sp1[m][:], AX.X, ALU.add)
                    dve.drain()
                    nc.vector.tensor_tensor(mag[m][:], mag[m][:], row_ps[m][:, :, B2], ALU.add)
                    dve.drain()
                    nc.vector.tensor_tensor(y[m][:], row_ps[m][:, :, DIR:DIR + D], per_row(mag[m][:], D), ALU.mult)
                    dve.drain()
                    nc.vector.scalar_tensor_tensor(out=y[m][:], in0=y[m][:], scalar=w["L2f_scale"][:], in1=k.XN[:, bass.ds(u * TPB, TPB), :],
                                                   op0=ALU.mult, op1=ALU.add)
                    dve.drain()
                    group_norm_rows(nc, dve, y[m], stats[m], mv[m])
                    nc.vector.tensor_scalar(rstd[m][:], mv[m][:, :, 1], 1e-5, None, ALU.add).then_inc(var_ready, 1)
                for m in range(2):
                    u = pair * 2 + m
                    dve.wait_ge(rstd_ready, u + 1)
                    for t in range(TPB):
                        nc.vector.tensor_scalar(y[m][:, t, :], y[m][:, t, :], mv[m][:, t, 0:1], rstd[m][:, t:t + 1], ALU.subtract, ALU.mult)
                    dve.drain()
                    nc.vector.tensor_tensor(y[m][:], y[m][:], over_tiles(w["L2f_gamma"]), ALU.mult)
                    dve.drain()
                    nc.vector.tensor_tensor(y[m][:], y[m][:], over_tiles(w["L2f_beta"]), ALU.add)
                    dve.drain()
                    x = k.X[:, bass.ds(u * TPB, TPB), :]
                    nc.vector.tensor_tensor(x, x, y[m][:], ALU.add).then_inc(done, 1)


def l1_attn_b(nc, k, name):
    H, HD, VD = 16, 4, 8
    FR, AR = H * HD, 96
    VC = 32
    LAMBDA_INIT = 0.8 - 0.6 * float(np.exp(-0.3 * 12))
    with Scope(nc, name) as s:
        names = [("L1b_wqk", [P, 2 * D]), ("L1b_wv", [P, D]), ("L1b_wo", [P, D]), ("L1b_bo", [1, TPB * D]), ("L1b_lam", [P, 4 * HD]),
                 ("L1b_sub", [P, VD]), ("c_head_rows", [AR, H])]
        w = {n: s.sb(n, shape) for n, shape in names}
        loaded = s.sem("loaded")
        layer_norm(nc, k, name + "_ln", loads=[(w[n][:], k.dram[n], loaded) for n, _ in names])
        lam, sub = s.sb("lam", [P, 2]), s.sb("sub", [P, D])
        prod = s.sb("prod", [P, 2, HD])
        xg = s.sb("xg", [P, SEQ])
        qt, kt = [s.sb(f"qt{i}", [AR, 2, SEQ]) for i in range(2)], s.sb("kt", [AR, 2, SEQ])
        q0 = s.sb("q0", [AR, 2, SEQ])
        masked = [s.sb(f"masked{i}", [AR, 2, H, SEQ]) for i in range(2)]
        spare = [k.XN[:, i * 8:(i + 1) * 8, :].rearrange("p t d -> p (t d)") for i in range(2)]
        vx = [spare[i].rearrange("p (t h d) -> p t h d", t=TPB, h=H) for i in range(2)]
        e = [k.PICK[:, i * 8:(i + 1) * 8, :].rearrange("p t n -> p (t n)").rearrange("p (t q) -> p t q", t=TPB) for i in range(3)]
        mixed = k.XN[:, 16:32, :].rearrange("p t d -> p (t d)").rearrange("p (i c q) -> p i c q", i=2, c=H // 4)
        top = s.sb("top", [P, 2, TPB, AR])
        rden, att = s.sb("rden", [P, 2, TPB * H]), s.sb("att", [P, 2, TPB * H, VD])
        o, sq, ms, minus = s.sb("o", [P, TPB * H, VD]), s.sb("sq", [P, TPB * H, VD]), s.sb("ms", [P, TPB * H]), s.sb("minus", [P, TPB * H])
        ot = s.sb("ot", [P, SEQ])
        misc = s.ps("misc", [P, 2, SEQ])
        misc2 = s.ps("misc2", [P, 2, SEQ])
        score_ps = [s.ps(f"score_ps{i}", [P, TPB, SEQ]) for i in range(2)]
        o_ps = s.ps("o_ps", [P, 2, H // 4, SEQ])
        o_flat = o_ps[:].rearrange("p i s q -> p (i s q)")
        max_banks = [b[:].rearrange("p t q -> p (t q)") for b in (*score_ps, misc)]
        NB = len(max_banks)
        sems = ("exped", "consts_ready", "xg_ready", "projected", "copied", "copied_k", "v_up", "v_ready", "masked_ready", "max_up", "max_ready",
                "top_ready", "turned", "turned_ready", "score_up", "e_ready", "o_up", "mixed_ready", "mixed_turned", "ms_ready", "rms_ready", "o_ready", "turned_o", "ot_ready",
                "y_ready", "done")
        (exped, consts_ready, xg_ready, projected, copied, copied_k, v_up, v_ready, masked_ready, max_up, max_ready, top_ready, turned, turned_ready,
         score_up, e_ready, o_up, mixed_ready, mixed_turned, ms_ready, rms_ready, o_ready, turned_o, ot_ready, y_ready, done) = (s.sem(n) for n in sems)
        block = s.block()
        MAXES, SCORES = 2 * TPB * H // 2, 2 * H

        @block.tensor
        def _(pe):
            pe.wait_ge(loaded, 16 * len(names))

            def project_qk(b):
                pe.wait_ge(xg_ready, b + 1)
                for j in range(2):
                    for i in range(2):
                        c = j * D + i * FR
                        last = nc.tensor.matmul((misc, misc2)[j][0:FR, i, :], w["L1b_wqk"][:, c:c + FR], xg[:], start=True, stop=True)
                last.then_inc(projected, 1)

            def project_v(b):
                pe.wait_ge(copied, b + 1)
                for t in range(TPB):
                    last = nc.tensor.matmul(misc[:, t, 0:D], xg[:, t * P:(t + 1) * P], w["L1b_wv"][:], start=True, stop=True)
                last.then_inc(v_up, 1)

            def turn_mixed(b):
                pe.wait_ge(mixed_ready, b * 2 + 2)
                for i in range(2):
                    for t in range(TPB):
                        for c in range(H // 4):
                            last = nc.tensor.transpose(o_flat[:, ((i * TPB + t) * 4 + c) * P:((i * TPB + t) * 4 + c + 1) * P],
                                                       mixed[:, i, c, t * P:(t + 1) * P], k.ident[:])
                last.then_inc(mixed_turned, 1)

            def turn_o(b):
                pe.wait_ge(o_ready, b + 1)
                for t in range(TPB):
                    last = nc.tensor.transpose(misc2[:, 0, t * P:(t + 1) * P], o[:, t * H:(t + 1) * H, :].rearrange("p h d -> p (h d)"), k.ident[:])
                last.then_inc(turned_o, 1)

            def project_o(b):
                pe.wait_ge(ot_ready, b + 1)
                nc.tensor.matmul(misc2[:, 1, :], k.ones_row[0:1, 0:P], w["L1b_bo"][:], start=True, stop=False, skip_group_check=True)
                for t in range(TPB):
                    last = nc.tensor.matmul(misc2[:, 1, t * D:(t + 1) * D], ot[:, t * P:(t + 1) * P], w["L1b_wo"][:], start=False, stop=True,
                                            skip_group_check=True)
                last.then_inc(y_ready, 1)

            def step(b, par, first, last_batch):
                pe.wait_ge(v_ready, b + 1)
                pe.wait_ge(masked_ready, b + 1)
                for n in range(MAXES):
                    i, t, h = n // (TPB * H // 2), n // (H // 2) % TPB, n % (H // 2) * 2
                    if n >= NB:
                        pe.wait_ge(max_ready, b * MAXES + (n - NB + 1))
                    nc.tensor.matmul(max_banks[n % NB], q0[:, i, t * P:(t + 1) * P],
                                     masked[par][:, i, h:h + 2, :].rearrange("p h q -> p (h q)"), start=True, stop=True).then_inc(max_up, 1)
                    if not first:
                        if n == 2:
                            turn_mixed(b - 1)
                        if n == 22:
                            turn_o(b - 1)
                        if n == 25:
                            project_o(b - 1)
                pe.wait_ge(top_ready, b + 1)
                for i in range(2):
                    for t in range(TPB):
                        last = nc.tensor.transpose(misc[0:AR, i, t * P:(t + 1) * P], top[:, i, t, :], k.ident[:])
                last.then_inc(turned, 1)
                pe.wait_ge(turned_ready, b + 1)

                def score(n):
                    i, h = divmod(n, H)
                    for t in range(TPB):
                        last = nc.tensor.matmul(score_ps[n % 2][:, t, :], masked[par][:, i, h, t * P:(t + 1) * P], qt[par][:, i, :], start=True, stop=True)
                    last.then_inc(score_up, 1)

                def mix(n):
                    i, h = divmod(n, H)
                    pe.wait_ge(e_ready, b * SCORES + (n + 1))
                    r = h % 4 * VC
                    for t in range(TPB):
                        last = nc.tensor.matmul(o_ps[r:r + VC, i, h // 4, :], vx[par][:, t, h, :], e[n % 3][:, t, :],
                                                start=(t == 0), stop=(t == TPB - 1))
                    return last

                score(0)
                for n in range(SCORES):
                    if n + 1 < SCORES:
                        score(n + 1)
                    last = mix(n)
                    if n % H == H - 1:
                        last.then_inc(o_up, 1)
                    if n == 2 and not last_batch:
                        if not first:
                            pe.wait_ge(done, b)
                        project_qk(b + 1)
                    if n == 9 and not last_batch:
                        project_v(b + 1)

            project_qk(0)
            project_v(0)
            over_pairs(pe, BATCH, step)
            turn_mixed(BATCH - 1)
            turn_o(BATCH - 1)
            project_o(BATCH - 1)

        @block.scalar
        def _(act):
            act.wait_ge(consts_ready, 1)
            nc.scalar.activation(lam[:], lam[:], ACT.Exp).then_inc(exped, 1)
            act.wait_ge(consts_ready, 2)

            def copy_x(b):
                nc.scalar.copy(xg[:], k.XNT[:, bass.ds(b * SEQ, SEQ)]).then_inc(xg_ready, 1)

            def keep_qk(b, par, part):
                if part == 0:
                    act.wait_ge(projected, b + 1)
                    nc.scalar.copy(kt[0:FR, :, :], misc2[0:FR, :, :]).then_inc(copied_k, 1)
                if part == 1:
                    nc.scalar.copy(q0[0:FR, :, :], misc[0:FR, :, :])
                if part == 2:
                    nc.scalar.copy(qt[par][0:FR, :, :], misc[0:FR, :, :]).then_inc(copied, 1)

            def keep_o(b):
                act.wait_ge(turned_o, b + 1)
                nc.scalar.copy(ot[:], misc2[:, 0, :]).then_inc(ot_ready, 1)

            def step(b, par, first, last_batch):
                if not first:
                    keep_o(b - 1)
                act.wait_ge(turned, b + 1)
                nc.scalar.copy(qt[par][FR:AR, :, :], misc[FR:AR, :, :]).then_inc(turned_ready, 1)
                for n in range(SCORES):
                    act.wait_ge(score_up, b * SCORES + (n + 1))
                    nc.scalar.activation(e[n % 3], score_ps[n % 2][:], ACT.Exp, scale=HD ** -0.5).then_inc(e_ready, 1)
                    if n == H:
                        act.wait_ge(o_up, b * 2 + 1)
                        nc.scalar.copy(mixed[:, 0, :, :], o_ps[:, 0, :, :]).then_inc(mixed_ready, 1)
                    if not last_batch:
                        if n == 0:
                            copy_x(b + 1)
                        if n in (4, 5, 6):
                            keep_qk(b + 1, 1 - par, n - 4)
                act.wait_ge(o_up, b * 2 + 2)
                nc.scalar.copy(mixed[:, 1, :, :], o_ps[:, 1, :, :]).then_inc(mixed_ready, 1)

            copy_x(0)
            for part in range(3):
                keep_qk(0, 0, part)
            over_pairs(act, BATCH, step)
            keep_o(BATCH - 1)

        @block.gpsimd
        def _(pool):
            nc.gpsimd.memset(minus[:], -0.5)
            pool.drain()
            with pool.Fori(0, BATCH) as b:
                pool.wait_ge(ms_ready, b + 1)
                nc.gpsimd.tensor_tensor(ms[:], ms[:], minus[:], ALU.pow).then_inc(rms_ready, 1)

        @block.vector
        def _(dve):
            dve.wait_ge(loaded, 16 * len(names))
            nc.vector.tensor_tensor(prod[:], w["L1b_lam"][:, 0:2 * HD].rearrange("p (i d) -> p i d", i=2),
                                    w["L1b_lam"][:, 2 * HD:4 * HD].rearrange("p (i d) -> p i d", i=2), ALU.mult)
            nc.vector.memset(kt[FR:AR, :, :], 1.0)
            nc.vector.memset(q0[FR:AR, :, :], 0.0)
            nc.vector.memset(top[:], 0.0)
            for buf in vx:
                nc.vector.memset(buf, 0.0)
            dve.drain()
            for buf in vx:
                nc.vector.memset(buf[:, :, :, VD:VD + 1], 1.0)
            nc.vector.tensor_scalar(sub[:].rearrange("p (h d) -> p h d", h=H),
                                    w["L1b_sub"][:].rearrange("p (a d) -> p a d", a=1).to_broadcast([P, H, VD]),
                                    1.0 - LAMBDA_INIT, None, ALU.mult)
            dve.drain()
            nc.vector.tensor_reduce(lam[:], prod[:], AX.X, ALU.add).then_inc(consts_ready, 1)
            dve.wait_ge(exped, 1)
            nc.vector.tensor_tensor(lam[:, 0:1], lam[:, 1:2], lam[:, 0:1], ALU.subtract)
            dve.drain()
            nc.vector.tensor_scalar(lam[:, 0:1], lam[:, 0:1], -LAMBDA_INIT, None, ALU.add).then_inc(consts_ready, 1)
            dve.drain()

            def mask_keys(b, par):
                dve.wait_ge(copied_k, b + 1)
                for i in range(2):
                    last = nc.vector.tensor_tensor(masked[par][:, i, :, :], kt[:, i, :].rearrange("p (a q) -> p a q", a=1).to_broadcast([AR, H, SEQ]),
                                                   w["c_head_rows"][:].rearrange("p (h a) -> p h a", a=1).to_broadcast([AR, H, SEQ]), ALU.mult)
                last.then_inc(masked_ready, 1)

            def keep_v(b, par):
                dve.wait_ge(v_up, b + 1)
                nc.vector.tensor_copy(vx[par][:, :, :, 0:VD], misc[:, :, 0:D].rearrange("p t (h d) -> p t h d", d=VD)).then_inc(v_ready, 1)

            def finish(b, part):
                heads = o_flat.rearrange("p (n c) -> p n c", c=VC)
                dve.drain()
                if part == 0:
                    dve.wait_ge(mixed_turned, b + 1)
                    nc.vector.reciprocal(rden[:].rearrange("p i n -> p (i n)"), heads[:, :, VD])
                if part == 1:
                    nc.vector.tensor_tensor(att[:].rearrange("p i n d -> p (i n) d"), heads[:, :, 0:VD],
                                            per_row(rden[:].rearrange("p i n -> p (i n)"), VD), ALU.mult)
                if part == 2:
                    nc.vector.scalar_tensor_tensor(out=o[:], in0=att[:, 1, :, :], scalar=lam[:, 0:1], in1=att[:, 0, :, :], op0=ALU.mult, op1=ALU.add)
                if part == 3:
                    nc.vector.tensor_tensor(sq[:], o[:], o[:], ALU.mult)
                if part == 4:
                    nc.vector.tensor_reduce(ms[:], sq[:], AX.X, ALU.add)
                if part == 5:
                    nc.vector.tensor_scalar(ms[:], ms[:], 1.0 / VD, 1e-5, ALU.mult, ALU.add).then_inc(ms_ready, 1)
                if part == 6:
                    dve.wait_ge(rms_ready, b + 1)
                    nc.vector.tensor_tensor(o[:], o[:], per_row(ms[:], VD), ALU.mult)
                if part == 7:
                    by_tile = o[:].rearrange("p (t h) d -> p t (h d)", t=TPB)
                    nc.vector.tensor_tensor(by_tile, by_tile, sub[:].rearrange("p (a n) -> p a n", a=1).to_broadcast([P, TPB, D]), ALU.mult).then_inc(o_ready, 1)

            def add_out(b):
                dve.wait_ge(y_ready, b + 1)
                x = k.X[:, bass.ds(b * TPB, TPB), :]
                nc.vector.tensor_tensor(x, x, misc2[:, 1, :].rearrange("p (t d) -> p t d", d=D), ALU.add).then_inc(done, 1)

            def step(b, par, first, last_batch):
                for n in range(MAXES):
                    i, t, h = n // (TPB * H // 2), n // (H // 2) % TPB, n % (H // 2) * 2
                    dve.wait_ge(max_up, b * MAXES + (n + 1))
                    nc.vector.tensor_reduce(top[:, i, t, FR + h:FR + h + 2], max_banks[n % NB].rearrange("p (h q) -> p h q", h=2), AX.X, ALU.max).then_inc(max_ready, 1)
                    if not first:
                        if 5 <= n <= 10:
                            finish(b - 1, n - 5)
                        if 18 <= n <= 19:
                            finish(b - 1, n - 12)
                        if n == 29:
                            add_out(b - 1)
                dve.drain()
                tops = top[:].rearrange("p i t n -> p (i t) n")[:, :, FR:FR + H]
                nc.vector.tensor_scalar(tops, tops, -1.0, None, ALU.mult).then_inc(top_ready, 1)
                if not last_batch:
                    mask_keys(b + 1, 1 - par)
                    keep_v(b + 1, 1 - par)

            mask_keys(0, 0)
            keep_v(0, 0)
            over_pairs(dve, BATCH, step)
            for part in range(8):
                finish(BATCH - 1, part)
            add_out(BATCH - 1)


def rows128(a):
    n, m = a.shape[0] // P, a.shape[1]
    return a.reshape(n, P, m).transpose(1, 0, 2).reshape(P, n * m)


def layouts(inp):
    a = {n: np.asarray(v) for n, v in inp.items()}
    o = {"x": a["L0_attn_a_x"].reshape(TILES, P, D).transpose(1, 0, 2), "c_ident": np.eye(P, dtype=np.float32)}
    o["L0_ffn_router"] = a["L0_ffn_router_w"].T
    o["L0_ffn_w1"] = a["L0_ffn_w1"].transpose(2, 0, 1).reshape(D, -1)
    o["L0_ffn_w2"] = rows128(a["L0_ffn_w2"].transpose(0, 2, 1).reshape(-1, D))
    o["L3_ffn_router"] = a["L3_ffn_router_w"].T
    o["L3_ffn_rb"] = np.broadcast_to(a["L3_ffn_router_b"], (P, 8))
    o["L3_ffn_w1"] = a["L3_ffn_w1"].transpose(2, 0, 1).reshape(D, -1)
    o["L3_ffn_b1"] = a["L3_ffn_b1"].reshape(8 * 8, P).T
    o["L3_ffn_w2"] = rows128(a["L3_ffn_w2"].transpose(0, 2, 1).reshape(-1, D))
    o["L3_ffn_b2"] = np.tile(a["L3_ffn_b2"], (P // 8, 1))
    o["c_own_tile"] = np.repeat(np.eye(P // 8, dtype=np.float32), 8, axis=0)
    o["L1_ffn_router"] = a["L1_ffn_Wg"]
    o["L1_ffn_w1"] = a["L1_ffn_W1"].transpose(1, 0, 2).reshape(D, -1)
    o["L1_ffn_w2"] = rows128(a["L1_ffn_W2"].reshape(-1, D))
    o["c_before"] = np.triu(np.ones((P, P), np.float32), 1)
    o["c_not_first_tile"] = np.broadcast_to((np.arange(8 * TILES) % TILES > 0).astype(np.float32), (P, 8 * TILES))
    o["c_early_first"] = np.broadcast_to(np.repeat(8 - np.arange(8, dtype=np.float32), TILES), (P, 8 * TILES))
    row = lambda v: np.tile(v, TPB).reshape(1, SEQ)
    spread = lambda v: np.broadcast_to(v, (P, v.shape[0]))
    col = lambda v: v.reshape(-1, P).T
    o["L0a_wqkv"] = np.concatenate([a["L0_attn_a_W" + n].T for n in "qkv"], axis=1)
    o["L0a_bqkv"] = spread(np.concatenate([a["L0_attn_a_b" + n] for n in "qkv"]))
    o["L0a_w1"], o["L0a_b1"] = a["L0_attn_a_W1"].T, col(a["L0_attn_a_b1"])
    o["L0a_w2"], o["L0a_b2"] = a["L0_attn_a_W2"].T, col(a["L0_attn_a_b2"])
    o["L0a_w3"], o["L0a_b3"] = rows128(a["L0_attn_a_W3"].T), row(a["L0_attn_a_b3"])
    o["L0b_w"] = np.concatenate([a["L0_attn_b_Wq"].T] + [a["L0_attn_b_W" + n][i].T for n in "kv" for i in range(2)], axis=1)
    o["L0b_b"] = spread(np.concatenate([a["L0_attn_b_bq"]] + [a["L0_attn_b_b" + n][i] for n in "kv" for i in range(2)]))
    o["L0b_wo"], o["L0b_bo"] = a["L0_attn_b_Wo"].T, row(a["L0_attn_b_bo"])
    o["L0b_g"], o["L0b_be"] = col(a["L0_attn_b_ln_g"]), col(a["L0_attn_b_ln_b"])
    o["L3b_w"] = np.concatenate([a["L3_attn_b_W" + n] for n in "qkv"], axis=1)
    o["L3b_b"] = spread(np.concatenate([a["L3_attn_b_b" + n] for n in "qkv"]))
    o["L3b_wo"], o["L3b_bo"] = a["L3_attn_b_Wo"], row(a["L3_attn_b_bo"])
    o["L3b_g1"], o["L3b_be1"] = col(a["L3_attn_b_g1"]), col(a["L3_attn_b_be1"])
    o["L3b_g2"], o["L3b_be2"] = spread(a["L3_attn_b_g2"]), spread(a["L3_attn_b_be2"])
    o["L3b_w1"], o["L3b_b1"] = a["L3_attn_b_W1"], col(a["L3_attn_b_b1"])
    o["L3b_w2"], o["L3b_b2"] = rows128(a["L3_attn_b_W2"]), row(a["L3_attn_b_b2"])
    o["L3a_wq"], o["L3a_wk"] = a["L3_attn_a_q_w"].T, np.tile(a["L3_attn_a_kv_w"][0:8].T, (1, 16))
    o["L3a_wv"] = np.tile(a["L3_attn_a_kv_w"][8:16].T, (1, 4))
    o["L3a_wo"], o["L3a_bo"] = a["L3_attn_a_proj_w"].T, row(a["L3_attn_a_proj_b"])
    o["c_head_of_row8"] = np.repeat(np.eye(16, dtype=np.float32), 8, axis=0)
    o["c_blocks32x8"] = np.kron(np.eye(4, dtype=np.float32), np.ones((32, 8), np.float32))
    o["c_pick"] = np.tile(np.eye(32, dtype=np.float32), (3, 1))
    o["L1a_win"] = a["L1_attn_a_in_proj_w"].T
    o["L1a_conv"] = a["L1_attn_a_conv_w"].reshape(2, P, 4).transpose(1, 0, 2).reshape(P, 8)
    o["L1a_wx"] = rows128(a["L1_attn_a_x_proj_w"].T)
    o["L1a_wdt"], o["L1a_bdt"] = a["L1_attn_a_dt_proj_w"].T, col(a["L1_attn_a_dt_proj_b"])
    o["L1a_alog"], o["L1a_d"] = rows128(a["L1_attn_a_A_log"]), col(a["L1_attn_a_D"])
    o["L1a_wout"] = rows128(a["L1_attn_a_out_proj_w"].T)
    even_odd = np.r_[0:16:2, 1:16:2]
    wx = np.zeros((65, 256), np.float32)
    wx[0:32], wx[32], wx[64] = a["L2_attn_a_W_x"][np.r_[even_odd, 16 + even_odd]], a["L2_attn_a_W_x"][32], a["L2_attn_a_W_x"][33]
    both = lambda n: np.concatenate([a[f"L2_attn_a_{c}_{n}"][even_odd] for c in "BC"]).reshape(32, 1)
    o["L2a_win"], o["L2a_wx"], o["L2a_wdt"] = a["L2_attn_a_W_in"].T, rows128(wx.T), a["L2_attn_a_W_dt"].T
    o["L2a_bdt"], o["L2a_d"] = col(a["L2_attn_a_b_dt"]), col(a["L2_attn_a_D"])
    o["L2a_alog"], o["L2a_wout"] = rows128(a["L2_attn_a_A_log"][:, even_odd]), rows128(a["L2_attn_a_W_out"].T)
    o["L2a_bias"], o["L2a_norm"] = both("bias"), both("norm_w")
    o["L2a_freq"] = np.tile(a["L2_attn_a_rope_freqs"], 4).reshape(32, 1)
    o["c_mean16"] = np.tile(np.kron(np.eye(2, dtype=np.float32), np.ones((16, 16), np.float32) / 16), (1, 4))
    quarter = np.kron(np.array([[0, 1], [-1, 0]], np.float32), np.eye(8, dtype=np.float32))
    o["c_quarter_turn"] = np.kron(np.eye(2, dtype=np.float32), quarter)
    o["c_not_first"] = np.broadcast_to((np.arange(GROUP) % SEQ > 0).astype(np.float32), (32, GROUP))
    swapped = np.arange(64) ^ 1
    heads = lambda v: v.reshape(D, 8, D)
    for n in "QK":
        o[f"L2b_w{n}"] = a[f"L2_attn_b_W_{n}"]
        o[f"L2b_w{n}s"] = heads(a[f"L2_attn_b_W_{n}"])[:, :, swapped].reshape(D, 512)
    o["L2b_wV"] = a["L2_attn_b_W_V"]
    o["L2b_g"], o["L2b_be"] = spread(a["L2_attn_b_gn_weight"]), spread(a["L2_attn_b_gn_bias"])
    inv_freq = 1.0 / 10000.0 ** (np.arange(0, 64, 2, dtype=np.float32) / 64)
    ang = np.repeat(np.arange(SEQ, dtype=np.float32)[:, None] * inv_freq[None, :], 2, axis=-1).astype(np.float32).T
    sign = np.where(np.arange(64) % 2 == 0, -1, 1).astype(np.float32)[:, None]
    o["c_cos"], o["c_sin"] = np.tile(np.cos(ang), (1, BPG)), np.tile(np.sin(ang) * sign, (1, BPG))
    diff = np.arange(SEQ)[:, None] - np.arange(SEQ)[None, :]
    decay = np.where(diff >= 0, np.float32(0.96875) ** np.maximum(diff, 0).astype(np.float32), 0).astype(np.float32)
    o["c_decay"] = np.concatenate([decay[0:P, 0:P], decay[P:, :]], axis=1)
    o["L2f_sig"] = a["L2_ffn_signatures_raw"].T
    o["L2f_temp"], o["L2f_knots"] = spread(a["L2_ffn_temperature"]), spread(a["L2_ffn_knot_values"])
    o["L2f_scale"] = spread(a["L2_ffn_output_scale"])
    o["L2f_cw1"], o["L2f_cb1"] = a["L2_ffn_compress_w1"], a["L2_ffn_compress_b1"].reshape(32, 1)
    o["L2f_cw2"], o["L2f_cb2"] = a["L2_ffn_compress_w2"], np.tile(a["L2_ffn_compress_b2"], TPB).reshape(1, 2 * TPB)
    table = np.concatenate([a["L2_ffn_spline_w1"].reshape(64, 32), a["L2_ffn_spline_b1"], a["L2_ffn_spline_w2"].reshape(64, 16),
                            a["L2_ffn_spline_b2"], a["L2_ffn_directions"]], axis=1)
    o["L2f_table"] = np.tile(table, (2, 1))
    o["L2f_gamma"], o["L2f_beta"] = spread(a["L2_ffn_norm_gamma"]), spread(a["L2_ffn_norm_beta"])
    o["c_first8"] = spread(8 - np.arange(8, dtype=np.float32))
    o["c_first64"] = spread(64 - np.arange(64, dtype=np.float32))
    o["c_minus_knot"] = spread(-np.arange(8, dtype=np.float32))
    o["L1b_wqk"], o["L1b_wv"] = a["L1_attn_b_W_qkv"][:, 0:2 * D], a["L1_attn_b_W_qkv"][:, 2 * D:]
    o["L1b_wo"], o["L1b_bo"] = a["L1_attn_b_W_proj"], np.tile(a["L1_attn_b_b_proj"], TPB).reshape(1, TPB * D)
    o["L1b_lam"] = spread(np.concatenate([a["L1_attn_b_lambda_" + n] for n in ("q1", "q2", "k1", "k2")]))
    o["L1b_sub"] = spread(a["L1_attn_b_subln_w"])
    o["c_head_rows"] = np.concatenate([np.repeat(np.eye(16, dtype=np.float32), 4, axis=0), np.eye(16, dtype=np.float32), np.zeros((16, 16), np.float32)])
    o["c_heads8"] = np.kron(np.eye(16, dtype=np.float32), np.ones((8, 8), np.float32))
    return o


RESIDENT = [("L0_ffn_router", "l0_ffn"),
            ("L1_ffn_router", "l1_ffn"),
            ("L3_ffn_router", "l3_ffn"), ("L3_ffn_rb", "l3_ffn"), ("L3_ffn_b1", "l3_ffn"),
            ("L3_ffn_b2", "l3_ffn"), ("c_own_tile", "l3_ffn")]
STEPS = {f.__name__: f for f in (l0_ffn, l3_ffn, l1_ffn, l0_attn_a, l0_attn_b,
                                l3_attn_a, l3_attn_b, l1_attn_a, l2_attn_a,
                                l1_attn_b, l2_attn_b, l2_ffn)}
PLAN = ["l0_attn_a",
        "l0_ffn",
        "l0_attn_b",
        "l0_ffn",
        "l1_attn_a",
        "l1_ffn",
        "l1_attn_b",
        "l1_ffn",
        "l2_attn_a",
        "l2_ffn",
        "l2_attn_b",
        "l2_ffn",
        "l3_attn_a",
        "l3_ffn",
        "l3_attn_b",
        "l3_ffn"]


def build(nc, dram, out, plan):
    k = Core(nc, dram)
    with k.stack:
        k.X = k.keep("X", [P, TILES, D])
        k.XN = k.keep("XN", [P, TILES, D])
        k.XNT = k.keep("XNT", [P, TOKENS])
        k.LOG = k.keep("LOG", [P, TILES, 72])
        k.PICK = k.keep("PICK", [P, TILES, 64])
        k.SIG = k.keep("SIG", [P, 72])
        k.ones = k.keep("ones", [P, P])
        k.ones_row = k.keep("ones_row", [1, GROUP])
        k.GATE = k.keep("GATE", [P, TILES, 8])
        k.ident = k.keep("c_ident", [P, P])
        k.up = k.keep("up", [P, max(dram[f"L{i}_ffn_w1"].shape[1] for i in (0, 1, 3))])
        k.down = k.keep("down", [P, max(dram[f"L{i}_ffn_w2"].shape[1] for i in (0, 1, 3))])
        k.weights_landed = k.stack.enter_context(nc.semaphore("weights_landed"))
        weights = ["c_ident"]
        for name, needed_by in RESIDENT:
            if any(p.startswith(needed_by) for p in plan):
                k.keep(name, list(dram[name].shape))
                weights.append(name)
        load_all(nc, k, weights)
        experts = [p for p in plan if p in ("l0_ffn", "l1_ffn", "l3_ffn")]
        landed = None
        if experts:
            start_expert_load(nc, k, experts[0])
        for n, step in enumerate(plan):
            if step in experts and landed != step:
                finish_expert_load(nc, k)
                landed = step
            STEPS[step](nc, k, f"s{n}_{step}")
            later = [p for p in plan[n + 1:] if p in experts]
            if step in experts and later and later[0] != step:
                start_expert_load(nc, k, later[0])
        store(nc, k, out)


def kernel(**inputs):
    import concourse.bacc as bacc
    from concourse.bass_utils import run_bass_kernel_spmd

    nc = bacc.Bacc("TRN2", target_bir_lowering=False, num_devices=1)
    arrays = {n: np.ascontiguousarray(a) for n, a in layouts(inputs).items()}
    dram = {n: nc.dram_tensor(f"in_{n}", a.shape, mybir.dt.from_np(a.dtype), kind="ExternalInput").ap()
            for n, a in arrays.items()}
    out = nc.dram_tensor("out_x", (BATCH, SEQ, D), F32, kind="ExternalOutput").ap()
    build(nc, dram, out.rearrange("b (t p) d -> p (b t) d", p=P), PLAN)
    r = run_bass_kernel_spmd(nc, [{f"in_{n}": a for n, a in arrays.items()}], core_ids=[0])
    return r.results[0]["out_x"]
```
